# Optimizing a Trainium2 kernel written in Bass

```python
import numpy as np
import jax
import jax.numpy as jnp

def _softmax(x, axis=-1):
    return jax.nn.softmax(x, axis=axis)

def _gelu(x):
    return jax.nn.gelu(x, approximate=True)

def _silu(x):
    return jax.nn.silu(x)

def _sigmoid(x):
    return jax.nn.sigmoid(x)

def _layernorm(x, axis=-1, eps=1e-05):
    m = jnp.mean(x, axis=axis, keepdims=True)
    v = jnp.var(x, axis=axis, keepdims=True)
    return (x - m) / jnp.sqrt(v + eps)

def _scatter_add(tgt, idx, src, axis=0):
    return tgt.at[idx].add(src)

def _segment_sum(src, seg, n):
    return jax.ops.segment_sum(src, seg, n)
kernel_name = 'mk_recurrent_d4_jaxref_r8_eb8825'

def setup_inputs(seed: int=0):
    np.random.seed(seed)
    _w = jnp.asarray

    def _L0_attn_setup():
        import jax, jax.numpy as jnp
        import numpy as np
        D_MODEL = 128
        N_HEADS = 16
        LATENT_HEADS = 8
        LATENT_DIM = 64
        N_LATENTS = 64
        WINDOW = 32
        HEAD_DIM = D_MODEL // N_HEADS
        LAT_HD = LATENT_DIM // LATENT_HEADS
        B, S = (2, 512)

        def _pool_to_latents(x):
            Bx, Sx, C = x.shape
            chunk = max(1, Sx // N_LATENTS)
            return x.reshape(Bx, N_LATENTS, chunk, C).mean(axis=2)

        def _local_window_attn(Q, K, V):
            Bx, H, Sx, D = Q.shape
            W = WINDOW
            nb = Sx // W
            Qb = Q.reshape(Bx, H, nb, W, D)
            Kp = jnp.pad(K, ((0, 0), (0, 0), (W, 0), (0, 0))).reshape(Bx, H, nb + 1, W, D)
            Vp = jnp.pad(V, ((0, 0), (0, 0), (W, 0), (0, 0))).reshape(Bx, H, nb + 1, W, D)
            Kw = jnp.concatenate([Kp[:, :, :-1], Kp[:, :, 1:]], axis=3)
            Vw = jnp.concatenate([Vp[:, :, :-1], Vp[:, :, 1:]], axis=3)
            i = jnp.arange(W)[:, None]
            j = jnp.arange(2 * W)[None, :]
            base = (j > i) & (j <= i + W)
            blk0 = (jnp.arange(nb) > 0)[:, None, None] | (j >= W)[None, :, :]
            mask = base[None, :, :] & blk0
            sc = jnp.einsum('bhnid,bhnjd->bhnij', Qb, Kw) / np.sqrt(D).astype(np.float32)
            sc = jnp.where(mask[None, None], sc, -jnp.inf)
            p = jax.nn.softmax(sc, axis=-1)
            out = jnp.einsum('bhnij,bhnjd->bhnid', p, Vw)
            return out.reshape(Bx, H, Sx, D)
        key = jax.random.key(seed)
        ks = jax.random.split(key, 11)
        std = 0.02
        w = lambda k, shp: jax.random.normal(k, shp, jnp.float32) * std
        return {'x': jax.random.normal(ks[0], (B, S, D_MODEL), jnp.float32), 'wq': w(ks[1], (D_MODEL, D_MODEL)), 'wk': w(ks[2], (D_MODEL, D_MODEL)), 'wv': w(ks[3], (D_MODEL, D_MODEL)), 'wgq': w(ks[4], (D_MODEL, LATENT_DIM)), 'wgk': w(ks[5], (D_MODEL, LATENT_DIM)), 'wgv': w(ks[6], (D_MODEL, LATENT_DIM)), 'r_out_w': w(ks[7], (LATENT_DIM, D_MODEL)), 'gate_local_w': w(ks[8], (N_HEADS, HEAD_DIM)), 'gate_remote_w': w(ks[9], (N_HEADS, HEAD_DIM)), 'w_out': w(ks[10], (D_MODEL, D_MODEL))}
    _L0_attn_in = _L0_attn_setup()

    def _L0_ffn_setup():
        import jax, jax.numpy as jnp
        import numpy as np
        BLOCK = 16
        _GRID = jnp.array([0.0, 0.5, 1.0, 1.5, 2.0, 3.0, 4.0, 6.0], dtype=jnp.float32)
        _MID = jnp.array([0.25, 0.75, 1.25, 1.75, 2.5, 3.5, 5.0], dtype=jnp.float32)

        def fp4_quant_dequant(x):
            shape = x.shape
            xb = x.reshape(shape[:-1] + (shape[-1] // BLOCK, BLOCK))
            scale = jnp.max(jnp.abs(xb), axis=-1, keepdims=True) / 6.0
            scale = jnp.maximum(scale, jnp.float32(1e-12))
            xn = xb / scale
            idx = jnp.searchsorted(_MID, jnp.abs(xn))
            q = _GRID[idx] * jnp.sign(xn) * scale
            return q.reshape(shape)

        def fp4_linear(x, w):
            xq = fp4_quant_dequant(x)
            wq = fp4_quant_dequant(w)
            return jnp.einsum('bsk,nk->bsn', xq, wq)
        key = jax.random.key(seed)
        k1, k2, k3, k4 = jax.random.split(key, 4)
        H, I = (128, 352)
        x = jax.random.normal(k1, (4, 512, H), dtype=jnp.float32)
        w_gate = jax.random.normal(k2, (I, H), dtype=jnp.float32) * 0.02
        w_up = jax.random.normal(k3, (I, H), dtype=jnp.float32) * 0.02
        w_down = jax.random.normal(k4, (H, I), dtype=jnp.float32) * 0.02
        return {'x': x, 'w_gate': w_gate, 'w_up': w_up, 'w_down': w_down}
    _L0_ffn_in = _L0_ffn_setup()

    def _L1_attn_setup():
        import jax, jax.numpy as jnp
        import numpy as np
        EMB, HEADS, HIDDEN = (128, 16, 64)
        BS, N = (2, 256)
        key = jax.random.key(seed)
        ks = jax.random.split(key, 7)
        s_in = 1.0 / np.sqrt(EMB)
        s_u = 1.0 / np.sqrt(HEADS * HIDDEN)
        return {'x': jax.random.normal(ks[0], (BS, N, EMB), dtype=jnp.float32), 'w_q': jax.random.uniform(ks[1], (EMB, HEADS * HIDDEN), jnp.float32, -s_in, s_in), 'w_k': jax.random.uniform(ks[2], (EMB, HEADS * HIDDEN), jnp.float32, -s_in, s_in), 'w_v': jax.random.uniform(ks[3], (EMB, HEADS * HIDDEN), jnp.float32, -s_in, s_in), 'w_u': jax.random.uniform(ks[4], (HEADS * HIDDEN, EMB), jnp.float32, -s_u, s_u), 'b_u': jax.random.uniform(ks[5], (EMB,), jnp.float32, -s_u, s_u)}
    _L1_attn_in = _L1_attn_setup()

    def _L1_ffn_setup():
        import jax, jax.numpy as jnp
        import numpy as np
        D_IN, D_HID = (128, 512)

        def _ternary(key, shape):
            return jax.random.randint(key, shape, -1, 2).astype(jnp.float32)

        def _tlin(x, w, s):
            return jnp.einsum('bsi,oi->bso', x, w) * s
        key = jax.random.key(seed)
        ks = jax.random.split(key, 12)
        inv = lambda fan: 1.0 / np.sqrt(fan).astype(np.float32)
        return {'x': jax.random.normal(ks[0], (4, 256, D_IN), dtype=jnp.float32), 'w1_w': _ternary(ks[1], (D_HID, D_IN)), 'w1_s': jax.random.uniform(ks[2], (D_HID,), dtype=jnp.float32) * inv(D_IN), 'w2_w': _ternary(ks[3], (D_HID, D_IN)), 'w2_s': jax.random.uniform(ks[4], (D_HID,), dtype=jnp.float32) * inv(D_IN), 'h1_w': _ternary(ks[5], (D_HID, D_HID)), 'h1_s': jax.random.uniform(ks[6], (D_HID,), dtype=jnp.float32) * inv(D_HID), 'h2_w': _ternary(ks[7], (D_HID, D_HID)), 'h2_s': jax.random.uniform(ks[8], (D_HID,), dtype=jnp.float32) * inv(D_HID), 'w3_w': _ternary(ks[9], (D_IN, D_HID)), 'w3_s': jax.random.uniform(ks[10], (D_IN,), dtype=jnp.float32) * inv(D_HID)}
    _L1_ffn_in = _L1_ffn_setup()

    def _L2_attn_setup():
        import jax, jax.numpy as jnp
        import numpy as np
        import math
        B, S, H = (4, 128, 128)
        NQ, NKV = (16, 8)
        HD = H // NQ
        G = HD * NKV
        DEPTH = 1
        LAMBDA_INIT = 0.8 - 0.6 * math.exp(-0.3 * DEPTH)
        key = jax.random.key(seed)
        ks = jax.random.split(key, 7)
        x = jax.random.normal(ks[0], (B, S, H), jnp.float32)
        Wqkv = jax.random.normal(ks[1], (H, 2 * H + 2 * G), jnp.float32) / math.sqrt(H)
        Wproj = jax.random.normal(ks[2], (H, H), jnp.float32) / math.sqrt(H)
        lambda_q1 = 0.1 * jax.random.normal(ks[3], (G,), jnp.float32)
        lambda_k1 = 0.1 * jax.random.normal(ks[4], (G,), jnp.float32)
        lambda_q2 = 0.1 * jax.random.normal(ks[5], (G,), jnp.float32)
        lambda_k2 = 0.1 * jax.random.normal(ks[6], (G,), jnp.float32)
        return {'x': x, 'Wqkv': Wqkv, 'Wproj': Wproj, 'lambda_q1': lambda_q1, 'lambda_k1': lambda_k1, 'lambda_q2': lambda_q2, 'lambda_k2': lambda_k2}
    _L2_attn_in = _L2_attn_setup()

    def _L2_ffn_setup():
        import jax, jax.numpy as jnp
        import numpy as np
        DIM = 128
        DEPTH = 6
        HEADS = 16
        DIM_HEAD = 64
        WINDOW = 32
        INNER = HEADS * DIM_HEAD
        DIM_INNER = int(DIM * 4 * 2 / 3)
        QK_SCALE = 8.0

        def shift_tokens(t):
            a, s = jnp.split(t, 2, -1)
            s = jnp.pad(s, ((0, 0), (1, 0), (0, 0)))[:, :-1]
            return jnp.concatenate([a, s], -1)

        def l2norm(t):
            return t / jnp.maximum(jnp.linalg.norm(t, axis=-1, keepdims=True), 1e-12)

        def rotate_half(x):
            x1, x2 = jnp.split(x, 2, -1)
            return jnp.concatenate([-x2, x1], -1)

        def rotary_tables(n):
            half = jnp.arange(0, DIM_HEAD, 2, dtype=jnp.float32)
            inv_freq = 1.0 / 10000.0 ** (half / DIM_HEAD)
            t = jnp.arange(n, dtype=jnp.float32)
            freqs = t[:, None] * inv_freq[None, :]
            freqs = jnp.concatenate([freqs, freqs], -1)
            base_scale = (half + 0.4 * DIM_HEAD) / (1.4 * DIM_HEAD)
            power = (t - n // 2) / (WINDOW // 2)
            scale = base_scale[None, :] ** power[:, None]
            scale = jnp.concatenate([scale, scale], -1)
            return (freqs, scale)

        def local_attention(q, k, v):
            b, h, n, d = q.shape
            w = WINDOW
            nw = n // w
            bq = q.reshape(b, h, nw, w, d)
            bk = k.reshape(b, h, nw, w, d)
            bv = v.reshape(b, h, nw, w, d)

            def look(t):
                p = jnp.pad(t, ((0, 0), (0, 0), (1, 0), (0, 0), (0, 0)))
                return jnp.concatenate([p[:, :, :nw], p[:, :, 1:]], axis=3)
            bk2, bv2 = (look(bk), look(bv))
            seq = jnp.arange(n).reshape(nw, w)
            seq_p = jnp.pad(seq, ((1, 0), (0, 0)), constant_values=-1)
            jt = jnp.concatenate([seq_p[:nw], seq_p[1:]], axis=1)
            it = seq[:, :, None]
            jb = jt[:, None, :]
            mask = (it < jb) | (it > jb + w) | (jb == -1)
            sim = jnp.einsum('bhwie,bhwje->bhwij', bq, bk2) * QK_SCALE
            sim = jnp.where(mask, -jnp.finfo(sim.dtype).max, sim)
            attn = jax.nn.softmax(sim, -1)
            out = jnp.einsum('bhwij,bhwje->bhwie', attn, bv2)
            return out.reshape(b, h, n, d)

        def attn_layer(x, Wqkv, qs, ksc, Wo):
            b, n, _ = x.shape
            qkv = x @ Wqkv
            q, k, v = jnp.split(qkv, 3, -1)
            sh = lambda t: t.reshape(b, n, HEADS, DIM_HEAD).transpose(0, 2, 1, 3)
            q, k, v = (sh(q), sh(k), sh(v))
            q = l2norm(q) * qs
            k = l2norm(k) * ksc
            freqs, scale = rotary_tables(n)
            cos, sin = (jnp.cos(freqs), jnp.sin(freqs))
            q = q * cos * scale + rotate_half(q) * sin * scale
            inv = 1.0 / scale
            k = k * cos * inv + rotate_half(k) * sin * inv
            out = local_attention(q, k, v)
            out = out.transpose(0, 2, 1, 3).reshape(b, n, INNER)
            return out @ Wo

        def ffn_layer(x, g, bln, W1, b1, W2, b2):
            mu = x.mean(-1, keepdims=True)
            var = ((x - mu) ** 2).mean(-1, keepdims=True)
            xn = (x - mu) / jnp.sqrt(var + 1e-05) * g + bln
            hg = xn @ W1 + b1
            a, gate = jnp.split(hg, 2, -1)
            return a * jax.nn.gelu(gate, approximate=False) @ W2 + b2
        key = jax.random.key(seed)
        ks = jax.random.split(key, 8)
        B, N = (2, 256)
        init = lambda k, shape: jax.random.normal(k, shape, jnp.float32) * 0.02
        return {'x': jax.random.normal(ks[0], (B, N, DIM), jnp.float32), 'Wqkv': init(ks[1], (DEPTH, DIM, 3 * INNER)), 'q_scale': jnp.ones((DEPTH, DIM_HEAD), jnp.float32), 'k_scale': jnp.ones((DEPTH, DIM_HEAD), jnp.float32), 'Wo': init(ks[2], (DEPTH, INNER, DIM)), 'ln_g': jnp.ones((DEPTH, DIM), jnp.float32), 'ln_b': jnp.zeros((DEPTH, DIM), jnp.float32), 'W1': init(ks[3], (DEPTH, DIM, 2 * DIM_INNER)), 'b1': jnp.zeros((DEPTH, 2 * DIM_INNER), jnp.float32), 'W2': init(ks[4], (DEPTH, DIM_INNER, DIM)), 'b2': jnp.zeros((DEPTH, DIM), jnp.float32)}
    _L2_ffn_in = _L2_ffn_setup()

    def _L3_attn_setup():
        import jax, jax.numpy as jnp
        import numpy as np
        LN_EPS = 1e-05
        key = jax.random.key(seed)
        ks = jax.random.split(key, 7)
        B, L, D, N = (8, 256, 128, 16)
        x = jax.random.normal(ks[0], (B, L, D), jnp.float32)
        A = jax.random.normal(ks[1], (D, N, N), jnp.float32) * (0.2 / np.sqrt(N))
        Bp = jax.random.normal(ks[2], (D, N), jnp.float32)
        Cp = jax.random.normal(ks[3], (D, N), jnp.float32)
        Dp = jax.random.normal(ks[4], (D,), jnp.float32)
        Wg = jax.random.normal(ks[5], (D, D), jnp.float32) / np.sqrt(D)
        bg = jnp.zeros((D,), jnp.float32)
        gamma = jnp.ones((D,), jnp.float32)
        beta = jnp.zeros((D,), jnp.float32)
        return dict(x=x, A=A, Bp=Bp, Cp=Cp, Dp=Dp, Wg=Wg, bg=bg, gamma=gamma, beta=beta)
    _L3_attn_in = _L3_attn_setup()

    def _L3_ffn_setup():
        import jax, jax.numpy as jnp
        import numpy as np
        DIM = 128
        DEPTH = 2
        HEADS = 8
        DIM_HEAD = 64
        WINDOW = 64
        INNER = HEADS * DIM_HEAD
        HID = int(DIM * 4 * 2 / 3)
        B, N = (2, 1024)
        QK_SCALE = 8.0

        def shift_token(t):
            t1, t2 = jnp.split(t, 2, axis=-1)
            t2 = jnp.pad(t2, ((0, 0), (1, 0), (0, 0)))[:, :-1]
            return jnp.concatenate([t1, t2], axis=-1)

        def l2norm(t):
            return t / jnp.clip(jnp.linalg.norm(t, axis=-1, keepdims=True), 1e-12)

        def rotate_half(x):
            x1, x2 = jnp.split(x, 2, axis=-1)
            return jnp.concatenate([-x2, x1], axis=-1)

        def rotary_xpos(q, k):
            n = q.shape[-2]
            half_idx = jnp.arange(0, DIM_HEAD, 2, dtype=jnp.float32)
            inv_freq = 1.0 / 10000.0 ** (half_idx / DIM_HEAD)
            t = jnp.arange(n, dtype=jnp.float32)
            freqs = t[:, None] * inv_freq[None, :]
            freqs = jnp.concatenate([freqs, freqs], axis=-1)
            base = (half_idx + 0.4 * DIM_HEAD) / (1.4 * DIM_HEAD)
            power = (t - n // 2) / float(WINDOW // 2)
            scale = base[None, :] ** power[:, None]
            scale = jnp.concatenate([scale, scale], axis=-1)
            cos, sin = (jnp.cos(freqs), jnp.sin(freqs))
            q = q * cos * scale + rotate_half(q) * sin * scale
            k = k * cos / scale + rotate_half(k) * sin / scale
            return (q, k)

        def local_attention(q, k, v):
            b, h, n, d = q.shape
            w = n // WINDOW
            bq = q.reshape(b, h, w, WINDOW, d) * QK_SCALE
            bk = k.reshape(b, h, w, WINDOW, d)
            bv = v.reshape(b, h, w, WINDOW, d)

            def look_around(t):
                p = jnp.pad(t, ((0, 0), (0, 0), (1, 0), (0, 0), (0, 0)))
                return jnp.concatenate([p[:, :, :w], p[:, :, 1:]], axis=3)
            bk, bv = (look_around(bk), look_around(bv))
            bt = jnp.arange(n).reshape(w, WINDOW)
            btp = jnp.pad(bt, ((1, 0), (0, 0)), constant_values=-1)
            btk = jnp.concatenate([btp[:w], btp[1:]], axis=1)
            sim = jnp.einsum('bhwid,bhwjd->bhwij', bq, bk)
            i = bt[:, :, None]
            j = btk[:, None, :]
            mask = (i < j) | (i > j + WINDOW) | (j == -1)
            sim = jnp.where(mask, -jnp.finfo(sim.dtype).max, sim)
            attn = jax.nn.softmax(sim, axis=-1)
            out = jnp.einsum('bhwij,bhwjd->bhwid', attn, bv)
            return out.reshape(b, h, n, d)

        def _layer(x, wqkv, qs, ksc, wo, lg, lb, w1, b1, w2, b2):
            b, n, _ = x.shape
            h = shift_token(x)
            qkv = h @ wqkv
            q, k, v = jnp.split(qkv, 3, axis=-1)
            to_heads = lambda t: t.reshape(b, n, HEADS, DIM_HEAD).transpose(0, 2, 1, 3)
            q, k, v = (to_heads(q), to_heads(k), to_heads(v))
            q = l2norm(q) * qs
            k = l2norm(k) * ksc
            q, k = rotary_xpos(q, k)
            o = local_attention(q, k, v)
            o = o.transpose(0, 2, 1, 3).reshape(b, n, INNER)
            x = x + o @ wo
            h = shift_token(x)
            mu = h.mean(-1, keepdims=True)
            var = h.var(-1, keepdims=True)
            h = (h - mu) / jnp.sqrt(var + 1e-05) * lg + lb
            h = h @ w1 + b1
            a, g = jnp.split(h, 2, axis=-1)
            h = a * jax.nn.gelu(g, approximate=False)
            x = x + h @ w2 + b2
            return x
        key = jax.random.key(seed)
        ks = jax.random.split(key, 6)
        return {'x': jax.random.normal(ks[0], (B, N, DIM), jnp.float32), 'wqkv': jax.random.normal(ks[1], (DEPTH, DIM, 3 * INNER), jnp.float32) * 0.02, 'q_scale': jnp.ones((DEPTH, DIM_HEAD), jnp.float32), 'k_scale': jnp.ones((DEPTH, DIM_HEAD), jnp.float32), 'wo': jax.random.normal(ks[2], (DEPTH, INNER, DIM), jnp.float32) * 0.02, 'ln_g': jnp.ones((DEPTH, DIM), jnp.float32), 'ln_b': jnp.zeros((DEPTH, DIM), jnp.float32), 'w1': jax.random.normal(ks[3], (DEPTH, DIM, 2 * HID), jnp.float32) * 0.02, 'b1': jnp.zeros((DEPTH, 2 * HID), jnp.float32), 'w2': jax.random.normal(ks[4], (DEPTH, HID, DIM), jnp.float32) * 0.02, 'b2': jnp.zeros((DEPTH, DIM), jnp.float32)}
    _L3_ffn_in = _L3_ffn_setup()
    _d = {'L0_attn_x': _L0_attn_in['x'], 'L0_attn_wq': _L0_attn_in['wq'], 'L0_attn_wk': _L0_attn_in['wk'], 'L0_attn_wv': _L0_attn_in['wv'], 'L0_attn_wgq': _L0_attn_in['wgq'], 'L0_attn_wgk': _L0_attn_in['wgk'], 'L0_attn_wgv': _L0_attn_in['wgv'], 'L0_attn_r_out_w': _L0_attn_in['r_out_w'], 'L0_attn_gate_local_w': _L0_attn_in['gate_local_w'], 'L0_attn_gate_remote_w': _L0_attn_in['gate_remote_w'], 'L0_attn_w_out': _L0_attn_in['w_out'], 'L0_ffn_w_gate': _L0_ffn_in['w_gate'], 'L0_ffn_w_up': _L0_ffn_in['w_up'], 'L0_ffn_w_down': _L0_ffn_in['w_down'], 'L1_attn_w_q': _L1_attn_in['w_q'], 'L1_attn_w_k': _L1_attn_in['w_k'], 'L1_attn_w_v': _L1_attn_in['w_v'], 'L1_attn_w_u': _L1_attn_in['w_u'], 'L1_attn_b_u': _L1_attn_in['b_u'], 'L1_ffn_w1_w': _L1_ffn_in['w1_w'], 'L1_ffn_w1_s': _L1_ffn_in['w1_s'], 'L1_ffn_w2_w': _L1_ffn_in['w2_w'], 'L1_ffn_w2_s': _L1_ffn_in['w2_s'], 'L1_ffn_h1_w': _L1_ffn_in['h1_w'], 'L1_ffn_h1_s': _L1_ffn_in['h1_s'], 'L1_ffn_h2_w': _L1_ffn_in['h2_w'], 'L1_ffn_h2_s': _L1_ffn_in['h2_s'], 'L1_ffn_w3_w': _L1_ffn_in['w3_w'], 'L1_ffn_w3_s': _L1_ffn_in['w3_s'], 'L2_attn_Wqkv': _L2_attn_in['Wqkv'], 'L2_attn_Wproj': _L2_attn_in['Wproj'], 'L2_attn_lambda_q1': _L2_attn_in['lambda_q1'], 'L2_attn_lambda_k1': _L2_attn_in['lambda_k1'], 'L2_attn_lambda_q2': _L2_attn_in['lambda_q2'], 'L2_attn_lambda_k2': _L2_attn_in['lambda_k2'], 'L2_ffn_Wqkv': _L2_ffn_in['Wqkv'], 'L2_ffn_q_scale': _L2_ffn_in['q_scale'], 'L2_ffn_k_scale': _L2_ffn_in['k_scale'], 'L2_ffn_Wo': _L2_ffn_in['Wo'], 'L2_ffn_ln_g': _L2_ffn_in['ln_g'], 'L2_ffn_ln_b': _L2_ffn_in['ln_b'], 'L2_ffn_W1': _L2_ffn_in['W1'], 'L2_ffn_b1': _L2_ffn_in['b1'], 'L2_ffn_W2': _L2_ffn_in['W2'], 'L2_ffn_b2': _L2_ffn_in['b2'], 'L3_attn_A': _L3_attn_in['A'], 'L3_attn_Bp': _L3_attn_in['Bp'], 'L3_attn_Cp': _L3_attn_in['Cp'], 'L3_attn_Dp': _L3_attn_in['Dp'], 'L3_attn_Wg': _L3_attn_in['Wg'], 'L3_attn_bg': _L3_attn_in['bg'], 'L3_attn_gamma': _L3_attn_in['gamma'], 'L3_attn_beta': _L3_attn_in['beta'], 'L3_ffn_wqkv': _L3_ffn_in['wqkv'], 'L3_ffn_q_scale': _L3_ffn_in['q_scale'], 'L3_ffn_k_scale': _L3_ffn_in['k_scale'], 'L3_ffn_wo': _L3_ffn_in['wo'], 'L3_ffn_ln_g': _L3_ffn_in['ln_g'], 'L3_ffn_ln_b': _L3_ffn_in['ln_b'], 'L3_ffn_w1': _L3_ffn_in['w1'], 'L3_ffn_b1': _L3_ffn_in['b1'], 'L3_ffn_w2': _L3_ffn_in['w2'], 'L3_ffn_b2': _L3_ffn_in['b2']}
    _x0 = _d['L0_attn_x']
    _d['L0_attn_x'] = jax.random.normal(jax.random.fold_in(jax.random.key(seed), 1), (4, 512, 128), dtype=_x0.dtype)
    del _x0
    return _d

def reference(L0_attn_x, L0_attn_wq, L0_attn_wk, L0_attn_wv, L0_attn_wgq, L0_attn_wgk, L0_attn_wgv, L0_attn_r_out_w, L0_attn_gate_local_w, L0_attn_gate_remote_w, L0_attn_w_out, L0_ffn_w_gate, L0_ffn_w_up, L0_ffn_w_down, L1_attn_w_q, L1_attn_w_k, L1_attn_w_v, L1_attn_w_u, L1_attn_b_u, L1_ffn_w1_w, L1_ffn_w1_s, L1_ffn_w2_w, L1_ffn_w2_s, L1_ffn_h1_w, L1_ffn_h1_s, L1_ffn_h2_w, L1_ffn_h2_s, L1_ffn_w3_w, L1_ffn_w3_s, L2_attn_Wqkv, L2_attn_Wproj, L2_attn_lambda_q1, L2_attn_lambda_k1, L2_attn_lambda_q2, L2_attn_lambda_k2, L2_ffn_Wqkv, L2_ffn_q_scale, L2_ffn_k_scale, L2_ffn_Wo, L2_ffn_ln_g, L2_ffn_ln_b, L2_ffn_W1, L2_ffn_b1, L2_ffn_W2, L2_ffn_b2, L3_attn_A, L3_attn_Bp, L3_attn_Cp, L3_attn_Dp, L3_attn_Wg, L3_attn_bg, L3_attn_gamma, L3_attn_beta, L3_ffn_wqkv, L3_ffn_q_scale, L3_ffn_k_scale, L3_ffn_wo, L3_ffn_ln_g, L3_ffn_ln_b, L3_ffn_w1, L3_ffn_b1, L3_ffn_w2, L3_ffn_b2):

    def _L0_attn_ref(x, wq, wk, wv, wgq, wgk, wgv, r_out_w, gate_local_w, gate_remote_w, w_out):
        import jax, jax.numpy as jnp
        import numpy as np
        D_MODEL = 128
        N_HEADS = 16
        LATENT_HEADS = 8
        LATENT_DIM = 64
        N_LATENTS = 64
        WINDOW = 32
        HEAD_DIM = D_MODEL // N_HEADS
        LAT_HD = LATENT_DIM // LATENT_HEADS
        B, S = (2, 512)

        def _pool_to_latents(x):
            Bx, Sx, C = x.shape
            chunk = max(1, Sx // N_LATENTS)
            return x.reshape(Bx, N_LATENTS, chunk, C).mean(axis=2)

        def _local_window_attn(Q, K, V):
            Bx, H, Sx, D = Q.shape
            W = WINDOW
            nb = Sx // W
            Qb = Q.reshape(Bx, H, nb, W, D)
            Kp = jnp.pad(K, ((0, 0), (0, 0), (W, 0), (0, 0))).reshape(Bx, H, nb + 1, W, D)
            Vp = jnp.pad(V, ((0, 0), (0, 0), (W, 0), (0, 0))).reshape(Bx, H, nb + 1, W, D)
            Kw = jnp.concatenate([Kp[:, :, :-1], Kp[:, :, 1:]], axis=3)
            Vw = jnp.concatenate([Vp[:, :, :-1], Vp[:, :, 1:]], axis=3)
            i = jnp.arange(W)[:, None]
            j = jnp.arange(2 * W)[None, :]
            base = (j > i) & (j <= i + W)
            blk0 = (jnp.arange(nb) > 0)[:, None, None] | (j >= W)[None, :, :]
            mask = base[None, :, :] & blk0
            sc = jnp.einsum('bhnid,bhnjd->bhnij', Qb, Kw) / np.sqrt(D).astype(np.float32)
            sc = jnp.where(mask[None, None], sc, -jnp.inf)
            p = jax.nn.softmax(sc, axis=-1)
            out = jnp.einsum('bhnij,bhnjd->bhnid', p, Vw)
            return out.reshape(Bx, H, Sx, D)
        Bx, Sx, _ = x.shape
        chunk = max(1, Sx // N_LATENTS)
        Q = (x @ wq).reshape(Bx, Sx, N_HEADS, HEAD_DIM).transpose(0, 2, 1, 3)
        K = (x @ wk).reshape(Bx, Sx, N_HEADS, HEAD_DIM).transpose(0, 2, 1, 3)
        V = (x @ wv).reshape(Bx, Sx, N_HEADS, HEAD_DIM).transpose(0, 2, 1, 3)
        local = _local_window_attn(Q, K, V)
        GQ = (x @ wgq).reshape(Bx, Sx, LATENT_HEADS, LAT_HD).transpose(0, 2, 1, 3)
        GK = _pool_to_latents(x @ wgk).reshape(Bx, N_LATENTS, LATENT_HEADS, LAT_HD).transpose(0, 2, 1, 3)
        GV = _pool_to_latents(x @ wgv).reshape(Bx, N_LATENTS, LATENT_HEADS, LAT_HD).transpose(0, 2, 1, 3)
        lsc = jnp.einsum('bhsd,bhnd->bhsn', GQ, GK) / np.sqrt(LAT_HD).astype(np.float32)
        lmask = jnp.arange(N_LATENTS)[None, :] <= (jnp.arange(Sx) // chunk)[:, None]
        lsc = jnp.where(lmask[None, None], lsc, -jnp.inf)
        lp = jax.nn.softmax(lsc, axis=-1)
        rem = jnp.einsum('bhsn,bhnd->bhsd', lp, GV)
        rem = rem.transpose(0, 2, 1, 3).reshape(Bx, Sx, LATENT_DIM) @ r_out_w
        rem = rem.reshape(Bx, Sx, N_HEADS, HEAD_DIM).transpose(0, 2, 1, 3)
        gl = jax.nn.sigmoid(jnp.einsum('bhsd,hd->bhs', Q, gate_local_w))[..., None]
        gr = jax.nn.sigmoid(jnp.einsum('bhsd,hd->bhs', Q, gate_remote_w))[..., None]
        out = gl * local + gr * rem
        out = out.transpose(0, 2, 1, 3).reshape(Bx, Sx, D_MODEL)
        return out @ w_out

    def _L0_ffn_ref(x, w_gate, w_up, w_down):
        import jax, jax.numpy as jnp
        import numpy as np
        BLOCK = 16
        _GRID = jnp.array([0.0, 0.5, 1.0, 1.5, 2.0, 3.0, 4.0, 6.0], dtype=jnp.float32)
        _MID = jnp.array([0.25, 0.75, 1.25, 1.75, 2.5, 3.5, 5.0], dtype=jnp.float32)

        def fp4_quant_dequant(x):
            shape = x.shape
            xb = x.reshape(shape[:-1] + (shape[-1] // BLOCK, BLOCK))
            scale = jnp.max(jnp.abs(xb), axis=-1, keepdims=True) / 6.0
            scale = jnp.maximum(scale, jnp.float32(1e-12))
            xn = xb / scale
            idx = jnp.searchsorted(_MID, jnp.abs(xn))
            q = _GRID[idx] * jnp.sign(xn) * scale
            return q.reshape(shape)

        def fp4_linear(x, w):
            xq = fp4_quant_dequant(x)
            wq = fp4_quant_dequant(w)
            return jnp.einsum('bsk,nk->bsn', xq, wq)
        gate = fp4_linear(x, w_gate)
        y = fp4_linear(x, w_up)
        h = jax.nn.silu(gate) * y
        return fp4_linear(h, w_down)

    def _L1_attn_ref(x, w_q, w_k, w_v, w_u, b_u):
        import jax, jax.numpy as jnp
        import numpy as np
        EMB, HEADS, HIDDEN = (128, 16, 64)
        BS, N = (2, 256)
        bs, n, emb = x.shape
        h, hd = (HEADS, HIDDEN)
        q = (x @ w_q).reshape(bs, n, h, hd)
        k = (x @ w_k).reshape(bs, n, h, hd)
        v = (x @ w_v).reshape(bs, n, h, hd)
        scale = 1.0 / jnp.sqrt(jnp.asarray(hd, dtype=x.dtype))
        q = q * scale
        k = k * scale
        dot = jnp.einsum('bqhd,bkhd->bhqk', q, k)
        causal = jnp.tril(jnp.ones((n, n), dtype=bool))
        dot = jnp.where(causal, dot, jnp.asarray(-jnp.inf, dtype=dot.dtype))
        att = jax.nn.softmax(dot, axis=-1)
        out = jnp.einsum('bhqk,bkhd->bqhd', att, v).reshape(bs, n, h * hd)
        return out @ w_u + b_u

    def _L1_ffn_ref(x, w1_w, w1_s, w2_w, w2_s, h1_w, h1_s, h2_w, h2_s, w3_w, w3_s):
        import jax, jax.numpy as jnp
        import numpy as np
        D_IN, D_HID = (128, 512)

        def _ternary(key, shape):
            return jax.random.randint(key, shape, -1, 2).astype(jnp.float32)

        def _tlin(x, w, s):
            return jnp.einsum('bsi,oi->bso', x, w) * s
        h = jax.nn.silu(_tlin(x, w1_w, w1_s)) * _tlin(x, w2_w, w2_s)
        h = jax.nn.gelu(_tlin(h, h1_w, h1_s), approximate=False)
        h = jax.nn.gelu(_tlin(h, h2_w, h2_s), approximate=False)
        return _tlin(h, w3_w, w3_s)

    def _L2_attn_ref(x, Wqkv, Wproj, lambda_q1, lambda_k1, lambda_q2, lambda_k2):
        import jax, jax.numpy as jnp
        import numpy as np
        import math
        B, S, H = (4, 128, 128)
        NQ, NKV = (16, 8)
        HD = H // NQ
        G = HD * NKV
        DEPTH = 1
        LAMBDA_INIT = 0.8 - 0.6 * math.exp(-0.3 * DEPTH)
        Bx, Sx, Hx = x.shape
        qkv = x @ Wqkv
        q = qkv[..., :2 * Hx].reshape(Bx, 2 * NQ, Sx, HD)
        k = qkv[..., 2 * Hx:2 * Hx + G].reshape(Bx, NKV, Sx, HD)
        v = qkv[..., 2 * Hx + G:].reshape(Bx, NKV, Sx, HD)
        k = jnp.repeat(k, 2 * NQ // NKV, axis=1)
        v = jnp.repeat(v, NQ // NKV, axis=1)
        scores = jnp.einsum('bhqd,bhkd->bhqk', q, k) / math.sqrt(HD)
        causal = jnp.tril(jnp.ones((Sx, Sx), dtype=bool))
        scores = jnp.where(causal, scores, -jnp.inf)
        aw = jax.nn.softmax(scores, axis=-1)
        lam1 = jnp.exp(jnp.sum(lambda_q1 * lambda_k1))
        lam2 = jnp.exp(jnp.sum(lambda_q2 * lambda_k2))
        lam = lam1 - lam2 + LAMBDA_INIT
        aw = aw.reshape(Bx, NQ, 2, Sx, Sx)
        aw = aw[:, :, 0] - lam * aw[:, :, 1]
        attn = jnp.einsum('bhqk,bhkd->bhqd', aw, v) * (1.0 - LAMBDA_INIT)
        attn = jnp.transpose(attn, (0, 2, 1, 3)).reshape(Bx, Sx, Hx)
        y = attn @ Wproj
        y = jnp.transpose(y, (0, 2, 1)).reshape(Bx, Sx, Hx)
        return y @ Wproj

    def _L2_ffn_ref(x, Wqkv, q_scale, k_scale, Wo, ln_g, ln_b, W1, b1, W2, b2):
        import jax, jax.numpy as jnp
        import numpy as np
        DIM = 128
        DEPTH = 6
        HEADS = 16
        DIM_HEAD = 64
        WINDOW = 32
        INNER = HEADS * DIM_HEAD
        DIM_INNER = int(DIM * 4 * 2 / 3)
        QK_SCALE = 8.0

        def shift_tokens(t):
            a, s = jnp.split(t, 2, -1)
            s = jnp.pad(s, ((0, 0), (1, 0), (0, 0)))[:, :-1]
            return jnp.concatenate([a, s], -1)

        def l2norm(t):
            return t / jnp.maximum(jnp.linalg.norm(t, axis=-1, keepdims=True), 1e-12)

        def rotate_half(x):
            x1, x2 = jnp.split(x, 2, -1)
            return jnp.concatenate([-x2, x1], -1)

        def rotary_tables(n):
            half = jnp.arange(0, DIM_HEAD, 2, dtype=jnp.float32)
            inv_freq = 1.0 / 10000.0 ** (half / DIM_HEAD)
            t = jnp.arange(n, dtype=jnp.float32)
            freqs = t[:, None] * inv_freq[None, :]
            freqs = jnp.concatenate([freqs, freqs], -1)
            base_scale = (half + 0.4 * DIM_HEAD) / (1.4 * DIM_HEAD)
            power = (t - n // 2) / (WINDOW // 2)
            scale = base_scale[None, :] ** power[:, None]
            scale = jnp.concatenate([scale, scale], -1)
            return (freqs, scale)

        def local_attention(q, k, v):
            b, h, n, d = q.shape
            w = WINDOW
            nw = n // w
            bq = q.reshape(b, h, nw, w, d)
            bk = k.reshape(b, h, nw, w, d)
            bv = v.reshape(b, h, nw, w, d)

            def look(t):
                p = jnp.pad(t, ((0, 0), (0, 0), (1, 0), (0, 0), (0, 0)))
                return jnp.concatenate([p[:, :, :nw], p[:, :, 1:]], axis=3)
            bk2, bv2 = (look(bk), look(bv))
            seq = jnp.arange(n).reshape(nw, w)
            seq_p = jnp.pad(seq, ((1, 0), (0, 0)), constant_values=-1)
            jt = jnp.concatenate([seq_p[:nw], seq_p[1:]], axis=1)
            it = seq[:, :, None]
            jb = jt[:, None, :]
            mask = (it < jb) | (it > jb + w) | (jb == -1)
            sim = jnp.einsum('bhwie,bhwje->bhwij', bq, bk2) * QK_SCALE
            sim = jnp.where(mask, -jnp.finfo(sim.dtype).max, sim)
            attn = jax.nn.softmax(sim, -1)
            out = jnp.einsum('bhwij,bhwje->bhwie', attn, bv2)
            return out.reshape(b, h, n, d)

        def attn_layer(x, Wqkv, qs, ksc, Wo):
            b, n, _ = x.shape
            qkv = x @ Wqkv
            q, k, v = jnp.split(qkv, 3, -1)
            sh = lambda t: t.reshape(b, n, HEADS, DIM_HEAD).transpose(0, 2, 1, 3)
            q, k, v = (sh(q), sh(k), sh(v))
            q = l2norm(q) * qs
            k = l2norm(k) * ksc
            freqs, scale = rotary_tables(n)
            cos, sin = (jnp.cos(freqs), jnp.sin(freqs))
            q = q * cos * scale + rotate_half(q) * sin * scale
            inv = 1.0 / scale
            k = k * cos * inv + rotate_half(k) * sin * inv
            out = local_attention(q, k, v)
            out = out.transpose(0, 2, 1, 3).reshape(b, n, INNER)
            return out @ Wo

        def ffn_layer(x, g, bln, W1, b1, W2, b2):
            mu = x.mean(-1, keepdims=True)
            var = ((x - mu) ** 2).mean(-1, keepdims=True)
            xn = (x - mu) / jnp.sqrt(var + 1e-05) * g + bln
            hg = xn @ W1 + b1
            a, gate = jnp.split(hg, 2, -1)
            return a * jax.nn.gelu(gate, approximate=False) @ W2 + b2
        for i in range(DEPTH):
            x = attn_layer(shift_tokens(x), Wqkv[i], q_scale[i], k_scale[i], Wo[i]) + x
            x = ffn_layer(shift_tokens(x), ln_g[i], ln_b[i], W1[i], b1[i], W2[i], b2[i]) + x
        return x

    def _L3_attn_ref(x, A, Bp, Cp, Dp, Wg, bg, gamma, beta):
        import jax, jax.numpy as jnp
        import numpy as np
        LN_EPS = 1e-05
        gate = jax.nn.sigmoid(jnp.einsum('bld,ed->ble', x, Wg) + bg)
        xg = x * gate
        Bsz, L, D = xg.shape
        N = A.shape[-1]

        def step(s, xt):
            s = jnp.einsum('bdn,dnm->bdm', s, A) + xt[..., None] * Bp
            y = jnp.einsum('bdn,dn->bd', s, Cp) + Dp * xt
            return (s, y)
        s0 = jnp.zeros((Bsz, D, N), xg.dtype)
        _, ys = jax.lax.scan(step, s0, jnp.moveaxis(xg, 1, 0))
        y = jnp.moveaxis(ys, 0, 1) + xg
        mu = jnp.mean(y, axis=-1, keepdims=True)
        var = jnp.var(y, axis=-1, keepdims=True)
        return (y - mu) * jax.lax.rsqrt(var + LN_EPS) * gamma + beta

    def _L3_ffn_ref(x, wqkv, q_scale, k_scale, wo, ln_g, ln_b, w1, b1, w2, b2):
        import jax, jax.numpy as jnp
        import numpy as np
        DIM = 128
        DEPTH = 2
        HEADS = 8
        DIM_HEAD = 64
        WINDOW = 64
        INNER = HEADS * DIM_HEAD
        HID = int(DIM * 4 * 2 / 3)
        B, N = (2, 1024)
        QK_SCALE = 8.0

        def shift_token(t):
            t1, t2 = jnp.split(t, 2, axis=-1)
            t2 = jnp.pad(t2, ((0, 0), (1, 0), (0, 0)))[:, :-1]
            return jnp.concatenate([t1, t2], axis=-1)

        def l2norm(t):
            return t / jnp.clip(jnp.linalg.norm(t, axis=-1, keepdims=True), 1e-12)

        def rotate_half(x):
            x1, x2 = jnp.split(x, 2, axis=-1)
            return jnp.concatenate([-x2, x1], axis=-1)

        def rotary_xpos(q, k):
            n = q.shape[-2]
            half_idx = jnp.arange(0, DIM_HEAD, 2, dtype=jnp.float32)
            inv_freq = 1.0 / 10000.0 ** (half_idx / DIM_HEAD)
            t = jnp.arange(n, dtype=jnp.float32)
            freqs = t[:, None] * inv_freq[None, :]
            freqs = jnp.concatenate([freqs, freqs], axis=-1)
            base = (half_idx + 0.4 * DIM_HEAD) / (1.4 * DIM_HEAD)
            power = (t - n // 2) / float(WINDOW // 2)
            scale = base[None, :] ** power[:, None]
            scale = jnp.concatenate([scale, scale], axis=-1)
            cos, sin = (jnp.cos(freqs), jnp.sin(freqs))
            q = q * cos * scale + rotate_half(q) * sin * scale
            k = k * cos / scale + rotate_half(k) * sin / scale
            return (q, k)

        def local_attention(q, k, v):
            b, h, n, d = q.shape
            w = n // WINDOW
            bq = q.reshape(b, h, w, WINDOW, d) * QK_SCALE
            bk = k.reshape(b, h, w, WINDOW, d)
            bv = v.reshape(b, h, w, WINDOW, d)

            def look_around(t):
                p = jnp.pad(t, ((0, 0), (0, 0), (1, 0), (0, 0), (0, 0)))
                return jnp.concatenate([p[:, :, :w], p[:, :, 1:]], axis=3)
            bk, bv = (look_around(bk), look_around(bv))
            bt = jnp.arange(n).reshape(w, WINDOW)
            btp = jnp.pad(bt, ((1, 0), (0, 0)), constant_values=-1)
            btk = jnp.concatenate([btp[:w], btp[1:]], axis=1)
            sim = jnp.einsum('bhwid,bhwjd->bhwij', bq, bk)
            i = bt[:, :, None]
            j = btk[:, None, :]
            mask = (i < j) | (i > j + WINDOW) | (j == -1)
            sim = jnp.where(mask, -jnp.finfo(sim.dtype).max, sim)
            attn = jax.nn.softmax(sim, axis=-1)
            out = jnp.einsum('bhwij,bhwjd->bhwid', attn, bv)
            return out.reshape(b, h, n, d)

        def _layer(x, wqkv, qs, ksc, wo, lg, lb, w1, b1, w2, b2):
            b, n, _ = x.shape
            h = shift_token(x)
            qkv = h @ wqkv
            q, k, v = jnp.split(qkv, 3, axis=-1)
            to_heads = lambda t: t.reshape(b, n, HEADS, DIM_HEAD).transpose(0, 2, 1, 3)
            q, k, v = (to_heads(q), to_heads(k), to_heads(v))
            q = l2norm(q) * qs
            k = l2norm(k) * ksc
            q, k = rotary_xpos(q, k)
            o = local_attention(q, k, v)
            o = o.transpose(0, 2, 1, 3).reshape(b, n, INNER)
            x = x + o @ wo
            h = shift_token(x)
            mu = h.mean(-1, keepdims=True)
            var = h.var(-1, keepdims=True)
            h = (h - mu) / jnp.sqrt(var + 1e-05) * lg + lb
            h = h @ w1 + b1
            a, g = jnp.split(h, 2, axis=-1)
            h = a * jax.nn.gelu(g, approximate=False)
            x = x + h @ w2 + b2
            return x
        for l in range(DEPTH):
            x = _layer(x, wqkv[l], q_scale[l], k_scale[l], wo[l], ln_g[l], ln_b[l], w1[l], b1[l], w2[l], b2[l])
        return x
    x = L0_attn_x
    xn = _layernorm(x, axis=-1)
    s = _L0_attn_ref(xn, L0_attn_wq, L0_attn_wk, L0_attn_wv, L0_attn_wgq, L0_attn_wgk, L0_attn_wgv, L0_attn_r_out_w, L0_attn_gate_local_w, L0_attn_gate_remote_w, L0_attn_w_out)
    g = _silu(_L0_ffn_ref(xn, L0_ffn_w_gate, L0_ffn_w_up, L0_ffn_w_down))
    x = x + s * g
    xn = _layernorm(x, axis=-1)
    s = _L1_attn_ref(xn, L1_attn_w_q, L1_attn_w_k, L1_attn_w_v, L1_attn_w_u, L1_attn_b_u)
    g = _silu(_L1_ffn_ref(xn, L1_ffn_w1_w, L1_ffn_w1_s, L1_ffn_w2_w, L1_ffn_w2_s, L1_ffn_h1_w, L1_ffn_h1_s, L1_ffn_h2_w, L1_ffn_h2_s, L1_ffn_w3_w, L1_ffn_w3_s))
    x = x + s * g
    xn = _layernorm(x, axis=-1)
    s = _L2_attn_ref(xn, L2_attn_Wqkv, L2_attn_Wproj, L2_attn_lambda_q1, L2_attn_lambda_k1, L2_attn_lambda_q2, L2_attn_lambda_k2)
    g = _silu(_L2_ffn_ref(xn, L2_ffn_Wqkv, L2_ffn_q_scale, L2_ffn_k_scale, L2_ffn_Wo, L2_ffn_ln_g, L2_ffn_ln_b, L2_ffn_W1, L2_ffn_b1, L2_ffn_W2, L2_ffn_b2))
    x = x + s * g
    xn = _layernorm(x, axis=-1)
    s = _L3_attn_ref(xn, L3_attn_A, L3_attn_Bp, L3_attn_Cp, L3_attn_Dp, L3_attn_Wg, L3_attn_bg, L3_attn_gamma, L3_attn_beta)
    g = _silu(_L3_ffn_ref(xn, L3_ffn_wqkv, L3_ffn_q_scale, L3_ffn_k_scale, L3_ffn_wo, L3_ffn_ln_g, L3_ffn_ln_b, L3_ffn_w1, L3_ffn_b1, L3_ffn_w2, L3_ffn_b2))
    x = x + s * g
    return x

_drawn_inputs = setup_inputs


def setup_inputs(seed=0):
    import zlib

    import numpy as np

    out = dict(_drawn_inputs(seed))
    spreads = {'L2_ffn_q_scale': (1.0, 0.2),
     'L2_ffn_k_scale': (1.0, 0.2),
     'L2_ffn_ln_g': (1.0, 0.2),
     'L2_ffn_ln_b': (0.0, 0.1),
     'L2_ffn_b1': (0.0, 0.1),
     'L2_ffn_b2': (0.0, 0.1),
     'L3_attn_bg': (0.0, 0.1),
     'L3_attn_gamma': (1.0, 0.2),
     'L3_attn_beta': (0.0, 0.1),
     'L3_ffn_q_scale': (1.0, 0.2),
     'L3_ffn_k_scale': (1.0, 0.2),
     'L3_ffn_ln_g': (1.0, 0.2),
     'L3_ffn_ln_b': (0.0, 0.1),
     'L3_ffn_b1': (0.0, 0.1),
     'L3_ffn_b2': (0.0, 0.1)}
    factors = {}
    for name, (base, spread) in spreads.items():
        noise = np.random.default_rng([zlib.crc32(name.encode()), seed]).standard_normal(out[name].shape)
        drawn = base * np.exp(spread * noise) if base else spread * noise
        out[name] = jnp.asarray(drawn.astype(out[name].dtype))
    for name, factor in factors.items():
        out[name] = (out[name] * factor).astype(out[name].dtype)
    return out
```

```python
from contextlib import ExitStack

import numpy as np
import concourse.bass as bass
from concourse import mybir

ALU = mybir.AluOpType
ACT = mybir.ActivationFunctionType
F32 = mybir.dt.float32
BF16 = mybir.dt.bfloat16
U32 = mybir.dt.uint32
X = mybir.AxisListType.X

P = 128
BATCH, SEQ, DIM = 4, 512, 128
TILES = BATCH * SEQ // P
TPB = SEQ // P
LN_EPS = 1e-5
MASKED = -1e30


class Event:

    def __init__(self, stage, name, per=1):
        self.sem = stage.sem(name)
        self.per = per

    def at(self, it, k=1):
        return it * self.per + k


class Stage:

    def __init__(self, nc, name):
        self.nc, self.name, self.ctx = nc, name, ExitStack()
        self.events, self.sems = [], []

    def __enter__(self):
        return self

    def __exit__(self, *exc):
        if exc[0] is None:
            self.clear(self.sems)
        return self.ctx.__exit__(*exc)

    def clear(self, sems):
        for sem in sems:
            self.nc.sync.sem_clear(sem)
        self.nc.all_engine_barrier()

    def sb(self, name, shape, dt=F32):
        return self.ctx.enter_context(self.nc.sbuf_tensor(f"{self.name}_{name}", shape, dt))

    def bank(self, name, shape=(P, 512), dt=F32):
        return self.ctx.enter_context(self.nc.psum_tensor(f"{self.name}_{name}", list(shape), dt))

    def sem(self, name):
        sem = self.ctx.enter_context(self.nc.semaphore(f"{self.name}_{name}"))
        self.sems.append(sem)
        return sem

    def event(self, name, per=1):
        e = Event(self, name, per)
        self.events.append(e)
        return e

    def restart(self):
        self.clear([e.sem for e in self.events])



def spread(ap, axis, n):
    a = ap.unsqueeze(axis)
    shape = list(a.shape)
    shape[axis] = n
    return a.to_broadcast(shape)


def load_inputs(nc, g, dram):
    with Stage(nc, "load") as st:
        loaded = st.sem("loaded")
        halved = st.sem("halved")
        with nc.Block() as block:

            @block.gpsimd
            def _(pool):
                pool.memset(g["half"][:, :], -0.5).then_inc(halved, 1)

            @block.sync
            def _(sp):
                sp.dma_start(g["x"][:, :, :], dram["L0_attn_x"].rearrange("b (t p) c -> p (b t) c", p=P)).then_inc(loaded, 16)
                sp.dma_start(g["ident"][:, :], dram["c_ident"]).then_inc(loaded, 16)
                sp.dma_start(g["identb"][:, :], dram["c_identb"]).then_inc(loaded, 16)
                sp.wait_ge(loaded, 3 * 16)


def layer_norm(nc, g, name):
    x, xn, xnT, ident = g["x"], g["xn"], g["xnT"], g["ident"]
    with Stage(nc, name) as st:
        stats = st.sb("stats", [P, TPB, 6])
        mv = st.sb("mv", [P, TPB, 2])
        vare = st.sb("vare", [P, TPB])
        rstd = st.sb("rstd", [P, TPB])
        staged = st.sb("staged", [P, TPB, P])
        turned = st.bank("turned")
        stepped = st.event("stepped", 5)
        rooted = st.event("rooted", 1)
        turned_up = st.event("turned_up", 1)
        with nc.Fori(0, BATCH) as b:
            with nc.Block() as block:
                @block.vector
                def _(v):
                    for t in range(TPB):
                        xt = x[:, bass.ds(b * TPB + t, 1), :].rearrange("p a c -> p (a c)")
                        v.bn_stats(stats[:, t, :], xt).then_inc(stepped.sem, 1)
                        v.wait_ge(stepped.sem, stepped.at(t, 1))
                        v.bn_aggr(mv[:, t, :], stats[:, t, :]).then_inc(stepped.sem, 1)
                        v.wait_ge(stepped.sem, stepped.at(t, 2))
                        v.tensor_scalar(vare[:, t:t + 1], mv[:, t, 1:2], LN_EPS, None, ALU.add).then_inc(stepped.sem, 1)
                        v.wait_ge(rooted.sem, rooted.at(t))
                        v.tensor_scalar(xn[:, bass.ds(b * TPB + t, 1), :].rearrange("p a c -> p (a c)"), xt,
                                        mv[:, t, 0:1], rstd[:, t:t + 1], ALU.subtract, ALU.mult).then_inc(stepped.sem, 1)
                        v.wait_ge(stepped.sem, stepped.at(t, 4))
                        v.tensor_copy(staged[:, t, :], xn[:, bass.ds(b * TPB + t, 1), :].rearrange("p a c -> p (a c)")).then_inc(stepped.sem, 1)

                @block.gpsimd
                def _(pool):
                    for t in range(TPB):
                        pool.wait_ge(stepped.sem, stepped.at(t, 3))
                        pool.tensor_tensor(rstd[:, t:t + 1], vare[:, t:t + 1], g["half"][:, 0:1], ALU.pow).then_inc(rooted.sem, 1)

                @block.tensor
                def _(pe):
                    for t in range(TPB):
                        pe.wait_ge(stepped.sem, stepped.at(t, 5))
                        pe.transpose(turned[:, t * P:(t + 1) * P], staged[:, t, :], ident[:, :]).then_inc(turned_up.sem, 1)

                @block.scalar
                def _(act):
                    act.wait_ge(turned_up.sem, TPB)
                    act.activation(xnT[:, bass.ds(b * SEQ, SEQ)], turned[:, :], ACT.Copy)
            st.restart()


def combine(nc, g, name):
    x, s, u = g["x"], g["s"], g["u"]
    with Stage(nc, name) as st:
        gated = st.sem("gated")
        product = st.sem("product")
        with nc.Block() as block:
            @block.scalar
            def _(act):
                act.activation(u[:, :, :], u[:, :, :], ACT.Silu).then_inc(gated, 1)

            @block.vector
            def _(v):
                v.wait_ge(gated, 1)
                v.tensor_tensor(s[:, :, :], s[:, :, :], u[:, :, :], ALU.mult).then_inc(product, 1)
                v.wait_ge(product, 1)
                v.tensor_tensor(x[:, :, :], x[:, :, :], s[:, :, :], ALU.add)


def store_output(nc, g, out):
    with Stage(nc, "store") as st:
        stored = st.sem("stored")
        with nc.Block() as block:

            @block.sync
            def _(sp):
                sp.dma_start(out.rearrange("b (t p) c -> p (b t) c", p=P), g["x"][:, :, :]).then_inc(stored, 16)
                sp.wait_ge(stored, 16)


def transformer(nc, g, dram, name, depth, heads, window, hid, wqkv, qs, ks, wo, ln_g, ln_b, w1, b1, w2, b2):
    HD = 64
    INNER = heads * HD
    PAIRS = heads // 2
    G4 = heads // 4
    QC = INNER // 512
    KEYS = window + P
    HC = [(c, min(P, hid - c)) for c in range(0, hid, P)]
    NH = len(HC)
    HL = HC[-1][1]
    u, ident, identb = g["u"], g["ident"], g["identb"]

    with Stage(nc, name) as st:
        w_qkv = st.sb("w_qkv", [P, 3 * INNER])
        w_o = st.sb("w_o", [P, PAIRS, DIM])
        w_1 = st.sb("w_1", [P, 2 * hid])
        w_2 = st.sb("w_2", [P, NH, DIM])
        b_1 = st.sb("b_1", [P, 2, NH])
        b_2 = st.sb("b_2", [1, DIM])
        lng = st.sb("lng", [P, 1])
        lnb = st.sb("lnb", [P, 1])
        scales = st.sb("scales", [P, 2, HD])
        base = st.sb("base", [P, 4, TPB, HD])
        rot = st.sb("rot", [P, 4, TPB, HD])
        mask = st.sb("mask", [P, 2, KEYS], BF16)
        maskt = st.sb("maskt", [P, 2, 2, P], BF16)
        sel = st.sb("sel", [2 * heads, heads, P], BF16)
        ones = st.sb("ones", [1, P])
        shT = st.sb("shT", [P, P + 1])
        sh2T = st.sb("sh2T", [P, P + 1])
        sq = st.sb("sq", [P, 2, 8, HD])
        ssq = st.sb("ssq", [P, 2 * heads])
        inv = st.sb("inv", [P, 2 * heads])
        qn = st.sb("qn", [P, 2, 8, HD])
        ra = st.sb("ra", [P, 2, 8, HD])
        rb = st.sb("rb", [P, 2, 8, HD])
        qT = st.sb("qT", [P, PAIRS, P])
        kT = st.sb("kT", [P, PAIRS, KEYS])
        va = st.sb("va", [P, heads, HD + 1])
        vc = st.sb("vc", [window, heads, HD + 1])
        nmax = st.sb("nmax", [P, heads])
        hl = st.sb("hl", [P, 2, heads], BF16)
        nmT = st.sb("nmT", [2 * heads, P], BF16)
        pt = st.sb("pt", [P, 2, 2, 2, P])
        pc = st.sb("pc", [window, 2, 2, 2, P])
        rden = st.sb("rden", [P, 2, 4])
        o = st.sb("o", [P, heads, HD])
        oT = st.sb("oT", [P, PAIRS, P])
        x0 = st.sb("x0", [P, DIM])
        x1 = st.sb("x1", [P, DIM])
        stats = st.sb("stats", [P, 6])
        mv = st.sb("mv", [P, 2])
        vare = st.sb("vare", [P, 1])
        rstd = st.sb("rstd", [P, 1])
        ln = st.sb("ln", [P, DIM])
        lnT = st.sb("lnT", [P, P])
        gg = st.sb("gg", [P, NH, P])
        hT = st.sb("hT", [P, NH, P])
        wide = st.bank("wide", [P, 4, 512])
        head = st.bank("head", [P, 2, 512])
        small = st.bank("small", [P, 512])
        misc = st.bank("misc", [P, 512])
        smallb = small[:, 0:P].bitcast(BF16)

        w_in = st.event("w_in")
        c_in = st.sem("c_in")
        zeroed = st.sem("zeroed")
        tables = st.event("tables", 4)
        x0_in = st.event("x0_in", 1)
        xT_up = st.event("xT_up", 1)
        carry0 = st.event("carry0", 1)
        sh_in = st.event("sh_in", 2)
        proj = st.event("proj", 3 * QC)
        sqd = st.event("sqd", 2 * QC)
        summed = st.event("summed", 2 * QC)
        floored = st.event("floored", 2 * QC)
        inved = st.event("inved", 2 * QC)
        normed = st.event("normed", 2 * QC)
        cosd = st.event("cosd", 2 * QC)
        sind = st.event("sind", 4 * QC)
        roped = st.event("roped", 2 * QC)
        turned = st.event("turned", 2 * QC)
        qk_in = st.event("qk_in", 2 * QC)
        v_in = st.event("v_in", QC)
        k_carried = st.event("k_carried", 1)
        v_carried = st.event("v_carried", 1)
        scored = st.event("scored", G4)
        maxed = st.event("maxed", G4)
        split = st.event("split", 2)
        m_up = st.event("m_up", 1)
        m_in = st.event("m_in", 1)
        shifted = st.event("shifted", G4)
        exped = st.event("exped", 2 * G4)
        weighed = st.event("weighed", G4)
        recip = st.event("recip", G4)
        o_in = st.event("o_in", G4)
        oT_up = st.event("oT_up", G4)
        oT_in = st.event("oT_in", G4)
        y_up = st.event("y_up", 1)
        x1_in = st.event("x1_in", 1)
        x1T_up = st.event("x1T_up", 1)
        carry1 = st.event("carry1", 1)
        sh2_in = st.event("sh2_in", 2)
        sh2_up = st.event("sh2_up", 1)
        lnd = st.event("lnd", 4)
        rooted = st.event("rooted", 1)
        lnT_up = st.event("lnT_up", 1)
        lnT_in = st.event("lnT_in", 1)
        gate_up = st.event("gate_up", 1)
        gelu_in = st.event("gelu_in", NH)
        h_in = st.event("h_in", NH)
        f_up = st.event("f_up", 1)
        tile_done = st.event("tile_done", 1)
        NW = 11 + (3 if HL < P else 0)
        with nc.Block() as block:
            @block.sync
            def _(sp):
                sp.dma_start(base[:, :, :, :], dram[f"c_rot{window}"]).then_inc(c_in, 16)
                sp.dma_start(mask[:, :, :], dram[f"c_mask{window}"]).then_inc(c_in, 16)
                sp.dma_start(maskt[:, :, :, :], dram[f"c_maskt{window}"]).then_inc(c_in, 16)
                sp.dma_start(sel[:, :, :], dram[f"c_sel{heads}"]).then_inc(c_in, 16)
                sp.wait_ge(c_in, 4 * 16)

            @block.gpsimd
            def _(pool):
                pool.memset(kT[:, :, :], 0.0).then_inc(zeroed, 1)
                pool.memset(va[:, :, :], 1.0).then_inc(zeroed, 1)
                pool.memset(shT[:, :], 0.0).then_inc(zeroed, 1)
                pool.memset(sh2T[:, :], 0.0).then_inc(zeroed, 1)
                pool.memset(ones[:, :], 1.0).then_inc(zeroed, 1)
                pool.wait_ge(zeroed, 5)

        with nc.Fori(0, depth) as l:
            with nc.Block() as block:
                @block.sync
                def _(sp):
                    lay = lambda a: a[bass.ds(l, 1)]
                    sp.dma_start(w_qkv[:, :], lay(wqkv).rearrange("a p n -> p (a n)")).then_inc(w_in.sem, 16)
                    sp.dma_start(w_o[:, :, :], lay(wo).rearrange("a (c p) n -> p (a c) n", p=P)).then_inc(w_in.sem, 16)
                    sp.dma_start(w_1[:, :], lay(w1).rearrange("a p n -> p (a n)")).then_inc(w_in.sem, 16)
                    sp.dma_start(lng[:, :], lay(ln_g).rearrange("a p -> p a"), allow_slow_non_contiguous=True).then_inc(w_in.sem, 16)
                    sp.dma_start(lnb[:, :], lay(ln_b).rearrange("a p -> p a"), allow_slow_non_contiguous=True).then_inc(w_in.sem, 16)
                    sp.dma_start(b_2[:, :], lay(b2)).then_inc(w_in.sem, 16)
                    sp.dma_start(scales[:, 0, :], lay(qs).to_broadcast([P, HD])).then_inc(w_in.sem, 16)
                    sp.dma_start(scales[:, 1, :], lay(ks).to_broadcast([P, HD])).then_inc(w_in.sem, 16)
                    full = (NH - 1) if HL < P else NH
                    w2l, b1l = lay(w2), lay(b1)
                    sp.dma_start(w_2[:, 0:full, :], w2l[:, 0:full * P, :].rearrange("a (c p) n -> p (a c) n", p=P)).then_inc(w_in.sem, 16)
                    for h in range(2):
                        sp.dma_start(b_1[:, h, 0:full], b1l[:, h * hid:h * hid + full * P].rearrange("a (c p) -> p (a c)", p=P), allow_slow_non_contiguous=True).then_inc(w_in.sem, 16)
                    if HL < P:
                        sp.dma_start(w_2[0:HL, full, :], w2l[:, full * P:hid, :].rearrange("a p n -> p (a n)")).then_inc(w_in.sem, 16)
                        for h in range(2):
                            sp.dma_start(b_1[0:HL, h, full:NH], b1l[:, h * hid + full * P:h * hid + hid].rearrange("a p -> p a"), allow_slow_non_contiguous=True).then_inc(w_in.sem, 16)
                    sp.wait_ge(w_in.sem, NW * 16)

                @block.vector
                def _(v):
                    v.wait_ge(w_in.sem, NW * 16)
                    for r in range(2):
                        s = scales[:, r, :]
                        v.tensor_tensor(rot[:, 2 * r], base[:, 2 * r], spread(s, 1, TPB), ALU.mult).then_inc(tables.sem, 1)
                        v.tensor_tensor(rot[:, 2 * r + 1, :, 0:32], base[:, 2 * r + 1, :, 0:32], spread(s[:, 32:64], 1, TPB), ALU.mult)
                        v.tensor_tensor(rot[:, 2 * r + 1, :, 32:64], base[:, 2 * r + 1, :, 32:64], spread(s[:, 0:32], 1, TPB),
                                        ALU.mult).then_inc(tables.sem, 1)

            with nc.Fori(0, BATCH) as b:
                with nc.Block() as block:
                    @block.gpsimd
                    def _(pool):
                        for t in range(TPB):
                            pool.wait_ge(tile_done.sem, t)
                            pool.tensor_copy(kT[:, :, 0:window], kT[:, :, P:P + window]).then_inc(k_carried.sem, 1)
                            def invert(c):
                                pool.wait_ge(floored.sem, floored.at(t, c + 1))
                                pool.tensor_tensor(inv[:, 8 * c:8 * c + 8], ssq[:, 8 * c:8 * c + 8], g["half"][:, 0:8],
                                                   ALU.pow).then_inc(inved.sem, 1)

                            invert(0)
                            for c in range(2 * QC):
                                if c + 1 < 2 * QC:
                                    invert(c + 1)
                                r = 2 * (c // QC)
                                cos = rot[:, r, t, :]
                                sin = rot[:, r + 1, t, :]
                                z = c % 2
                                pool.wait_ge(normed.sem, normed.at(t, c + 1))
                                if c >= 2:
                                    pool.wait_ge(roped.sem, roped.at(t, c - 1))
                                    pool.wait_ge(turned.sem, turned.at(t, c - 1))
                                pool.tensor_tensor(ra[:, z], qn[:, z], spread(cos, 1, 8), ALU.mult).then_inc(cosd.sem, 1)
                                pool.tensor_tensor(rb[:, z, :, 0:32], qn[:, z, :, 32:64], spread(sin[:, 0:32], 1, 8), ALU.mult).then_inc(sind.sem, 1)
                                pool.tensor_tensor(rb[:, z, :, 32:64], qn[:, z, :, 0:32], spread(sin[:, 32:64], 1, 8), ALU.mult).then_inc(sind.sem, 1)
                            pool.wait_ge(lnd.sem, lnd.at(t, 3))
                            pool.tensor_tensor(rstd[:, :], vare[:, :], g["half"][:, 0:1], ALU.pow).then_inc(rooted.sem, 1)

                    @block.tensor
                    def _(pe):
                        for t in range(TPB):
                            pe.wait_ge(tile_done.sem, t)
                            pe.wait_ge(x0_in.sem, x0_in.at(t))
                            pe.transpose(misc[:, 0:P], x0[:, :], ident[:, :]).then_inc(xT_up.sem, 1)
                            pe.wait_ge(sh_in.sem, sh_in.at(t, 2))
                            for c in range(3 * QC):
                                if 4 <= c:
                                    pe.wait_ge(normed.sem, normed.at(t, c - 3))
                                pe.matmul(wide[:, c % 4, :], shT[:, 0:P], w_qkv[:, c * 512:(c + 1) * 512],
                                          start=True, stop=True).then_inc(proj.sem, 1)
                            for c in range(2 * QC):
                                pe.wait_ge(roped.sem, roped.at(t, c + 1))
                                if c >= 2:
                                    pe.wait_ge(qk_in.sem, qk_in.at(t, c - 1))
                                for j in range(4):
                                    m = pe.transpose(head[:, c % 2, j * P:(j + 1) * P],
                                                     ra[:, c % 2, 2 * j:2 * j + 2, :].rearrange("p h d -> p (h d)"), ident[:, :])
                                m.then_inc(turned.sem, 1)
                            pe.wait_ge(qk_in.sem, qk_in.at(t, 2 * QC))
                            pe.wait_ge(v_in.sem, v_in.at(t, QC))
                            pe.wait_ge(k_carried.sem, k_carried.at(t))
                            for q in range(G4):
                                if q >= 2:
                                    pe.wait_ge(maxed.sem, maxed.at(t, q - 1))
                                for h2 in range(2):
                                    rows = slice(64 * h2, 64 * h2 + 64)
                                    bank = wide[:, 2 * (q % 2) + h2, :].rearrange("p (h k) -> p h k", h=2)[:, :, 0:KEYS]
                                    pe.matmul(bank, identb[:, :], spread(mask[:, min(t, 1), :], 1, 2),
                                              start=True, stop=False, skip_group_check=True)
                                    for j in range(2):
                                        m = pe.matmul(bank[:, j, :], qT[rows, 2 * q + j, :], kT[rows, 2 * q + j, :],
                                                      start=False, stop=True, skip_group_check=True)
                                m.then_inc(scored.sem, 1)
                            pe.wait_ge(split.sem, split.at(t, 2))
                            pe.transpose(smallb[0:2 * heads, 0:P], hl[:, :, :].rearrange("p a h -> p (a h)"), identb[:, :]).then_inc(m_up.sem, 1)
                            pe.wait_ge(m_in.sem, m_in.at(t))
                            pe.wait_ge(v_carried.sem, v_carried.at(t))

                            def shift(q):
                                if q >= 2:
                                    pe.wait_ge(exped.sem, exped.at(t, 2 * (q - 1)))
                                for p in range(2):
                                    bank = wide[:, 2 * (q % 2) + p, :].rearrange("p (a j k) -> p a j k", a=2, j=2)
                                    rows = slice(64 * p, 64 * p + 64)
                                    pe.matmul(bank, identb[:, :], spread(maskt[:, min(t, 1), :, :], 2, 2),
                                              start=True, stop=False, skip_group_check=True)
                                    for j in range(2):
                                        col = 4 * q + 2 * p + j
                                        own, car = bank[:, 0, j, :], bank[0:window, 1, j, :]
                                        pe.matmul(own, sel[:, col, :], nmT[:, :], start=False, stop=False, skip_group_check=True)
                                        pe.matmul(car, sel[:, col, 0:window], nmT[:, :], start=False, stop=False, skip_group_check=True)
                                        pe.matmul(own, kT[rows, 2 * q + j, window:KEYS], qT[rows, 2 * q + j, :],
                                                  start=False, stop=True, skip_group_check=True)
                                        m = pe.matmul(car, kT[rows, 2 * q + j, 0:window], qT[rows, 2 * q + j, :],
                                                      start=False, stop=True, skip_group_check=True)
                                m.then_inc(shifted.sem, 1)

                            def weigh(q):
                                pe.wait_ge(exped.sem, exped.at(t, 2 * q + 2))
                                if q >= 2:
                                    pe.wait_ge(o_in.sem, o_in.at(t, q - 1))
                                for hh in range(4):
                                    out = head[:, q % 2, hh * 65:hh * 65 + 65]
                                    pe.matmul(out, pt[:, q % 2, hh % 2, hh // 2, :], va[:, 4 * q + hh, :], start=True, stop=False, skip_group_check=True)
                                    m = pe.matmul(out, pc[:, q % 2, hh % 2, hh // 2, :], vc[:, 4 * q + hh, :], start=False, stop=True, skip_group_check=True)
                                m.then_inc(weighed.sem, 1)

                            def turn_out(q):
                                pe.wait_ge(o_in.sem, o_in.at(t, q + 1))
                                if q >= 2:
                                    pe.wait_ge(oT_in.sem, oT_in.at(t, q - 1))
                                for j in range(2):
                                    m = pe.transpose((small, misc)[q % 2][:, j * P:(j + 1) * P],
                                                     o[:, 4 * q + 2 * j:4 * q + 2 * j + 2, :].rearrange("p h d -> p (h d)"), ident[:, :])
                                m.then_inc(oT_up.sem, 1)

                            for q in range(G4 + 2):
                                if q < G4:
                                    shift(q)
                                if 1 <= q <= G4:
                                    weigh(q - 1)
                                if q >= 2:
                                    turn_out(q - 2)
                            pe.wait_ge(oT_in.sem, oT_in.at(t, G4))
                            for c in range(PAIRS):
                                m = pe.matmul(misc[:, 0:DIM], oT[:, c, :], w_o[:, c, :], start=(c == 0), stop=(c == PAIRS - 1))
                            m.then_inc(y_up.sem, 1)
                            pe.wait_ge(x1_in.sem, x1_in.at(t))
                            pe.transpose(misc[:, P:2 * P], x1[:, :], ident[:, :]).then_inc(x1T_up.sem, 1)
                            pe.wait_ge(sh2_in.sem, sh2_in.at(t, 2))
                            pe.transpose(misc[:, 2 * P:3 * P], sh2T[:, 0:P], ident[:, :]).then_inc(sh2_up.sem, 1)
                            pe.wait_ge(lnd.sem, lnd.at(t, 4))
                            pe.transpose(misc[:, 3 * P:4 * P], ln[:, :], ident[:, :]).then_inc(lnT_up.sem, 1)
                            pe.wait_ge(lnT_in.sem, lnT_in.at(t))
                            for half in range(2):
                                for c, (at, size) in enumerate(HC):
                                    lo = (1 - half) * hid + at
                                    m = pe.matmul(head[0:size, half, c * P:(c + 1) * P], w_1[:, lo:lo + size], lnT[:, :], start=True, stop=True)
                            m.then_inc(gate_up.sem, 1)
                            pe.wait_ge(h_in.sem, h_in.at(t, NH))
                            for c, (at, size) in enumerate(HC):
                                pe.matmul(misc[:, 0:DIM], hT[0:size, c, :], w_2[0:size, c, :], start=(c == 0), stop=False)
                            pe.matmul(misc[:, 0:DIM], ones[:, :], b_2[:, :], start=False, stop=True).then_inc(f_up.sem, 1)

                    @block.scalar
                    def _(act):
                        for t in range(TPB):
                            act.wait_ge(tile_done.sem, t)

                            act.activation(vc[:, :, :], va[P - window:P, :, :], ACT.Copy).then_inc(v_carried.sem, 1)

                            def copy_turned(c):
                                act.wait_ge(turned.sem, turned.at(t, c + 1))
                                cc = c % QC
                                dst = qT[:, 4 * cc:4 * cc + 4, :] if c < QC else kT[:, 4 * cc:4 * cc + 4, window:KEYS]
                                if c == QC:
                                    act.wait_ge(k_carried.sem, k_carried.at(t))
                                act.activation(dst, head[:, c % 2, :].rearrange("p (j k) -> p j k", j=4), ACT.Copy).then_inc(qk_in.sem, 1)

                            for c in range(2 * QC):
                                act.wait_ge(proj.sem, proj.at(t, c + 1))
                                if c >= 2:
                                    act.wait_ge(summed.sem, summed.at(t, c - 1))
                                act.activation(sq[:, c % 2].rearrange("p h d -> p (h d)"), wide[:, c % 4, :], ACT.Square).then_inc(sqd.sem, 1)
                                if c >= 2:
                                    copy_turned(c - 2)
                            act.wait_ge(v_carried.sem, v_carried.at(t))
                            for c in range(QC):
                                act.wait_ge(proj.sem, proj.at(t, 2 * QC + c + 1))
                                act.activation(va[:, 8 * c:8 * c + 8, 0:HD], wide[:, (2 * QC + c) % 4, :].rearrange("p (h d) -> p h d", h=8),
                                               ACT.Copy).then_inc(v_in.sem, 1)
                            copy_turned(2 * QC - 2)
                            copy_turned(2 * QC - 1)

                            def copy_out(q):
                                act.wait_ge(oT_up.sem, oT_up.at(t, q + 1))
                                act.activation(oT[:, 2 * q:2 * q + 2, :].rearrange("p a b -> p (a b)"), (small, misc)[q % 2][:, 0:256],
                                               ACT.Copy).then_inc(oT_in.sem, 1)

                            for q in range(G4 + 3):
                                if q < G4:
                                    act.wait_ge(shifted.sem, shifted.at(t, q + 1))
                                    if q >= 2:
                                        act.wait_ge(weighed.sem, weighed.at(t, q - 1))
                                    pair = wide[:, 2 * (q % 2):2 * (q % 2) + 2, :]
                                    act.activation(pt[:, q % 2].rearrange("p a j k -> p a (j k)"), pair[:, :, 0:256], ACT.Exp).then_inc(exped.sem, 1)
                                    act.activation(pc[:, q % 2].rearrange("p a j k -> p a (j k)"), pair[0:window, :, 256:512], ACT.Exp).then_inc(exped.sem, 1)
                                if q >= 3:
                                    copy_out(q - 3)
                            act.wait_ge(lnT_up.sem, lnT_up.at(t))
                            act.activation(lnT[:, :], misc[:, 3 * P:4 * P], ACT.Identity, bias=lnb[:, :], scale=lng[:, 0:1]).then_inc(lnT_in.sem, 1)
                            act.wait_ge(gate_up.sem, gate_up.at(t))
                            for c, (at, size) in enumerate(HC):
                                act.activation(gg[0:size, c, :], head[0:size, 0, c * P:(c + 1) * P], ACT.Gelu,
                                               bias=b_1[0:size, 1, c:c + 1]).then_inc(gelu_in.sem, 1)

                    @block.vector
                    def _(v):
                        for t in range(TPB):
                            ut = u[:, bass.ds(b * TPB + t, 1), :].rearrange("p a c -> p (a c)")
                            v.wait_ge(tile_done.sem, t)
                            v.tensor_copy(x0[:, :], ut).then_inc(x0_in.sem, 1)
                            v.tensor_scalar(shT[64:P, 0:1], shT[64:P, P:P + 1], float(t > 0), None, ALU.mult).then_inc(carry0.sem, 1)
                            v.wait_ge(carry0.sem, carry0.at(t))
                            v.wait_ge(xT_up.sem, xT_up.at(t))
                            v.tensor_copy(shT[0:64, 0:P], misc[0:64, 0:P]).then_inc(sh_in.sem, 1)
                            v.tensor_copy(shT[64:P, 1:P + 1], misc[64:P, 0:P]).then_inc(sh_in.sem, 1)

                            def finish_rope(c):
                                z = c % 2
                                v.wait_ge(cosd.sem, cosd.at(t, c + 1))
                                v.wait_ge(sind.sem, sind.at(t, 2 * c + 2))
                                v.tensor_tensor(ra[:, z], ra[:, z], rb[:, z], ALU.add).then_inc(roped.sem, 1)

                            for c in range(2 * QC):
                                z = c % 2
                                v.wait_ge(sqd.sem, sqd.at(t, c + 1))
                                v.tensor_reduce(ssq[:, 8 * c:8 * c + 8], sq[:, z], X, ALU.add).then_inc(summed.sem, 1)
                                v.wait_ge(summed.sem, summed.at(t, c + 1))
                                v.tensor_scalar(ssq[:, 8 * c:8 * c + 8], ssq[:, 8 * c:8 * c + 8], 1e-24, None, ALU.max).then_inc(floored.sem, 1)
                                v.wait_ge(inved.sem, inved.at(t, c + 1))
                                if c >= 2:
                                    v.wait_ge(sind.sem, sind.at(t, 2 * c - 2))
                                v.tensor_tensor(qn[:, z], wide[:, c % 4, :].rearrange("p (h d) -> p h d", h=8),
                                                spread(inv[:, 8 * c:8 * c + 8], 2, HD), ALU.mult).then_inc(normed.sem, 1)
                                if c >= 1:
                                    finish_rope(c - 1)
                            finish_rope(2 * QC - 1)
                            for q in range(G4):
                                v.wait_ge(scored.sem, scored.at(t, q + 1))
                                v.tensor_reduce(nmax[:, 4 * q:4 * q + 4],
                                                wide[:, 2 * (q % 2):2 * (q % 2) + 2, :].rearrange("p b (h k) -> p (b h) k", h=2)[:, :, 0:KEYS],
                                                X, ALU.max, negate=True).then_inc(maxed.sem, 1)
                            v.wait_ge(maxed.sem, maxed.at(t, G4))
                            v.tensor_copy(hl[:, 0, :], nmax[:, :]).then_inc(split.sem, 1)
                            v.wait_ge(split.sem, split.at(t, 1))
                            v.tensor_tensor(hl[:, 1, :], nmax[:, :], hl[:, 0, :], ALU.subtract).then_inc(split.sem, 1)
                            v.wait_ge(m_up.sem, m_up.at(t))
                            v.tensor_copy(nmT[:, :], smallb[0:2 * heads, 0:P]).then_inc(m_in.sem, 1)
                            for q in range(G4):
                                v.wait_ge(weighed.sem, weighed.at(t, q + 1))
                                out = head[:, q % 2, 0:4 * 65].rearrange("p (h d) -> p h d", h=4)
                                v.reciprocal(rden[:, q % 2, :], out[:, :, HD]).then_inc(recip.sem, 1)
                                v.wait_ge(recip.sem, recip.at(t, q + 1))
                                v.tensor_tensor(o[:, 4 * q:4 * q + 4, :], out[:, :, 0:HD], spread(rden[:, q % 2, :], 2, HD),
                                                ALU.mult).then_inc(o_in.sem, 1)
                            v.wait_ge(y_up.sem, y_up.at(t))
                            v.tensor_tensor(x1[:, :], misc[:, 0:DIM], x0[:, :], ALU.add).then_inc(x1_in.sem, 1)
                            v.tensor_scalar(sh2T[64:P, 0:1], sh2T[64:P, P:P + 1], float(t > 0), None, ALU.mult).then_inc(carry1.sem, 1)
                            v.wait_ge(carry1.sem, carry1.at(t))
                            v.wait_ge(x1T_up.sem, x1T_up.at(t))
                            v.tensor_copy(sh2T[0:64, 0:P], misc[0:64, P:2 * P]).then_inc(sh2_in.sem, 1)
                            v.tensor_copy(sh2T[64:P, 1:P + 1], misc[64:P, P:2 * P]).then_inc(sh2_in.sem, 1)
                            v.wait_ge(sh2_up.sem, sh2_up.at(t))
                            v.bn_stats(stats[:, :], misc[:, 2 * P:3 * P]).then_inc(lnd.sem, 1)
                            v.wait_ge(lnd.sem, lnd.at(t, 1))
                            v.bn_aggr(mv[:, :], stats[:, :]).then_inc(lnd.sem, 1)
                            v.wait_ge(lnd.sem, lnd.at(t, 2))
                            v.tensor_scalar(vare[:, :], mv[:, 1:2], LN_EPS, None, ALU.add).then_inc(lnd.sem, 1)
                            v.wait_ge(rooted.sem, rooted.at(t))
                            v.tensor_scalar(ln[:, :], misc[:, 2 * P:3 * P], mv[:, 0:1], rstd[:, 0:1], ALU.subtract, ALU.mult).then_inc(lnd.sem, 1)
                            for c, (at, size) in enumerate(HC):
                                v.wait_ge(gelu_in.sem, gelu_in.at(t, c + 1))
                                v.scalar_tensor_tensor(out=hT[0:size, c, :], in0=head[0:size, 1, c * P:(c + 1) * P], scalar=b_1[0:size, 0, c:c + 1],
                                                       in1=gg[0:size, c, :], op0=ALU.add, op1=ALU.mult).then_inc(h_in.sem, 1)
                            v.wait_ge(f_up.sem, f_up.at(t))
                            v.wait_ge(x1_in.sem, x1_in.at(t))
                            v.tensor_tensor(ut, misc[:, 0:DIM], x1[:, :], ALU.add).then_inc(tile_done.sem, 1)

                st.restart()


def attention0(nc, g, d):
    H, HD, LH, WIN, LAT = 16, 8, 8, 32, 64
    G, LG = H // 4, LH // 4
    CHUNK = SEQ // LAT
    s, ident, identb, xnT = g["s"], g["ident"], g["identb"], g["xnT"]
    with Stage(nc, "a0") as st:
        wqs = st.sb("wqs", [P, G, 4, 32])
        wks = st.sb("wks", [P, G, 4, 32])
        wgqs = st.sb("wgqs", [P, LG, 4, 32])
        wgks = st.sb("wgks", [P, LG, 4, 32])
        wq = st.sb("wq", [P, DIM])
        wv = st.sb("wv", [P, DIM])
        wgv = st.sb("wgv", [P, LAT])
        wr = st.sb("wr", [LAT, DIM])
        wo = st.sb("wo", [P, DIM])
        gw = st.sb("gw", [P, 2, DIM])
        mask = st.sb("mask", [P, 2, WIN + P], BF16)
        maskt = st.sb("maskt", [P, 2, 2, P], BF16)
        maskl = st.sb("maskl", [P, TPB, LAT], BF16)
        masklt = st.sb("masklt", [LAT, TPB, P], BF16)
        sel = st.sb("sel", [64, H, P], BF16)
        xb = st.sb("xb", [P, SEQ])
        qT = st.sb("qT", [P, G, SEQ])
        kT = st.sb("kT", [P, G, SEQ])
        gqT = st.sb("gqT", [P, LG, SEQ])
        gkT = st.sb("gkT", [P, LG, LAT])
        gvT = st.sb("gvT", [LAT, LAT])
        va = st.sb("va", [P, TPB, H, HD + 1])
        vc = st.sb("vc", [WIN, TPB, H, HD + 1])
        gva = st.sb("gva", [LAT, LH, HD + 1])
        gprod = st.sb("gprod", [P, 2, DIM])
        logit = st.sb("logit", [P, TPB, 2, H])
        gates = st.sb("gates", [P, TPB, 2, H])
        nmax = st.sb("nmax", [P, H])
        hl = st.sb("hl", [P, 2, H], BF16)
        nmT = st.sb("nmT", [64, P], BF16)
        pt = st.sb("pt", [P, 4, G, P])
        pc = st.sb("pc", [WIN, 4, G, P])
        ptl = st.sb("ptl", [LAT, 4, LG, P])
        rden = st.sb("rden", [P, H])
        rdl = st.sb("rdl", [P, LH])
        loc = st.sb("loc", [P, DIM])
        rem = st.sb("rem", [P, LAT])
        remT = st.sb("remT", [LAT, P])
        remg = st.sb("remg", [P, DIM])
        mix = st.sb("mix", [P, DIM])
        mixT = st.sb("mixT", [P, P])
        all8 = st.bank("all8", [P, 8, 512])
        bank = [all8[:, i, :] for i in range(8)]
        loaded, zeroed = st.sem("loaded"), st.sem("zeroed")
        with nc.Block() as block:
            @block.gpsimd
            def _(pool):
                for z in (wqs, wks, wgqs, wgks):
                    pool.memset(z[:, :, :, :], 0.0).then_inc(zeroed, 1)
                pool.memset(sel[:, :, :], 0.0).then_inc(zeroed, 1)
                pool.memset(nmT[:, :], 0.0).then_inc(zeroed, 1)
                pool.memset(hl[:, :, :], 0.0).then_inc(zeroed, 1)
                pool.memset(va[:, :, :, :], 1.0).then_inc(zeroed, 1)
                pool.memset(gva[:, :, :], 1.0).then_inc(zeroed, 1)

            @block.sync
            def _(sp):
                sp.wait_ge(zeroed, 9)
                for dst, name, groups in ((wqs, "wq", G), (wks, "wk", G), (wgqs, "wgq", LG), (wgks, "wgk", LG)):
                    for c in range(groups):
                        sp.dma_start(dst[:, c, :, 0:HD], d[f"L0_attn_{name}"][:, c * 32:(c + 1) * 32].rearrange("p (j e) -> p j e", e=HD)).then_inc(loaded, 16)
                sp.dma_start(wq[:, :], d["L0_attn_wq"]).then_inc(loaded, 16)
                sp.dma_start(wv[:, :], d["L0_attn_wv"]).then_inc(loaded, 16)
                sp.dma_start(wgv[:, :], d["L0_attn_wgv"]).then_inc(loaded, 16)
                sp.dma_start(wr[:, :], d["L0_attn_r_out_w"]).then_inc(loaded, 16)
                sp.dma_start(wo[:, :], d["L0_attn_w_out"]).then_inc(loaded, 16)
                for k, name in enumerate(("local", "remote")):
                    sp.dma_start(gw[:, k, :], d[f"L0_attn_gate_{name}_w"].rearrange("h e -> (h e)").rearrange("(a n) -> a n", a=1).to_broadcast([P, DIM])).then_inc(loaded, 16)
                sp.dma_start(mask[:, :, :], d["c_mask31"]).then_inc(loaded, 16)
                sp.dma_start(maskt[:, :, :, :], d["c_maskt31"]).then_inc(loaded, 16)
                sp.dma_start(maskl[:, :, :], d["c_maskl"]).then_inc(loaded, 16)
                sp.dma_start(masklt[:, :, :], d["c_masklt"]).then_inc(loaded, 16)
                sp.dma_start(sel[0:2 * H, :, :], d["c_sel16"]).then_inc(loaded, 16)
                sp.wait_ge(loaded, (2 * G + 2 * LG + 12) * 16)

        xb_in = st.event("xb_in")
        proj = st.event("proj")
        even_in = st.event("even_in")
        odd_in = st.event("odd_in")
        lat_up = st.event("lat_up")
        lat_in = st.event("lat_in")
        carried = st.event("carried")
        gate_up = st.event("gate_up")
        gate_mul = st.event("gate_mul")
        gate_sum = st.event("gate_sum")
        gates_in = st.event("gates_in")
        with nc.Fori(0, BATCH) as b:
            JOBS = ([("q", c) for c in range(G)] + [("k", c) for c in range(G)] + [("gq", 0), ("gk", 0), ("gq", 1), ("gk", 1)]
                    + [("v", 0), ("gv", 0)] + [("v", t) for t in range(1, TPB)])
            NP = len(JOBS)
            with nc.Block() as block:
                @block.gpsimd
                def _(pool):
                    pool.tensor_copy(xb[:, :], xnT[:, bass.ds(b * SEQ, SEQ)]).then_inc(xb_in.sem, 1)

                @block.tensor
                def _(pe):
                    pe.wait_ge(xb_in.sem, 1)
                    for n in range(NP):
                        if n >= 8:
                            pe.wait_ge((even_in, odd_in)[n % 2].sem, (n - 8) // 2 + 1)
                        kind, c = JOBS[n]
                        if kind == "gv":
                            m = pe.matmul(bank[n % 8][0:LAT, :], wgv[:, :], xb[:, :], start=True, stop=True)
                        elif kind == "v":
                            m = pe.matmul(bank[n % 8][:, 0:DIM], xb[:, c * P:(c + 1) * P], wv[:, :], start=True, stop=True)
                        else:
                            w = {"q": wqs, "k": wks, "gq": wgqs, "gk": wgks}[kind]
                            m = pe.matmul(bank[n % 8], w[:, c, :, :].rearrange("p j e -> p (j e)"), xb[:, :], start=True, stop=True)
                        m.then_inc(proj.sem, 1)
                    pe.wait_ge(even_in.sem, (NP + 1) // 2)
                    pe.wait_ge(odd_in.sem, NP // 2)
                    pe.transpose(bank[0][0:LAT, 0:LAT], gvT[:, :], ident[0:LAT, 0:LAT]).then_inc(lat_up.sem, 1)
                    for t in range(TPB):
                        pe.matmul(bank[1 + t][:, 0:DIM], xb[:, t * P:(t + 1) * P], wq[:, :], start=True, stop=True).then_inc(gate_up.sem, 1)

                def place(n, copy, pooled):
                    src = bank[n % 8]
                    kind, c = JOBS[n]
                    if kind == "q":
                        return copy(qT[:, c, :], src, HD ** -0.5)
                    if kind == "k":
                        return copy(kT[:, c, :], src, 1.0)
                    if kind == "gq":
                        return copy(gqT[:, c, :], src, HD ** -0.5 / CHUNK)
                    if kind == "gk":
                        return pooled(gkT[:, c, :], src)
                    if kind == "gv":
                        return pooled(gvT[:, :], src[0:LAT, :])
                    return copy(va[:, c, :, 0:HD], src[:, 0:DIM].rearrange("p (h e) -> p h e", e=HD), 1.0)

                @block.scalar
                def _(act):
                    for n in range(0, NP, 2):
                        act.wait_ge(proj.sem, n + 1)
                        place(n, lambda dst, src, k: act.activation(dst, src, ACT.Copy, scale=k), None).then_inc(even_in.sem, 1)
                    act.wait_ge(even_in.sem, (NP + 1) // 2)
                    act.wait_ge(odd_in.sem, NP // 2)
                    for t in range(1, TPB):
                        act.activation(vc[:, t, :, :], va[P - WIN:P, t - 1, :, :], ACT.Copy).then_inc(carried.sem, 1)
                    act.wait_ge(gate_sum.sem, TPB)
                    act.activation(gates[:, :, :, :], logit[:, :, :, :], ACT.Sigmoid).then_inc(gates_in.sem, 1)

                @block.vector
                def _(v):
                    def pooled(dst, src):
                        return v.tensor_reduce(dst, src.rearrange("p (n k) -> p n k", k=CHUNK), X, ALU.add)

                    for n in range(1, NP, 2):
                        v.wait_ge(proj.sem, n + 1)
                        place(n, lambda dst, src, k: v.tensor_scalar(dst, src, k, None, ALU.mult), pooled).then_inc(odd_in.sem, 1)
                    v.wait_ge(lat_up.sem, 1)
                    v.tensor_scalar(gva[:, :, 0:HD], bank[0][0:LAT, 0:LAT].rearrange("p (h e) -> p h e", e=HD), 1.0 / CHUNK, None, ALU.mult).then_inc(lat_in.sem, 1)
                    for t in range(TPB):
                        v.wait_ge(gate_up.sem, t + 1)
                        if t:
                            v.wait_ge(gate_sum.sem, t)
                        v.tensor_tensor(gprod[:, :, :], gw[:, :, :], spread(bank[1 + t][:, 0:DIM], 1, 2), ALU.mult).then_inc(gate_mul.sem, 1)
                        v.wait_ge(gate_mul.sem, t + 1)
                        v.tensor_reduce(logit[:, t, :, :].rearrange("p a h -> p (a h)"), gprod[:, :, :].rearrange("p a (h e) -> p (a h) e", e=HD),
                                        X, ALU.add).then_inc(gate_sum.sem, 1)
            st.restart()

            t_scored = st.event("t_scored", 3)
            t_maxed = st.event("t_maxed", 3)
            t_split = st.event("t_split", 4)
            t_m_up = st.event("t_m_up", 2)
            t_m_in = st.event("t_m_in", 2)
            t_shifted = st.event("t_shifted", 2)
            t_exped = st.event("t_exped", 2)
            t_weighed = st.event("t_weighed", 2)
            t_norm = st.event("t_norm", 5)
            t_remT_up = st.event("t_remT_up", 1)
            t_remT_in = st.event("t_remT_in", 1)
            t_rem_up = st.event("t_rem_up", 1)
            t_mix = st.event("t_mix", 2)
            t_mixT_up = st.event("t_mixT_up", 1)
            t_mixT_in = st.event("t_mixT_in", 1)
            t_y_up = st.event("t_y_up", 1)
            t_done = st.event("t_done", 1)
            strip = lambda j: slice(32 * j, 32 * j + HD)
            with nc.Block() as block:
                @block.tensor
                def _(pe):
                    for t in range(TPB):
                        f, own = min(t, 1), slice(t * P, (t + 1) * P)
                        carry = WIN if t else 0
                        pe.wait_ge(t_done.sem, t)
                        for half in range(2):
                            for j in range(4):
                                out = bank[2 * j + half].rearrange("p (a k) -> p a k", a=2)[:, :, WIN - carry:WIN + P]
                                pe.matmul(out, identb[:, :], spread(mask[:, f, WIN - carry:], 1, 2), start=True, stop=False, skip_group_check=True)
                                for c2 in range(2):
                                    c = 2 * half + c2
                                    m = pe.matmul(out[:, c2, :], qT[strip(j), c, own], kT[strip(j), c, t * P - carry:(t + 1) * P],
                                                  start=False, stop=True, skip_group_check=True, tile_position=(32 * j, 0))
                            m.then_inc(t_scored.sem, 1)
                        pe.wait_ge(t_split.sem, t_split.at(t, 2))
                        pe.transpose(bank[0].bitcast(BF16)[0:2 * H, 0:P], hl[:, :, :].rearrange("p a h -> p (a h)"), identb[:, :]).then_inc(t_m_up.sem, 1)
                        pe.wait_ge(t_m_in.sem, t_m_in.at(t, 1))
                        for j in range(4):
                            for a in range(1 + f):
                                n = (P, WIN)[a]
                                out = bank[2 * j + a][0:n].rearrange("p (c k) -> p c k", c=G)
                                lo = (t * P, t * P - WIN)[a]
                                pe.matmul(out, identb[:, 0:n], spread(maskt[:, f, a, :], 1, G), start=True, stop=False, skip_group_check=True)
                                for c in range(G):
                                    col = 4 * j + c
                                    pe.matmul(out[:, c, :], sel[:, col, 0:n], nmT[:, :], start=False, stop=False, skip_group_check=True)
                                    m = pe.matmul(out[:, c, :], kT[strip(j), c, lo:lo + n], qT[strip(j), c, own],
                                                  start=False, stop=True, skip_group_check=True, tile_position=(32 * j, 0))
                        m.then_inc(t_shifted.sem, 1)
                        pe.wait_ge(t_exped.sem, t_exped.at(t, 1))
                        for j in range(4):
                            for c in range(G):
                                h = 4 * c + j
                                out = bank[0][:, h * 9:h * 9 + 9]
                                m = pe.matmul(out, pt[:, j, c, :], va[:, t, h, :], start=True, stop=not t, skip_group_check=True)
                                if t:
                                    m = pe.matmul(out, pc[:, j, c, :], vc[:, t, h, :], start=False, stop=True, skip_group_check=True)
                        m.then_inc(t_weighed.sem, 1)
                        for j in range(4):
                            out = bank[2 * j + 1][:, 0:LG * LAT].rearrange("p (c k) -> p c k", c=LG)
                            pe.matmul(out, identb[:, :], spread(maskl[:, t, :], 1, LG), start=True, stop=False, skip_group_check=True)
                            for c in range(LG):
                                m = pe.matmul(out[:, c, :], gqT[strip(j), c, own], gkT[strip(j), c, :],
                                              start=False, stop=True, skip_group_check=True, tile_position=(32 * j, 0))
                        m.then_inc(t_scored.sem, 1)
                        pe.wait_ge(t_split.sem, t_split.at(t, 4))
                        pe.transpose(bank[2].bitcast(BF16)[0:2 * H, 0:P], hl[:, :, :].rearrange("p a h -> p (a h)"), identb[:, :]).then_inc(t_m_up.sem, 1)
                        pe.wait_ge(t_m_in.sem, t_m_in.at(t, 2))
                        for j in range(4):
                            out = bank[2 * j + 1][0:LAT, 0:LG * P].rearrange("p (c k) -> p c k", c=LG)
                            pe.matmul(out, identb[0:LAT, 0:LAT], spread(masklt[:, t, :], 1, LG), start=True, stop=False, skip_group_check=True)
                            for c in range(LG):
                                pe.matmul(out[:, c, :], sel[:, LG * j + c, 0:LAT], nmT[:, :], start=False, stop=False, skip_group_check=True)
                                m = pe.matmul(out[:, c, :], gkT[strip(j), c, :], gqT[strip(j), c, own],
                                              start=False, stop=True, skip_group_check=True, tile_position=(32 * j, 0))
                        m.then_inc(t_shifted.sem, 1)
                        pe.wait_ge(t_exped.sem, t_exped.at(t, 2))
                        for j in range(4):
                            for c in range(LG):
                                h = 4 * c + j
                                m = pe.matmul(bank[2][:, h * 9:h * 9 + 9], ptl[:, j, c, :], gva[:, h, :], start=True, stop=True, skip_group_check=True)
                        m.then_inc(t_weighed.sem, 1)
                        pe.wait_ge(t_norm.sem, t_norm.at(t, 5))
                        pe.transpose(bank[4][0:LAT, 0:P], rem[:, :], ident[:, :]).then_inc(t_remT_up.sem, 1)
                        pe.wait_ge(t_remT_in.sem, t + 1)
                        pe.matmul(bank[4][:, 0:DIM], remT[:, :], wr[:, :], start=True, stop=True).then_inc(t_rem_up.sem, 1)
                        pe.wait_ge(t_mix.sem, t_mix.at(t, 2))
                        pe.transpose(bank[6][:, 0:P], mix[:, :], ident[:, :]).then_inc(t_mixT_up.sem, 1)
                        pe.wait_ge(t_mixT_in.sem, t + 1)
                        pe.matmul(bank[6][:, P:P + DIM], mixT[:, :], wo[:, :], start=True, stop=True).then_inc(t_y_up.sem, 1)

                @block.scalar
                def _(act):
                    for t in range(TPB):
                        act.wait_ge(t_shifted.sem, t_shifted.at(t, 1))
                        own = all8[:, 0:8:2, :]
                        m = act.activation(pt[:, :, :, :].rearrange("p j c k -> p j (c k)"), own, ACT.Exp)
                        if t:
                            m = act.activation(pc[:, :, :, :].rearrange("p j c k -> p j (c k)"), all8[0:WIN, 1:8:2, :], ACT.Exp)
                        m.then_inc(t_exped.sem, 1)
                        act.wait_ge(t_shifted.sem, t_shifted.at(t, 2))
                        act.activation(ptl[:, :, :, :].rearrange("p j c k -> p j (c k)"), all8[0:LAT, 1:8:2, 0:LG * P], ACT.Exp).then_inc(t_exped.sem, 1)
                        act.wait_ge(t_remT_up.sem, t + 1)
                        act.activation(remT[:, :], bank[4][0:LAT, 0:P], ACT.Copy).then_inc(t_remT_in.sem, 1)
                        act.wait_ge(t_mixT_up.sem, t + 1)
                        act.activation(mixT[:, :], bank[6][:, 0:P], ACT.Copy).then_inc(t_mixT_in.sem, 1)

                @block.vector
                def _(v):
                    def split(t, k, src, up, n):
                        v.tensor_copy(hl[:, 0, 0:n], nmax[:, 0:n]).then_inc(t_split.sem, 1)
                        v.wait_ge(t_split.sem, t_split.at(t, 2 * k + 1))
                        v.tensor_tensor(hl[:, 1, 0:n], nmax[:, 0:n], hl[:, 0, 0:n], ALU.subtract).then_inc(t_split.sem, 1)
                        v.wait_ge(t_m_up.sem, t_m_up.at(t, k + 1))
                        v.tensor_copy(nmT[0:2 * H, :], src).then_inc(t_m_in.sem, 1)

                    for t in range(TPB):
                        carry = WIN if t else 0
                        for half in range(2):
                            v.wait_ge(t_scored.sem, t_scored.at(t, half + 1))
                            for j in range(4):
                                m = v.tensor_reduce(nmax[:, 4 * j + 2 * half:4 * j + 2 * half + 2],
                                                    bank[2 * j + half].rearrange("p (a k) -> p a k", a=2)[:, :, WIN - carry:WIN + P],
                                                    X, ALU.max, negate=True)
                            m.then_inc(t_maxed.sem, 1)
                        v.wait_ge(t_maxed.sem, t_maxed.at(t, 2))
                        split(t, 0, bank[0].bitcast(BF16)[0:2 * H, 0:P], t_m_up, H)
                        v.wait_ge(t_weighed.sem, t_weighed.at(t, 1))
                        out = bank[0][:, 0:H * 9].rearrange("p (h e) -> p h e", e=9)
                        v.reciprocal(rden[:, :], out[:, :, HD]).then_inc(t_norm.sem, 1)
                        v.wait_ge(t_norm.sem, t_norm.at(t, 1))
                        v.tensor_tensor(rden[:, :], rden[:, :], gates[:, t, 0, :], ALU.mult).then_inc(t_norm.sem, 1)
                        v.wait_ge(t_norm.sem, t_norm.at(t, 2))
                        v.tensor_tensor(loc[:, :].rearrange("p (h e) -> p h e", e=HD), out[:, :, 0:HD], spread(rden[:, :], 2, HD), ALU.mult).then_inc(t_norm.sem, 1)
                        v.wait_ge(t_scored.sem, t_scored.at(t, 3))
                        for j in range(4):
                            m = v.tensor_reduce(nmax[:, LG * j:LG * j + LG], bank[2 * j + 1][:, 0:LG * LAT].rearrange("p (c k) -> p c k", c=LG),
                                                X, ALU.max, negate=True)
                        m.then_inc(t_maxed.sem, 1)
                        v.wait_ge(t_maxed.sem, t_maxed.at(t, 3))
                        split(t, 1, bank[2].bitcast(BF16)[0:2 * H, 0:P], t_m_up, LH)
                        v.wait_ge(t_weighed.sem, t_weighed.at(t, 2))
                        outl = bank[2][:, 0:LH * 9].rearrange("p (h e) -> p h e", e=9)
                        v.reciprocal(rdl[:, :], outl[:, :, HD]).then_inc(t_norm.sem, 1)
                        v.wait_ge(t_norm.sem, t_norm.at(t, 4))
                        v.tensor_tensor(rem[:, :].rearrange("p (h e) -> p h e", e=HD), outl[:, :, 0:HD], spread(rdl[:, :], 2, HD), ALU.mult).then_inc(t_norm.sem, 1)
                        v.wait_ge(t_rem_up.sem, t + 1)
                        v.tensor_tensor(remg[:, :].rearrange("p (h e) -> p h e", e=HD), bank[4][:, 0:DIM].rearrange("p (h e) -> p h e", e=HD),
                                        spread(gates[:, t, 1, :], 2, HD), ALU.mult).then_inc(t_mix.sem, 1)
                        v.wait_ge(t_mix.sem, t_mix.at(t, 1))
                        v.tensor_tensor(mix[:, :], loc[:, :], remg[:, :], ALU.add).then_inc(t_mix.sem, 1)
                        v.wait_ge(t_y_up.sem, t + 1)
                        v.tensor_copy(s[:, bass.ds(b * TPB + t, 1), :].rearrange("p a c -> p (a c)"), bank[6][:, P:P + DIM]).then_inc(t_done.sem, 1)
            st.restart()


def ffn0(nc, g, d):
    HID, BL = 352, 16
    HC = [(c, min(P, HID - c)) for c in range(0, HID, P)]
    u, ident, xn = g["u"], g["ident"], g["xn"]
    MAXN = TPB * HID
    with Stage(nc, "f0") as st:
        wgu = st.sb("wgu", [P, 2, len(HC), DIM])
        wd = st.sb("wd", [P, HID])
        wguT = st.sb("wguT", [P, 2, HID])
        wdT = st.sb("wdT", [P, len(HC), DIM])
        src = st.sb("src", [P, MAXN])
        mag = st.sb("mag", [P, MAXN])
        sgn = st.sb("sgn", [P, MAXN])
        acc = st.sb("acc", [P, MAXN])
        low = st.sb("low", [P, MAXN])
        scale = st.sb("scale", [P, MAXN // BL])
        inverse = st.sb("inverse", [P, MAXN // BL])
        xqT = st.sb("xqT", [P, SEQ])
        sil = st.sb("sil", [P, 2, HID])
        hqT = st.sb("hqT", [P, len(HC), SEQ])
        bank = [st.bank(f"bank{i}") for i in range(8)]
        loaded = st.sem("loaded")
        zeroed = st.sem("zeroed")

        STEPS = 14

        def round_fp4(v, stepped, base, signed, sign_at, n):
            a, q, lo = (z[:, 0:n] for z in (mag, acc, low))
            blk = lambda z: z.rearrange("p (k e) -> p k e", e=BL)
            sc = scale[:, 0:n // BL]
            k = base

            def step(m):
                nonlocal k
                k += 1
                m.then_inc(stepped.sem, 1)
                v.wait_ge(stepped.sem, k)

            v.wait_ge(signed.sem, sign_at)
            step(v.tensor_reduce(sc, blk(a), X, ALU.max))
            step(v.tensor_scalar(sc, sc, 1.0 / 6.0, 1e-12, ALU.mult, ALU.max))
            step(v.reciprocal(inverse[:, 0:n // BL], sc))
            step(v.tensor_tensor(blk(a), blk(a), spread(inverse[:, 0:n // BL], 2, BL), ALU.mult))
            step(v.tensor_scalar(q, a, 5.0, 2.0, ALU.is_gt, ALU.mult))
            for mid in (3.5, 2.5):
                step(v.scalar_tensor_tensor(out=q, in0=a, scalar=mid, in1=q, op0=ALU.is_gt, op1=ALU.add))
            step(v.tensor_scalar(lo, a, 1.75, None, ALU.is_gt))
            for mid in (1.25, 0.75, 0.25):
                step(v.scalar_tensor_tensor(out=lo, in0=a, scalar=mid, in1=lo, op0=ALU.is_gt, op1=ALU.add))
            step(v.scalar_tensor_tensor(out=q, in0=lo, scalar=0.5, in1=q, op0=ALU.mult, op1=ALU.add))
            step(v.tensor_tensor(q, q, sgn[:, 0:n], ALU.mult))
            step(v.tensor_tensor(blk(q), blk(q), spread(sc, 2, BL), ALU.mult))

        stepped = st.event("stepped")
        staged = st.event("staged")
        signed = st.event("signed")
        turned = st.event("turned")
        placed = st.event("placed")
        NW = 2 * len(HC) * DIM
        with nc.Block() as block:
            @block.gpsimd
            def _(pool):
                pool.memset(wgu[:, :, :, :], 0.0).then_inc(zeroed, 1)

            @block.sync
            def _(sp):
                sp.wait_ge(zeroed, 1)
                for k, name in enumerate(("gate", "up")):
                    w = d[f"L0_ffn_w_{name}"]
                    sp.dma_start(wgu[:, k, 0:2, :], w[0:2 * P, :].rearrange("(c p) n -> p c n", p=P)).then_inc(loaded, 16)
                    sp.dma_start(wgu[0:HID - 2 * P, k, 2, :], w[2 * P:HID, :]).then_inc(loaded, 16)
                sp.dma_start(wd[:, :], d["L0_ffn_w_down"]).then_inc(loaded, 16)
                sp.wait_ge(loaded, 5 * 16)

            @block.vector
            def _(v):
                v.wait_ge(loaded, 5 * 16)
                v.wait_ge(zeroed, 1)
                v.tensor_copy(src[:, 0:NW], wgu[:, :, :, :].rearrange("p a c n -> p (a c n)")).then_inc(staged.sem, 1)
                v.tensor_copy(src[:, NW:NW + HID], wd[:, :]).then_inc(staged.sem, 1)
                v.wait_ge(staged.sem, 2)
                round_fp4(v, stepped, 0, signed, 2, NW + HID)

            @block.scalar
            def _(act):
                act.wait_ge(staged.sem, 2)
                act.activation(mag[:, 0:NW + HID], src[:, 0:NW + HID], ACT.Abs).then_inc(signed.sem, 1)
                act.activation(sgn[:, 0:NW + HID], src[:, 0:NW + HID], ACT.Sign).then_inc(signed.sem, 1)
                for k in range(2):
                    act.wait_ge(turned.sem, k + 1)
                    act.activation(wguT[:, k, :], bank[k][:, 0:HID], ACT.Copy).then_inc(placed.sem, 1)
                act.wait_ge(turned.sem, 3)
                for c, (at, size) in enumerate(HC):
                    act.activation(wdT[0:size, c, :], bank[2][0:size, c * P:(c + 1) * P], ACT.Copy).then_inc(placed.sem, 1)

            @block.tensor
            def _(pe):
                pe.wait_ge(stepped.sem, STEPS)
                for k in range(2):
                    for c, (at, size) in enumerate(HC):
                        lo = (k * len(HC) + c) * DIM
                        m = pe.transpose(bank[k][:, at:at + size], acc[0:size, lo:lo + DIM], ident[0:size, 0:size])
                    m.then_inc(turned.sem, 1)
                for c, (at, size) in enumerate(HC):
                    m = pe.transpose(bank[2][0:size, c * P:c * P + P], acc[:, NW + at:NW + at + size], ident[:, :])
                m.then_inc(turned.sem, 1)
        st.restart()

        xqT_up = st.event("xqT_up")
        xqT_in = st.event("xqT_in")
        hid_up = st.event("hid_up")
        silued = st.event("silued")
        hid_in = st.event("hid_in")
        hqT_up = st.event("hqT_up")
        hqT_in = st.event("hqT_in")
        y_up = st.event("y_up")
        y_in = st.event("y_in")
        with nc.Fori(0, BATCH) as b:
            with nc.Block() as block:
                @block.vector
                def _(v):
                    v.tensor_copy(src[:, 0:TPB * DIM], xn[:, bass.ds(b * TPB, TPB), :].rearrange("p t c -> p (t c)")).then_inc(staged.sem, 1)
                    v.wait_ge(staged.sem, 1)
                    round_fp4(v, stepped, 0, signed, 2, TPB * DIM)
                    for t in range(TPB):
                        v.wait_ge(silued.sem, t + 1)
                        v.tensor_tensor(src[:, t * HID:(t + 1) * HID], sil[:, t % 2, :], bank[2 * (t % 2) + 1][:, 0:HID], ALU.mult).then_inc(hid_in.sem, 1)
                    v.wait_ge(hid_in.sem, TPB)
                    v.wait_ge(xqT_up.sem, 1)
                    round_fp4(v, stepped, STEPS, signed, 4, MAXN)
                    for t in range(TPB):
                        v.wait_ge(y_up.sem, t + 1)
                        v.tensor_copy(u[:, bass.ds(b * TPB + t, 1), :].rearrange("p a c -> p (a c)"), bank[4 + t][:, 0:DIM]).then_inc(y_in.sem, 1)

                @block.scalar
                def _(act):
                    act.wait_ge(staged.sem, 1)
                    act.activation(mag[:, 0:TPB * DIM], src[:, 0:TPB * DIM], ACT.Abs).then_inc(signed.sem, 1)
                    act.activation(sgn[:, 0:TPB * DIM], src[:, 0:TPB * DIM], ACT.Sign).then_inc(signed.sem, 1)
                    act.wait_ge(xqT_up.sem, 1)
                    act.activation(xqT[:, :], bank[4][:, :], ACT.Copy).then_inc(xqT_in.sem, 1)
                    for t in range(TPB):
                        act.wait_ge(hid_up.sem, t + 1)
                        if t >= 2:
                            act.wait_ge(hid_in.sem, t - 1)
                        act.activation(sil[:, t % 2, :], bank[2 * (t % 2)][:, 0:HID], ACT.Silu).then_inc(silued.sem, 1)
                    act.wait_ge(hid_in.sem, TPB)
                    act.activation(mag[:, :], src[:, :], ACT.Abs).then_inc(signed.sem, 1)
                    act.activation(sgn[:, :], src[:, :], ACT.Sign).then_inc(signed.sem, 1)
                    for c, (at, size) in enumerate(HC):
                        act.wait_ge(hqT_up.sem, c + 1)
                        act.activation(hqT[0:size, c, :], bank[c][0:size, :], ACT.Copy).then_inc(hqT_in.sem, 1)

                @block.tensor
                def _(pe):
                    pe.wait_ge(stepped.sem, STEPS)
                    for t in range(TPB):
                        m = pe.transpose(bank[4][:, t * P:(t + 1) * P], acc[:, t * DIM:(t + 1) * DIM], ident[:, :])
                    m.then_inc(xqT_up.sem, 1)
                    pe.wait_ge(xqT_in.sem, 1)
                    for t in range(TPB):
                        if t >= 2:
                            pe.wait_ge(hid_in.sem, t - 1)
                        pe.matmul(bank[2 * (t % 2)][:, 0:HID], xqT[:, t * P:(t + 1) * P], wguT[:, 0, :], start=True, stop=True)
                        pe.matmul(bank[2 * (t % 2) + 1][:, 0:HID], xqT[:, t * P:(t + 1) * P], wguT[:, 1, :], start=True, stop=True).then_inc(hid_up.sem, 1)
                    pe.wait_ge(stepped.sem, 2 * STEPS)
                    for c, (at, size) in enumerate(HC):
                        for t in range(TPB):
                            m = pe.transpose(bank[c][0:size, t * P:(t + 1) * P], acc[:, t * HID + at:t * HID + at + size], ident[:, :])
                        m.then_inc(hqT_up.sem, 1)
                    pe.wait_ge(hqT_in.sem, len(HC))
                    for t in range(TPB):
                        for c, (at, size) in enumerate(HC):
                            m = pe.matmul(bank[4 + t][:, 0:DIM], hqT[0:size, c, t * P:(t + 1) * P], wdT[0:size, c, :],
                                          start=(c == 0), stop=(c == len(HC) - 1))
                        m.then_inc(y_up.sem, 1)
            st.restart()


def attention1(nc, g, d):
    H, HD = 16, 64
    PAIRS = H // 2
    s, ident, identb, xnT = g["s"], g["ident"], g["identb"], g["xnT"]
    with Stage(nc, "a1") as st:
        wq = st.sb("wq", [P, H * HD])
        wk = st.sb("wk", [P, H * HD])
        wv = st.sb("wv", [P, H * HD])
        wu = st.sb("wu", [P, PAIRS, DIM])
        bu = st.sb("bu", [1, DIM])
        ones = st.sb("ones", [1, P])
        maskq = st.sb("maskq", [P, P], BF16)
        maskk = st.sb("maskk", [P, P], BF16)
        sel = st.sb("sel", [2 * H, H, P], BF16)
        xb = st.sb("xb", [P, SEQ])
        qT = st.sb("qT", [P, PAIRS, SEQ])
        kT = st.sb("kT", [P, PAIRS, SEQ])
        va = st.sb("va", [P, TPB, H, HD + 1])
        nmax = st.sb("nmax", [P, TPB, H])
        hl = st.sb("hl", [P, TPB, 2, H], BF16)
        nmT = st.sb("nmT", [2 * H, SEQ], BF16)
        pt = st.sb("pt", [P, 2, TPB, SEQ])
        rden = st.sb("rden", [P, 2, TPB])
        o = st.sb("o", [P, TPB, H * HD])
        oT = st.sb("oT", [P, 2, PAIRS, P])
        bank = [st.bank(f"bank{i}") for i in range(8)]
        loaded = st.sem("loaded")
        zeroed = st.sem("zeroed")
        xb_in = st.event("xb_in")
        NPROJ = 2 * PAIRS + 2 * TPB
        proj = st.event("proj", NPROJ)
        proj_in = st.event("proj_in")
        projv_in = st.event("projv_in")
        scored = st.event("scored")
        maxed = st.event("maxed")
        split = st.event("split")
        m_up = st.event("m_up")
        m_in = st.event("m_in")
        shifted = st.event("shifted")
        exped = st.event("exped", 3)
        weighed = st.event("weighed")
        recip = st.event("recip")
        o_in = st.event("o_in")
        oT_up = st.event("oT_up")
        oT_in = st.event("oT_in")
        y_up = st.event("y_up")
        y_in = st.event("y_in")

        with nc.Block() as block:
            @block.sync
            def _(sp):
                sp.dma_start(wq[:, :], d["L1_attn_w_q"]).then_inc(loaded, 16)
                sp.dma_start(wk[:, :], d["L1_attn_w_k"]).then_inc(loaded, 16)
                sp.dma_start(wv[:, :], d["L1_attn_w_v"]).then_inc(loaded, 16)
                sp.dma_start(wu[:, :, :], d["L1_attn_w_u"].rearrange("(c p) n -> p c n", p=P)).then_inc(loaded, 16)
                sp.dma_start(bu[:, :], d["L1_attn_b_u"].rearrange("(a n) -> a n", a=1)).then_inc(loaded, 16)
                sp.dma_start(maskq[:, :], d["c_causal"][0]).then_inc(loaded, 16)
                sp.dma_start(maskk[:, :], d["c_causal"][1]).then_inc(loaded, 16)
                sp.dma_start(sel[:, :, :], d["c_sel16"]).then_inc(loaded, 16)
                sp.wait_ge(loaded, 8 * 16)

            @block.gpsimd
            def _(pool):
                pool.memset(va[:, :, :, :], 1.0).then_inc(zeroed, 1)
                pool.memset(ones[:, :], 1.0).then_inc(zeroed, 1)

        def spot(j):
            return {0: (0, 0), 1: (1, 0), 2: (2, 0), 3: (1, 3 * P)}[j]

        with nc.Fori(0, BATCH) as b:
            with nc.Block() as block:
                @block.tensor
                def _(pe):
                    pe.wait_ge(xb_in.sem, 1)
                    for n in range(NPROJ):
                        if n >= 8:
                            pe.wait_ge((proj_in, projv_in)[n % 2].sem, (n - 8) // 2 + 1)
                        if n < 2 * PAIRS:
                            w = (wq, wk)[n // PAIRS]
                            c = n % PAIRS
                            m = pe.matmul(bank[n % 8][:, :], w[:, c * P:(c + 1) * P], xb[:, :], start=True, stop=True)
                        else:
                            t, c = divmod(n - 2 * PAIRS, 2)
                            m = pe.matmul(bank[n % 8][:, :], xb[:, t * P:(t + 1) * P], wv[:, c * 512:(c + 1) * 512], start=True, stop=True)
                        m.then_inc(proj.sem, 1)
                    pe.wait_ge(proj_in.sem, NPROJ // 2)
                    pe.wait_ge(projv_in.sem, NPROJ // 2)
                    for t in range(TPB):
                        for c in range(PAIRS):
                            n = t * PAIRS + c
                            if n >= 4:
                                pe.wait_ge(maxed.sem, n - 3)
                            for p in range(2):
                                rows = slice(64 * p, 64 * p + 64)
                                out = bank[2 * (n % 4) + p]
                                pe.matmul(out[:, 0:(t + 1) * P], qT[rows, c, t * P:(t + 1) * P], kT[rows, c, 0:(t + 1) * P],
                                          start=True, stop=False, skip_group_check=True)
                                m = pe.matmul(out[:, t * P:(t + 1) * P], identb[:, :], maskq[:, :],
                                              start=False, stop=True, skip_group_check=True)
                            m.then_inc(scored.sem, 1)
                    pe.wait_ge(split.sem, 2)
                    for t in range(TPB):
                        m = pe.transpose(bank[7][:, 0:SEQ // 2].bitcast(BF16)[0:2 * H, t * P:(t + 1) * P], hl[:, t, :, :].rearrange("p a h -> p (a h)"),
                                         identb[:, :])
                    m.then_inc(m_up.sem, 1)
                    pe.wait_ge(m_in.sem, 1)

                    def shift(h):
                        p, c = h % 2, h // 2
                        rows = slice(64 * p, 64 * p + 64)
                        if h >= 2:
                            pe.wait_ge(exped.sem, 3 * (h - 1))
                        for j in range(TPB):
                            k, at = spot(j)
                            n = (TPB - j) * P
                            out = bank[3 * p + k][:, at:at + n]
                            pe.matmul(out, sel[:, h, :], nmT[:, j * P:SEQ], start=True, stop=False, skip_group_check=True)
                            pe.matmul(out[:, 0:P], identb[:, :], maskk[:, :], start=False, stop=False, skip_group_check=True)
                            m = pe.matmul(out, kT[rows, c, j * P:(j + 1) * P], qT[rows, c, j * P:SEQ],
                                          start=False, stop=True, skip_group_check=True)
                        m.then_inc(shifted.sem, 1)

                    def weigh(h):
                        pe.wait_ge(exped.sem, 3 * (h + 1))
                        if h >= 2:
                            pe.wait_ge(o_in.sem, h - 1)
                        for i in range(TPB):
                            for j in range(i + 1):
                                m = pe.matmul(bank[6 + h % 2][:, i * 65:i * 65 + 65], pt[:, h % 2, j, i * P:(i + 1) * P], va[:, j, h, :],
                                              start=(j == 0), stop=(j == i), skip_group_check=True)
                        m.then_inc(weighed.sem, 1)

                    for h in range(H + 1):
                        if h < H:
                            shift(h)
                        if h >= 1:
                            weigh(h - 1)
                    pe.wait_ge(o_in.sem, H)
                    for t in range(TPB):
                        for half in range(2):
                            n = 2 * t + half
                            if n >= 4:
                                pe.wait_ge(oT_in.sem, n - 3)
                            for j in range(4):
                                c = 4 * half + j
                                m = pe.transpose(bank[n % 4][:, j * P:(j + 1) * P], o[:, t, c * P:(c + 1) * P], ident[:, :])
                            m.then_inc(oT_up.sem, 1)
                        pe.wait_ge(oT_in.sem, 2 * t + 2)
                        if t >= 2:
                            pe.wait_ge(y_in.sem, t - 1)
                        for c in range(PAIRS):
                            pe.matmul(bank[4 + t % 2][:, 0:DIM], oT[:, t % 2, c, :], wu[:, c, :], start=(c == 0), stop=False)
                        pe.matmul(bank[4 + t % 2][:, 0:DIM], ones[:, :], bu[:, :], start=False, stop=True).then_inc(y_up.sem, 1)

                def evacuate(n, copy):
                    src = bank[n % 8]
                    if n < PAIRS:
                        return copy(qT[:, n, :], src[:, :], 1.0 / HD)
                    if n < 2 * PAIRS:
                        return copy(kT[:, n - PAIRS, :], src[:, :], 1.0)
                    t, c = divmod(n - 2 * PAIRS, 2)
                    return copy(va[:, t, 8 * c:8 * c + 8, 0:HD], src[:, :].rearrange("p (h d) -> p h d", h=8), 1.0)

                @block.scalar
                def _(act):
                    act.activation(xb[:, :], xnT[:, bass.ds(b * SEQ, SEQ)], ACT.Copy).then_inc(xb_in.sem, 1)
                    for n in range(0, NPROJ, 2):
                        act.wait_ge(proj.sem, n + 1)
                        evacuate(n, lambda dst, src, k: act.activation(dst, src, ACT.Copy, scale=k)).then_inc(proj_in.sem, 1)
                    for h in range(H):
                        act.wait_ge(shifted.sem, h + 1)
                        if h >= 2:
                            act.wait_ge(weighed.sem, h - 1)
                        for js in ((0,), (1, 3), (2,)):
                            for j in js:
                                k, at = spot(j)
                                m = act.activation(pt[:, h % 2, j, j * P:SEQ], bank[3 * (h % 2) + k][:, at:at + (TPB - j) * P], ACT.Exp)
                            m.then_inc(exped.sem, 1)
                    for n in range(2 * TPB):
                        act.wait_ge(oT_up.sem, n + 1)
                        if n >= 4:
                            act.wait_ge(y_in.sem, n // 2 - 1)
                        act.activation(oT[:, (n // 2) % 2, 4 * (n % 2):4 * (n % 2) + 4, :].rearrange("p a b -> p (a b)"), bank[n % 4][:, :],
                                       ACT.Copy).then_inc(oT_in.sem, 1)

                @block.vector
                def _(v):
                    for n in range(1, NPROJ, 2):
                        v.wait_ge(proj.sem, n + 1)
                        evacuate(n, lambda dst, src, k: v.tensor_scalar(dst, src, k, None, ALU.mult)).then_inc(projv_in.sem, 1)
                    for t in range(TPB):
                        for c in range(PAIRS):
                            n = t * PAIRS + c
                            v.wait_ge(scored.sem, n + 1)
                            for p in range(2):
                                m = v.tensor_reduce(nmax[:, t, 2 * c + p:2 * c + p + 1], bank[2 * (n % 4) + p][:, 0:(t + 1) * P], X, ALU.max, negate=True)
                            m.then_inc(maxed.sem, 1)
                    v.wait_ge(maxed.sem, TPB * PAIRS)
                    v.tensor_copy(hl[:, :, 0, :], nmax[:, :, :]).then_inc(split.sem, 1)
                    v.wait_ge(split.sem, 1)
                    v.tensor_tensor(hl[:, :, 1, :], nmax[:, :, :], hl[:, :, 0, :], ALU.subtract).then_inc(split.sem, 1)
                    v.wait_ge(m_up.sem, 1)
                    v.tensor_copy(nmT[:, :], bank[7][:, 0:SEQ // 2].bitcast(BF16)[0:2 * H, :]).then_inc(m_in.sem, 1)
                    for h in range(H):
                        v.wait_ge(weighed.sem, h + 1)
                        out = bank[6 + h % 2][:, 0:TPB * 65].rearrange("p (t e) -> p t e", t=TPB)
                        v.reciprocal(rden[:, h % 2, :], out[:, :, HD]).then_inc(recip.sem, 1)
                        v.wait_ge(recip.sem, h + 1)
                        v.tensor_tensor(o[:, :, h * HD:(h + 1) * HD], out[:, :, 0:HD], spread(rden[:, h % 2, :], 2, HD), ALU.mult).then_inc(o_in.sem, 1)
                    for t in range(TPB):
                        v.wait_ge(y_up.sem, t + 1)
                        v.tensor_copy(s[:, bass.ds(b * TPB + t, 1), :].rearrange("p a c -> p (a c)"), bank[4 + t % 2][:, 0:DIM]).then_inc(y_in.sem, 1)
            st.restart()


def ffn1(nc, g, d):
    HID, C = 512, 4
    u, xnT = g["u"], g["xnT"]
    with Stage(nc, "f1") as st:
        w1 = st.sb("w1", [P, HID])
        w2 = st.sb("w2", [P, HID])
        h1 = st.sb("h1", [P, C, HID])
        h2 = st.sb("h2", [P, C, HID])
        w3 = st.sb("w3", [P, C, DIM])
        sc = st.sb("sc", [P, 4, C])
        s3 = st.sb("s3", [P, DIM])
        xb = st.sb("xb", [P, SEQ])
        a1 = st.sb("a1", [P, C, SEQ])
        a2 = st.sb("a2", [P, C, SEQ])
        a3 = st.sb("a3", [P, C, SEQ])
        bank = [st.bank(f"bank{i}") for i in range(8)]
        loaded = st.sem("loaded")
        xb_in = st.event("xb_in")
        first = st.event("first", C)
        silued = st.event("silued", C)
        gated = st.event("gated", C)
        second = st.event("second", C)
        gelu1 = st.event("gelu1", C)
        third = st.event("third", C)
        gelu2 = st.event("gelu2", C)
        y_up = st.event("y_up", TPB)
        y_in = st.event("y_in", TPB)
        with nc.Block() as block:
            @block.sync
            def _(sp):
                sp.dma_start(w1[:, :], d["t_L1_ffn_w1_w"]).then_inc(loaded, 16)
                sp.dma_start(w2[:, :], d["t_L1_ffn_w2_w"]).then_inc(loaded, 16)
                sp.dma_start(h1[:, :, :], d["t_L1_ffn_h1_w"].rearrange("(c p) n -> p c n", p=P)).then_inc(loaded, 16)
                sp.dma_start(h2[:, :, :], d["t_L1_ffn_h2_w"].rearrange("(c p) n -> p c n", p=P)).then_inc(loaded, 16)
                sp.dma_start(w3[:, :, :], d["t_L1_ffn_w3_w"].rearrange("(c p) n -> p c n", p=P)).then_inc(loaded, 16)
                for k, name in enumerate(("w1", "w2", "h1", "h2")):
                    sp.dma_start(sc[:, k, :], d[f"L1_ffn_{name}_s"].rearrange("(c p) -> p c", p=P), allow_slow_non_contiguous=True).then_inc(loaded, 16)
                sp.dma_start(s3[:, :], d["L1_ffn_w3_s"].rearrange("(a n) -> a n", a=1).to_broadcast([P, DIM])).then_inc(loaded, 16)
                sp.wait_ge(loaded, 10 * 16)

        with nc.Fori(0, BATCH) as b:
            with nc.Block() as block:
                @block.gpsimd
                def _(pool):
                    pool.tensor_copy(xb[:, :], xnT[:, bass.ds(b * SEQ, SEQ)]).then_inc(xb_in.sem, 1)

                @block.tensor
                def _(pe):
                    pe.wait_ge(xb_in.sem, 1)
                    for c in range(C):
                        pe.matmul(bank[2 * c][:, :], w1[:, c * P:(c + 1) * P], xb[:, :], start=True, stop=True)
                        pe.matmul(bank[2 * c + 1][:, :], w2[:, c * P:(c + 1) * P], xb[:, :], start=True, stop=True).then_inc(first.sem, 1)
                    for w, src, ready, done, last in ((h1, a2, gated, second, gated), (h2, a3, gelu1, third, gelu1)):
                        pe.wait_ge(ready.sem, C)
                        for c in range(C):
                            out = bank[c if w is h1 else 4 + c]
                            for k in range(C):
                                m = pe.matmul(out[:, :], w[:, k, c * P:(c + 1) * P], src[:, k, :], start=(k == 0), stop=(k == C - 1))
                            m.then_inc(done.sem, 1)
                    pe.wait_ge(gelu2.sem, C)
                    for t in range(TPB):
                        for k in range(C):
                            m = pe.matmul(bank[t][:, 0:DIM], a2[:, k, t * P:(t + 1) * P], w3[:, k, :], start=(k == 0), stop=(k == C - 1))
                        m.then_inc(y_up.sem, 1)

                @block.scalar
                def _(act):
                    for c in range(C):
                        act.wait_ge(first.sem, c + 1)
                        act.activation(a1[:, c, :], bank[2 * c][:, :], ACT.Silu, scale=sc[:, 0, c:c + 1]).then_inc(silued.sem, 1)
                    for c in range(C):
                        act.wait_ge(second.sem, c + 1)
                        act.activation(a3[:, c, :], bank[c][:, :], ACT.Gelu, scale=sc[:, 2, c:c + 1]).then_inc(gelu1.sem, 1)
                    for c in range(C):
                        act.wait_ge(third.sem, c + 1)
                        act.activation(a2[:, c, :], bank[4 + c][:, :], ACT.Gelu, scale=sc[:, 3, c:c + 1]).then_inc(gelu2.sem, 1)

                @block.vector
                def _(v):
                    for c in range(C):
                        v.wait_ge(silued.sem, c + 1)
                        v.scalar_tensor_tensor(out=a2[:, c, :], in0=bank[2 * c + 1][:, :], scalar=sc[:, 1, c:c + 1], in1=a1[:, c, :],
                                               op0=ALU.mult, op1=ALU.mult).then_inc(gated.sem, 1)
                    for t in range(TPB):
                        v.wait_ge(y_up.sem, t + 1)
                        v.tensor_tensor(u[:, bass.ds(b * TPB + t, 1), :].rearrange("p a c -> p (a c)"), bank[t][:, 0:DIM], s3[:, :],
                                        ALU.mult).then_inc(y_in.sem, 1)
            st.restart()


def attention2(nc, g, d):
    HD, NQ, NKV = 8, 32, 8
    GH = NQ // NKV
    MAPS = BATCH * GH
    LAMBDA_INIT = 0.8 - 0.6 * float(np.exp(-0.3))
    QG, KG = 2 * DIM // HD, NKV * HD // HD
    s, ident, identb, xnT = g["s"], g["ident"], g["identb"], g["xnT"]
    with Stage(nc, "a2") as st:
        w = st.sb("w", [P, 2 * DIM + 2 * NKV * HD + 32])
        wp = st.sb("wp", [P, DIM])
        lam = st.sb("lam", [P, 4, NKV * HD])
        lprod = st.sb("lprod", [P, 2, NKV * HD])
        lsum = st.sb("lsum", [P, 2])
        lexp = st.sb("lexp", [P, 2])
        nlam = st.sb("nlam", [P, 1])
        maskq = st.sb("maskq", [P, P], BF16)
        maskk = st.sb("maskk", [P, P], BF16)
        sel = st.sb("sel", [64, MAPS, P], BF16)
        qT = st.sb("qT", [P, NQ * SEQ])
        kT = st.sb("kT", [P, NKV * SEQ])
        vT = st.sb("vT", [P, NKV * SEQ])
        va = st.sb("va", [P, NKV, TPB, BATCH, HD + 1])
        qs = st.sb("qs", [P, GH, SEQ])
        ks = st.sb("ks", [P, SEQ])
        vs = st.sb("vs", [P, TPB, BATCH, HD + 1])
        nmax = st.sb("nmax", [P, TPB, MAPS])
        hl = st.sb("hl", [P, TPB, 2, MAPS], BF16)
        nmT = st.sb("nmT", [64, SEQ], BF16)
        pt = st.sb("pt", [P, 2, TPB, SEQ])
        rden = st.sb("rden", [P, 2, GH, TPB])
        on = st.sb("on", [P, 2, GH, TPB, HD])
        att = st.sb("att", [P, BATCH, TPB, DIM])
        attT = st.sb("attT", [P, SEQ])
        y1 = st.sb("y1", [P, TPB, DIM])
        y2T = st.sb("y2T", [P, SEQ])
        bank = [st.bank(f"bank{i}") for i in range(8)]
        loaded = st.sem("loaded")
        zeroed = st.sem("zeroed")
        lamd = st.sem("lamd")
        lamx = st.sem("lamx")

        proj = st.event("proj")
        even_in = st.event("even_in")
        odd_in = st.event("odd_in")
        v_up = st.event("v_up")
        v_in = st.event("v_in")
        NG = QG + 2 * KG
        with nc.Block() as block:
            @block.gpsimd
            def _(pool):
                pool.memset(w[:, 2 * DIM + 2 * NKV * HD:], 0.0).then_inc(zeroed, 1)
                pool.memset(va[:, :, :, :, :], 1.0).then_inc(zeroed, 1)
                pool.memset(nmT[:, :], 0.0).then_inc(zeroed, 1)
                pool.memset(sel[:, :, :], 0.0).then_inc(zeroed, 1)

            @block.sync
            def _(sp):
                sp.dma_start(w[:, 0:2 * DIM + 2 * NKV * HD], d["L2_attn_Wqkv"]).then_inc(loaded, 16)
                sp.dma_start(wp[:, :], d["L2_attn_Wproj"]).then_inc(loaded, 16)
                for k, name in enumerate(("q1", "k1", "q2", "k2")):
                    sp.dma_start(lam[:, k, :], d[f"L2_attn_lambda_{name}"].rearrange("(a n) -> a n", a=1).to_broadcast([P, NKV * HD])).then_inc(loaded, 16)
                sp.dma_start(maskq[:, :], d["c_causal"][0]).then_inc(loaded, 16)
                sp.dma_start(maskk[:, :], d["c_causal"][1]).then_inc(loaded, 16)
                sp.wait_ge(zeroed, 4)
                sp.dma_start(sel[0:2 * MAPS, :, :], d["c_sel16"]).then_inc(loaded, 16)
                sp.wait_ge(loaded, 9 * 16)

            @block.tensor
            def _(pe):
                pe.wait_ge(loaded, 9 * 16)
                for n in range(NG):
                    if n >= 8:
                        pe.wait_ge((even_in, odd_in)[n % 2].sem, (n - 8) // 2 + 1)
                    for b in range(BATCH):
                        m = pe.matmul(bank[n % 8][32 * b:32 * b + 32, :], w[:, n * HD:n * HD + 32], xnT[:, b * SEQ:(b + 1) * SEQ],
                                      start=True, stop=True, tile_position=(0, 32 * b))
                    m.then_inc(proj.sem, 1)
                pe.wait_ge(even_in.sem, NG // 2)
                pe.wait_ge(odd_in.sem, NG // 2)
                for h in range(NKV):
                    for t in range(TPB):
                        m = pe.transpose(bank[h][:, t * P:(t + 1) * P], vT[:, h * SEQ + t * P:h * SEQ + (t + 1) * P], ident[:, :])
                    m.then_inc(v_up.sem, 1)

            def place(n, copy):
                if n < QG:
                    return copy(qT[:, :].rearrange("p (t r) -> p t r", r=QG)[:, :, n], bank[n % 8][:, :], HD ** -0.5)
                to, r = (kT, n - QG) if n < QG + KG else (vT, n - QG - KG)
                return copy(to[:, :].rearrange("p (t r) -> p t r", r=KG)[:, :, r], bank[n % 8][:, :], 1.0)

            @block.scalar
            def _(act):
                for n in range(0, NG, 2):
                    act.wait_ge(proj.sem, n + 1)
                    place(n, lambda dst, src, k: act.activation(dst, src, ACT.Copy, scale=k)).then_inc(even_in.sem, 1)
                act.wait_ge(lamd, 2)
                act.activation(lexp[:, :], lsum[:, :], ACT.Exp).then_inc(lamx, 1)

            @block.vector
            def _(v):
                v.wait_ge(loaded, 9 * 16)
                lm = lam[:, :, :].rearrange("p (a c) n -> p a c n", c=2)
                v.tensor_tensor(lprod[:, :, :], lm[:, :, 0, :], lm[:, :, 1, :], ALU.mult).then_inc(lamd, 1)
                v.wait_ge(lamd, 1)
                v.tensor_reduce(lsum[:, :], lprod[:, :, :], X, ALU.add).then_inc(lamd, 1)
                for n in range(1, NG, 2):
                    v.wait_ge(proj.sem, n + 1)
                    place(n, lambda dst, src, k: v.tensor_scalar(dst, src, k, None, ALU.mult)).then_inc(odd_in.sem, 1)
                v.wait_ge(zeroed, 4)
                for h in range(NKV):
                    v.wait_ge(v_up.sem, h + 1)
                    v.tensor_copy(va[:, h, :, :, 0:HD].rearrange("p t b e -> p (t b) e"),
                                  bank[h][:, :].rearrange("p (x e) -> p x e", e=32)[:, :, 0:HD]).then_inc(v_in.sem, 1)
                v.wait_ge(lamx, 1)
                v.tensor_tensor(nlam[:, :], lexp[:, 1:2], lexp[:, 0:1], ALU.subtract).then_inc(lamd, 1)
                v.wait_ge(lamd, 3)
                v.tensor_scalar(nlam[:, :], nlam[:, :], -LAMBDA_INIT, None, ALU.add)
        st.restart()

        staged = st.event("staged")
        scored = st.event("scored")
        maxed = st.event("maxed")
        split = st.event("split")
        m_up = st.event("m_up")
        m_in = st.event("m_in")
        shifted = st.event("shifted")
        exped = st.event("exped")
        weighed = st.event("weighed")
        recip = st.event("recip")
        normed = st.event("normed")
        FILLS = [(0, 0, 4), (1, 0, 2), (1, 2, 2)] + [(t, h, 1) for t in (2, 3) for h in range(GH)]
        SPOT = {0: (0, 0), 1: (1, 0), 2: (2, 0), 3: (1, 3 * P)}

        with nc.Fori(0, NKV) as kv:
            with nc.Block() as block:
                @block.gpsimd
                def _(pool):
                    pool.tensor_copy(qs[:, :, :].rearrange("p h q -> p (h q)"), qT[:, bass.ds(kv * (GH * SEQ), GH * SEQ)]).then_inc(staged.sem, 1)
                    pool.wait_ge(staged.sem, 1)
                    pool.tensor_copy(ks[:, :], kT[:, bass.ds(kv * SEQ, SEQ)]).then_inc(staged.sem, 1)
                    pool.wait_ge(staged.sem, 2)
                    pool.tensor_copy(vs[:, :, :, :].rearrange("p t b e -> p (t b e)"),
                                     va[:, bass.ds(kv, 1), :, :, :].rearrange("p a t b e -> p (a t b e)")).then_inc(staged.sem, 1)

                @block.tensor
                def _(pe):
                    pe.wait_ge(staged.sem, 3)
                    n = 0
                    for b in range(BATCH):
                        rows = slice(32 * b, 32 * b + HD)
                        for t, h0, nh in FILLS:
                            if n >= 8:
                                pe.wait_ge(maxed.sem, n - 7)
                            keys = (t + 1) * P
                            for h in range(nh):
                                out = bank[n % 8][:, h * keys:(h + 1) * keys]
                                pe.matmul(out, qs[rows, h0 + h, t * P:(t + 1) * P], ks[rows, 0:keys],
                                          start=True, stop=False, skip_group_check=True, tile_position=(32 * b, 0))
                                m = pe.matmul(out[:, t * P:keys], identb[:, :], maskq[:, :], start=False, stop=True, skip_group_check=True)
                            m.then_inc(scored.sem, 1)
                            n += 1
                    pe.wait_ge(split.sem, 2)
                    for t in range(TPB):
                        m = pe.transpose(bank[7][:, 0:SEQ // 2].bitcast(BF16)[0:2 * MAPS, t * P:(t + 1) * P],
                                         hl[:, t, :, :].rearrange("p a h -> p (a h)"), identb[:, :])
                    m.then_inc(m_up.sem, 1)
                    pe.wait_ge(m_in.sem, 1)

                    def shift(x):
                        b, h = divmod(x, GH)
                        rows = slice(32 * b, 32 * b + HD)
                        if x >= 2:
                            pe.wait_ge(exped.sem, x - 1)
                        for j in range(TPB):
                            k, at = SPOT[j]
                            n = (TPB - j) * P
                            out = bank[3 * (x % 2) + k][:, at:at + n]
                            pe.matmul(out, sel[:, x, :], nmT[:, j * P:SEQ], start=True, stop=False, skip_group_check=True)
                            pe.matmul(out[:, 0:P], identb[:, :], maskk[:, :], start=False, stop=False, skip_group_check=True)
                            m = pe.matmul(out, ks[rows, j * P:(j + 1) * P], qs[rows, h, j * P:SEQ],
                                          start=False, stop=True, skip_group_check=True, tile_position=(32 * b, 0))
                        m.then_inc(shifted.sem, 1)

                    def weigh(x):
                        b, h = divmod(x, GH)
                        pe.wait_ge(exped.sem, x + 1)
                        if h == 0 and b >= 2:
                            pe.wait_ge(normed.sem, 2 * (b - 1))
                        for i in range(TPB):
                            for j in range(i + 1):
                                at = (h * TPB + i) * (HD + 1)
                                m = pe.matmul(bank[6 + b % 2][:, at:at + HD + 1], pt[:, x % 2, j, i * P:(i + 1) * P], vs[:, j, b, :],
                                              start=(j == 0), stop=(j == i), skip_group_check=True)
                        m.then_inc(weighed.sem, 1)

                    for x in range(MAPS + 1):
                        if x < MAPS:
                            shift(x)
                        if x >= 1:
                            weigh(x - 1)

                @block.scalar
                def _(act):
                    for x in range(MAPS):
                        act.wait_ge(shifted.sem, x + 1)
                        if x >= 2:
                            act.wait_ge(weighed.sem, x - 1)
                        for j in range(TPB):
                            k, at = SPOT[j]
                            m = act.activation(pt[:, x % 2, j, j * P:SEQ], bank[3 * (x % 2) + k][:, at:at + (TPB - j) * P], ACT.Exp)
                        m.then_inc(exped.sem, 1)

                @block.vector
                def _(v):
                    n = 0
                    for b in range(BATCH):
                        for t, h0, nh in FILLS:
                            v.wait_ge(scored.sem, n + 1)
                            v.tensor_reduce(nmax[:, t, b * GH + h0:b * GH + h0 + nh],
                                            bank[n % 8][:, 0:nh * (t + 1) * P].rearrange("p (h k) -> p h k", h=nh),
                                            X, ALU.max, negate=True).then_inc(maxed.sem, 1)
                            n += 1
                    v.wait_ge(maxed.sem, n)
                    v.tensor_copy(hl[:, :, 0, :], nmax[:, :, :]).then_inc(split.sem, 1)
                    v.wait_ge(split.sem, 1)
                    v.tensor_tensor(hl[:, :, 1, :], nmax[:, :, :], hl[:, :, 0, :], ALU.subtract).then_inc(split.sem, 1)
                    v.wait_ge(m_up.sem, 1)
                    v.tensor_copy(nmT[0:2 * MAPS, :], bank[7][:, 0:SEQ // 2].bitcast(BF16)[0:2 * MAPS, :]).then_inc(m_in.sem, 1)
                    for b in range(BATCH):
                        v.wait_ge(weighed.sem, GH * (b + 1))
                        out = bank[6 + b % 2][:, 0:GH * TPB * (HD + 1)].rearrange("p (x e) -> p x e", e=HD + 1)
                        rd = rden[:, b % 2].rearrange("p h t -> p (h t)")
                        v.reciprocal(rd, out[:, :, HD]).then_inc(recip.sem, 1)
                        v.wait_ge(recip.sem, b + 1)
                        v.tensor_tensor(on[:, b % 2].rearrange("p h t e -> p (h t) e"), out[:, :, 0:HD], spread(rd, 2, HD), ALU.mult).then_inc(normed.sem, 1)
                        v.wait_ge(normed.sem, 2 * b + 1)
                        for k in range(2):
                            m = v.scalar_tensor_tensor(out=att[:, b, :, bass.ds(kv * (2 * HD) + k * HD, HD)], in0=on[:, b % 2, 2 * k + 1], scalar=nlam[:, 0:1],
                                                       in1=on[:, b % 2, 2 * k], op0=ALU.mult, op1=ALU.add)
                        m.then_inc(normed.sem, 1)
            st.restart()

        at_up = st.event("at_up")
        at_in = st.event("at_in")
        y1_up = st.event("y1_up")
        y1_in = st.event("y1_in")
        y2_up = st.event("y2_up")
        y2_in = st.event("y2_in")
        y3_up = st.event("y3_up")
        y3_in = st.event("y3_in")
        with nc.Block() as block:
            @block.tensor
            def _(pe):
                for b in range(BATCH):
                    for t in range(TPB):
                        m = pe.transpose(bank[0][:, t * P:(t + 1) * P], att[:, b, t, :], ident[:, :])
                    m.then_inc(at_up.sem, 1)
                    pe.wait_ge(at_in.sem, b + 1)
                    for t in range(TPB):
                        m = pe.matmul(bank[1][:, t * P:(t + 1) * P], attT[:, t * P:(t + 1) * P], wp[:, :], start=True, stop=True)
                    m.then_inc(y1_up.sem, 1)
                    pe.wait_ge(y1_in.sem, b + 1)
                    pe.matmul(bank[2][:, :], wp[:, :], y1[:, :, :].rearrange("p t m -> p (t m)"), start=True, stop=True).then_inc(y2_up.sem, 1)
                    pe.wait_ge(y2_in.sem, b + 1)
                    for t in range(TPB):
                        m = pe.transpose(bank[3][:, t * P:(t + 1) * P], y2T[:, t * P:(t + 1) * P], ident[:, :])
                    m.then_inc(y3_up.sem, 1)
                    pe.wait_ge(y3_in.sem, b + 1)

            @block.scalar
            def _(act):
                for b in range(BATCH):
                    act.wait_ge(at_up.sem, b + 1)
                    act.activation(attT[:, :], bank[0][:, :], ACT.Copy, scale=1.0 - LAMBDA_INIT).then_inc(at_in.sem, 1)
                    act.wait_ge(y2_up.sem, b + 1)
                    act.activation(y2T[:, :].rearrange("p (m t) -> p t m", t=TPB), bank[2][:, :].rearrange("p (t m) -> p t m", t=TPB),
                                   ACT.Copy).then_inc(y2_in.sem, 1)

            @block.vector
            def _(v):
                for b in range(BATCH):
                    v.wait_ge(y1_up.sem, b + 1)
                    v.tensor_copy(y1[:, :, :].rearrange("p t m -> p (t m)"), bank[1][:, :]).then_inc(y1_in.sem, 1)
                    v.wait_ge(y3_up.sem, b + 1)
                    v.tensor_copy(s[:, b * TPB:(b + 1) * TPB, :].rearrange("p t m -> p (t m)"), bank[3][:, :]).then_inc(y3_in.sem, 1)


def attention3(nc, g, d):
    N, T = 16, 16
    CH = SEQ // T
    R = BATCH * CH
    s, ident, xnT = g["s"], g["ident"], g["xnT"]
    with Stage(nc, "a3") as st:
        A = st.sb("A", [P, N, N])
        Bp = st.sb("Bp", [P, N])
        Cp = st.sb("Cp", [P, N])
        Dp = st.sb("Dp", [P, 1])
        wg = st.sb("wg", [P, P])
        bg = st.sb("bg", [P, 1])
        gam = st.sb("gam", [P, DIM])
        bet = st.sb("bet", [P, DIM])
        gate = st.sb("gate", [P, TILES * P])
        xg = st.sb("xg", [P, TILES * P])
        V = st.sb("V", [P, T, N])
        W = st.sb("W", [P, T + 1, N])
        h = st.sb("h", [P, T])
        h0 = st.sb("h0", [P, 1])
        pw = st.sb("pw", [P, 2, N, N])
        prod = st.sb("prod", [P, N, N, N])
        tmp = st.sb("tmp", [P, N, N])
        y = st.sb("y", [P, R, T])
        U = st.sb("U", [P, N, R])
        S = st.sb("S", [P, CH + 1, BATCH, N])
        rec = st.sb("rec", [P, BATCH, N])
        stats = st.sb("stats", [P, TPB, 6])
        mv = st.sb("mv", [P, TPB, 2])
        vare = st.sb("vare", [P, TPB])
        rstd = st.sb("rstd", [P, TPB])
        ln = st.sb("ln", [P, TPB, DIM])
        bank = [st.bank(f"bank{i}") for i in range(8)]
        loaded = st.sem("loaded")

        gated_up = st.event("gated_up")
        sig_in = st.event("sig_in")
        xg_in = st.event("xg_in")
        did = st.event("did")
        powd = st.event("powd")
        with nc.Block() as block:
            @block.sync
            def _(sp):
                sp.dma_start(A[:, :, :], d["L3_attn_A"]).then_inc(loaded, 16)
                sp.dma_start(Bp[:, :], d["L3_attn_Bp"]).then_inc(loaded, 16)
                sp.dma_start(Cp[:, :], d["L3_attn_Cp"]).then_inc(loaded, 16)
                sp.dma_start(Dp[:, :], d["L3_attn_Dp"].rearrange("(p a) -> p a", a=1)).then_inc(loaded, 16)
                sp.dma_start(wg[:, :], d["t_L3_attn_Wg"]).then_inc(loaded, 16)
                sp.dma_start(bg[:, :], d["L3_attn_bg"].rearrange("(p a) -> p a", a=1)).then_inc(loaded, 16)
                sp.dma_start(gam[:, :], d["L3_attn_gamma"].rearrange("(a n) -> a n", a=1).to_broadcast([P, DIM])).then_inc(loaded, 16)
                sp.dma_start(bet[:, :], d["L3_attn_beta"].rearrange("(a n) -> a n", a=1).to_broadcast([P, DIM])).then_inc(loaded, 16)
                sp.wait_ge(loaded, 8 * 16)

            @block.tensor
            def _(pe):
                pe.wait_ge(loaded, 8 * 16)
                for b in range(BATCH):
                    pe.matmul(bank[b][:, :], wg[:, :], xnT[:, b * SEQ:(b + 1) * SEQ], start=True, stop=True).then_inc(gated_up.sem, 1)

            @block.scalar
            def _(act):
                for b in range(BATCH):
                    act.wait_ge(gated_up.sem, b + 1)
                    act.activation(gate[:, b * SEQ:(b + 1) * SEQ], bank[b][:, :], ACT.Sigmoid, bias=bg[:, :]).then_inc(sig_in.sem, 1)

            @block.gpsimd
            def _(pool):
                pool.wait_ge(loaded, 8 * 16)
                for b in range(BATCH):
                    pool.wait_ge(sig_in.sem, b + 1)
                    if b:
                        pool.wait_ge(xg_in.sem, b)
                    pool.tensor_tensor(xg[:, b * SEQ:(b + 1) * SEQ], xnT[:, b * SEQ:(b + 1) * SEQ], gate[:, b * SEQ:(b + 1) * SEQ],
                                       ALU.mult).then_inc(xg_in.sem, 1)

            @block.vector
            def _(v):
                n = 0

                def step(m):
                    nonlocal n
                    n += 1
                    m.then_inc(did.sem, 1)
                    v.wait_ge(did.sem, n)

                v.wait_ge(loaded, 8 * 16)
                At = A[:, :, :].rearrange("p n m -> p m n")
                step(v.tensor_copy(V[:, 0, :], Bp[:, :]))
                step(v.tensor_copy(W[:, 0, :], Cp[:, :]))
                for k in range(1, T + 1):
                    if k < T:
                        step(v.tensor_tensor(tmp[:, :, :], At, spread(V[:, k - 1, :], 1, N), ALU.mult))
                        step(v.tensor_reduce(V[:, k, :], tmp[:, :, :], X, ALU.add))
                    step(v.tensor_tensor(tmp[:, :, :], A[:, :, :], spread(W[:, k - 1, :], 1, N), ALU.mult))
                    step(v.tensor_reduce(W[:, k, :], tmp[:, :, :], X, ALU.add))
                step(v.tensor_tensor(tmp[:, :, :], V[:, :, :], spread(Cp[:, :], 1, T), ALU.mult))
                step(v.tensor_reduce(h[:, :], tmp[:, :, :], X, ALU.add))
                src = A
                for k in range(4):
                    a = A[:, :, :] if k == 0 else pw[:, (k - 1) % 2]
                    step(v.tensor_tensor(prod[:, :, :, :], spread(a, 2, N), spread(a.rearrange("p n m -> p m n"), 1, N), ALU.mult))
                    step(v.tensor_reduce(pw[:, k % 2], prod[:, :, :, :], X, ALU.add))
                step(v.tensor_scalar(h0[:, :], h[:, 0:1], Dp[:, 0:1], 1.0, ALU.add, ALU.add))
                v.wait_ge(xg_in.sem, BATCH)
                x = xg[:, :].rearrange("p (r t) -> p r t", t=T)
                step(v.tensor_scalar(y[:, :, :], x, h0[:, 0:1], None, ALU.mult))
                for k in range(1, T):
                    step(v.scalar_tensor_tensor(out=y[:, :, k:T], in0=x[:, :, 0:T - k], scalar=h[:, k:k + 1], in1=y[:, :, k:T],
                                                op0=ALU.mult, op1=ALU.add))
                step(v.memset(S[:, 0, :, :], 0.0))
        st.restart()

        added = st.event("added")
        with nc.Fori(0, N // 2) as m:
            with nc.Block() as block:
                @block.vector
                def _(v):
                    x = xg[:, :].rearrange("p (r t) -> p r t", t=T)
                    for j in range(T):
                        if j:
                            v.wait_ge(added.sem, j)
                        for k in range(2):
                            out = U[:, bass.ds(2 * m + k, 1), :].rearrange("p a r -> p (a r)")
                            vk = V[:, T - 1 - j, bass.ds(2 * m + k, 1)]
                            if j == 0:
                                i = v.tensor_scalar(out, x[:, :, j], vk, None, ALU.mult)
                            else:
                                i = v.scalar_tensor_tensor(out=out, in0=x[:, :, j], scalar=vk, in1=out, op0=ALU.mult, op1=ALU.add)
                        i.then_inc(added.sem, 1)
            st.restart()

        multiplied = st.event("multiplied", 3)
        UNROLL = 4
        with nc.Fori(0, CH // UNROLL) as c:
            with nc.Block() as block:
                @block.vector
                def _(v):
                    last = pw[:, 1]
                    Uc = U[:, :, :].rearrange("p n (b c) -> p c b n", b=BATCH)
                    for k in range(UNROLL):
                        if k:
                            v.wait_ge(multiplied.sem, 3 * k)
                        now = S[:, bass.ds(UNROLL * c + k, 1), :, :].rearrange("p a b n -> p (a b) n")
                        nxt = S[:, bass.ds(UNROLL * c + k + 1, 1), :, :].rearrange("p a b n -> p (a b) n")
                        v.tensor_tensor(prod[:, 0:BATCH, :, :], spread(now, 2, N), spread(last.rearrange("p n m -> p m n"), 1, BATCH),
                                        ALU.mult).then_inc(multiplied.sem, 1)
                        v.wait_ge(multiplied.sem, 3 * k + 1)
                        v.tensor_reduce(rec[:, :, :], prod[:, 0:BATCH, :, :], X, ALU.add).then_inc(multiplied.sem, 1)
                        v.wait_ge(multiplied.sem, 3 * k + 2)
                        v.tensor_tensor(nxt, rec[:, :, :], Uc[:, bass.ds(UNROLL * c + k, 1), :, :].rearrange("p a b n -> p (a b) n"), ALU.add).then_inc(multiplied.sem, 1)
            st.restart()

        with nc.Fori(0, T // 2) as i:
            with nc.Block() as block:
                @block.vector
                def _(v):
                    yv = y[:, :, :].rearrange("p (b c) t -> p b c t", b=BATCH)
                    Sv = S[:, 0:CH, :, :].rearrange("p c b n -> p b c n")
                    for n in range(N):
                        if n:
                            v.wait_ge(added.sem, n)
                        for k in range(2):
                            out = yv[:, :, :, bass.ds(2 * i + k, 1)].rearrange("p b c a -> p b (c a)")
                            m = v.scalar_tensor_tensor(out=out, in0=Sv[:, :, :, n], scalar=W[:, bass.ds(2 * i + k + 1, 1), n],
                                                       in1=out, op0=ALU.mult, op1=ALU.add)
                        m.then_inc(added.sem, 1)
            st.restart()

        yT_up = st.event("yT_up")
        stepped = st.event("stepped")
        rooted = st.event("rooted")
        with nc.Fori(0, BATCH) as b:
            with nc.Block() as block:
                @block.gpsimd
                def _(pool):
                    pool.tensor_copy(gate[:, 0:SEQ], y[:, bass.ds(b * CH, CH), :].rearrange("p r t -> p (r t)")).then_inc(powd.sem, 1)
                    pool.wait_ge(stepped.sem, 3)
                    pool.tensor_tensor(rstd[:, :], vare[:, :], g["half"][:, 0:TPB], ALU.pow).then_inc(rooted.sem, 1)

                @block.tensor
                def _(pe):
                    pe.wait_ge(powd.sem, 1)
                    for t in range(TPB):
                        m = pe.transpose(bank[0][:, t * P:(t + 1) * P], gate[:, t * P:(t + 1) * P], ident[:, :])
                    m.then_inc(yT_up.sem, 1)

                @block.vector
                def _(v):
                    v.wait_ge(yT_up.sem, 1)
                    for t in range(TPB):
                        m = v.bn_stats(stats[:, t, :], bank[0][:, t * P:(t + 1) * P])
                    m.then_inc(stepped.sem, 1)
                    v.wait_ge(stepped.sem, 1)
                    for t in range(TPB):
                        m = v.bn_aggr(mv[:, t, :], stats[:, t, :])
                    m.then_inc(stepped.sem, 1)
                    v.wait_ge(stepped.sem, 2)
                    v.tensor_scalar(vare[:, :], mv[:, :, 1], LN_EPS, None, ALU.add).then_inc(stepped.sem, 1)
                    v.wait_ge(rooted.sem, 1)
                    for t in range(TPB):
                        m = v.tensor_scalar(ln[:, t, :], bank[0][:, t * P:(t + 1) * P], mv[:, t, 0:1], rstd[:, t:t + 1], ALU.subtract, ALU.mult)
                    m.then_inc(stepped.sem, 1)
                    v.wait_ge(stepped.sem, 4)
                    v.tensor_tensor(ln[:, :, :], ln[:, :, :], spread(gam[:, :], 1, TPB), ALU.mult).then_inc(stepped.sem, 1)
                    v.wait_ge(stepped.sem, 5)
                    v.tensor_tensor(s[:, bass.ds(b * TPB, TPB), :], ln[:, :, :], spread(bet[:, :], 1, TPB), ALU.add).then_inc(stepped.sem, 1)
            st.restart()


def program(nc, dram, out):
    with ExitStack() as ctx:
        def keep(name, shape, dt=F32):
            return ctx.enter_context(nc.sbuf_tensor(name, shape, dt))

        g = {
            "x": keep("x", [P, TILES, DIM]),
            "xn": keep("xn", [P, TILES, DIM]),
            "xnT": keep("xnT", [P, TILES * P]),
            "s": keep("s", [P, TILES, DIM]),
            "u": keep("u", [P, TILES, DIM]),
            "half": keep("half", [P, 32]),
            "ident": keep("ident", [P, P]),
            "identb": keep("identb", [P, P], BF16),
        }
        load_inputs(nc, g, dram)
        for layer in range(4):
            layer_norm(nc, g, f"norm{layer}")
            ATTENTION[layer](nc, g, dram)
            FFN[layer](nc, g, dram)
            combine(nc, g, f"combine{layer}")
        store_output(nc, g, out)


def copy_xn(nc, g, name):
    with Stage(nc, name) as st:
        with nc.Block() as block:

            @block.vector
            def _(v):
                v.tensor_copy(g["u"][:, :, :], g["xn"][:, :, :])


def ffn2(nc, g, d):
    copy_xn(nc, g, "copy2")
    transformer(nc, g, d, "t2", 6, 16, 32, 341, d["L2_ffn_Wqkv"], d["L2_ffn_q_scale"], d["L2_ffn_k_scale"], d["L2_ffn_Wo"],
                d["L2_ffn_ln_g"], d["L2_ffn_ln_b"], d["L2_ffn_W1"], d["L2_ffn_b1"], d["L2_ffn_W2"], d["L2_ffn_b2"])


def ffn3(nc, g, d):
    copy_xn(nc, g, "copy3")
    transformer(nc, g, d, "t3", 2, 8, 64, 341, d["L3_ffn_wqkv"], d["L3_ffn_q_scale"], d["L3_ffn_k_scale"], d["L3_ffn_wo"],
                d["L3_ffn_ln_g"], d["L3_ffn_ln_b"], d["L3_ffn_w1"], d["L3_ffn_b1"], d["L3_ffn_w2"], d["L3_ffn_b2"])


ATTENTION = [attention0, attention1, attention2, attention3]
FFN = [ffn0, ffn1, ffn2, ffn3]


def rotary_table(window):
    half = np.arange(0, 64, 2, dtype=np.float32)
    inv_freq = (1.0 / np.float32(10000.0) ** (half / 64)).astype(np.float32)
    t = np.arange(SEQ, dtype=np.float32)
    freqs = t[:, None] * inv_freq[None, :]
    freqs = np.concatenate([freqs, freqs], -1)
    base = ((half + np.float32(0.4 * 64)) / np.float32(1.4 * 64)).astype(np.float32)
    power = (t - SEQ // 2) / np.float32(window // 2)
    scale = (base[None, :] ** power[:, None]).astype(np.float32)
    scale = np.concatenate([scale, scale], -1)
    cos, sin = np.cos(freqs), np.sin(freqs)
    sin = np.concatenate([-sin[:, :32], sin[:, 32:]], -1)
    tab = np.stack([cos * scale * 8, sin * scale * 8, cos / scale, sin / scale])
    return np.ascontiguousarray(tab.reshape(4, TPB, P, 64).transpose(2, 0, 1, 3).astype(np.float32))


def band_masks(window, first):
    q = np.arange(P)[:, None]
    k = np.arange(window + P)[None, :] - window
    ok = (k <= q) & (k >= q - first)
    tiles = []
    for i in range(2):
        m = ok & (k >= 0) if i == 0 else ok
        tiles.append(np.where(m, 0.0, MASKED))
    m = np.stack(tiles, 1).astype(np.dtype("bfloat16"))
    mt = np.zeros((P, 2, 2, P), m.dtype)
    mt[:, :, 0] = m[:, :, window:].transpose(2, 1, 0)
    mt[:window, :, 1] = m[:, :, :window].transpose(2, 1, 0)
    return m, mt


def shape_constants():
    bf = np.dtype("bfloat16")
    c = {"c_ident": np.eye(P, dtype=np.float32), "c_identb": np.eye(P, dtype=np.float32).astype(bf)}
    for window in (32, 64):
        c[f"c_rot{window}"] = rotary_table(window)
        c[f"c_mask{window}"], c[f"c_maskt{window}"] = band_masks(window, window)
    c["c_mask31"], c["c_maskt31"] = band_masks(32, 31)
    q, n, t = np.arange(P)[:, None, None], np.arange(64)[None, None, :], np.arange(TPB)[None, :, None]
    latent = np.where(n <= (t * P + q) // 8, 0.0, MASKED)
    c["c_maskl"] = latent.astype(bf)
    c["c_masklt"] = np.ascontiguousarray(latent.transpose(2, 1, 0)).astype(bf)
    q, k = np.arange(P)[:, None], np.arange(P)[None, :]
    c["c_causal"] = np.stack([np.where(k <= q, 0.0, MASKED), np.where(q <= k, 0.0, MASKED)]).astype(bf)
    for heads in (8, 16):
        sel = np.zeros((2, heads, heads, P), np.float32)
        for h in range(heads):
            sel[:, h, h, :] = 1.0
        c[f"c_sel{heads}"] = sel.reshape(2 * heads, heads, P).astype(bf)
    return c


TRANSPOSED = ["L3_attn_Wg", "L1_ffn_w1_w", "L1_ffn_w2_w", "L1_ffn_h1_w", "L1_ffn_h2_w", "L1_ffn_w3_w"]


def kernel(**inputs):
    import concourse.bacc as _bacc
    from concourse.bass_utils import run_bass_kernel_spmd as _run

    nc = _bacc.Bacc("TRN2", target_bir_lowering=False, num_devices=1)
    arrays, dram = {}, {}
    for name in list(inputs):
        a = np.ascontiguousarray(inputs[name])
        arrays[f"in_{name}"] = a
        dram[name] = nc.dram_tensor(f"in_{name}", a.shape, mybir.dt.from_np(a.dtype), kind="ExternalInput").ap()
    for name in TRANSPOSED:
        arrays[f"t_{name}"] = a = np.ascontiguousarray(inputs[name].T)
        dram[f"t_{name}"] = nc.dram_tensor(f"t_{name}", a.shape, mybir.dt.from_np(a.dtype), kind="ExternalInput").ap()
    for name, a in shape_constants().items():
        arrays[name] = a
        dram[name] = nc.dram_tensor(name, a.shape, mybir.dt.from_np(a.dtype), kind="ExternalInput").ap()
    out = nc.dram_tensor("out_0_dram", (BATCH, SEQ, DIM), F32, kind="ExternalOutput").ap()
    program(nc, dram, out)
    r = _run(nc, [arrays], core_ids=[0])
    return r.results[0]["out_0_dram"]
```

```python
from contextlib import ExitStack

import numpy as np
import concourse.bass as bass
from concourse import mybir

ALU = mybir.AluOpType
ACT = mybir.ActivationFunctionType
F32 = mybir.dt.float32
BF16 = mybir.dt.bfloat16
U32 = mybir.dt.uint32
X = mybir.AxisListType.X

P = 128
BATCH, SEQ, DIM = 4, 512, 128
TILES = BATCH * SEQ // P
TPB = SEQ // P
LN_EPS = 1e-5
MASKED = -1e30


class Event:

    def __init__(self, stage, name, per=1):
        self.sem = stage.sem(name)
        self.per = per

    def at(self, it, k=1):
        return it * self.per + k


class Stage:

    def __init__(self, nc, name):
        self.nc, self.name, self.ctx = nc, name, ExitStack()
        self.events, self.sems = [], []

    def __enter__(self):
        return self

    def __exit__(self, *exc):
        if exc[0] is None:
            self.clear(self.sems)
        return self.ctx.__exit__(*exc)

    def clear(self, sems):
        for sem in sems:
            self.nc.sync.sem_clear(sem)
        self.nc.all_engine_barrier()

    def sb(self, name, shape, dt=F32):
        return self.ctx.enter_context(self.nc.sbuf_tensor(f"{self.name}_{name}", shape, dt))

    def bank(self, name, shape=(P, 512), dt=F32):
        return self.ctx.enter_context(self.nc.psum_tensor(f"{self.name}_{name}", list(shape), dt))

    def sem(self, name):
        sem = self.ctx.enter_context(self.nc.semaphore(f"{self.name}_{name}"))
        self.sems.append(sem)
        return sem

    def event(self, name, per=1):
        e = Event(self, name, per)
        self.events.append(e)
        return e

    def restart(self):
        self.clear([e.sem for e in self.events])



def spread(ap, axis, n):
    a = ap.unsqueeze(axis)
    shape = list(a.shape)
    shape[axis] = n
    return a.to_broadcast(shape)


def load_inputs(nc, g, dram):
    with Stage(nc, "load") as st:
        loaded = st.sem("loaded")
        halved = st.sem("halved")
        with nc.Block() as block:

            @block.gpsimd
            def _(pool):
                pool.memset(g["half"][:, :], -0.5).then_inc(halved, 1)

            @block.sync
            def _(sp):
                sp.dma_start(g["x"][:, :, :], dram["L0_attn_x"].rearrange("b (t p) c -> p (b t) c", p=P)).then_inc(loaded, 16)
                sp.dma_start(g["ident"][:, :], dram["c_ident"]).then_inc(loaded, 16)
                sp.dma_start(g["identb"][:, :], dram["c_identb"]).then_inc(loaded, 16)
                sp.wait_ge(loaded, 3 * 16)


def layer_norm(nc, g, name):
    x, xn, xnT, ident = g["x"], g["xn"], g["xnT"], g["ident"]
    with Stage(nc, name) as st:
        stats = st.sb("stats", [P, TPB, 6])
        mv = st.sb("mv", [P, TPB, 2])
        vare = st.sb("vare", [P, TPB])
        rstd = st.sb("rstd", [P, TPB])
        staged = st.sb("staged", [P, TPB, P])
        turned = st.bank("turned")
        stepped = st.event("stepped", 5)
        rooted = st.event("rooted", 1)
        turned_up = st.event("turned_up", 1)
        with nc.Fori(0, BATCH) as b:
            with nc.Block() as block:
                @block.vector
                def _(v):
                    for t in range(TPB):
                        xt = x[:, bass.ds(b * TPB + t, 1), :].rearrange("p a c -> p (a c)")
                        v.bn_stats(stats[:, t, :], xt).then_inc(stepped.sem, 1)
                        v.wait_ge(stepped.sem, stepped.at(t, 1))
                        v.bn_aggr(mv[:, t, :], stats[:, t, :]).then_inc(stepped.sem, 1)
                        v.wait_ge(stepped.sem, stepped.at(t, 2))
                        v.tensor_scalar(vare[:, t:t + 1], mv[:, t, 1:2], LN_EPS, None, ALU.add).then_inc(stepped.sem, 1)
                        v.wait_ge(rooted.sem, rooted.at(t))
                        v.tensor_scalar(xn[:, bass.ds(b * TPB + t, 1), :].rearrange("p a c -> p (a c)"), xt,
                                        mv[:, t, 0:1], rstd[:, t:t + 1], ALU.subtract, ALU.mult).then_inc(stepped.sem, 1)
                        v.wait_ge(stepped.sem, stepped.at(t, 4))
                        v.tensor_copy(staged[:, t, :], xn[:, bass.ds(b * TPB + t, 1), :].rearrange("p a c -> p (a c)")).then_inc(stepped.sem, 1)

                @block.gpsimd
                def _(pool):
                    for t in range(TPB):
                        pool.wait_ge(stepped.sem, stepped.at(t, 3))
                        pool.tensor_tensor(rstd[:, t:t + 1], vare[:, t:t + 1], g["half"][:, 0:1], ALU.pow).then_inc(rooted.sem, 1)

                @block.tensor
                def _(pe):
                    for t in range(TPB):
                        pe.wait_ge(stepped.sem, stepped.at(t, 5))
                        pe.transpose(turned[:, t * P:(t + 1) * P], staged[:, t, :], ident[:, :]).then_inc(turned_up.sem, 1)

                @block.scalar
                def _(act):
                    act.wait_ge(turned_up.sem, TPB)
                    act.activation(xnT[:, bass.ds(b * SEQ, SEQ)], turned[:, :], ACT.Copy)
            st.restart()


def combine(nc, g, name):
    x, s, u = g["x"], g["s"], g["u"]
    with Stage(nc, name) as st:
        gated = st.sem("gated")
        product = st.sem("product")
        with nc.Block() as block:
            @block.scalar
            def _(act):
                act.activation(u[:, :, :], u[:, :, :], ACT.Silu).then_inc(gated, 1)

            @block.vector
            def _(v):
                v.wait_ge(gated, 1)
                v.tensor_tensor(s[:, :, :], s[:, :, :], u[:, :, :], ALU.mult).then_inc(product, 1)
                v.wait_ge(product, 1)
                v.tensor_tensor(x[:, :, :], x[:, :, :], s[:, :, :], ALU.add)


def store_output(nc, g, out):
    with Stage(nc, "store") as st:
        stored = st.sem("stored")
        with nc.Block() as block:

            @block.sync
            def _(sp):
                sp.dma_start(out.rearrange("b (t p) c -> p (b t) c", p=P), g["x"][:, :, :]).then_inc(stored, 16)
                sp.wait_ge(stored, 16)


def transformer(nc, g, dram, name, depth, heads, window, hid, wqkv, qs, ks, wo, ln_g, ln_b, w1, b1, w2, b2):
    HD = 64
    INNER = heads * HD
    PAIRS = heads // 2
    G4 = heads // 4
    QC = INNER // 512
    KEYS = window + P
    HC = [(c, min(P, hid - c)) for c in range(0, hid, P)]
    NH = len(HC)
    TB = 8
    HL = HC[-1][1]
    u, ident, identb = g["u"], g["ident"], g["identb"]

    with Stage(nc, name) as st:
        w_qkv = st.sb("w_qkv", [P, 3 * INNER])
        w_o = st.sb("w_o", [P, PAIRS, DIM])
        w_1 = st.sb("w_1", [P, 2 * hid])
        w_2 = st.sb("w_2", [P, NH, DIM])
        b_1 = st.sb("b_1", [P, 2, NH])
        b_2 = st.sb("b_2", [1, DIM])
        lng = st.sb("lng", [P, 1])
        lnb = st.sb("lnb", [P, 1])
        scales = st.sb("scales", [P, 2, HD])
        base = st.sb("base", [P, 4, TPB, HD])
        rot = st.sb("rot", [P, 4, TPB, HD])
        mask = st.sb("mask", [P, KEYS], BF16)
        maskt = st.sb("maskt", [P, P], BF16)
        maskp = st.sb("maskp", [P, window], BF16)
        sel = st.sb("sel", [2 * heads, heads, P], BF16)
        ones = st.sb("ones", [1, P])
        shT = st.sb("shT", [P, P + 1])
        sh2T = st.sb("sh2T", [P, P + 1])
        sq = st.sb("sq", [P, 2, 8, HD])
        ssq = st.sb("ssq", [P, 2 * heads])
        inv = st.sb("inv", [P, 2 * heads])
        qn = st.sb("qn", [P, 2, 8, HD])
        ra = st.sb("ra", [P, 2 * QC, 8, HD])
        rb = st.sb("rb", [P, 2, 8, HD])
        qz = st.sb("qz", [P, 2, heads, P])
        kT = st.sb("kT", [P, 3, PAIRS, P])
        va = st.sb("va", [P, 3, heads, HD + 2])
        nmax = st.sb("nmax", [P, heads])
        hl = st.sb("hl", [P, 2, heads], BF16)
        nmT = st.sb("nmT", [2 * heads, P], BF16)
        pt = st.sb("pt", [P, 2, 4, P])
        pc = st.sb("pc", [P, heads, window])
        rden = st.sb("rden", [P, 2, 4])
        o = st.sb("o", [P, heads, HD])
        oT = st.sb("oT", [P, PAIRS, P])
        x0 = st.sb("x0", [P, 2, DIM])
        x1 = st.sb("x1", [P, DIM])
        stats = st.sb("stats", [P, 6])
        mv = st.sb("mv", [P, 2])
        vare = st.sb("vare", [P, 1])
        rstd = st.sb("rstd", [P, 1])
        ln = st.sb("ln", [P, DIM])
        lnT = st.sb("lnT", [P, P])
        gg = st.sb("gg", [P, NH, P])
        hT = st.sb("hT", [P, NH, P])
        wa = st.bank("wa", [P, 2, 512])
        tr = st.bank("tr", [P, 512])
        wide = st.bank("wide", [P, 4, 512])
        misc = st.bank("misc", [P, 512])
        miscb = misc[:, 0:P].bitcast(BF16)

        w_in = st.event("w_in")
        c_in = st.sem("c_in")
        zeroed = st.sem("zeroed")
        tables = st.event("tables", 4)
        x0_in = st.event("x0_in", 1)
        xT_up = st.event("xT_up", 1)
        carry0 = st.event("carry0", 1)
        sh_in = st.event("sh_in", 2)
        proj = st.event("proj", 3 * QC)
        sqd = st.event("sqd", 2 * QC)
        summed = st.event("summed", 2 * QC)
        floored = st.event("floored", 2 * QC)
        inved = st.event("inved", 2 * QC)
        normed = st.event("normed", 2 * QC)
        cosd = st.event("cosd", 2 * QC)
        sind = st.event("sind", 4 * QC)
        roped = st.event("roped", 2 * QC)
        turned = st.event("turned", 2 * QC)
        qk_in = st.event("qk_in", 2 * QC)
        v_in = st.event("v_in", QC)
        scored = st.event("scored", G4)
        maxed = st.event("maxed", G4)
        split = st.event("split", 2)
        m_up = st.event("m_up", 1)
        m_in = st.event("m_in", 1)
        shifted = st.event("shifted", G4)
        shiftp = st.event("shiftp", 1)
        expp = st.event("expp", 1)
        exped = st.event("exped", G4)
        weighed = st.event("weighed", G4)
        recip = st.event("recip", G4)
        o_in = st.event("o_in", G4)
        oT_up = st.event("oT_up", G4)
        oT_in = st.event("oT_in", G4)
        y_up = st.event("y_up", 1)
        x1_in = st.event("x1_in", 1)
        x1T_up = st.event("x1T_up", 1)
        carry1 = st.event("carry1", 1)
        sh2_in = st.event("sh2_in", 2)
        sh2_up = st.event("sh2_up", 1)
        lnd = st.event("lnd", 4)
        rooted = st.event("rooted", 1)
        lnT_up = st.event("lnT_up", 1)
        lnT_in = st.event("lnT_in", 1)
        gate_up = st.event("gate_up", 1)
        gelu_in = st.event("gelu_in", NH)
        h_in = st.event("h_in", NH)
        f_up = st.event("f_up", 1)
        tile_done = st.event("tile_done", 1)
        NW = 11 + (3 if HL < P else 0)
        with nc.Block() as block:
            @block.sync
            def _(sp):
                sp.dma_start(base[:, :, :, :], dram[f"c_rot{window}"]).then_inc(c_in, 16)
                sp.dma_start(mask[:, :], dram[f"c_mask{window}"][:, 1, :]).then_inc(c_in, 16)
                sp.dma_start(maskt[:, :], dram[f"c_maskt{window}"][:, 1, 0, :]).then_inc(c_in, 16)
                sp.dma_start(maskp[:, :], dram[f"c_maskp{window}"]).then_inc(c_in, 16)
                sp.dma_start(sel[:, :, :], dram[f"c_sel{heads}"]).then_inc(c_in, 16)
                sp.wait_ge(c_in, 5 * 16)

            @block.gpsimd
            def _(pool):
                pool.memset(qz[:, :, :, :], 0.0).then_inc(zeroed, 1)
                pool.memset(va[:, :, :, :], 1.0).then_inc(zeroed, 1)
                pool.memset(shT[:, :], 0.0).then_inc(zeroed, 1)
                pool.memset(sh2T[:, :], 0.0).then_inc(zeroed, 1)
                pool.memset(ones[:, :], 1.0).then_inc(zeroed, 1)

        with nc.Fori(0, depth) as l:
            with nc.Block() as block:
                @block.sync
                def _(sp):
                    lay = lambda a: a[bass.ds(l, 1)]
                    sp.dma_start(w_qkv[:, :], lay(wqkv).rearrange("a p n -> p (a n)")).then_inc(w_in.sem, 16)
                    sp.dma_start(w_o[:, :, :], lay(wo).rearrange("a (c p) n -> p (a c) n", p=P)).then_inc(w_in.sem, 16)
                    sp.dma_start(w_1[:, :], lay(w1).rearrange("a p n -> p (a n)")).then_inc(w_in.sem, 16)
                    sp.dma_start(lng[:, :], lay(ln_g).rearrange("a p -> p a"), allow_slow_non_contiguous=True).then_inc(w_in.sem, 16)
                    sp.dma_start(lnb[:, :], lay(ln_b).rearrange("a p -> p a"), allow_slow_non_contiguous=True).then_inc(w_in.sem, 16)
                    sp.dma_start(b_2[:, :], lay(b2)).then_inc(w_in.sem, 16)
                    sp.dma_start(scales[:, 0, :], lay(qs).to_broadcast([P, HD])).then_inc(w_in.sem, 16)
                    sp.dma_start(scales[:, 1, :], lay(ks).to_broadcast([P, HD])).then_inc(w_in.sem, 16)
                    full = (NH - 1) if HL < P else NH
                    w2l, b1l = lay(w2), lay(b1)
                    sp.dma_start(w_2[:, 0:full, :], w2l[:, 0:full * P, :].rearrange("a (c p) n -> p (a c) n", p=P)).then_inc(w_in.sem, 16)
                    for h in range(2):
                        sp.dma_start(b_1[:, h, 0:full], b1l[:, h * hid:h * hid + full * P].rearrange("a (c p) -> p (a c)", p=P), allow_slow_non_contiguous=True).then_inc(w_in.sem, 16)
                    if HL < P:
                        sp.dma_start(w_2[0:HL, full, :], w2l[:, full * P:hid, :].rearrange("a p n -> p (a n)")).then_inc(w_in.sem, 16)
                        for h in range(2):
                            sp.dma_start(b_1[0:HL, h, full:NH], b1l[:, h * hid + full * P:h * hid + hid].rearrange("a p -> p a"), allow_slow_non_contiguous=True).then_inc(w_in.sem, 16)
                    sp.wait_ge(w_in.sem, NW * 16)

                @block.vector
                def _(v):
                    v.wait_ge(w_in.sem, NW * 16)
                    for r in range(2):
                        s = scales[:, r, :]
                        v.tensor_tensor(rot[:, 2 * r], base[:, 2 * r], spread(s, 1, TPB), ALU.mult).then_inc(tables.sem, 1)
                        v.tensor_tensor(rot[:, 2 * r + 1, :, 0:32], base[:, 2 * r + 1, :, 0:32], spread(s[:, 32:64], 1, TPB), ALU.mult)
                        v.tensor_tensor(rot[:, 2 * r + 1, :, 32:64], base[:, 2 * r + 1, :, 32:64], spread(s[:, 0:32], 1, TPB),
                                        ALU.mult).then_inc(tables.sem, 1)

            with nc.Fori(0, TILES // TB) as b:
                with nc.Block() as block:
                    NJ = max(G4 + 1, 2 * QC + 2, 3 * QC)
                    first = lambda t: t % TPB == 0

                    @block.gpsimd
                    def _(pool):
                        for t in range(-1, TB):
                            n = t + 1
                            if n < TB:
                                for j in range(2 * QC + 1):
                                    if j < 2 * QC:
                                        pool.wait_ge(floored.sem, floored.at(n, j + 1))
                                        pool.tensor_tensor(inv[:, 8 * j:8 * j + 8], ssq[:, 8 * j:8 * j + 8], g["half"][:, 0:8],
                                                           ALU.pow).then_inc(inved.sem, 1)
                                    if j:
                                        c = j - 1
                                        r, z = 2 * (c // QC), c % 2
                                        cos, sin = rot[:, r, n % TPB, :], rot[:, r + 1, n % TPB, :]
                                        pool.wait_ge(normed.sem, normed.at(n, c + 1))
                                        if c >= 2:
                                            pool.wait_ge(roped.sem, roped.at(n, c - 1))
                                        if c == 0:
                                            if n:
                                                pool.wait_ge(turned.sem, turned.at(n, 0))
                                        pool.tensor_tensor(ra[:, c], qn[:, z], spread(cos, 1, 8), ALU.mult).then_inc(cosd.sem, 1)
                                        pool.tensor_tensor(rb[:, z, :, 0:32], qn[:, z, :, 32:64], spread(sin[:, 0:32], 1, 8), ALU.mult).then_inc(sind.sem, 1)
                                        pool.tensor_tensor(rb[:, z, :, 32:64], qn[:, z, :, 0:32], spread(sin[:, 32:64], 1, 8), ALU.mult).then_inc(sind.sem, 1)
                            if t >= 0:
                                pool.wait_ge(lnd.sem, lnd.at(t, 3))
                                pool.tensor_tensor(rstd[:, :], vare[:, :], g["half"][:, 0:1], ALU.pow).then_inc(rooted.sem, 1)

                    @block.tensor
                    def _(pe):
                        def score(t, q):
                            if q == 0:
                                pe.wait_ge(qk_in.sem, qk_in.at(t, 2 * QC))
                                if t:
                                    pe.wait_ge(h_in.sem, h_in.at(t - 1, NH))
                            if q >= 2:
                                pe.wait_ge(maxed.sem, maxed.at(t, q - 1))
                            lo = window if first(t) else 0
                            for h2 in range(2):
                                bank = wide[:, 2 * (q % 2) + h2, :].rearrange("p (h k) -> p h k", h=2)
                                pe.matmul(bank[:, :, lo:KEYS], identb[:, :], spread(mask[:, lo:KEYS], 1, 2),
                                          start=True, stop=False, skip_group_check=True)
                                for j in range(2):
                                    h = 4 * q + 2 * h2 + j
                                    if not first(t):
                                        pe.matmul(bank[:, j, 0:window], qz[:, t % 2, h, :], kT[:, (t - 1) % 3, h // 2, P - window:P],
                                                  start=False, stop=False, skip_group_check=True)
                                    m = pe.matmul(bank[:, j, window:KEYS], qz[:, t % 2, h, :], kT[:, t % 3, h // 2, :],
                                                  start=False, stop=True, skip_group_check=True)
                            m.then_inc(scored.sem, 1)

                        def x_up(n):
                            pe.wait_ge(x0_in.sem, x0_in.at(n))
                            if n:
                                pe.wait_ge(qk_in.sem, qk_in.at(n, 0))
                            pe.transpose(tr[:, 0:P], x0[:, n % 2, :], ident[:, :]).then_inc(xT_up.sem, 1)

                        def project(n, c):
                            if c == 0:
                                pe.wait_ge(sh_in.sem, sh_in.at(n, 2))
                            k = n * 3 * QC + c
                            if k >= 2:
                                pn, pc_ = divmod(k - 2, 3 * QC)
                                if pc_ < 2 * QC:
                                    pe.wait_ge(normed.sem, normed.at(pn, pc_ + 1))
                                else:
                                    pe.wait_ge(v_in.sem, v_in.at(pn, pc_ - 2 * QC + 1))
                            pe.matmul(wa[:, k % 2, :], shT[:, 0:P], w_qkv[:, c * 512:(c + 1) * 512],
                                      start=True, stop=True).then_inc(proj.sem, 1)

                        def turn(n, c):
                            pe.wait_ge(roped.sem, roped.at(n, c + 1))
                            if c:
                                pe.wait_ge(qk_in.sem, qk_in.at(n, c))
                            for j in range(4):
                                m = pe.transpose(tr[:, j * P:(j + 1) * P], ra[:, c, 2 * j:2 * j + 2, :].rearrange("p h d -> p (h d)"), ident[:, :])
                            m.then_inc(turned.sem, 1)

                        def shift_before(t):
                            bank = misc[:, 0:heads * window].rearrange("p (h k) -> p h k", h=heads)
                            pe.matmul(bank, identb[:, :], spread(maskp[:, :], 1, heads), start=True, stop=False, skip_group_check=True)
                            for h in range(heads):
                                pe.matmul(bank[:, h, :], sel[:, h, :], nmT[:, 0:window], start=False, stop=False, skip_group_check=True)
                                m = pe.matmul(bank[:, h, :], kT[:, (t - 1) % 3, h // 2, :], qz[:, t % 2, h, 0:window],
                                              start=False, stop=True, skip_group_check=True)
                            m.then_inc(shiftp.sem, 1)

                        def shift(t, q):
                            if q >= 2:
                                pe.wait_ge(exped.sem, exped.at(t, q - 1))
                            bank = wide[:, q % 2, :].rearrange("p (h k) -> p h k", h=4)
                            pe.matmul(bank, identb[:, :], spread(maskt[:, :], 1, 4), start=True, stop=False, skip_group_check=True)
                            for j in range(4):
                                h = 4 * q + j
                                pe.matmul(bank[:, j, :], sel[:, h, :], nmT[:, :], start=False, stop=False, skip_group_check=True)
                                m = pe.matmul(bank[:, j, :], kT[:, t % 3, h // 2, :], qz[:, t % 2, h, :],
                                              start=False, stop=True, skip_group_check=True)
                            m.then_inc(shifted.sem, 1)

                        def weigh(t, q):
                            pe.wait_ge(exped.sem, exped.at(t, q + 1))
                            if q == 0:
                                pe.wait_ge(v_in.sem, v_in.at(t, QC))
                                if not first(t):
                                    pe.wait_ge(expp.sem, expp.at(sum(not first(x) for x in range(t))))
                            if q >= 2:
                                pe.wait_ge(o_in.sem, o_in.at(t, q - 1))
                            for j in range(4):
                                h = 4 * q + j
                                out = wide[:, 2 + q % 2, j * 66:j * 66 + 66]
                                m = pe.matmul(out, pt[:, q % 2, j, :], va[:, t % 3, h, :], start=True, stop=first(t), skip_group_check=True)
                                if not first(t):
                                    m = pe.matmul(out[0:window], pc[:, h, :], va[:, (t - 1) % 3, h, :], start=False, stop=True, skip_group_check=True)
                            m.then_inc(weighed.sem, 1)

                        def turn_out(t, q):
                            pe.wait_ge(o_in.sem, o_in.at(t, q + 1))
                            if q >= 2:
                                pe.wait_ge(oT_in.sem, oT_in.at(t, q - 1))
                            for j in range(2):
                                m = pe.transpose(wide[:, q % 2, j * P:(j + 1) * P],
                                                 o[:, 4 * q + 2 * j:4 * q + 2 * j + 2, :].rearrange("p h d -> p (h d)"), ident[:, :])
                            m.then_inc(oT_up.sem, 1)

                        for t in range(-1, TB):
                            n = t + 1
                            A, B = n < TB, t >= 0
                            if A:
                                x_up(n)
                            if B:
                                for q in range(G4):
                                    score(t, q)
                            if A:
                                project(n, 0)
                                project(n, 1)
                            if B:
                                pe.wait_ge(split.sem, split.at(t, 2))
                                pe.transpose(miscb[0:2 * heads, 0:P], hl[:, :, :].rearrange("p a h -> p (a h)"), identb[:, :]).then_inc(m_up.sem, 1)
                                pe.wait_ge(m_in.sem, m_in.at(t))
                            for j in range(NJ):
                                if B and j < G4:
                                    shift(t, j)
                                    if j == 0 and not first(t):
                                        shift_before(t)
                                if A and j + 2 < 3 * QC:
                                    project(n, j + 2)
                                if B and 1 <= j <= G4:
                                    weigh(t, j - 1)
                            if B:
                                for q in range(G4):
                                    turn_out(t, q)
                                pe.wait_ge(oT_in.sem, oT_in.at(t, G4))
                                for c in range(PAIRS):
                                    m = pe.matmul(misc[:, 0:DIM], oT[:, c, :], w_o[:, c, :], start=(c == 0), stop=(c == PAIRS - 1))
                                m.then_inc(y_up.sem, 1)
                            if A:
                                turn(n, 0)
                            if B:
                                pe.wait_ge(x1_in.sem, x1_in.at(t))
                                pe.transpose(misc[:, P:2 * P], x1[:, :], ident[:, :]).then_inc(x1T_up.sem, 1)
                            if A:
                                turn(n, 1)
                            if B:
                                pe.wait_ge(sh2_in.sem, sh2_in.at(t, 2))
                                pe.transpose(misc[:, 2 * P:3 * P], sh2T[:, 0:P], ident[:, :]).then_inc(sh2_up.sem, 1)
                            if A and QC > 1:
                                turn(n, 2)
                            if B:
                                pe.wait_ge(lnd.sem, lnd.at(t, 4))
                                pe.transpose(misc[:, 3 * P:4 * P], ln[:, :], ident[:, :]).then_inc(lnT_up.sem, 1)
                            if A and QC > 1:
                                turn(n, 3)
                            if B:
                                pe.wait_ge(lnT_in.sem, lnT_in.at(t))
                                for half in range(2):
                                    for c, (at, size) in enumerate(HC):
                                        lo = (1 - half) * hid + at
                                        m = pe.matmul(wide[0:size, half, c * P:(c + 1) * P], w_1[:, lo:lo + size], lnT[:, :], start=True, stop=True)
                                m.then_inc(gate_up.sem, 1)
                                pe.wait_ge(h_in.sem, h_in.at(t, NH))
                                for c, (at, size) in enumerate(HC):
                                    pe.matmul(misc[:, 0:DIM], hT[0:size, c, :], w_2[0:size, c, :], start=(c == 0), stop=False)
                                pe.matmul(misc[:, 0:DIM], ones[:, :], b_2[:, :], start=False, stop=True).then_inc(f_up.sem, 1)

                    @block.scalar
                    def _(act):
                        def square(n, c):
                            act.wait_ge(proj.sem, proj.at(n, c + 1))
                            k = n * 2 * QC + c
                            if k >= 2:
                                act.wait_ge(summed.sem, k - 1)
                            act.activation(sq[:, c % 2].rearrange("p h d -> p (h d)"), wa[:, (n * 3 * QC + c) % 2, :], ACT.Square).then_inc(sqd.sem, 1)

                        def values(n, c):
                            act.wait_ge(proj.sem, proj.at(n, 2 * QC + c + 1))
                            if n >= 3:
                                act.wait_ge(weighed.sem, weighed.at(n - 2, G4))
                            act.activation(va[:, n % 3, 8 * c:8 * c + 8, 0:HD],
                                           wa[:, (n * 3 * QC + 2 * QC + c) % 2, :].rearrange("p (h d) -> p h d", h=8), ACT.Copy).then_inc(v_in.sem, 1)

                        def copy_turned(n, c):
                            act.wait_ge(turned.sem, turned.at(n, c + 1))
                            src = tr[:, :].rearrange("p (j k) -> p j k", j=4)
                            if c < QC:
                                heads_ = qz[:, n % 2, 8 * c:8 * c + 8, :].rearrange("p (j a) k -> p a j k", a=2)
                                act.activation(heads_[0:64, 0], src[0:64], ACT.Copy)
                                act.activation(heads_[64:P, 1], src[64:P], ACT.Copy).then_inc(qk_in.sem, 1)
                            else:
                                act.activation(kT[:, n % 3, 4 * (c - QC):4 * (c - QC) + 4, :], src, ACT.Copy).then_inc(qk_in.sem, 1)

                        for t in range(-1, TB):
                            n = t + 1
                            A, B = n < TB, t >= 0
                            for j in range(NJ):
                                if A and j < 2 * QC:
                                    square(n, j)
                                elif A and j < 3 * QC:
                                    values(n, j - 2 * QC)
                                if B and j < G4:
                                    act.wait_ge(shifted.sem, shifted.at(t, j + 1))
                                    if j >= 2:
                                        act.wait_ge(weighed.sem, weighed.at(t, j - 1))
                                    act.activation(pt[:, j % 2].rearrange("p h k -> p (h k)"), wide[:, j % 2, :], ACT.Exp).then_inc(exped.sem, 1)
                                    if j == 0 and not first(t):
                                        act.wait_ge(shiftp.sem, sum(not first(x) for x in range(t + 1)))
                                        act.activation(pc[:, :, :].rearrange("p h k -> p (h k)"), misc[:, 0:heads * window], ACT.Exp).then_inc(expp.sem, 1)
                            if B:
                                for q in range(G4):
                                    act.wait_ge(oT_up.sem, oT_up.at(t, q + 1))
                                    act.activation(oT[:, 2 * q:2 * q + 2, :].rearrange("p a b -> p (a b)"), wide[:, q % 2, 0:256],
                                                   ACT.Copy).then_inc(oT_in.sem, 1)
                            if A:
                                for c in range(min(3, 2 * QC)):
                                    copy_turned(n, c)
                            if B:
                                act.wait_ge(lnT_up.sem, lnT_up.at(t))
                                act.activation(lnT[:, :], misc[:, 3 * P:4 * P], ACT.Identity, bias=lnb[:, :], scale=lng[:, 0:1]).then_inc(lnT_in.sem, 1)
                            if A and QC > 1:
                                copy_turned(n, 3)
                            if B:
                                act.wait_ge(gate_up.sem, gate_up.at(t))
                                for c, (at, size) in enumerate(HC):
                                    act.activation(gg[0:size, c, :], wide[0:size, 0, c * P:(c + 1) * P], ACT.Gelu,
                                                   bias=b_1[0:size, 1, c:c + 1]).then_inc(gelu_in.sem, 1)

                    @block.vector
                    def _(v):
                        def tile(t):
                            return u[:, bass.ds(b * TB + t, 1), :].rearrange("p a c -> p (a c)")

                        def sums(n, c):
                            v.wait_ge(sqd.sem, sqd.at(n, c + 1))
                            cols = slice(8 * c, 8 * c + 8)
                            v.tensor_reduce(ssq[:, cols], sq[:, c % 2], X, ALU.add).then_inc(summed.sem, 1)
                            v.wait_ge(summed.sem, summed.at(n, c + 1))
                            v.tensor_scalar(ssq[:, cols], ssq[:, cols], 1e-24, None, ALU.max).then_inc(floored.sem, 1)

                        def normalise(n, c):
                            v.wait_ge(inved.sem, inved.at(n, c + 1))
                            k = n * 2 * QC + c
                            if k >= 2:
                                v.wait_ge(sind.sem, 2 * (k - 1))
                            v.tensor_tensor(qn[:, c % 2], wa[:, (n * 3 * QC + c) % 2, :].rearrange("p (h d) -> p h d", h=8),
                                            spread(inv[:, 8 * c:8 * c + 8], 2, HD), ALU.mult).then_inc(normed.sem, 1)

                        def finish_rope(n, c):
                            v.wait_ge(cosd.sem, cosd.at(n, c + 1))
                            v.wait_ge(sind.sem, sind.at(n, 2 * c + 2))
                            v.tensor_tensor(ra[:, c], ra[:, c], rb[:, c % 2], ALU.add).then_inc(roped.sem, 1)

                        for t in range(-1, TB):
                            n = t + 1
                            A, B = n < TB, t >= 0
                            if A:
                                v.tensor_copy(x0[:, n % 2, :], tile(n)).then_inc(x0_in.sem, 1)
                                if n:
                                    v.wait_ge(proj.sem, proj.at(n, 0))
                                v.tensor_scalar(shT[64:P, 0:1], shT[64:P, P:P + 1], float(not first(n)), None, ALU.mult).then_inc(carry0.sem, 1)
                                v.wait_ge(carry0.sem, carry0.at(n))
                                v.wait_ge(xT_up.sem, xT_up.at(n))
                                v.tensor_copy(shT[0:64, 0:P], tr[0:64, 0:P]).then_inc(sh_in.sem, 1)
                                v.tensor_copy(shT[64:P, 1:P + 1], tr[64:P, 0:P]).then_inc(sh_in.sem, 1)
                            if B:
                                lo = window if first(t) else 0
                                for q in range(G4):
                                    v.wait_ge(scored.sem, scored.at(t, q + 1))
                                    v.tensor_reduce(nmax[:, 4 * q:4 * q + 4],
                                                    wide[:, 2 * (q % 2):2 * (q % 2) + 2, :].rearrange("p b (h k) -> p (b h) k", h=2)[:, :, lo:KEYS],
                                                    X, ALU.max, negate=True).then_inc(maxed.sem, 1)
                                v.wait_ge(maxed.sem, maxed.at(t, G4))
                                v.tensor_copy(hl[:, 0, :], nmax[:, :]).then_inc(split.sem, 1)
                                v.wait_ge(split.sem, split.at(t, 1))
                                v.tensor_tensor(hl[:, 1, :], nmax[:, :], hl[:, 0, :], ALU.subtract).then_inc(split.sem, 1)
                                v.wait_ge(m_up.sem, m_up.at(t))
                                v.tensor_copy(nmT[:, :], miscb[0:2 * heads, 0:P]).then_inc(m_in.sem, 1)
                            for j in range(NJ):
                                if A and j < 2 * QC:
                                    sums(n, j)
                                if A and 2 <= j < 2 * QC + 2:
                                    finish_rope(n, j - 2)
                                if A and j < 2 * QC:
                                    normalise(n, j)
                                if B and 1 <= j <= G4:
                                    q = j - 1
                                    v.wait_ge(weighed.sem, weighed.at(t, q + 1))
                                    out = wide[:, 2 + q % 2, 0:4 * 66].rearrange("p (h d) -> p h d", h=4)
                                    v.reciprocal(rden[:, q % 2, :], out[:, :, HD]).then_inc(recip.sem, 1)
                                    v.wait_ge(recip.sem, recip.at(t, q + 1))
                                    v.tensor_tensor(o[:, 4 * q:4 * q + 4, :], out[:, :, 0:HD], spread(rden[:, q % 2, :], 2, HD),
                                                    ALU.mult).then_inc(o_in.sem, 1)
                            if B:
                                v.wait_ge(y_up.sem, y_up.at(t))
                                v.tensor_tensor(x1[:, :], misc[:, 0:DIM], x0[:, t % 2, :], ALU.add).then_inc(x1_in.sem, 1)
                                v.tensor_scalar(sh2T[64:P, 0:1], sh2T[64:P, P:P + 1], float(not first(t)), None, ALU.mult).then_inc(carry1.sem, 1)
                                v.wait_ge(carry1.sem, carry1.at(t))
                                v.wait_ge(x1T_up.sem, x1T_up.at(t))
                                v.tensor_copy(sh2T[0:64, 0:P], misc[0:64, P:2 * P]).then_inc(sh2_in.sem, 1)
                                v.tensor_copy(sh2T[64:P, 1:P + 1], misc[64:P, P:2 * P]).then_inc(sh2_in.sem, 1)
                                v.wait_ge(sh2_up.sem, sh2_up.at(t))
                                v.bn_stats(stats[:, :], misc[:, 2 * P:3 * P]).then_inc(lnd.sem, 1)
                                v.wait_ge(lnd.sem, lnd.at(t, 1))
                                v.bn_aggr(mv[:, :], stats[:, :]).then_inc(lnd.sem, 1)
                                v.wait_ge(lnd.sem, lnd.at(t, 2))
                                v.tensor_scalar(vare[:, :], mv[:, 1:2], LN_EPS, None, ALU.add).then_inc(lnd.sem, 1)
                                v.wait_ge(rooted.sem, rooted.at(t))
                                v.tensor_scalar(ln[:, :], misc[:, 2 * P:3 * P], mv[:, 0:1], rstd[:, 0:1], ALU.subtract, ALU.mult).then_inc(lnd.sem, 1)
                                for c, (at, size) in enumerate(HC):
                                    v.wait_ge(gelu_in.sem, gelu_in.at(t, c + 1))
                                    v.scalar_tensor_tensor(out=hT[0:size, c, :], in0=wide[0:size, 1, c * P:(c + 1) * P], scalar=b_1[0:size, 0, c:c + 1],
                                                           in1=gg[0:size, c, :], op0=ALU.add, op1=ALU.mult).then_inc(h_in.sem, 1)
                                v.wait_ge(f_up.sem, f_up.at(t))
                                v.tensor_tensor(tile(t), misc[:, 0:DIM], x1[:, :], ALU.add).then_inc(tile_done.sem, 1)
                st.restart()


def attention0(nc, g, d):
    H, HD, LH, WIN, LAT = 16, 8, 8, 32, 64
    G, LG = H // 4, LH // 4
    CHUNK = SEQ // LAT
    s, ident, identb, xnT = g["s"], g["ident"], g["identb"], g["xnT"]
    with Stage(nc, "a0") as st:
        wqs = st.sb("wqs", [P, G, 4, 32])
        wks = st.sb("wks", [P, G, 4, 32])
        wgqs = st.sb("wgqs", [P, LG, 4, 32])
        wgks = st.sb("wgks", [P, LG, 4, 32])
        wq = st.sb("wq", [P, DIM])
        wv = st.sb("wv", [P, DIM])
        wgv = st.sb("wgv", [P, LAT])
        wr = st.sb("wr", [LAT, DIM])
        wo = st.sb("wo", [P, DIM])
        gw = st.sb("gw", [P, 2, DIM])
        mask = st.sb("mask", [P, 2, WIN + P], BF16)
        maskt = st.sb("maskt", [P, 2, 2, P], BF16)
        maskl = st.sb("maskl", [P, TPB, LAT], BF16)
        masklt = st.sb("masklt", [LAT, TPB, P], BF16)
        sel = st.sb("sel", [64, H, P], BF16)
        xb = st.sb("xb", [P, SEQ])
        qT = st.sb("qT", [P, G, SEQ])
        kT = st.sb("kT", [P, G, SEQ])
        gqT = st.sb("gqT", [P, LG, SEQ])
        gkT = st.sb("gkT", [P, LG, LAT])
        gvT = st.sb("gvT", [LAT, LAT])
        va = st.sb("va", [P, TPB, H, HD + 1])
        vc = st.sb("vc", [WIN, TPB, H, HD + 1])
        gva = st.sb("gva", [LAT, LH, HD + 1])
        gprod = st.sb("gprod", [P, 2, DIM])
        logit = st.sb("logit", [P, TPB, 2, H])
        gates = st.sb("gates", [P, TPB, 2, H])
        nmax = st.sb("nmax", [P, H])
        hl = st.sb("hl", [P, 2, H], BF16)
        nmT = st.sb("nmT", [64, P], BF16)
        pt = st.sb("pt", [P, 4, G, P])
        pc = st.sb("pc", [WIN, 4, G, P])
        ptl = st.sb("ptl", [LAT, 4, LG, P])
        rden = st.sb("rden", [P, H])
        rdl = st.sb("rdl", [P, LH])
        loc = st.sb("loc", [P, DIM])
        rem = st.sb("rem", [P, LAT])
        remT = st.sb("remT", [LAT, P])
        remg = st.sb("remg", [P, DIM])
        mix = st.sb("mix", [P, DIM])
        mixT = st.sb("mixT", [P, P])
        all8 = st.bank("all8", [P, 8, 512])
        bank = [all8[:, i, :] for i in range(8)]
        loaded, zeroed = st.sem("loaded"), st.sem("zeroed")
        with nc.Block() as block:
            @block.gpsimd
            def _(pool):
                for z in (wqs, wks, wgqs, wgks):
                    pool.memset(z[:, :, :, :], 0.0).then_inc(zeroed, 1)
                pool.memset(sel[:, :, :], 0.0).then_inc(zeroed, 1)
                pool.memset(nmT[:, :], 0.0).then_inc(zeroed, 1)
                pool.memset(hl[:, :, :], 0.0).then_inc(zeroed, 1)
                pool.memset(va[:, :, :, :], 1.0).then_inc(zeroed, 1)
                pool.memset(gva[:, :, :], 1.0).then_inc(zeroed, 1)

            @block.sync
            def _(sp):
                sp.wait_ge(zeroed, 9)
                for dst, name, groups in ((wqs, "wq", G), (wks, "wk", G), (wgqs, "wgq", LG), (wgks, "wgk", LG)):
                    for c in range(groups):
                        sp.dma_start(dst[:, c, :, 0:HD], d[f"L0_attn_{name}"][:, c * 32:(c + 1) * 32].rearrange("p (j e) -> p j e", e=HD)).then_inc(loaded, 16)
                sp.dma_start(wq[:, :], d["L0_attn_wq"]).then_inc(loaded, 16)
                sp.dma_start(wv[:, :], d["L0_attn_wv"]).then_inc(loaded, 16)
                sp.dma_start(wgv[:, :], d["L0_attn_wgv"]).then_inc(loaded, 16)
                sp.dma_start(wr[:, :], d["L0_attn_r_out_w"]).then_inc(loaded, 16)
                sp.dma_start(wo[:, :], d["L0_attn_w_out"]).then_inc(loaded, 16)
                for k, name in enumerate(("local", "remote")):
                    sp.dma_start(gw[:, k, :], d[f"L0_attn_gate_{name}_w"].rearrange("h e -> (h e)").rearrange("(a n) -> a n", a=1).to_broadcast([P, DIM])).then_inc(loaded, 16)
                sp.dma_start(mask[:, :, :], d["c_mask31"]).then_inc(loaded, 16)
                sp.dma_start(maskt[:, :, :, :], d["c_maskt31"]).then_inc(loaded, 16)
                sp.dma_start(maskl[:, :, :], d["c_maskl"]).then_inc(loaded, 16)
                sp.dma_start(masklt[:, :, :], d["c_masklt"]).then_inc(loaded, 16)
                sp.dma_start(sel[0:2 * H, :, :], d["c_sel16"]).then_inc(loaded, 16)
                sp.wait_ge(loaded, (2 * G + 2 * LG + 12) * 16)

        xb_in = st.event("xb_in")
        proj = st.event("proj")
        even_in = st.event("even_in")
        odd_in = st.event("odd_in")
        lat_up = st.event("lat_up")
        lat_in = st.event("lat_in")
        carried = st.event("carried")
        gate_up = st.event("gate_up")
        gate_mul = st.event("gate_mul")
        gate_sum = st.event("gate_sum")
        gates_in = st.event("gates_in")
        with nc.Fori(0, BATCH) as b:
            JOBS = ([("q", c) for c in range(G)] + [("k", c) for c in range(G)] + [("gq", 0), ("gk", 0), ("gq", 1), ("gk", 1)]
                    + [("v", 0), ("gv", 0)] + [("v", t) for t in range(1, TPB)])
            NP = len(JOBS)
            with nc.Block() as block:
                @block.gpsimd
                def _(pool):
                    pool.tensor_copy(xb[:, :], xnT[:, bass.ds(b * SEQ, SEQ)]).then_inc(xb_in.sem, 1)

                @block.tensor
                def _(pe):
                    pe.wait_ge(xb_in.sem, 1)
                    for n in range(NP):
                        if n >= 8:
                            pe.wait_ge((even_in, odd_in)[n % 2].sem, (n - 8) // 2 + 1)
                        kind, c = JOBS[n]
                        if kind == "gv":
                            m = pe.matmul(bank[n % 8][0:LAT, :], wgv[:, :], xb[:, :], start=True, stop=True)
                        elif kind == "v":
                            m = pe.matmul(bank[n % 8][:, 0:DIM], xb[:, c * P:(c + 1) * P], wv[:, :], start=True, stop=True)
                        else:
                            w = {"q": wqs, "k": wks, "gq": wgqs, "gk": wgks}[kind]
                            m = pe.matmul(bank[n % 8], w[:, c, :, :].rearrange("p j e -> p (j e)"), xb[:, :], start=True, stop=True)
                        m.then_inc(proj.sem, 1)
                    pe.wait_ge(even_in.sem, (NP + 1) // 2)
                    pe.wait_ge(odd_in.sem, NP // 2)
                    pe.transpose(bank[0][0:LAT, 0:LAT], gvT[:, :], ident[0:LAT, 0:LAT]).then_inc(lat_up.sem, 1)
                    for t in range(TPB):
                        pe.matmul(bank[1 + t][:, 0:DIM], xb[:, t * P:(t + 1) * P], wq[:, :], start=True, stop=True).then_inc(gate_up.sem, 1)

                def place(n, copy, pooled):
                    src = bank[n % 8]
                    kind, c = JOBS[n]
                    if kind == "q":
                        return copy(qT[:, c, :], src, HD ** -0.5)
                    if kind == "k":
                        return copy(kT[:, c, :], src, 1.0)
                    if kind == "gq":
                        return copy(gqT[:, c, :], src, HD ** -0.5 / CHUNK)
                    if kind == "gk":
                        return pooled(gkT[:, c, :], src)
                    if kind == "gv":
                        return pooled(gvT[:, :], src[0:LAT, :])
                    return copy(va[:, c, :, 0:HD], src[:, 0:DIM].rearrange("p (h e) -> p h e", e=HD), 1.0)

                @block.scalar
                def _(act):
                    for n in range(0, NP, 2):
                        act.wait_ge(proj.sem, n + 1)
                        place(n, lambda dst, src, k: act.activation(dst, src, ACT.Copy, scale=k), None).then_inc(even_in.sem, 1)
                    act.wait_ge(even_in.sem, (NP + 1) // 2)
                    act.wait_ge(odd_in.sem, NP // 2)
                    for t in range(1, TPB):
                        act.activation(vc[:, t, :, :], va[P - WIN:P, t - 1, :, :], ACT.Copy).then_inc(carried.sem, 1)
                    act.wait_ge(gate_sum.sem, TPB)
                    act.activation(gates[:, :, :, :], logit[:, :, :, :], ACT.Sigmoid).then_inc(gates_in.sem, 1)

                @block.vector
                def _(v):
                    def pooled(dst, src):
                        return v.tensor_reduce(dst, src.rearrange("p (n k) -> p n k", k=CHUNK), X, ALU.add)

                    for n in range(1, NP, 2):
                        v.wait_ge(proj.sem, n + 1)
                        place(n, lambda dst, src, k: v.tensor_scalar(dst, src, k, None, ALU.mult), pooled).then_inc(odd_in.sem, 1)
                    v.wait_ge(lat_up.sem, 1)
                    v.tensor_scalar(gva[:, :, 0:HD], bank[0][0:LAT, 0:LAT].rearrange("p (h e) -> p h e", e=HD), 1.0 / CHUNK, None, ALU.mult).then_inc(lat_in.sem, 1)
                    for t in range(TPB):
                        v.wait_ge(gate_up.sem, t + 1)
                        if t:
                            v.wait_ge(gate_sum.sem, t)
                        v.tensor_tensor(gprod[:, :, :], gw[:, :, :], spread(bank[1 + t][:, 0:DIM], 1, 2), ALU.mult).then_inc(gate_mul.sem, 1)
                        v.wait_ge(gate_mul.sem, t + 1)
                        v.tensor_reduce(logit[:, t, :, :].rearrange("p a h -> p (a h)"), gprod[:, :, :].rearrange("p a (h e) -> p (a h) e", e=HD),
                                        X, ALU.add).then_inc(gate_sum.sem, 1)
            st.restart()

            t_scored = st.event("t_scored", 3)
            t_maxed = st.event("t_maxed", 3)
            t_split = st.event("t_split", 4)
            t_m_up = st.event("t_m_up", 2)
            t_m_in = st.event("t_m_in", 2)
            t_shifted = st.event("t_shifted", 2)
            t_exped = st.event("t_exped", 2)
            t_weighed = st.event("t_weighed", 2)
            t_norm = st.event("t_norm", 5)
            t_remT_up = st.event("t_remT_up", 1)
            t_remT_in = st.event("t_remT_in", 1)
            t_rem_up = st.event("t_rem_up", 1)
            t_mix = st.event("t_mix", 2)
            t_mixT_up = st.event("t_mixT_up", 1)
            t_mixT_in = st.event("t_mixT_in", 1)
            t_y_up = st.event("t_y_up", 1)
            t_done = st.event("t_done", 1)
            strip = lambda j: slice(32 * j, 32 * j + HD)
            with nc.Block() as block:
                @block.tensor
                def _(pe):
                    for t in range(TPB):
                        f, own = min(t, 1), slice(t * P, (t + 1) * P)
                        carry = WIN if t else 0
                        pe.wait_ge(t_done.sem, t)
                        for half in range(2):
                            for j in range(4):
                                out = bank[2 * j + half].rearrange("p (a k) -> p a k", a=2)[:, :, WIN - carry:WIN + P]
                                pe.matmul(out, identb[:, :], spread(mask[:, f, WIN - carry:], 1, 2), start=True, stop=False, skip_group_check=True)
                                for c2 in range(2):
                                    c = 2 * half + c2
                                    m = pe.matmul(out[:, c2, :], qT[strip(j), c, own], kT[strip(j), c, t * P - carry:(t + 1) * P],
                                                  start=False, stop=True, skip_group_check=True, tile_position=(32 * j, 0))
                            m.then_inc(t_scored.sem, 1)
                        pe.wait_ge(t_split.sem, t_split.at(t, 2))
                        pe.transpose(bank[0].bitcast(BF16)[0:2 * H, 0:P], hl[:, :, :].rearrange("p a h -> p (a h)"), identb[:, :]).then_inc(t_m_up.sem, 1)
                        pe.wait_ge(t_m_in.sem, t_m_in.at(t, 1))
                        for j in range(4):
                            for a in range(1 + f):
                                n = (P, WIN)[a]
                                out = bank[2 * j + a][0:n].rearrange("p (c k) -> p c k", c=G)
                                lo = (t * P, t * P - WIN)[a]
                                pe.matmul(out, identb[:, 0:n], spread(maskt[:, f, a, :], 1, G), start=True, stop=False, skip_group_check=True)
                                for c in range(G):
                                    col = 4 * j + c
                                    pe.matmul(out[:, c, :], sel[:, col, 0:n], nmT[:, :], start=False, stop=False, skip_group_check=True)
                                    m = pe.matmul(out[:, c, :], kT[strip(j), c, lo:lo + n], qT[strip(j), c, own],
                                                  start=False, stop=True, skip_group_check=True, tile_position=(32 * j, 0))
                        m.then_inc(t_shifted.sem, 1)
                        pe.wait_ge(t_exped.sem, t_exped.at(t, 1))
                        for j in range(4):
                            for c in range(G):
                                h = 4 * c + j
                                out = bank[0][:, h * 9:h * 9 + 9]
                                m = pe.matmul(out, pt[:, j, c, :], va[:, t, h, :], start=True, stop=not t, skip_group_check=True)
                                if t:
                                    m = pe.matmul(out, pc[:, j, c, :], vc[:, t, h, :], start=False, stop=True, skip_group_check=True)
                        m.then_inc(t_weighed.sem, 1)
                        for j in range(4):
                            out = bank[2 * j + 1][:, 0:LG * LAT].rearrange("p (c k) -> p c k", c=LG)
                            pe.matmul(out, identb[:, :], spread(maskl[:, t, :], 1, LG), start=True, stop=False, skip_group_check=True)
                            for c in range(LG):
                                m = pe.matmul(out[:, c, :], gqT[strip(j), c, own], gkT[strip(j), c, :],
                                              start=False, stop=True, skip_group_check=True, tile_position=(32 * j, 0))
                        m.then_inc(t_scored.sem, 1)
                        pe.wait_ge(t_split.sem, t_split.at(t, 4))
                        pe.transpose(bank[2].bitcast(BF16)[0:2 * H, 0:P], hl[:, :, :].rearrange("p a h -> p (a h)"), identb[:, :]).then_inc(t_m_up.sem, 1)
                        pe.wait_ge(t_m_in.sem, t_m_in.at(t, 2))
                        for j in range(4):
                            out = bank[2 * j + 1][0:LAT, 0:LG * P].rearrange("p (c k) -> p c k", c=LG)
                            pe.matmul(out, identb[0:LAT, 0:LAT], spread(masklt[:, t, :], 1, LG), start=True, stop=False, skip_group_check=True)
                            for c in range(LG):
                                pe.matmul(out[:, c, :], sel[:, LG * j + c, 0:LAT], nmT[:, :], start=False, stop=False, skip_group_check=True)
                                m = pe.matmul(out[:, c, :], gkT[strip(j), c, :], gqT[strip(j), c, own],
                                              start=False, stop=True, skip_group_check=True, tile_position=(32 * j, 0))
                        m.then_inc(t_shifted.sem, 1)
                        pe.wait_ge(t_exped.sem, t_exped.at(t, 2))
                        for j in range(4):
                            for c in range(LG):
                                h = 4 * c + j
                                m = pe.matmul(bank[2][:, h * 9:h * 9 + 9], ptl[:, j, c, :], gva[:, h, :], start=True, stop=True, skip_group_check=True)
                        m.then_inc(t_weighed.sem, 1)
                        pe.wait_ge(t_norm.sem, t_norm.at(t, 5))
                        pe.transpose(bank[4][0:LAT, 0:P], rem[:, :], ident[:, :]).then_inc(t_remT_up.sem, 1)
                        pe.wait_ge(t_remT_in.sem, t + 1)
                        pe.matmul(bank[4][:, 0:DIM], remT[:, :], wr[:, :], start=True, stop=True).then_inc(t_rem_up.sem, 1)
                        pe.wait_ge(t_mix.sem, t_mix.at(t, 2))
                        pe.transpose(bank[6][:, 0:P], mix[:, :], ident[:, :]).then_inc(t_mixT_up.sem, 1)
                        pe.wait_ge(t_mixT_in.sem, t + 1)
                        pe.matmul(bank[6][:, P:P + DIM], mixT[:, :], wo[:, :], start=True, stop=True).then_inc(t_y_up.sem, 1)

                @block.scalar
                def _(act):
                    for t in range(TPB):
                        act.wait_ge(t_shifted.sem, t_shifted.at(t, 1))
                        own = all8[:, 0:8:2, :]
                        m = act.activation(pt[:, :, :, :].rearrange("p j c k -> p j (c k)"), own, ACT.Exp)
                        if t:
                            m = act.activation(pc[:, :, :, :].rearrange("p j c k -> p j (c k)"), all8[0:WIN, 1:8:2, :], ACT.Exp)
                        m.then_inc(t_exped.sem, 1)
                        act.wait_ge(t_shifted.sem, t_shifted.at(t, 2))
                        act.activation(ptl[:, :, :, :].rearrange("p j c k -> p j (c k)"), all8[0:LAT, 1:8:2, 0:LG * P], ACT.Exp).then_inc(t_exped.sem, 1)
                        act.wait_ge(t_remT_up.sem, t + 1)
                        act.activation(remT[:, :], bank[4][0:LAT, 0:P], ACT.Copy).then_inc(t_remT_in.sem, 1)
                        act.wait_ge(t_mixT_up.sem, t + 1)
                        act.activation(mixT[:, :], bank[6][:, 0:P], ACT.Copy).then_inc(t_mixT_in.sem, 1)

                @block.vector
                def _(v):
                    def split(t, k, src, up, n):
                        v.tensor_copy(hl[:, 0, 0:n], nmax[:, 0:n]).then_inc(t_split.sem, 1)
                        v.wait_ge(t_split.sem, t_split.at(t, 2 * k + 1))
                        v.tensor_tensor(hl[:, 1, 0:n], nmax[:, 0:n], hl[:, 0, 0:n], ALU.subtract).then_inc(t_split.sem, 1)
                        v.wait_ge(t_m_up.sem, t_m_up.at(t, k + 1))
                        v.tensor_copy(nmT[0:2 * H, :], src).then_inc(t_m_in.sem, 1)

                    for t in range(TPB):
                        carry = WIN if t else 0
                        for half in range(2):
                            v.wait_ge(t_scored.sem, t_scored.at(t, half + 1))
                            for j in range(4):
                                m = v.tensor_reduce(nmax[:, 4 * j + 2 * half:4 * j + 2 * half + 2],
                                                    bank[2 * j + half].rearrange("p (a k) -> p a k", a=2)[:, :, WIN - carry:WIN + P],
                                                    X, ALU.max, negate=True)
                            m.then_inc(t_maxed.sem, 1)
                        v.wait_ge(t_maxed.sem, t_maxed.at(t, 2))
                        split(t, 0, bank[0].bitcast(BF16)[0:2 * H, 0:P], t_m_up, H)
                        v.wait_ge(t_weighed.sem, t_weighed.at(t, 1))
                        out = bank[0][:, 0:H * 9].rearrange("p (h e) -> p h e", e=9)
                        v.reciprocal(rden[:, :], out[:, :, HD]).then_inc(t_norm.sem, 1)
                        v.wait_ge(t_norm.sem, t_norm.at(t, 1))
                        v.tensor_tensor(rden[:, :], rden[:, :], gates[:, t, 0, :], ALU.mult).then_inc(t_norm.sem, 1)
                        v.wait_ge(t_norm.sem, t_norm.at(t, 2))
                        v.tensor_tensor(loc[:, :].rearrange("p (h e) -> p h e", e=HD), out[:, :, 0:HD], spread(rden[:, :], 2, HD), ALU.mult).then_inc(t_norm.sem, 1)
                        v.wait_ge(t_scored.sem, t_scored.at(t, 3))
                        for j in range(4):
                            m = v.tensor_reduce(nmax[:, LG * j:LG * j + LG], bank[2 * j + 1][:, 0:LG * LAT].rearrange("p (c k) -> p c k", c=LG),
                                                X, ALU.max, negate=True)
                        m.then_inc(t_maxed.sem, 1)
                        v.wait_ge(t_maxed.sem, t_maxed.at(t, 3))
                        split(t, 1, bank[2].bitcast(BF16)[0:2 * H, 0:P], t_m_up, LH)
                        v.wait_ge(t_weighed.sem, t_weighed.at(t, 2))
                        outl = bank[2][:, 0:LH * 9].rearrange("p (h e) -> p h e", e=9)
                        v.reciprocal(rdl[:, :], outl[:, :, HD]).then_inc(t_norm.sem, 1)
                        v.wait_ge(t_norm.sem, t_norm.at(t, 4))
                        v.tensor_tensor(rem[:, :].rearrange("p (h e) -> p h e", e=HD), outl[:, :, 0:HD], spread(rdl[:, :], 2, HD), ALU.mult).then_inc(t_norm.sem, 1)
                        v.wait_ge(t_rem_up.sem, t + 1)
                        v.tensor_tensor(remg[:, :].rearrange("p (h e) -> p h e", e=HD), bank[4][:, 0:DIM].rearrange("p (h e) -> p h e", e=HD),
                                        spread(gates[:, t, 1, :], 2, HD), ALU.mult).then_inc(t_mix.sem, 1)
                        v.wait_ge(t_mix.sem, t_mix.at(t, 1))
                        v.tensor_tensor(mix[:, :], loc[:, :], remg[:, :], ALU.add).then_inc(t_mix.sem, 1)
                        v.wait_ge(t_y_up.sem, t + 1)
                        v.tensor_copy(s[:, bass.ds(b * TPB + t, 1), :].rearrange("p a c -> p (a c)"), bank[6][:, P:P + DIM]).then_inc(t_done.sem, 1)
            st.restart()


def ffn0(nc, g, d):
    HID, BL = 352, 16
    HC = [(c, min(P, HID - c)) for c in range(0, HID, P)]
    u, ident, xn = g["u"], g["ident"], g["xn"]
    MAXN = TPB * HID
    with Stage(nc, "f0") as st:
        wgu = st.sb("wgu", [P, 2, len(HC), DIM])
        wd = st.sb("wd", [P, HID])
        wguT = st.sb("wguT", [P, 2, HID])
        wdT = st.sb("wdT", [P, len(HC), DIM])
        src = st.sb("src", [P, MAXN])
        mag = st.sb("mag", [P, MAXN])
        sgn = st.sb("sgn", [P, MAXN])
        acc = st.sb("acc", [P, MAXN])
        low = st.sb("low", [P, MAXN])
        scale = st.sb("scale", [P, MAXN // BL])
        inverse = st.sb("inverse", [P, MAXN // BL])
        xqT = st.sb("xqT", [P, SEQ])
        sil = st.sb("sil", [P, 2, HID])
        hqT = st.sb("hqT", [P, len(HC), SEQ])
        bank = [st.bank(f"bank{i}") for i in range(8)]
        loaded = st.sem("loaded")
        zeroed = st.sem("zeroed")

        STEPS = 14

        def round_fp4(v, stepped, base, signed, sign_at, n):
            a, q, lo = (z[:, 0:n] for z in (mag, acc, low))
            blk = lambda z: z.rearrange("p (k e) -> p k e", e=BL)
            sc = scale[:, 0:n // BL]
            k = base

            def step(m):
                nonlocal k
                k += 1
                m.then_inc(stepped.sem, 1)
                v.wait_ge(stepped.sem, k)

            v.wait_ge(signed.sem, sign_at)
            step(v.tensor_reduce(sc, blk(a), X, ALU.max))
            step(v.tensor_scalar(sc, sc, 1.0 / 6.0, 1e-12, ALU.mult, ALU.max))
            step(v.reciprocal(inverse[:, 0:n // BL], sc))
            step(v.tensor_tensor(blk(a), blk(a), spread(inverse[:, 0:n // BL], 2, BL), ALU.mult))
            step(v.tensor_scalar(q, a, 5.0, 2.0, ALU.is_gt, ALU.mult))
            for mid in (3.5, 2.5):
                step(v.scalar_tensor_tensor(out=q, in0=a, scalar=mid, in1=q, op0=ALU.is_gt, op1=ALU.add))
            step(v.tensor_scalar(lo, a, 1.75, None, ALU.is_gt))
            for mid in (1.25, 0.75, 0.25):
                step(v.scalar_tensor_tensor(out=lo, in0=a, scalar=mid, in1=lo, op0=ALU.is_gt, op1=ALU.add))
            step(v.scalar_tensor_tensor(out=q, in0=lo, scalar=0.5, in1=q, op0=ALU.mult, op1=ALU.add))
            step(v.tensor_tensor(q, q, sgn[:, 0:n], ALU.mult))
            step(v.tensor_tensor(blk(q), blk(q), spread(sc, 2, BL), ALU.mult))

        stepped = st.event("stepped")
        staged = st.event("staged")
        signed = st.event("signed")
        turned = st.event("turned")
        placed = st.event("placed")
        NW = 2 * len(HC) * DIM
        with nc.Block() as block:
            @block.gpsimd
            def _(pool):
                pool.memset(wgu[:, :, :, :], 0.0).then_inc(zeroed, 1)

            @block.sync
            def _(sp):
                sp.wait_ge(zeroed, 1)
                for k, name in enumerate(("gate", "up")):
                    w = d[f"L0_ffn_w_{name}"]
                    sp.dma_start(wgu[:, k, 0:2, :], w[0:2 * P, :].rearrange("(c p) n -> p c n", p=P)).then_inc(loaded, 16)
                    sp.dma_start(wgu[0:HID - 2 * P, k, 2, :], w[2 * P:HID, :]).then_inc(loaded, 16)
                sp.dma_start(wd[:, :], d["L0_ffn_w_down"]).then_inc(loaded, 16)
                sp.wait_ge(loaded, 5 * 16)

            @block.vector
            def _(v):
                v.wait_ge(loaded, 5 * 16)
                v.wait_ge(zeroed, 1)
                v.tensor_copy(src[:, 0:NW], wgu[:, :, :, :].rearrange("p a c n -> p (a c n)")).then_inc(staged.sem, 1)
                v.tensor_copy(src[:, NW:NW + HID], wd[:, :]).then_inc(staged.sem, 1)
                v.wait_ge(staged.sem, 2)
                round_fp4(v, stepped, 0, signed, 2, NW + HID)

            @block.scalar
            def _(act):
                act.wait_ge(staged.sem, 2)
                act.activation(mag[:, 0:NW + HID], src[:, 0:NW + HID], ACT.Abs).then_inc(signed.sem, 1)
                act.activation(sgn[:, 0:NW + HID], src[:, 0:NW + HID], ACT.Sign).then_inc(signed.sem, 1)
                for k in range(2):
                    act.wait_ge(turned.sem, k + 1)
                    act.activation(wguT[:, k, :], bank[k][:, 0:HID], ACT.Copy).then_inc(placed.sem, 1)
                act.wait_ge(turned.sem, 3)
                for c, (at, size) in enumerate(HC):
                    act.activation(wdT[0:size, c, :], bank[2][0:size, c * P:(c + 1) * P], ACT.Copy).then_inc(placed.sem, 1)

            @block.tensor
            def _(pe):
                pe.wait_ge(stepped.sem, STEPS)
                for k in range(2):
                    for c, (at, size) in enumerate(HC):
                        lo = (k * len(HC) + c) * DIM
                        m = pe.transpose(bank[k][:, at:at + size], acc[0:size, lo:lo + DIM], ident[0:size, 0:size])
                    m.then_inc(turned.sem, 1)
                for c, (at, size) in enumerate(HC):
                    m = pe.transpose(bank[2][0:size, c * P:c * P + P], acc[:, NW + at:NW + at + size], ident[:, :])
                m.then_inc(turned.sem, 1)
        st.restart()

        xqT_up = st.event("xqT_up")
        xqT_in = st.event("xqT_in")
        hid_up = st.event("hid_up")
        silued = st.event("silued")
        hid_in = st.event("hid_in")
        hqT_up = st.event("hqT_up")
        hqT_in = st.event("hqT_in")
        y_up = st.event("y_up")
        y_in = st.event("y_in")
        with nc.Fori(0, BATCH) as b:
            with nc.Block() as block:
                @block.vector
                def _(v):
                    v.tensor_copy(src[:, 0:TPB * DIM], xn[:, bass.ds(b * TPB, TPB), :].rearrange("p t c -> p (t c)")).then_inc(staged.sem, 1)
                    v.wait_ge(staged.sem, 1)
                    round_fp4(v, stepped, 0, signed, 2, TPB * DIM)
                    for t in range(TPB):
                        v.wait_ge(silued.sem, t + 1)
                        v.tensor_tensor(src[:, t * HID:(t + 1) * HID], sil[:, t % 2, :], bank[2 * (t % 2) + 1][:, 0:HID], ALU.mult).then_inc(hid_in.sem, 1)
                    v.wait_ge(hid_in.sem, TPB)
                    v.wait_ge(xqT_up.sem, 1)
                    round_fp4(v, stepped, STEPS, signed, 4, MAXN)
                    for t in range(TPB):
                        v.wait_ge(y_up.sem, t + 1)
                        v.tensor_copy(u[:, bass.ds(b * TPB + t, 1), :].rearrange("p a c -> p (a c)"), bank[4 + t][:, 0:DIM]).then_inc(y_in.sem, 1)

                @block.scalar
                def _(act):
                    act.wait_ge(staged.sem, 1)
                    act.activation(mag[:, 0:TPB * DIM], src[:, 0:TPB * DIM], ACT.Abs).then_inc(signed.sem, 1)
                    act.activation(sgn[:, 0:TPB * DIM], src[:, 0:TPB * DIM], ACT.Sign).then_inc(signed.sem, 1)
                    act.wait_ge(xqT_up.sem, 1)
                    act.activation(xqT[:, :], bank[4][:, :], ACT.Copy).then_inc(xqT_in.sem, 1)
                    for t in range(TPB):
                        act.wait_ge(hid_up.sem, t + 1)
                        if t >= 2:
                            act.wait_ge(hid_in.sem, t - 1)
                        act.activation(sil[:, t % 2, :], bank[2 * (t % 2)][:, 0:HID], ACT.Silu).then_inc(silued.sem, 1)
                    act.wait_ge(hid_in.sem, TPB)
                    act.activation(mag[:, :], src[:, :], ACT.Abs).then_inc(signed.sem, 1)
                    act.activation(sgn[:, :], src[:, :], ACT.Sign).then_inc(signed.sem, 1)
                    for c, (at, size) in enumerate(HC):
                        act.wait_ge(hqT_up.sem, c + 1)
                        act.activation(hqT[0:size, c, :], bank[c][0:size, :], ACT.Copy).then_inc(hqT_in.sem, 1)

                @block.tensor
                def _(pe):
                    pe.wait_ge(stepped.sem, STEPS)
                    for t in range(TPB):
                        m = pe.transpose(bank[4][:, t * P:(t + 1) * P], acc[:, t * DIM:(t + 1) * DIM], ident[:, :])
                    m.then_inc(xqT_up.sem, 1)
                    pe.wait_ge(xqT_in.sem, 1)
                    for t in range(TPB):
                        if t >= 2:
                            pe.wait_ge(hid_in.sem, t - 1)
                        pe.matmul(bank[2 * (t % 2)][:, 0:HID], xqT[:, t * P:(t + 1) * P], wguT[:, 0, :], start=True, stop=True)
                        pe.matmul(bank[2 * (t % 2) + 1][:, 0:HID], xqT[:, t * P:(t + 1) * P], wguT[:, 1, :], start=True, stop=True).then_inc(hid_up.sem, 1)
                    pe.wait_ge(stepped.sem, 2 * STEPS)
                    for c, (at, size) in enumerate(HC):
                        for t in range(TPB):
                            m = pe.transpose(bank[c][0:size, t * P:(t + 1) * P], acc[:, t * HID + at:t * HID + at + size], ident[:, :])
                        m.then_inc(hqT_up.sem, 1)
                    pe.wait_ge(hqT_in.sem, len(HC))
                    for t in range(TPB):
                        for c, (at, size) in enumerate(HC):
                            m = pe.matmul(bank[4 + t][:, 0:DIM], hqT[0:size, c, t * P:(t + 1) * P], wdT[0:size, c, :],
                                          start=(c == 0), stop=(c == len(HC) - 1))
                        m.then_inc(y_up.sem, 1)
            st.restart()


def attention1(nc, g, d):
    H, HD = 16, 64
    PAIRS = H // 2
    s, ident, identb, xnT = g["s"], g["ident"], g["identb"], g["xnT"]
    with Stage(nc, "a1") as st:
        wq = st.sb("wq", [P, H * HD])
        wk = st.sb("wk", [P, H * HD])
        wv = st.sb("wv", [P, H * HD])
        wu = st.sb("wu", [P, PAIRS, DIM])
        bu = st.sb("bu", [1, DIM])
        ones = st.sb("ones", [1, P])
        maskq = st.sb("maskq", [P, P], BF16)
        maskk = st.sb("maskk", [P, P], BF16)
        sel = st.sb("sel", [2 * H, H, P], BF16)
        xb = st.sb("xb", [P, SEQ])
        qT = st.sb("qT", [P, PAIRS, SEQ])
        kT = st.sb("kT", [P, PAIRS, SEQ])
        va = st.sb("va", [P, TPB, H, HD + 1])
        nmax = st.sb("nmax", [P, TPB, H])
        hl = st.sb("hl", [P, TPB, 2, H], BF16)
        nmT = st.sb("nmT", [2 * H, SEQ], BF16)
        pt = st.sb("pt", [P, 2, TPB, SEQ])
        rden = st.sb("rden", [P, 2, TPB])
        o = st.sb("o", [P, TPB, H * HD])
        oT = st.sb("oT", [P, 2, PAIRS, P])
        bank = [st.bank(f"bank{i}") for i in range(8)]
        loaded = st.sem("loaded")
        zeroed = st.sem("zeroed")
        xb_in = st.event("xb_in")
        NPROJ = 2 * PAIRS + 2 * TPB
        proj = st.event("proj", NPROJ)
        proj_in = st.event("proj_in")
        projv_in = st.event("projv_in")
        scored = st.event("scored")
        maxed = st.event("maxed")
        split = st.event("split")
        m_up = st.event("m_up")
        m_in = st.event("m_in")
        shifted = st.event("shifted")
        exped = st.event("exped", 3)
        weighed = st.event("weighed")
        recip = st.event("recip")
        o_in = st.event("o_in")
        oT_up = st.event("oT_up")
        oT_in = st.event("oT_in")
        y_up = st.event("y_up")
        y_in = st.event("y_in")

        with nc.Block() as block:
            @block.sync
            def _(sp):
                sp.dma_start(wq[:, :], d["L1_attn_w_q"]).then_inc(loaded, 16)
                sp.dma_start(wk[:, :], d["L1_attn_w_k"]).then_inc(loaded, 16)
                sp.dma_start(wv[:, :], d["L1_attn_w_v"]).then_inc(loaded, 16)
                sp.dma_start(wu[:, :, :], d["L1_attn_w_u"].rearrange("(c p) n -> p c n", p=P)).then_inc(loaded, 16)
                sp.dma_start(bu[:, :], d["L1_attn_b_u"].rearrange("(a n) -> a n", a=1)).then_inc(loaded, 16)
                sp.dma_start(maskq[:, :], d["c_causal"][0]).then_inc(loaded, 16)
                sp.dma_start(maskk[:, :], d["c_causal"][1]).then_inc(loaded, 16)
                sp.dma_start(sel[:, :, :], d["c_sel16"]).then_inc(loaded, 16)
                sp.wait_ge(loaded, 8 * 16)

            @block.gpsimd
            def _(pool):
                pool.memset(va[:, :, :, :], 1.0).then_inc(zeroed, 1)
                pool.memset(ones[:, :], 1.0).then_inc(zeroed, 1)

        def spot(j):
            return {0: (0, 0), 1: (1, 0), 2: (2, 0), 3: (1, 3 * P)}[j]

        with nc.Fori(0, BATCH) as b:
            with nc.Block() as block:
                @block.tensor
                def _(pe):
                    pe.wait_ge(xb_in.sem, 1)
                    for n in range(NPROJ):
                        if n >= 8:
                            pe.wait_ge((proj_in, projv_in)[n % 2].sem, (n - 8) // 2 + 1)
                        if n < 2 * PAIRS:
                            w = (wq, wk)[n // PAIRS]
                            c = n % PAIRS
                            m = pe.matmul(bank[n % 8][:, :], w[:, c * P:(c + 1) * P], xb[:, :], start=True, stop=True)
                        else:
                            t, c = divmod(n - 2 * PAIRS, 2)
                            m = pe.matmul(bank[n % 8][:, :], xb[:, t * P:(t + 1) * P], wv[:, c * 512:(c + 1) * 512], start=True, stop=True)
                        m.then_inc(proj.sem, 1)
                    pe.wait_ge(proj_in.sem, NPROJ // 2)
                    pe.wait_ge(projv_in.sem, NPROJ // 2)
                    for t in range(TPB):
                        for c in range(PAIRS):
                            n = t * PAIRS + c
                            if n >= 4:
                                pe.wait_ge(maxed.sem, n - 3)
                            for p in range(2):
                                rows = slice(64 * p, 64 * p + 64)
                                out = bank[2 * (n % 4) + p]
                                pe.matmul(out[:, 0:(t + 1) * P], qT[rows, c, t * P:(t + 1) * P], kT[rows, c, 0:(t + 1) * P],
                                          start=True, stop=False, skip_group_check=True)
                                m = pe.matmul(out[:, t * P:(t + 1) * P], identb[:, :], maskq[:, :],
                                              start=False, stop=True, skip_group_check=True)
                            m.then_inc(scored.sem, 1)
                    pe.wait_ge(split.sem, 2)
                    for t in range(TPB):
                        m = pe.transpose(bank[7][:, 0:SEQ // 2].bitcast(BF16)[0:2 * H, t * P:(t + 1) * P], hl[:, t, :, :].rearrange("p a h -> p (a h)"),
                                         identb[:, :])
                    m.then_inc(m_up.sem, 1)
                    pe.wait_ge(m_in.sem, 1)

                    def shift(h):
                        p, c = h % 2, h // 2
                        rows = slice(64 * p, 64 * p + 64)
                        if h >= 2:
                            pe.wait_ge(exped.sem, 3 * (h - 1))
                        for j in range(TPB):
                            k, at = spot(j)
                            n = (TPB - j) * P
                            out = bank[3 * p + k][:, at:at + n]
                            pe.matmul(out, sel[:, h, :], nmT[:, j * P:SEQ], start=True, stop=False, skip_group_check=True)
                            pe.matmul(out[:, 0:P], identb[:, :], maskk[:, :], start=False, stop=False, skip_group_check=True)
                            m = pe.matmul(out, kT[rows, c, j * P:(j + 1) * P], qT[rows, c, j * P:SEQ],
                                          start=False, stop=True, skip_group_check=True)
                        m.then_inc(shifted.sem, 1)

                    def weigh(h):
                        pe.wait_ge(exped.sem, 3 * (h + 1))
                        if h >= 2:
                            pe.wait_ge(o_in.sem, h - 1)
                        for i in range(TPB):
                            for j in range(i + 1):
                                m = pe.matmul(bank[6 + h % 2][:, i * 65:i * 65 + 65], pt[:, h % 2, j, i * P:(i + 1) * P], va[:, j, h, :],
                                              start=(j == 0), stop=(j == i), skip_group_check=True)
                        m.then_inc(weighed.sem, 1)

                    for h in range(H + 1):
                        if h < H:
                            shift(h)
                        if h >= 1:
                            weigh(h - 1)
                    pe.wait_ge(o_in.sem, H)
                    for t in range(TPB):
                        for half in range(2):
                            n = 2 * t + half
                            if n >= 4:
                                pe.wait_ge(oT_in.sem, n - 3)
                            for j in range(4):
                                c = 4 * half + j
                                m = pe.transpose(bank[n % 4][:, j * P:(j + 1) * P], o[:, t, c * P:(c + 1) * P], ident[:, :])
                            m.then_inc(oT_up.sem, 1)
                        pe.wait_ge(oT_in.sem, 2 * t + 2)
                        if t >= 2:
                            pe.wait_ge(y_in.sem, t - 1)
                        for c in range(PAIRS):
                            pe.matmul(bank[4 + t % 2][:, 0:DIM], oT[:, t % 2, c, :], wu[:, c, :], start=(c == 0), stop=False)
                        pe.matmul(bank[4 + t % 2][:, 0:DIM], ones[:, :], bu[:, :], start=False, stop=True).then_inc(y_up.sem, 1)

                def evacuate(n, copy):
                    src = bank[n % 8]
                    if n < PAIRS:
                        return copy(qT[:, n, :], src[:, :], 1.0 / HD)
                    if n < 2 * PAIRS:
                        return copy(kT[:, n - PAIRS, :], src[:, :], 1.0)
                    t, c = divmod(n - 2 * PAIRS, 2)
                    return copy(va[:, t, 8 * c:8 * c + 8, 0:HD], src[:, :].rearrange("p (h d) -> p h d", h=8), 1.0)

                @block.scalar
                def _(act):
                    act.activation(xb[:, :], xnT[:, bass.ds(b * SEQ, SEQ)], ACT.Copy).then_inc(xb_in.sem, 1)
                    for n in range(0, NPROJ, 2):
                        act.wait_ge(proj.sem, n + 1)
                        evacuate(n, lambda dst, src, k: act.activation(dst, src, ACT.Copy, scale=k)).then_inc(proj_in.sem, 1)
                    for h in range(H):
                        act.wait_ge(shifted.sem, h + 1)
                        if h >= 2:
                            act.wait_ge(weighed.sem, h - 1)
                        for js in ((0,), (1, 3), (2,)):
                            for j in js:
                                k, at = spot(j)
                                m = act.activation(pt[:, h % 2, j, j * P:SEQ], bank[3 * (h % 2) + k][:, at:at + (TPB - j) * P], ACT.Exp)
                            m.then_inc(exped.sem, 1)
                    for n in range(2 * TPB):
                        act.wait_ge(oT_up.sem, n + 1)
                        if n >= 4:
                            act.wait_ge(y_in.sem, n // 2 - 1)
                        act.activation(oT[:, (n // 2) % 2, 4 * (n % 2):4 * (n % 2) + 4, :].rearrange("p a b -> p (a b)"), bank[n % 4][:, :],
                                       ACT.Copy).then_inc(oT_in.sem, 1)

                @block.vector
                def _(v):
                    for n in range(1, NPROJ, 2):
                        v.wait_ge(proj.sem, n + 1)
                        evacuate(n, lambda dst, src, k: v.tensor_scalar(dst, src, k, None, ALU.mult)).then_inc(projv_in.sem, 1)
                    for t in range(TPB):
                        for c in range(PAIRS):
                            n = t * PAIRS + c
                            v.wait_ge(scored.sem, n + 1)
                            for p in range(2):
                                m = v.tensor_reduce(nmax[:, t, 2 * c + p:2 * c + p + 1], bank[2 * (n % 4) + p][:, 0:(t + 1) * P], X, ALU.max, negate=True)
                            m.then_inc(maxed.sem, 1)
                    v.wait_ge(maxed.sem, TPB * PAIRS)
                    v.tensor_copy(hl[:, :, 0, :], nmax[:, :, :]).then_inc(split.sem, 1)
                    v.wait_ge(split.sem, 1)
                    v.tensor_tensor(hl[:, :, 1, :], nmax[:, :, :], hl[:, :, 0, :], ALU.subtract).then_inc(split.sem, 1)
                    v.wait_ge(m_up.sem, 1)
                    v.tensor_copy(nmT[:, :], bank[7][:, 0:SEQ // 2].bitcast(BF16)[0:2 * H, :]).then_inc(m_in.sem, 1)
                    for h in range(H):
                        v.wait_ge(weighed.sem, h + 1)
                        out = bank[6 + h % 2][:, 0:TPB * 65].rearrange("p (t e) -> p t e", t=TPB)
                        v.reciprocal(rden[:, h % 2, :], out[:, :, HD]).then_inc(recip.sem, 1)
                        v.wait_ge(recip.sem, h + 1)
                        v.tensor_tensor(o[:, :, h * HD:(h + 1) * HD], out[:, :, 0:HD], spread(rden[:, h % 2, :], 2, HD), ALU.mult).then_inc(o_in.sem, 1)
                    for t in range(TPB):
                        v.wait_ge(y_up.sem, t + 1)
                        v.tensor_copy(s[:, bass.ds(b * TPB + t, 1), :].rearrange("p a c -> p (a c)"), bank[4 + t % 2][:, 0:DIM]).then_inc(y_in.sem, 1)
            st.restart()


def ffn1(nc, g, d):
    HID, C = 512, 4
    u, xnT = g["u"], g["xnT"]
    with Stage(nc, "f1") as st:
        w1 = st.sb("w1", [P, HID])
        w2 = st.sb("w2", [P, HID])
        h1 = st.sb("h1", [P, C, HID])
        h2 = st.sb("h2", [P, C, HID])
        w3 = st.sb("w3", [P, C, DIM])
        sc = st.sb("sc", [P, 4, C])
        s3 = st.sb("s3", [P, DIM])
        xb = st.sb("xb", [P, SEQ])
        a1 = st.sb("a1", [P, C, SEQ])
        a2 = st.sb("a2", [P, C, SEQ])
        a3 = st.sb("a3", [P, C, SEQ])
        bank = [st.bank(f"bank{i}") for i in range(8)]
        loaded = st.sem("loaded")
        xb_in = st.event("xb_in")
        first = st.event("first", C)
        silued = st.event("silued", C)
        gated = st.event("gated", C)
        second = st.event("second", C)
        gelu1 = st.event("gelu1", C)
        third = st.event("third", C)
        gelu2 = st.event("gelu2", C)
        y_up = st.event("y_up", TPB)
        y_in = st.event("y_in", TPB)
        with nc.Block() as block:
            @block.sync
            def _(sp):
                sp.dma_start(w1[:, :], d["t_L1_ffn_w1_w"]).then_inc(loaded, 16)
                sp.dma_start(w2[:, :], d["t_L1_ffn_w2_w"]).then_inc(loaded, 16)
                sp.dma_start(h1[:, :, :], d["t_L1_ffn_h1_w"].rearrange("(c p) n -> p c n", p=P)).then_inc(loaded, 16)
                sp.dma_start(h2[:, :, :], d["t_L1_ffn_h2_w"].rearrange("(c p) n -> p c n", p=P)).then_inc(loaded, 16)
                sp.dma_start(w3[:, :, :], d["t_L1_ffn_w3_w"].rearrange("(c p) n -> p c n", p=P)).then_inc(loaded, 16)
                for k, name in enumerate(("w1", "w2", "h1", "h2")):
                    sp.dma_start(sc[:, k, :], d[f"L1_ffn_{name}_s"].rearrange("(c p) -> p c", p=P), allow_slow_non_contiguous=True).then_inc(loaded, 16)
                sp.dma_start(s3[:, :], d["L1_ffn_w3_s"].rearrange("(a n) -> a n", a=1).to_broadcast([P, DIM])).then_inc(loaded, 16)
                sp.wait_ge(loaded, 10 * 16)

        with nc.Fori(0, BATCH) as b:
            with nc.Block() as block:
                @block.gpsimd
                def _(pool):
                    pool.tensor_copy(xb[:, :], xnT[:, bass.ds(b * SEQ, SEQ)]).then_inc(xb_in.sem, 1)

                @block.tensor
                def _(pe):
                    pe.wait_ge(xb_in.sem, 1)
                    for c in range(C):
                        pe.matmul(bank[2 * c][:, :], w1[:, c * P:(c + 1) * P], xb[:, :], start=True, stop=True)
                        pe.matmul(bank[2 * c + 1][:, :], w2[:, c * P:(c + 1) * P], xb[:, :], start=True, stop=True).then_inc(first.sem, 1)
                    for w, src, ready, done, last in ((h1, a2, gated, second, gated), (h2, a3, gelu1, third, gelu1)):
                        pe.wait_ge(ready.sem, C)
                        for c in range(C):
                            out = bank[c if w is h1 else 4 + c]
                            for k in range(C):
                                m = pe.matmul(out[:, :], w[:, k, c * P:(c + 1) * P], src[:, k, :], start=(k == 0), stop=(k == C - 1))
                            m.then_inc(done.sem, 1)
                    pe.wait_ge(gelu2.sem, C)
                    for t in range(TPB):
                        for k in range(C):
                            m = pe.matmul(bank[t][:, 0:DIM], a2[:, k, t * P:(t + 1) * P], w3[:, k, :], start=(k == 0), stop=(k == C - 1))
                        m.then_inc(y_up.sem, 1)

                @block.scalar
                def _(act):
                    for c in range(C):
                        act.wait_ge(first.sem, c + 1)
                        act.activation(a1[:, c, :], bank[2 * c][:, :], ACT.Silu, scale=sc[:, 0, c:c + 1]).then_inc(silued.sem, 1)
                    for c in range(C):
                        act.wait_ge(second.sem, c + 1)
                        act.activation(a3[:, c, :], bank[c][:, :], ACT.Gelu, scale=sc[:, 2, c:c + 1]).then_inc(gelu1.sem, 1)
                    for c in range(C):
                        act.wait_ge(third.sem, c + 1)
                        act.activation(a2[:, c, :], bank[4 + c][:, :], ACT.Gelu, scale=sc[:, 3, c:c + 1]).then_inc(gelu2.sem, 1)

                @block.vector
                def _(v):
                    for c in range(C):
                        v.wait_ge(silued.sem, c + 1)
                        v.scalar_tensor_tensor(out=a2[:, c, :], in0=bank[2 * c + 1][:, :], scalar=sc[:, 1, c:c + 1], in1=a1[:, c, :],
                                               op0=ALU.mult, op1=ALU.mult).then_inc(gated.sem, 1)
                    for t in range(TPB):
                        v.wait_ge(y_up.sem, t + 1)
                        v.tensor_tensor(u[:, bass.ds(b * TPB + t, 1), :].rearrange("p a c -> p (a c)"), bank[t][:, 0:DIM], s3[:, :],
                                        ALU.mult).then_inc(y_in.sem, 1)
            st.restart()


def attention2(nc, g, d):
    HD, NQ, NKV = 8, 32, 8
    GH = NQ // NKV
    MAPS = BATCH * GH
    LAMBDA_INIT = 0.8 - 0.6 * float(np.exp(-0.3))
    QG, KG = 2 * DIM // HD, NKV * HD // HD
    s, ident, identb, xnT = g["s"], g["ident"], g["identb"], g["xnT"]
    with Stage(nc, "a2") as st:
        w = st.sb("w", [P, 2 * DIM + 2 * NKV * HD + 32])
        wp = st.sb("wp", [P, DIM])
        lam = st.sb("lam", [P, 4, NKV * HD])
        lprod = st.sb("lprod", [P, 2, NKV * HD])
        lsum = st.sb("lsum", [P, 2])
        lexp = st.sb("lexp", [P, 2])
        nlam = st.sb("nlam", [P, 1])
        maskq = st.sb("maskq", [P, P], BF16)
        maskk = st.sb("maskk", [P, P], BF16)
        sel = st.sb("sel", [64, MAPS, P], BF16)
        qT = st.sb("qT", [P, NQ * SEQ])
        kT = st.sb("kT", [P, NKV * SEQ])
        vT = st.sb("vT", [P, NKV * SEQ])
        va = st.sb("va", [P, NKV, TPB, BATCH, HD + 1])
        qs = st.sb("qs", [P, GH, SEQ])
        ks = st.sb("ks", [P, SEQ])
        vs = st.sb("vs", [P, TPB, BATCH, HD + 1])
        nmax = st.sb("nmax", [P, TPB, MAPS])
        hl = st.sb("hl", [P, TPB, 2, MAPS], BF16)
        nmT = st.sb("nmT", [64, SEQ], BF16)
        pt = st.sb("pt", [P, 2, TPB, SEQ])
        rden = st.sb("rden", [P, 2, GH, TPB])
        on = st.sb("on", [P, 2, GH, TPB, HD])
        att = st.sb("att", [P, BATCH, TPB, DIM])
        attT = st.sb("attT", [P, SEQ])
        y1 = st.sb("y1", [P, TPB, DIM])
        y2T = st.sb("y2T", [P, SEQ])
        bank = [st.bank(f"bank{i}") for i in range(8)]
        loaded = st.sem("loaded")
        zeroed = st.sem("zeroed")
        lamd = st.sem("lamd")
        lamx = st.sem("lamx")

        proj = st.event("proj")
        even_in = st.event("even_in")
        odd_in = st.event("odd_in")
        v_up = st.event("v_up")
        v_in = st.event("v_in")
        NG = QG + 2 * KG
        with nc.Block() as block:
            @block.gpsimd
            def _(pool):
                pool.memset(w[:, 2 * DIM + 2 * NKV * HD:], 0.0).then_inc(zeroed, 1)
                pool.memset(va[:, :, :, :, :], 1.0).then_inc(zeroed, 1)
                pool.memset(nmT[:, :], 0.0).then_inc(zeroed, 1)
                pool.memset(sel[:, :, :], 0.0).then_inc(zeroed, 1)

            @block.sync
            def _(sp):
                sp.dma_start(w[:, 0:2 * DIM + 2 * NKV * HD], d["L2_attn_Wqkv"]).then_inc(loaded, 16)
                sp.dma_start(wp[:, :], d["L2_attn_Wproj"]).then_inc(loaded, 16)
                for k, name in enumerate(("q1", "k1", "q2", "k2")):
                    sp.dma_start(lam[:, k, :], d[f"L2_attn_lambda_{name}"].rearrange("(a n) -> a n", a=1).to_broadcast([P, NKV * HD])).then_inc(loaded, 16)
                sp.dma_start(maskq[:, :], d["c_causal"][0]).then_inc(loaded, 16)
                sp.dma_start(maskk[:, :], d["c_causal"][1]).then_inc(loaded, 16)
                sp.wait_ge(zeroed, 4)
                sp.dma_start(sel[0:2 * MAPS, :, :], d["c_sel16"]).then_inc(loaded, 16)
                sp.wait_ge(loaded, 9 * 16)

            @block.tensor
            def _(pe):
                pe.wait_ge(loaded, 9 * 16)
                for n in range(NG):
                    if n >= 8:
                        pe.wait_ge((even_in, odd_in)[n % 2].sem, (n - 8) // 2 + 1)
                    for b in range(BATCH):
                        m = pe.matmul(bank[n % 8][32 * b:32 * b + 32, :], w[:, n * HD:n * HD + 32], xnT[:, b * SEQ:(b + 1) * SEQ],
                                      start=True, stop=True, tile_position=(0, 32 * b))
                    m.then_inc(proj.sem, 1)
                pe.wait_ge(even_in.sem, NG // 2)
                pe.wait_ge(odd_in.sem, NG // 2)
                for h in range(NKV):
                    for t in range(TPB):
                        m = pe.transpose(bank[h][:, t * P:(t + 1) * P], vT[:, h * SEQ + t * P:h * SEQ + (t + 1) * P], ident[:, :])
                    m.then_inc(v_up.sem, 1)

            def place(n, copy):
                if n < QG:
                    return copy(qT[:, :].rearrange("p (t r) -> p t r", r=QG)[:, :, n], bank[n % 8][:, :], HD ** -0.5)
                to, r = (kT, n - QG) if n < QG + KG else (vT, n - QG - KG)
                return copy(to[:, :].rearrange("p (t r) -> p t r", r=KG)[:, :, r], bank[n % 8][:, :], 1.0)

            @block.scalar
            def _(act):
                for n in range(0, NG, 2):
                    act.wait_ge(proj.sem, n + 1)
                    place(n, lambda dst, src, k: act.activation(dst, src, ACT.Copy, scale=k)).then_inc(even_in.sem, 1)
                act.wait_ge(lamd, 2)
                act.activation(lexp[:, :], lsum[:, :], ACT.Exp).then_inc(lamx, 1)

            @block.vector
            def _(v):
                v.wait_ge(loaded, 9 * 16)
                lm = lam[:, :, :].rearrange("p (a c) n -> p a c n", c=2)
                v.tensor_tensor(lprod[:, :, :], lm[:, :, 0, :], lm[:, :, 1, :], ALU.mult).then_inc(lamd, 1)
                v.wait_ge(lamd, 1)
                v.tensor_reduce(lsum[:, :], lprod[:, :, :], X, ALU.add).then_inc(lamd, 1)
                for n in range(1, NG, 2):
                    v.wait_ge(proj.sem, n + 1)
                    place(n, lambda dst, src, k: v.tensor_scalar(dst, src, k, None, ALU.mult)).then_inc(odd_in.sem, 1)
                v.wait_ge(zeroed, 4)
                for h in range(NKV):
                    v.wait_ge(v_up.sem, h + 1)
                    v.tensor_copy(va[:, h, :, :, 0:HD].rearrange("p t b e -> p (t b) e"),
                                  bank[h][:, :].rearrange("p (x e) -> p x e", e=32)[:, :, 0:HD]).then_inc(v_in.sem, 1)
                v.wait_ge(lamx, 1)
                v.tensor_tensor(nlam[:, :], lexp[:, 1:2], lexp[:, 0:1], ALU.subtract).then_inc(lamd, 1)
                v.wait_ge(lamd, 3)
                v.tensor_scalar(nlam[:, :], nlam[:, :], -LAMBDA_INIT, None, ALU.add)
        st.restart()

        staged = st.event("staged")
        scored = st.event("scored")
        maxed = st.event("maxed")
        split = st.event("split")
        m_up = st.event("m_up")
        m_in = st.event("m_in")
        shifted = st.event("shifted")
        exped = st.event("exped")
        weighed = st.event("weighed")
        recip = st.event("recip")
        normed = st.event("normed")
        FILLS = [(0, 0, 4), (1, 0, 2), (1, 2, 2)] + [(t, h, 1) for t in (2, 3) for h in range(GH)]
        SPOT = {0: (0, 0), 1: (1, 0), 2: (2, 0), 3: (1, 3 * P)}

        with nc.Fori(0, NKV) as kv:
            with nc.Block() as block:
                @block.gpsimd
                def _(pool):
                    pool.tensor_copy(qs[:, :, :].rearrange("p h q -> p (h q)"), qT[:, bass.ds(kv * (GH * SEQ), GH * SEQ)]).then_inc(staged.sem, 1)
                    pool.wait_ge(staged.sem, 1)
                    pool.tensor_copy(ks[:, :], kT[:, bass.ds(kv * SEQ, SEQ)]).then_inc(staged.sem, 1)
                    pool.wait_ge(staged.sem, 2)
                    pool.tensor_copy(vs[:, :, :, :].rearrange("p t b e -> p (t b e)"),
                                     va[:, bass.ds(kv, 1), :, :, :].rearrange("p a t b e -> p (a t b e)")).then_inc(staged.sem, 1)

                @block.tensor
                def _(pe):
                    pe.wait_ge(staged.sem, 3)
                    n = 0
                    for b in range(BATCH):
                        rows = slice(32 * b, 32 * b + HD)
                        for t, h0, nh in FILLS:
                            if n >= 8:
                                pe.wait_ge(maxed.sem, n - 7)
                            keys = (t + 1) * P
                            for h in range(nh):
                                out = bank[n % 8][:, h * keys:(h + 1) * keys]
                                pe.matmul(out, qs[rows, h0 + h, t * P:(t + 1) * P], ks[rows, 0:keys],
                                          start=True, stop=False, skip_group_check=True, tile_position=(32 * b, 0))
                                m = pe.matmul(out[:, t * P:keys], identb[:, :], maskq[:, :], start=False, stop=True, skip_group_check=True)
                            m.then_inc(scored.sem, 1)
                            n += 1
                    pe.wait_ge(split.sem, 2)
                    for t in range(TPB):
                        m = pe.transpose(bank[7][:, 0:SEQ // 2].bitcast(BF16)[0:2 * MAPS, t * P:(t + 1) * P],
                                         hl[:, t, :, :].rearrange("p a h -> p (a h)"), identb[:, :])
                    m.then_inc(m_up.sem, 1)
                    pe.wait_ge(m_in.sem, 1)

                    def shift(x):
                        b, h = divmod(x, GH)
                        rows = slice(32 * b, 32 * b + HD)
                        if x >= 2:
                            pe.wait_ge(exped.sem, x - 1)
                        for j in range(TPB):
                            k, at = SPOT[j]
                            n = (TPB - j) * P
                            out = bank[3 * (x % 2) + k][:, at:at + n]
                            pe.matmul(out, sel[:, x, :], nmT[:, j * P:SEQ], start=True, stop=False, skip_group_check=True)
                            pe.matmul(out[:, 0:P], identb[:, :], maskk[:, :], start=False, stop=False, skip_group_check=True)
                            m = pe.matmul(out, ks[rows, j * P:(j + 1) * P], qs[rows, h, j * P:SEQ],
                                          start=False, stop=True, skip_group_check=True, tile_position=(32 * b, 0))
                        m.then_inc(shifted.sem, 1)

                    def weigh(x):
                        b, h = divmod(x, GH)
                        pe.wait_ge(exped.sem, x + 1)
                        if h == 0 and b >= 2:
                            pe.wait_ge(normed.sem, 2 * (b - 1))
                        for i in range(TPB):
                            for j in range(i + 1):
                                at = (h * TPB + i) * (HD + 1)
                                m = pe.matmul(bank[6 + b % 2][:, at:at + HD + 1], pt[:, x % 2, j, i * P:(i + 1) * P], vs[:, j, b, :],
                                              start=(j == 0), stop=(j == i), skip_group_check=True)
                        m.then_inc(weighed.sem, 1)

                    for x in range(MAPS + 1):
                        if x < MAPS:
                            shift(x)
                        if x >= 1:
                            weigh(x - 1)

                @block.scalar
                def _(act):
                    for x in range(MAPS):
                        act.wait_ge(shifted.sem, x + 1)
                        if x >= 2:
                            act.wait_ge(weighed.sem, x - 1)
                        for j in range(TPB):
                            k, at = SPOT[j]
                            m = act.activation(pt[:, x % 2, j, j * P:SEQ], bank[3 * (x % 2) + k][:, at:at + (TPB - j) * P], ACT.Exp)
                        m.then_inc(exped.sem, 1)

                @block.vector
                def _(v):
                    n = 0
                    for b in range(BATCH):
                        for t, h0, nh in FILLS:
                            v.wait_ge(scored.sem, n + 1)
                            v.tensor_reduce(nmax[:, t, b * GH + h0:b * GH + h0 + nh],
                                            bank[n % 8][:, 0:nh * (t + 1) * P].rearrange("p (h k) -> p h k", h=nh),
                                            X, ALU.max, negate=True).then_inc(maxed.sem, 1)
                            n += 1
                    v.wait_ge(maxed.sem, n)
                    v.tensor_copy(hl[:, :, 0, :], nmax[:, :, :]).then_inc(split.sem, 1)
                    v.wait_ge(split.sem, 1)
                    v.tensor_tensor(hl[:, :, 1, :], nmax[:, :, :], hl[:, :, 0, :], ALU.subtract).then_inc(split.sem, 1)
                    v.wait_ge(m_up.sem, 1)
                    v.tensor_copy(nmT[0:2 * MAPS, :], bank[7][:, 0:SEQ // 2].bitcast(BF16)[0:2 * MAPS, :]).then_inc(m_in.sem, 1)
                    for b in range(BATCH):
                        v.wait_ge(weighed.sem, GH * (b + 1))
                        out = bank[6 + b % 2][:, 0:GH * TPB * (HD + 1)].rearrange("p (x e) -> p x e", e=HD + 1)
                        rd = rden[:, b % 2].rearrange("p h t -> p (h t)")
                        v.reciprocal(rd, out[:, :, HD]).then_inc(recip.sem, 1)
                        v.wait_ge(recip.sem, b + 1)
                        v.tensor_tensor(on[:, b % 2].rearrange("p h t e -> p (h t) e"), out[:, :, 0:HD], spread(rd, 2, HD), ALU.mult).then_inc(normed.sem, 1)
                        v.wait_ge(normed.sem, 2 * b + 1)
                        for k in range(2):
                            m = v.scalar_tensor_tensor(out=att[:, b, :, bass.ds(kv * (2 * HD) + k * HD, HD)], in0=on[:, b % 2, 2 * k + 1], scalar=nlam[:, 0:1],
                                                       in1=on[:, b % 2, 2 * k], op0=ALU.mult, op1=ALU.add)
                        m.then_inc(normed.sem, 1)
            st.restart()

        at_up = st.event("at_up")
        at_in = st.event("at_in")
        y1_up = st.event("y1_up")
        y1_in = st.event("y1_in")
        y2_up = st.event("y2_up")
        y2_in = st.event("y2_in")
        y3_up = st.event("y3_up")
        y3_in = st.event("y3_in")
        with nc.Block() as block:
            @block.tensor
            def _(pe):
                for b in range(BATCH):
                    for t in range(TPB):
                        m = pe.transpose(bank[0][:, t * P:(t + 1) * P], att[:, b, t, :], ident[:, :])
                    m.then_inc(at_up.sem, 1)
                    pe.wait_ge(at_in.sem, b + 1)
                    for t in range(TPB):
                        m = pe.matmul(bank[1][:, t * P:(t + 1) * P], attT[:, t * P:(t + 1) * P], wp[:, :], start=True, stop=True)
                    m.then_inc(y1_up.sem, 1)
                    pe.wait_ge(y1_in.sem, b + 1)
                    pe.matmul(bank[2][:, :], wp[:, :], y1[:, :, :].rearrange("p t m -> p (t m)"), start=True, stop=True).then_inc(y2_up.sem, 1)
                    pe.wait_ge(y2_in.sem, b + 1)
                    for t in range(TPB):
                        m = pe.transpose(bank[3][:, t * P:(t + 1) * P], y2T[:, t * P:(t + 1) * P], ident[:, :])
                    m.then_inc(y3_up.sem, 1)
                    pe.wait_ge(y3_in.sem, b + 1)

            @block.scalar
            def _(act):
                for b in range(BATCH):
                    act.wait_ge(at_up.sem, b + 1)
                    act.activation(attT[:, :], bank[0][:, :], ACT.Copy, scale=1.0 - LAMBDA_INIT).then_inc(at_in.sem, 1)
                    act.wait_ge(y2_up.sem, b + 1)
                    act.activation(y2T[:, :].rearrange("p (m t) -> p t m", t=TPB), bank[2][:, :].rearrange("p (t m) -> p t m", t=TPB),
                                   ACT.Copy).then_inc(y2_in.sem, 1)

            @block.vector
            def _(v):
                for b in range(BATCH):
                    v.wait_ge(y1_up.sem, b + 1)
                    v.tensor_copy(y1[:, :, :].rearrange("p t m -> p (t m)"), bank[1][:, :]).then_inc(y1_in.sem, 1)
                    v.wait_ge(y3_up.sem, b + 1)
                    v.tensor_copy(s[:, b * TPB:(b + 1) * TPB, :].rearrange("p t m -> p (t m)"), bank[3][:, :]).then_inc(y3_in.sem, 1)


def attention3(nc, g, d):
    N, T = 16, 16
    CH = SEQ // T
    R = BATCH * CH
    s, ident, xnT = g["s"], g["ident"], g["xnT"]
    with Stage(nc, "a3") as st:
        A = st.sb("A", [P, N, N])
        Bp = st.sb("Bp", [P, N])
        Cp = st.sb("Cp", [P, N])
        Dp = st.sb("Dp", [P, 1])
        wg = st.sb("wg", [P, P])
        bg = st.sb("bg", [P, 1])
        gam = st.sb("gam", [P, DIM])
        bet = st.sb("bet", [P, DIM])
        gate = st.sb("gate", [P, TILES * P])
        xg = st.sb("xg", [P, TILES * P])
        V = st.sb("V", [P, T, N])
        W = st.sb("W", [P, T + 1, N])
        h = st.sb("h", [P, T])
        h0 = st.sb("h0", [P, 1])
        pw = st.sb("pw", [P, 2, N, N])
        prod = st.sb("prod", [P, N, N, N])
        tmp = st.sb("tmp", [P, N, N])
        y = st.sb("y", [P, R, T])
        U = st.sb("U", [P, N, R])
        S = st.sb("S", [P, CH + 1, BATCH, N])
        rec = st.sb("rec", [P, BATCH, N])
        stats = st.sb("stats", [P, TPB, 6])
        mv = st.sb("mv", [P, TPB, 2])
        vare = st.sb("vare", [P, TPB])
        rstd = st.sb("rstd", [P, TPB])
        ln = st.sb("ln", [P, TPB, DIM])
        bank = [st.bank(f"bank{i}") for i in range(8)]
        loaded = st.sem("loaded")

        gated_up = st.event("gated_up")
        sig_in = st.event("sig_in")
        xg_in = st.event("xg_in")
        did = st.event("did")
        powd = st.event("powd")
        with nc.Block() as block:
            @block.sync
            def _(sp):
                sp.dma_start(A[:, :, :], d["L3_attn_A"]).then_inc(loaded, 16)
                sp.dma_start(Bp[:, :], d["L3_attn_Bp"]).then_inc(loaded, 16)
                sp.dma_start(Cp[:, :], d["L3_attn_Cp"]).then_inc(loaded, 16)
                sp.dma_start(Dp[:, :], d["L3_attn_Dp"].rearrange("(p a) -> p a", a=1)).then_inc(loaded, 16)
                sp.dma_start(wg[:, :], d["t_L3_attn_Wg"]).then_inc(loaded, 16)
                sp.dma_start(bg[:, :], d["L3_attn_bg"].rearrange("(p a) -> p a", a=1)).then_inc(loaded, 16)
                sp.dma_start(gam[:, :], d["L3_attn_gamma"].rearrange("(a n) -> a n", a=1).to_broadcast([P, DIM])).then_inc(loaded, 16)
                sp.dma_start(bet[:, :], d["L3_attn_beta"].rearrange("(a n) -> a n", a=1).to_broadcast([P, DIM])).then_inc(loaded, 16)
                sp.wait_ge(loaded, 8 * 16)

            @block.tensor
            def _(pe):
                pe.wait_ge(loaded, 8 * 16)
                for b in range(BATCH):
                    pe.matmul(bank[b][:, :], wg[:, :], xnT[:, b * SEQ:(b + 1) * SEQ], start=True, stop=True).then_inc(gated_up.sem, 1)

            @block.scalar
            def _(act):
                for b in range(BATCH):
                    act.wait_ge(gated_up.sem, b + 1)
                    act.activation(gate[:, b * SEQ:(b + 1) * SEQ], bank[b][:, :], ACT.Sigmoid, bias=bg[:, :]).then_inc(sig_in.sem, 1)

            @block.gpsimd
            def _(pool):
                pool.wait_ge(loaded, 8 * 16)
                for b in range(BATCH):
                    pool.wait_ge(sig_in.sem, b + 1)
                    if b:
                        pool.wait_ge(xg_in.sem, b)
                    pool.tensor_tensor(xg[:, b * SEQ:(b + 1) * SEQ], xnT[:, b * SEQ:(b + 1) * SEQ], gate[:, b * SEQ:(b + 1) * SEQ],
                                       ALU.mult).then_inc(xg_in.sem, 1)

            @block.vector
            def _(v):
                n = 0

                def step(m):
                    nonlocal n
                    n += 1
                    m.then_inc(did.sem, 1)
                    v.wait_ge(did.sem, n)

                v.wait_ge(loaded, 8 * 16)
                At = A[:, :, :].rearrange("p n m -> p m n")
                step(v.tensor_copy(V[:, 0, :], Bp[:, :]))
                step(v.tensor_copy(W[:, 0, :], Cp[:, :]))
                for k in range(1, T + 1):
                    if k < T:
                        step(v.tensor_tensor(tmp[:, :, :], At, spread(V[:, k - 1, :], 1, N), ALU.mult))
                        step(v.tensor_reduce(V[:, k, :], tmp[:, :, :], X, ALU.add))
                    step(v.tensor_tensor(tmp[:, :, :], A[:, :, :], spread(W[:, k - 1, :], 1, N), ALU.mult))
                    step(v.tensor_reduce(W[:, k, :], tmp[:, :, :], X, ALU.add))
                step(v.tensor_tensor(tmp[:, :, :], V[:, :, :], spread(Cp[:, :], 1, T), ALU.mult))
                step(v.tensor_reduce(h[:, :], tmp[:, :, :], X, ALU.add))
                src = A
                for k in range(4):
                    a = A[:, :, :] if k == 0 else pw[:, (k - 1) % 2]
                    step(v.tensor_tensor(prod[:, :, :, :], spread(a, 2, N), spread(a.rearrange("p n m -> p m n"), 1, N), ALU.mult))
                    step(v.tensor_reduce(pw[:, k % 2], prod[:, :, :, :], X, ALU.add))
                step(v.tensor_scalar(h0[:, :], h[:, 0:1], Dp[:, 0:1], 1.0, ALU.add, ALU.add))
                v.wait_ge(xg_in.sem, BATCH)
                x = xg[:, :].rearrange("p (r t) -> p r t", t=T)
                step(v.tensor_scalar(y[:, :, :], x, h0[:, 0:1], None, ALU.mult))
                for k in range(1, T):
                    step(v.scalar_tensor_tensor(out=y[:, :, k:T], in0=x[:, :, 0:T - k], scalar=h[:, k:k + 1], in1=y[:, :, k:T],
                                                op0=ALU.mult, op1=ALU.add))
                step(v.memset(S[:, 0, :, :], 0.0))
        st.restart()

        added = st.event("added")
        with nc.Fori(0, N // 2) as m:
            with nc.Block() as block:
                @block.vector
                def _(v):
                    x = xg[:, :].rearrange("p (r t) -> p r t", t=T)
                    for j in range(T):
                        if j:
                            v.wait_ge(added.sem, j)
                        for k in range(2):
                            out = U[:, bass.ds(2 * m + k, 1), :].rearrange("p a r -> p (a r)")
                            vk = V[:, T - 1 - j, bass.ds(2 * m + k, 1)]
                            if j == 0:
                                i = v.tensor_scalar(out, x[:, :, j], vk, None, ALU.mult)
                            else:
                                i = v.scalar_tensor_tensor(out=out, in0=x[:, :, j], scalar=vk, in1=out, op0=ALU.mult, op1=ALU.add)
                        i.then_inc(added.sem, 1)
            st.restart()

        multiplied = st.event("multiplied", 3)
        UNROLL = 4
        with nc.Fori(0, CH // UNROLL) as c:
            with nc.Block() as block:
                @block.vector
                def _(v):
                    last = pw[:, 1]
                    Uc = U[:, :, :].rearrange("p n (b c) -> p c b n", b=BATCH)
                    for k in range(UNROLL):
                        if k:
                            v.wait_ge(multiplied.sem, 3 * k)
                        now = S[:, bass.ds(UNROLL * c + k, 1), :, :].rearrange("p a b n -> p (a b) n")
                        nxt = S[:, bass.ds(UNROLL * c + k + 1, 1), :, :].rearrange("p a b n -> p (a b) n")
                        v.tensor_tensor(prod[:, 0:BATCH, :, :], spread(now, 2, N), spread(last.rearrange("p n m -> p m n"), 1, BATCH),
                                        ALU.mult).then_inc(multiplied.sem, 1)
                        v.wait_ge(multiplied.sem, 3 * k + 1)
                        v.tensor_reduce(rec[:, :, :], prod[:, 0:BATCH, :, :], X, ALU.add).then_inc(multiplied.sem, 1)
                        v.wait_ge(multiplied.sem, 3 * k + 2)
                        v.tensor_tensor(nxt, rec[:, :, :], Uc[:, bass.ds(UNROLL * c + k, 1), :, :].rearrange("p a b n -> p (a b) n"), ALU.add).then_inc(multiplied.sem, 1)
            st.restart()

        with nc.Fori(0, T // 2) as i:
            with nc.Block() as block:
                @block.vector
                def _(v):
                    yv = y[:, :, :].rearrange("p (b c) t -> p b c t", b=BATCH)
                    Sv = S[:, 0:CH, :, :].rearrange("p c b n -> p b c n")
                    for n in range(N):
                        if n:
                            v.wait_ge(added.sem, n)
                        for k in range(2):
                            out = yv[:, :, :, bass.ds(2 * i + k, 1)].rearrange("p b c a -> p b (c a)")
                            m = v.scalar_tensor_tensor(out=out, in0=Sv[:, :, :, n], scalar=W[:, bass.ds(2 * i + k + 1, 1), n],
                                                       in1=out, op0=ALU.mult, op1=ALU.add)
                        m.then_inc(added.sem, 1)
            st.restart()

        yT_up = st.event("yT_up")
        stepped = st.event("stepped")
        rooted = st.event("rooted")
        with nc.Fori(0, BATCH) as b:
            with nc.Block() as block:
                @block.gpsimd
                def _(pool):
                    pool.tensor_copy(gate[:, 0:SEQ], y[:, bass.ds(b * CH, CH), :].rearrange("p r t -> p (r t)")).then_inc(powd.sem, 1)
                    pool.wait_ge(stepped.sem, 3)
                    pool.tensor_tensor(rstd[:, :], vare[:, :], g["half"][:, 0:TPB], ALU.pow).then_inc(rooted.sem, 1)

                @block.tensor
                def _(pe):
                    pe.wait_ge(powd.sem, 1)
                    for t in range(TPB):
                        m = pe.transpose(bank[0][:, t * P:(t + 1) * P], gate[:, t * P:(t + 1) * P], ident[:, :])
                    m.then_inc(yT_up.sem, 1)

                @block.vector
                def _(v):
                    v.wait_ge(yT_up.sem, 1)
                    for t in range(TPB):
                        m = v.bn_stats(stats[:, t, :], bank[0][:, t * P:(t + 1) * P])
                    m.then_inc(stepped.sem, 1)
                    v.wait_ge(stepped.sem, 1)
                    for t in range(TPB):
                        m = v.bn_aggr(mv[:, t, :], stats[:, t, :])
                    m.then_inc(stepped.sem, 1)
                    v.wait_ge(stepped.sem, 2)
                    v.tensor_scalar(vare[:, :], mv[:, :, 1], LN_EPS, None, ALU.add).then_inc(stepped.sem, 1)
                    v.wait_ge(rooted.sem, 1)
                    for t in range(TPB):
                        m = v.tensor_scalar(ln[:, t, :], bank[0][:, t * P:(t + 1) * P], mv[:, t, 0:1], rstd[:, t:t + 1], ALU.subtract, ALU.mult)
                    m.then_inc(stepped.sem, 1)
                    v.wait_ge(stepped.sem, 4)
                    v.tensor_tensor(ln[:, :, :], ln[:, :, :], spread(gam[:, :], 1, TPB), ALU.mult).then_inc(stepped.sem, 1)
                    v.wait_ge(stepped.sem, 5)
                    v.tensor_tensor(s[:, bass.ds(b * TPB, TPB), :], ln[:, :, :], spread(bet[:, :], 1, TPB), ALU.add).then_inc(stepped.sem, 1)
            st.restart()


def program(nc, dram, out):
    with ExitStack() as ctx:
        def keep(name, shape, dt=F32):
            return ctx.enter_context(nc.sbuf_tensor(name, shape, dt))

        g = {
            "x": keep("x", [P, TILES, DIM]),
            "xn": keep("xn", [P, TILES, DIM]),
            "xnT": keep("xnT", [P, TILES * P]),
            "s": keep("s", [P, TILES, DIM]),
            "u": keep("u", [P, TILES, DIM]),
            "half": keep("half", [P, 32]),
            "ident": keep("ident", [P, P]),
            "identb": keep("identb", [P, P], BF16),
        }
        load_inputs(nc, g, dram)
        for layer in range(4):
            layer_norm(nc, g, f"norm{layer}")
            ATTENTION[layer](nc, g, dram)
            FFN[layer](nc, g, dram)
            combine(nc, g, f"combine{layer}")
        store_output(nc, g, out)


def copy_xn(nc, g, name):
    with Stage(nc, name) as st:
        with nc.Block() as block:

            @block.vector
            def _(v):
                v.tensor_copy(g["u"][:, :, :], g["xn"][:, :, :])


def ffn2(nc, g, d):
    copy_xn(nc, g, "copy2")
    transformer(nc, g, d, "t2", 6, 16, 32, 341, d["L2_ffn_Wqkv"], d["L2_ffn_q_scale"], d["L2_ffn_k_scale"], d["L2_ffn_Wo"],
                d["L2_ffn_ln_g"], d["L2_ffn_ln_b"], d["L2_ffn_W1"], d["L2_ffn_b1"], d["L2_ffn_W2"], d["L2_ffn_b2"])


def ffn3(nc, g, d):
    copy_xn(nc, g, "copy3")
    transformer(nc, g, d, "t3", 2, 8, 64, 341, d["L3_ffn_wqkv"], d["L3_ffn_q_scale"], d["L3_ffn_k_scale"], d["L3_ffn_wo"],
                d["L3_ffn_ln_g"], d["L3_ffn_ln_b"], d["L3_ffn_w1"], d["L3_ffn_b1"], d["L3_ffn_w2"], d["L3_ffn_b2"])


ATTENTION = [attention0, attention1, attention2, attention3]
FFN = [ffn0, ffn1, ffn2, ffn3]


def rotary_table(window):
    half = np.arange(0, 64, 2, dtype=np.float32)
    inv_freq = (1.0 / np.float32(10000.0) ** (half / 64)).astype(np.float32)
    t = np.arange(SEQ, dtype=np.float32)
    freqs = t[:, None] * inv_freq[None, :]
    freqs = np.concatenate([freqs, freqs], -1)
    base = ((half + np.float32(0.4 * 64)) / np.float32(1.4 * 64)).astype(np.float32)
    power = (t - SEQ // 2) / np.float32(window // 2)
    scale = (base[None, :] ** power[:, None]).astype(np.float32)
    scale = np.concatenate([scale, scale], -1)
    cos, sin = np.cos(freqs), np.sin(freqs)
    sin = np.concatenate([-sin[:, :32], sin[:, 32:]], -1)
    tab = np.stack([cos * scale * 8, sin * scale * 8, cos / scale, sin / scale])
    return np.ascontiguousarray(tab.reshape(4, TPB, P, 64).transpose(2, 0, 1, 3).astype(np.float32))


def band_masks(window, first):
    q = np.arange(P)[:, None]
    k = np.arange(window + P)[None, :] - window
    ok = (k <= q) & (k >= q - first)
    tiles = []
    for i in range(2):
        m = ok & (k >= 0) if i == 0 else ok
        tiles.append(np.where(m, 0.0, MASKED))
    m = np.stack(tiles, 1).astype(np.dtype("bfloat16"))
    mt = np.zeros((P, 2, 2, P), m.dtype)
    mt[:, :, 0] = m[:, :, window:].transpose(2, 1, 0)
    mt[:window, :, 1] = m[:, :, :window].transpose(2, 1, 0)
    return m, mt


def shape_constants():
    bf = np.dtype("bfloat16")
    c = {"c_ident": np.eye(P, dtype=np.float32), "c_identb": np.eye(P, dtype=np.float32).astype(bf)}
    for window in (32, 64):
        c[f"c_rot{window}"] = rotary_table(window)
        c[f"c_mask{window}"], c[f"c_maskt{window}"] = band_masks(window, window)
        k, q = np.arange(P)[:, None] - P, np.arange(window)[None, :]
        c[f"c_maskp{window}"] = np.where(k >= q - window, 0.0, MASKED).astype(bf)
    c["c_mask31"], c["c_maskt31"] = band_masks(32, 31)
    q, n, t = np.arange(P)[:, None, None], np.arange(64)[None, None, :], np.arange(TPB)[None, :, None]
    latent = np.where(n <= (t * P + q) // 8, 0.0, MASKED)
    c["c_maskl"] = latent.astype(bf)
    c["c_masklt"] = np.ascontiguousarray(latent.transpose(2, 1, 0)).astype(bf)
    q, k = np.arange(P)[:, None], np.arange(P)[None, :]
    c["c_causal"] = np.stack([np.where(k <= q, 0.0, MASKED), np.where(q <= k, 0.0, MASKED)]).astype(bf)
    for heads in (8, 16):
        sel = np.zeros((2, heads, heads, P), np.float32)
        for h in range(heads):
            sel[:, h, h, :] = 1.0
        c[f"c_sel{heads}"] = sel.reshape(2 * heads, heads, P).astype(bf)
    return c


TRANSPOSED = ["L3_attn_Wg", "L1_ffn_w1_w", "L1_ffn_w2_w", "L1_ffn_h1_w", "L1_ffn_h2_w", "L1_ffn_w3_w"]


def kernel(**inputs):
    import concourse.bacc as _bacc
    from concourse.bass_utils import run_bass_kernel_spmd as _run

    nc = _bacc.Bacc("TRN2", target_bir_lowering=False, num_devices=1)
    arrays, dram = {}, {}
    for name in list(inputs):
        a = np.ascontiguousarray(inputs[name])
        arrays[f"in_{name}"] = a
        dram[name] = nc.dram_tensor(f"in_{name}", a.shape, mybir.dt.from_np(a.dtype), kind="ExternalInput").ap()
    for name in TRANSPOSED:
        arrays[f"t_{name}"] = a = np.ascontiguousarray(inputs[name].T)
        dram[f"t_{name}"] = nc.dram_tensor(f"t_{name}", a.shape, mybir.dt.from_np(a.dtype), kind="ExternalInput").ap()
    for name, a in shape_constants().items():
        arrays[name] = a
        dram[name] = nc.dram_tensor(name, a.shape, mybir.dt.from_np(a.dtype), kind="ExternalInput").ap()
    out = nc.dram_tensor("out_0_dram", (BATCH, SEQ, DIM), F32, kind="ExternalOutput").ap()
    program(nc, dram, out)
    r = _run(nc, [arrays], core_ids=[0])
    return r.results[0]["out_0_dram"]
```

```python
from contextlib import ExitStack

import numpy as np
import concourse.bass as bass
from concourse import mybir

ALU = mybir.AluOpType
ACT = mybir.ActivationFunctionType
F32 = mybir.dt.float32
BF16 = mybir.dt.bfloat16
U32 = mybir.dt.uint32
X = mybir.AxisListType.X

P = 128
BATCH, SEQ, DIM = 4, 512, 128
TILES = BATCH * SEQ // P
TPB = SEQ // P
LN_EPS = 1e-5
MASKED = -1e30


class Event:

    def __init__(self, stage, name, per=1):
        self.sem = stage.sem(name)
        self.per = per

    def at(self, it, k=1):
        return it * self.per + k


class Stage:

    def __init__(self, nc, name):
        self.nc, self.name, self.ctx = nc, name, ExitStack()
        self.events, self.sems = [], []

    def __enter__(self):
        return self

    def __exit__(self, *exc):
        if exc[0] is None:
            self.clear(self.sems)
        return self.ctx.__exit__(*exc)

    def clear(self, sems):
        for sem in sems:
            self.nc.sync.sem_clear(sem)
        self.nc.all_engine_barrier()

    def sb(self, name, shape, dt=F32):
        return self.ctx.enter_context(self.nc.sbuf_tensor(f"{self.name}_{name}", shape, dt))

    def bank(self, name, shape=(P, 512), dt=F32):
        return self.ctx.enter_context(self.nc.psum_tensor(f"{self.name}_{name}", list(shape), dt))

    def sem(self, name):
        sem = self.ctx.enter_context(self.nc.semaphore(f"{self.name}_{name}"))
        self.sems.append(sem)
        return sem

    def event(self, name, per=1):
        e = Event(self, name, per)
        self.events.append(e)
        return e

    def restart(self):
        self.clear([e.sem for e in self.events])



def spread(ap, axis, n):
    a = ap.unsqueeze(axis)
    shape = list(a.shape)
    shape[axis] = n
    return a.to_broadcast(shape)


def load_inputs(nc, g, dram):
    with Stage(nc, "load") as st:
        loaded = st.sem("loaded")
        halved = st.sem("halved")
        with nc.Block() as block:

            @block.gpsimd
            def _(pool):
                pool.memset(g["half"][:, :], -0.5).then_inc(halved, 1)

            @block.sync
            def _(sp):
                sp.dma_start(g["x"][:, :, :], dram["L0_attn_x"].rearrange("b (t p) c -> p (b t) c", p=P)).then_inc(loaded, 16)
                sp.dma_start(g["ident"][:, :], dram["c_ident"]).then_inc(loaded, 16)
                sp.dma_start(g["identb"][:, :], dram["c_identb"]).then_inc(loaded, 16)
                sp.wait_ge(loaded, 3 * 16)


def layer_norm(nc, g, name):
    x, xn, xnT, ident = g["x"], g["xn"], g["xnT"], g["ident"]
    with Stage(nc, name) as st:
        stats = st.sb("stats", [P, TPB, 6])
        mv = st.sb("mv", [P, TPB, 2])
        vare = st.sb("vare", [P, TPB])
        rstd = st.sb("rstd", [P, TPB])
        staged = st.sb("staged", [P, TPB, P])
        turned = st.bank("turned")
        stepped = st.event("stepped", 5)
        rooted = st.event("rooted", 1)
        turned_up = st.event("turned_up", 1)
        with nc.Fori(0, BATCH) as b:
            with nc.Block() as block:
                @block.vector
                def _(v):
                    for t in range(TPB):
                        xt = x[:, bass.ds(b * TPB + t, 1), :].rearrange("p a c -> p (a c)")
                        v.bn_stats(stats[:, t, :], xt).then_inc(stepped.sem, 1)
                        v.wait_ge(stepped.sem, stepped.at(t, 1))
                        v.bn_aggr(mv[:, t, :], stats[:, t, :]).then_inc(stepped.sem, 1)
                        v.wait_ge(stepped.sem, stepped.at(t, 2))
                        v.tensor_scalar(vare[:, t:t + 1], mv[:, t, 1:2], LN_EPS, None, ALU.add).then_inc(stepped.sem, 1)
                        v.wait_ge(rooted.sem, rooted.at(t))
                        v.tensor_scalar(xn[:, bass.ds(b * TPB + t, 1), :].rearrange("p a c -> p (a c)"), xt,
                                        mv[:, t, 0:1], rstd[:, t:t + 1], ALU.subtract, ALU.mult).then_inc(stepped.sem, 1)
                        v.wait_ge(stepped.sem, stepped.at(t, 4))
                        v.tensor_copy(staged[:, t, :], xn[:, bass.ds(b * TPB + t, 1), :].rearrange("p a c -> p (a c)")).then_inc(stepped.sem, 1)

                @block.gpsimd
                def _(pool):
                    for t in range(TPB):
                        pool.wait_ge(stepped.sem, stepped.at(t, 3))
                        pool.tensor_tensor(rstd[:, t:t + 1], vare[:, t:t + 1], g["half"][:, 0:1], ALU.pow).then_inc(rooted.sem, 1)

                @block.tensor
                def _(pe):
                    for t in range(TPB):
                        pe.wait_ge(stepped.sem, stepped.at(t, 5))
                        pe.transpose(turned[:, t * P:(t + 1) * P], staged[:, t, :], ident[:, :]).then_inc(turned_up.sem, 1)

                @block.scalar
                def _(act):
                    act.wait_ge(turned_up.sem, TPB)
                    act.activation(xnT[:, bass.ds(b * SEQ, SEQ)], turned[:, :], ACT.Copy)
            st.restart()


def combine(nc, g, name):
    x, s, u = g["x"], g["s"], g["u"]
    with Stage(nc, name) as st:
        gated = st.sem("gated")
        product = st.sem("product")
        with nc.Block() as block:
            @block.scalar
            def _(act):
                act.activation(u[:, :, :], u[:, :, :], ACT.Silu).then_inc(gated, 1)

            @block.vector
            def _(v):
                v.wait_ge(gated, 1)
                v.tensor_tensor(s[:, :, :], s[:, :, :], u[:, :, :], ALU.mult).then_inc(product, 1)
                v.wait_ge(product, 1)
                v.tensor_tensor(x[:, :, :], x[:, :, :], s[:, :, :], ALU.add)


def store_output(nc, g, out):
    with Stage(nc, "store") as st:
        stored = st.sem("stored")
        with nc.Block() as block:

            @block.sync
            def _(sp):
                sp.dma_start(out.rearrange("b (t p) c -> p (b t) c", p=P), g["x"][:, :, :]).then_inc(stored, 16)
                sp.wait_ge(stored, 16)


def transformer(nc, g, dram, name, depth, heads, window, hid, wqkv, qs, ks, wo, ln_g, ln_b, w1, b1, w2, b2):
    HD = 64
    INNER = heads * HD
    PAIRS = heads // 2
    G4 = heads // 4
    QC = INNER // 512
    KEYS = window + P
    HC = [(c, min(P, hid - c)) for c in range(0, hid, P)]
    NH = len(HC)
    HL = HC[-1][1]
    u, ident, identb = g["u"], g["ident"], g["identb"]

    with Stage(nc, name) as st:
        w_qkv = st.sb("w_qkv", [P, 3 * INNER])
        w_o = st.sb("w_o", [P, PAIRS, DIM])
        w_1 = st.sb("w_1", [P, 2 * hid])
        w_2 = st.sb("w_2", [P, NH, DIM])
        b_1 = st.sb("b_1", [P, 2, NH])
        b_2 = st.sb("b_2", [1, DIM])
        lng = st.sb("lng", [P, 1])
        lnb = st.sb("lnb", [P, 1])
        scales = st.sb("scales", [P, 2, HD])
        base = st.sb("base", [P, 4, TPB, HD])
        rot = st.sb("rot", [P, 4, TPB, HD])
        mask = st.sb("mask", [P, KEYS], BF16)
        maskt = st.sb("maskt", [P, P], BF16)
        maskp = st.sb("maskp", [P, window], BF16)
        sel = st.sb("sel", [2 * heads, heads, P], BF16)
        ones = st.sb("ones", [1, P])
        onesb = st.sb("onesb", [2 * heads, P], BF16)
        shT = st.sb("shT", [P, P + 1])
        sh2T = st.sb("sh2T", [P, P + 1])
        raw = st.sb("raw", [P, 2 * QC, 8, HD])
        sq = st.sb("sq", [P, 2 * QC, 8, HD])
        ssq = st.sb("ssq", [P, 2 * heads])
        inv = st.sb("inv", [P, 2 * heads])
        qn = st.sb("qn", [P, 2, 8, HD])
        ra = st.sb("ra", [P, 2 * QC, 8, HD])
        rb = st.sb("rb", [P, 2, 8, HD])
        qz = st.sb("qz", [P, 2, heads, P])
        kT = st.sb("kT", [P, 3, PAIRS, KEYS])
        va = st.sb("va", [P, 3, heads, HD + 2])
        nmax = st.sb("nmax", [P, heads])
        hl = st.sb("hl", [P, 2, heads], BF16)
        nmT = st.sb("nmT", [2 * heads, P], BF16)
        pt = st.sb("pt", [P, 2, 4, P])
        nmS = st.sb("nmS", [2 * heads, heads, window], BF16)
        pc = st.sb("pc", [P, heads, window])
        rden = st.sb("rden", [P, 2, 4])
        o = st.sb("o", [P, heads, HD])
        oT = st.sb("oT", [P, PAIRS, P])
        x0 = st.sb("x0", [P, 2, DIM])
        x1 = st.sb("x1", [P, DIM])
        stats = st.sb("stats", [P, 6])
        mv = st.sb("mv", [P, 2])
        vare = st.sb("vare", [P, 1])
        rstd = st.sb("rstd", [P, 1])
        ln = st.sb("ln", [P, DIM])
        lnT = st.sb("lnT", [P, P])
        gg = st.sb("gg", [P, NH, P])
        hT = st.sb("hT", [P, NH, P])
        wa = st.bank("wa", [P, 2, 512])
        tr = st.bank("tr", [P, 512])
        wide = st.bank("wide", [P, 4, 512])
        misc = st.bank("misc", [P, 512])
        miscb = misc[:, 0:P].bitcast(BF16)

        w_in = st.event("w_in")
        c_in = st.sem("c_in")
        zeroed = st.sem("zeroed")
        tables = st.event("tables", 4)
        x0_in = st.event("x0_in", 1)
        xT_up = st.event("xT_up", 1)
        carry0 = st.event("carry0", 1)
        sh_in = st.event("sh_in", 2)
        proj = st.event("proj", 3 * QC)
        sqd = st.event("sqd", 2 * QC)
        summed = st.event("summed", 2 * QC)
        floored = st.event("floored", 2 * QC)
        inved = st.event("inved", 2 * QC)
        normed = st.event("normed", 2 * QC)
        cosd = st.event("cosd", 2 * QC)
        sind = st.event("sind", 4 * QC)
        roped = st.event("roped", 2 * QC)
        turned = st.event("turned", 2 * QC)
        qk_in = st.event("qk_in", 2 * QC)
        v_in = st.event("v_in", QC)
        scored = st.event("scored", G4)
        maxed = st.event("maxed", G4)
        split = st.event("split", 2)
        m_up = st.event("m_up", 1)
        m_in = st.event("m_in", 1)
        mS_in = st.event("mS_in", 1)
        shifted = st.event("shifted", G4)
        shiftp = st.event("shiftp", 1)
        expp = st.event("expp", 1)
        exped = st.event("exped", G4)
        weighed = st.event("weighed", G4)
        recip = st.event("recip", G4)
        o_in = st.event("o_in", G4)
        oT_up = st.event("oT_up", G4)
        oT_in = st.event("oT_in", G4)
        y_up = st.event("y_up", 1)
        x1_in = st.event("x1_in", 1)
        x1T_up = st.event("x1T_up", 1)
        carry1 = st.event("carry1", 1)
        sh2_in = st.event("sh2_in", 2)
        sh2_up = st.event("sh2_up", 1)
        lnd = st.event("lnd", 4)
        rooted = st.event("rooted", 1)
        lnT_up = st.event("lnT_up", 1)
        lnT_in = st.event("lnT_in", 1)
        gate_up = st.event("gate_up", 1)
        gelu_in = st.event("gelu_in", NH)
        h_in = st.event("h_in", NH)
        f_up = st.event("f_up", 1)
        tile_done = st.event("tile_done", 1)
        NW = 11 + (3 if HL < P else 0)
        with nc.Block() as block:
            @block.sync
            def _(sp):
                sp.dma_start(base[:, :, :, :], dram[f"c_rot{window}"]).then_inc(c_in, 16)
                sp.dma_start(mask[:, :], dram[f"c_mask{window}"][:, 1, :]).then_inc(c_in, 16)
                sp.dma_start(maskt[:, :], dram[f"c_maskt{window}"][:, 1, 0, :]).then_inc(c_in, 16)
                sp.dma_start(maskp[:, :], dram[f"c_maskp{window}"]).then_inc(c_in, 16)
                sp.dma_start(sel[:, :, :], dram[f"c_sel{heads}"]).then_inc(c_in, 16)
                sp.wait_ge(c_in, 5 * 16)

            @block.gpsimd
            def _(pool):
                pool.memset(qz[:, :, :, :], 0.0).then_inc(zeroed, 1)
                pool.memset(va[:, :, :, :], 1.0).then_inc(zeroed, 1)
                pool.memset(shT[:, :], 0.0).then_inc(zeroed, 1)
                pool.memset(sh2T[:, :], 0.0).then_inc(zeroed, 1)
                pool.memset(ones[:, :], 1.0).then_inc(zeroed, 1)
                pool.memset(onesb[:, :], 1.0).then_inc(zeroed, 1)
                pool.memset(pc[:, :, :], 0.0).then_inc(zeroed, 1)

        with nc.Fori(0, depth) as l:
            with nc.Block() as block:
                @block.sync
                def _(sp):
                    lay = lambda a: a[bass.ds(l, 1)]
                    sp.dma_start(w_qkv[:, :], lay(wqkv).rearrange("a p n -> p (a n)")).then_inc(w_in.sem, 16)
                    sp.dma_start(w_o[:, :, :], lay(wo).rearrange("a (c p) n -> p (a c) n", p=P)).then_inc(w_in.sem, 16)
                    sp.dma_start(w_1[:, :], lay(w1).rearrange("a p n -> p (a n)")).then_inc(w_in.sem, 16)
                    sp.dma_start(lng[:, :], lay(ln_g).rearrange("a p -> p a"), allow_slow_non_contiguous=True).then_inc(w_in.sem, 16)
                    sp.dma_start(lnb[:, :], lay(ln_b).rearrange("a p -> p a"), allow_slow_non_contiguous=True).then_inc(w_in.sem, 16)
                    sp.dma_start(b_2[:, :], lay(b2)).then_inc(w_in.sem, 16)
                    sp.dma_start(scales[:, 0, :], lay(qs).to_broadcast([P, HD])).then_inc(w_in.sem, 16)
                    sp.dma_start(scales[:, 1, :], lay(ks).to_broadcast([P, HD])).then_inc(w_in.sem, 16)
                    full = (NH - 1) if HL < P else NH
                    w2l, b1l = lay(w2), lay(b1)
                    sp.dma_start(w_2[:, 0:full, :], w2l[:, 0:full * P, :].rearrange("a (c p) n -> p (a c) n", p=P)).then_inc(w_in.sem, 16)
                    for h in range(2):
                        sp.dma_start(b_1[:, h, 0:full], b1l[:, h * hid:h * hid + full * P].rearrange("a (c p) -> p (a c)", p=P), allow_slow_non_contiguous=True).then_inc(w_in.sem, 16)
                    if HL < P:
                        sp.dma_start(w_2[0:HL, full, :], w2l[:, full * P:hid, :].rearrange("a p n -> p (a n)")).then_inc(w_in.sem, 16)
                        for h in range(2):
                            sp.dma_start(b_1[0:HL, h, full:NH], b1l[:, h * hid + full * P:h * hid + hid].rearrange("a p -> p a"), allow_slow_non_contiguous=True).then_inc(w_in.sem, 16)
                    sp.wait_ge(w_in.sem, NW * 16)

                @block.vector
                def _(v):
                    v.wait_ge(w_in.sem, NW * 16)
                    for r in range(2):
                        s = scales[:, r, :]
                        v.tensor_tensor(rot[:, 2 * r], base[:, 2 * r], spread(s, 1, TPB), ALU.mult).then_inc(tables.sem, 1)
                        v.tensor_tensor(rot[:, 2 * r + 1, :, 0:32], base[:, 2 * r + 1, :, 0:32], spread(s[:, 32:64], 1, TPB), ALU.mult)
                        v.tensor_tensor(rot[:, 2 * r + 1, :, 32:64], base[:, 2 * r + 1, :, 32:64], spread(s[:, 0:32], 1, TPB),
                                        ALU.mult).then_inc(tables.sem, 1)

            with nc.Block() as block:
                NJ = max(G4 + 1, 2 * QC + 2)
                first = lambda t: t % TPB == 0
                later = lambda t: sum(not first(x) for x in range(t + 1))

                @block.gpsimd
                def _(pool):
                    for t in range(-1, TILES):
                        n = t + 1
                        if n < TILES:
                            for j in range(2 * QC + 1):
                                if j < 2 * QC:
                                    pool.wait_ge(floored.sem, floored.at(n, j + 1))
                                    pool.tensor_tensor(inv[:, 8 * j:8 * j + 8], ssq[:, 8 * j:8 * j + 8], g["half"][:, 0:8],
                                                       ALU.pow).then_inc(inved.sem, 1)
                                if j:
                                    c = j - 1
                                    r, z = 2 * (c // QC), c % 2
                                    cos, sin = rot[:, r, n % TPB, :], rot[:, r + 1, n % TPB, :]
                                    pool.wait_ge(normed.sem, normed.at(n, c + 1))
                                    if c >= 2:
                                        pool.wait_ge(roped.sem, roped.at(n, c - 1))
                                    if c == 0:
                                        if n:
                                            pool.wait_ge(turned.sem, turned.at(n, 0))
                                    pool.tensor_tensor(ra[:, c], qn[:, z], spread(cos, 1, 8), ALU.mult).then_inc(cosd.sem, 1)
                                    pool.tensor_tensor(rb[:, z, :, 0:32], qn[:, z, :, 32:64], spread(sin[:, 0:32], 1, 8), ALU.mult).then_inc(sind.sem, 1)
                                    pool.tensor_tensor(rb[:, z, :, 32:64], qn[:, z, :, 0:32], spread(sin[:, 32:64], 1, 8), ALU.mult).then_inc(sind.sem, 1)
                        if t >= 0:
                            pool.wait_ge(lnd.sem, lnd.at(t, 3))
                            pool.tensor_tensor(rstd[:, :], vare[:, :], g["half"][:, 0:1], ALU.pow).then_inc(rooted.sem, 1)

                @block.tensor
                def _(pe):
                    def score(t, q):
                        if q == 0:
                            pe.wait_ge(qk_in.sem, qk_in.at(t, 2 * QC))
                            if t:
                                pe.wait_ge(h_in.sem, h_in.at(t - 1, NH))
                        if q >= 2:
                            pe.wait_ge(maxed.sem, maxed.at(t, q - 1))
                        lo = window if first(t) else 0
                        for h2 in range(2):
                            bank = wide[:, 2 * (q % 2) + h2, :].rearrange("p (h k) -> p h k", h=2)
                            pe.matmul(bank[:, :, lo:KEYS], identb[:, :], spread(mask[:, lo:KEYS], 1, 2),
                                      start=True, stop=False, skip_group_check=True)
                            for j in range(2):
                                h = 4 * q + 2 * h2 + j
                                m = pe.matmul(bank[:, j, lo:KEYS], qz[:, t % 2, h, :], kT[:, t % 3, h // 2, lo:KEYS],
                                              start=False, stop=True, skip_group_check=True)
                        m.then_inc(scored.sem, 1)

                    def x_up(n):
                        pe.wait_ge(x0_in.sem, x0_in.at(n))
                        if n:
                            pe.wait_ge(qk_in.sem, qk_in.at(n, 0))
                        pe.transpose(tr[:, 0:P], x0[:, n % 2, :], ident[:, :]).then_inc(xT_up.sem, 1)

                    def project(n, c):
                        if c == 0:
                            pe.wait_ge(sh_in.sem, sh_in.at(n, 2))
                        k = n * 3 * QC + c
                        if k >= 2:
                            pn, pc_ = divmod(k - 2, 3 * QC)
                            if pc_ < 2 * QC:
                                pe.wait_ge(sqd.sem, sqd.at(pn, pc_ + 1))
                            else:
                                pe.wait_ge(v_in.sem, v_in.at(pn, pc_ - 2 * QC + 1))
                        pe.matmul(wa[:, k % 2, :], shT[:, 0:P], w_qkv[:, c * 512:(c + 1) * 512],
                                  start=True, stop=True).then_inc(proj.sem, 1)

                    def turn(n, c):
                        pe.wait_ge(roped.sem, roped.at(n, c + 1))
                        if c:
                            pe.wait_ge(qk_in.sem, qk_in.at(n, c))
                        for j in range(4):
                            m = pe.transpose(tr[:, j * P:(j + 1) * P], ra[:, c, 2 * j:2 * j + 2, :].rearrange("p h d -> p (h d)"), ident[:, :])
                        m.then_inc(turned.sem, 1)

                    def shift_before(t):
                        pe.wait_ge(mS_in.sem, later(t))
                        bank = misc[:, 0:heads * window].rearrange("p (h k) -> p h k", h=heads)
                        pe.matmul(bank, identb[:, :], spread(maskp[:, :], 1, heads), start=True, stop=False, skip_group_check=True)
                        pe.matmul(bank, onesb[:, :], nmS[:, :, :], start=False, stop=False, skip_group_check=True)
                        for h in range(heads):
                            m = pe.matmul(bank[P - window:P, h, :], kT[:, t % 3, h // 2, 0:window], qz[:, t % 2, h, 0:window],
                                          start=False, stop=True, skip_group_check=True, tile_position=(0, P - window))
                        m.then_inc(shiftp.sem, 1)

                    def shift(t, q):
                        if q >= 2:
                            pe.wait_ge(exped.sem, exped.at(t, q - 1))
                        bank = wide[:, q % 2, :].rearrange("p (h k) -> p h k", h=4)
                        pe.matmul(bank, identb[:, :], spread(maskt[:, :], 1, 4), start=True, stop=False, skip_group_check=True)
                        for j in range(4):
                            h = 4 * q + j
                            pe.matmul(bank[:, j, :], sel[:, h, :], nmT[:, :], start=False, stop=False, skip_group_check=True)
                            m = pe.matmul(bank[:, j, :], kT[:, t % 3, h // 2, window:KEYS], qz[:, t % 2, h, :],
                                          start=False, stop=True, skip_group_check=True)
                        m.then_inc(shifted.sem, 1)

                    def weigh(t, q):
                        pe.wait_ge(exped.sem, exped.at(t, q + 1))
                        if q == 0:
                            pe.wait_ge(v_in.sem, v_in.at(t, QC))
                            if not first(t):
                                pe.wait_ge(expp.sem, later(t))
                        if q >= 2:
                            pe.wait_ge(o_in.sem, o_in.at(t, q - 1))
                        for j in range(4):
                            h = 4 * q + j
                            out = wide[:, 2 + q % 2, j * 66:j * 66 + 66]
                            m = pe.matmul(out, pt[:, q % 2, j, :], va[:, t % 3, h, :], start=True, stop=first(t), skip_group_check=True)
                            if not first(t):
                                m = pe.matmul(out[0:window], pc[:, h, :], va[:, (t - 1) % 3, h, :], start=False, stop=True, skip_group_check=True)
                        m.then_inc(weighed.sem, 1)

                    def turn_out(t, q):
                        pe.wait_ge(o_in.sem, o_in.at(t, q + 1))
                        if q >= 2:
                            pe.wait_ge(oT_in.sem, oT_in.at(t, q - 1))
                        for j in range(2):
                            m = pe.transpose(wide[:, q % 2, j * P:(j + 1) * P],
                                             o[:, 4 * q + 2 * j:4 * q + 2 * j + 2, :].rearrange("p h d -> p (h d)"), ident[:, :])
                        m.then_inc(oT_up.sem, 1)

                    for t in range(-1, TILES):
                        n = t + 1
                        A, B = n < TILES, t >= 0
                        if A:
                            x_up(n)
                        for q in range(max(2, G4)):
                            if B and q < G4:
                                score(t, q)
                            if A and q == max(1, G4 - 2):
                                project(n, 0)
                        if A:
                            project(n, 1)
                        if B:
                            pe.wait_ge(split.sem, split.at(t, 2))
                            pe.transpose(miscb[0:2 * heads, 0:P], hl[:, :, :].rearrange("p a h -> p (a h)"), identb[:, :]).then_inc(m_up.sem, 1)
                            pe.wait_ge(m_in.sem, m_in.at(t))
                        for j in range(NJ):
                            if B and j < G4:
                                shift(t, j)
                                if j == 0 and not first(t):
                                    shift_before(t)
                            if B and 1 <= j <= G4:
                                weigh(t, j - 1)
                            if A and j + 2 < 2 * QC:
                                project(n, j + 2)
                        if B:
                            for q in range(G4):
                                turn_out(t, q)
                            pe.wait_ge(oT_in.sem, oT_in.at(t, G4))
                            for c in range(PAIRS):
                                m = pe.matmul(misc[:, 0:DIM], oT[:, c, :], w_o[:, c, :], start=(c == 0), stop=(c == PAIRS - 1))
                            m.then_inc(y_up.sem, 1)
                        if A:
                            turn(n, 0)
                            if QC > 1:
                                project(n, 2 * QC)
                        if B:
                            pe.wait_ge(x1_in.sem, x1_in.at(t))
                            pe.transpose(misc[:, P:2 * P], x1[:, :], ident[:, :]).then_inc(x1T_up.sem, 1)
                        if A:
                            turn(n, 1)
                        if B:
                            pe.wait_ge(sh2_in.sem, sh2_in.at(t, 2))
                            pe.transpose(misc[:, 2 * P:3 * P], sh2T[:, 0:P], ident[:, :]).then_inc(sh2_up.sem, 1)
                        if A and QC > 1:
                            turn(n, 2)
                        if B:
                            pe.wait_ge(lnd.sem, lnd.at(t, 4))
                            pe.transpose(misc[:, 3 * P:4 * P], ln[:, :], ident[:, :]).then_inc(lnT_up.sem, 1)
                        if A and QC > 1:
                            turn(n, 3)
                        if B:
                            pe.wait_ge(lnT_in.sem, lnT_in.at(t))
                            for half in range(2):
                                for c, (at, size) in enumerate(HC):
                                    lo = (1 - half) * hid + at
                                    m = pe.matmul(wide[0:size, half, c * P:(c + 1) * P], w_1[:, lo:lo + size], lnT[:, :], start=True, stop=True)
                            m.then_inc(gate_up.sem, 1)
                        if A:
                            project(n, 3 * QC - 1)
                        if B:
                            pe.wait_ge(h_in.sem, h_in.at(t, NH))
                            for c, (at, size) in enumerate(HC):
                                pe.matmul(misc[:, 0:DIM], hT[0:size, c, :], w_2[0:size, c, :], start=(c == 0), stop=False)
                            pe.matmul(misc[:, 0:DIM], ones[:, :], b_2[:, :], start=False, stop=True).then_inc(f_up.sem, 1)

                @block.scalar
                def _(act):
                    def square(n, c):
                        act.wait_ge(proj.sem, proj.at(n, c + 1))
                        if n:
                            act.wait_ge(normed.sem, normed.at(n - 1, c + 1))
                        bank = wa[:, (n * 3 * QC + c) % 2, :]
                        act.activation(sq[:, c].rearrange("p h d -> p (h d)"), bank, ACT.Square)
                        act.activation(raw[:, c].rearrange("p h d -> p (h d)"), bank, ACT.Copy).then_inc(sqd.sem, 1)

                    def values(n, c):
                        act.wait_ge(proj.sem, proj.at(n, 2 * QC + c + 1))
                        if n >= 3:
                            act.wait_ge(weighed.sem, weighed.at(n - 2, G4))
                        act.activation(va[:, n % 3, 8 * c:8 * c + 8, 0:HD],
                                       wa[:, (n * 3 * QC + 2 * QC + c) % 2, :].rearrange("p (h d) -> p h d", h=8), ACT.Copy).then_inc(v_in.sem, 1)

                    def copy_turned(n, c):
                        act.wait_ge(turned.sem, turned.at(n, c + 1))
                        src = tr[:, :].rearrange("p (j k) -> p j k", j=4)
                        if c < QC:
                            heads_ = qz[:, n % 2, 8 * c:8 * c + 8, :].rearrange("p (j a) k -> p a j k", a=2)
                            act.activation(heads_[0:64, 0], src[0:64], ACT.Copy)
                            act.activation(heads_[64:P, 1], src[64:P], ACT.Copy).then_inc(qk_in.sem, 1)
                        else:
                            pairs = slice(4 * (c - QC), 4 * (c - QC) + 4)
                            if not first(n + 1):
                                act.activation(kT[:, (n + 1) % 3, pairs, 0:window], src[:, :, P - window:P], ACT.Copy)
                            act.activation(kT[:, n % 3, pairs, window:KEYS], src, ACT.Copy).then_inc(qk_in.sem, 1)

                    for t in range(-1, TILES):
                        n = t + 1
                        A, B = n < TILES, t >= 0
                        for j in range(NJ):
                            if A and j < 2 * QC:
                                square(n, j)
                            if B and j < G4:
                                act.wait_ge(shifted.sem, shifted.at(t, j + 1))
                                if j >= 2:
                                    act.wait_ge(weighed.sem, weighed.at(t, j - 1))
                                act.activation(pt[:, j % 2].rearrange("p h k -> p (h k)"), wide[:, j % 2, :], ACT.Exp).then_inc(exped.sem, 1)
                                if j == 0 and not first(t):
                                    act.wait_ge(shiftp.sem, later(t))
                                    act.activation(pc[P - window:P, :, :].rearrange("p h k -> p (h k)"), misc[P - window:P, 0:heads * window],
                                                   ACT.Exp).then_inc(expp.sem, 1)
                        if B:
                            for q in range(G4):
                                act.wait_ge(oT_up.sem, oT_up.at(t, q + 1))
                                act.activation(oT[:, 2 * q:2 * q + 2, :].rearrange("p a b -> p (a b)"), wide[:, q % 2, 0:256],
                                               ACT.Copy).then_inc(oT_in.sem, 1)
                        if A:
                            for c in range(min(3, 2 * QC)):
                                copy_turned(n, c)
                                if c == 0 and QC > 1:
                                    values(n, 0)
                        if B:
                            act.wait_ge(lnT_up.sem, lnT_up.at(t))
                            act.activation(lnT[:, :], misc[:, 3 * P:4 * P], ACT.Identity, bias=lnb[:, :], scale=lng[:, 0:1]).then_inc(lnT_in.sem, 1)
                        if A and QC > 1:
                            copy_turned(n, 3)
                        if B:
                            act.wait_ge(gate_up.sem, gate_up.at(t))
                            for c, (at, size) in enumerate(HC):
                                act.activation(gg[0:size, c, :], wide[0:size, 0, c * P:(c + 1) * P], ACT.Gelu,
                                               bias=b_1[0:size, 1, c:c + 1]).then_inc(gelu_in.sem, 1)
                        if A:
                            values(n, QC - 1)

                @block.vector
                def _(v):
                    def tile(t):
                        return u[:, t, :]

                    def sums(n, c):
                        v.wait_ge(sqd.sem, sqd.at(n, c + 1))
                        cols = slice(8 * c, 8 * c + 8)
                        v.tensor_reduce(ssq[:, cols], sq[:, c], X, ALU.add).then_inc(summed.sem, 1)
                        v.wait_ge(summed.sem, summed.at(n, c + 1))
                        v.tensor_scalar(ssq[:, cols], ssq[:, cols], 1e-24, None, ALU.max).then_inc(floored.sem, 1)

                    def normalise(n, c):
                        v.wait_ge(inved.sem, inved.at(n, c + 1))
                        k = n * 2 * QC + c
                        if k >= 2:
                            v.wait_ge(sind.sem, 2 * (k - 1))
                        v.tensor_tensor(qn[:, c % 2], raw[:, c],
                                        spread(inv[:, 8 * c:8 * c + 8], 2, HD), ALU.mult).then_inc(normed.sem, 1)

                    def finish_rope(n, c):
                        v.wait_ge(cosd.sem, cosd.at(n, c + 1))
                        v.wait_ge(sind.sem, sind.at(n, 2 * c + 2))
                        v.tensor_tensor(ra[:, c], ra[:, c], rb[:, c % 2], ALU.add).then_inc(roped.sem, 1)

                    for n in range(2):
                        v.tensor_copy(x0[:, n, :], tile(n)).then_inc(x0_in.sem, 1)
                    for t in range(-1, TILES):
                        n = t + 1
                        A, B = n < TILES, t >= 0
                        if A:
                            if n:
                                v.wait_ge(proj.sem, proj.at(n, 0))
                            v.tensor_scalar(shT[64:P, 0:1], shT[64:P, P:P + 1], float(not first(n)), None, ALU.mult).then_inc(carry0.sem, 1)
                            v.wait_ge(carry0.sem, carry0.at(n))
                            v.wait_ge(xT_up.sem, xT_up.at(n))
                            v.tensor_copy(shT[0:64, 0:P], tr[0:64, 0:P]).then_inc(sh_in.sem, 1)
                            v.tensor_copy(shT[64:P, 1:P + 1], tr[64:P, 0:P]).then_inc(sh_in.sem, 1)
                        lo = window if first(t) else 0
                        if B:
                            for q in range(G4):
                                v.wait_ge(scored.sem, scored.at(t, q + 1))
                                v.tensor_reduce(nmax[:, 4 * q:4 * q + 4],
                                                wide[:, 2 * (q % 2):2 * (q % 2) + 2, :].rearrange("p b (h k) -> p (b h) k", h=2)[:, :, lo:KEYS],
                                                X, ALU.max, negate=True).then_inc(maxed.sem, 1)
                        if B:
                            v.wait_ge(maxed.sem, maxed.at(t, G4))
                            v.tensor_copy(hl[:, 0, :], nmax[:, :]).then_inc(split.sem, 1)
                            v.wait_ge(split.sem, split.at(t, 1))
                            v.tensor_tensor(hl[:, 1, :], nmax[:, :], hl[:, 0, :], ALU.subtract).then_inc(split.sem, 1)
                            v.wait_ge(m_up.sem, m_up.at(t))
                            v.tensor_copy(nmT[:, :], miscb[0:2 * heads, 0:P]).then_inc(m_in.sem, 1)
                            if not first(t):
                                v.tensor_tensor(nmS[:, :, :], spread(miscb[0:2 * heads, 0:window], 1, heads), sel[:, :, 0:window],
                                                ALU.mult).then_inc(mS_in.sem, 1)
                        for j in range(NJ):
                            if A and j < 2 * QC:
                                sums(n, j)
                            if B and 1 <= j <= G4:
                                q = j - 1
                                v.wait_ge(weighed.sem, weighed.at(t, q + 1))
                                out = wide[:, 2 + q % 2, 0:4 * 66].rearrange("p (h d) -> p h d", h=4)
                                v.reciprocal(rden[:, q % 2, :], out[:, :, HD]).then_inc(recip.sem, 1)
                                v.wait_ge(recip.sem, recip.at(t, q + 1))
                                v.tensor_tensor(o[:, 4 * q:4 * q + 4, :], out[:, :, 0:HD], spread(rden[:, q % 2, :], 2, HD),
                                                ALU.mult).then_inc(o_in.sem, 1)
                            if A and 2 <= j < 2 * QC + 2:
                                finish_rope(n, j - 2)
                            if A and j < 2 * QC:
                                normalise(n, j)
                        if B:
                            v.wait_ge(y_up.sem, y_up.at(t))
                            v.tensor_tensor(x1[:, :], misc[:, 0:DIM], x0[:, t % 2, :], ALU.add).then_inc(x1_in.sem, 1)
                            v.tensor_scalar(sh2T[64:P, 0:1], sh2T[64:P, P:P + 1], float(not first(t)), None, ALU.mult).then_inc(carry1.sem, 1)
                            v.wait_ge(carry1.sem, carry1.at(t))
                            v.wait_ge(x1T_up.sem, x1T_up.at(t))
                            v.tensor_copy(sh2T[0:64, 0:P], misc[0:64, P:2 * P]).then_inc(sh2_in.sem, 1)
                            v.tensor_copy(sh2T[64:P, 1:P + 1], misc[64:P, P:2 * P]).then_inc(sh2_in.sem, 1)
                            if t + 2 < TILES:
                                v.tensor_copy(x0[:, t % 2, :], tile(t + 2)).then_inc(x0_in.sem, 1)
                            v.wait_ge(sh2_up.sem, sh2_up.at(t))
                            v.bn_stats(stats[:, :], misc[:, 2 * P:3 * P]).then_inc(lnd.sem, 1)
                            v.wait_ge(lnd.sem, lnd.at(t, 1))
                            v.bn_aggr(mv[:, :], stats[:, :]).then_inc(lnd.sem, 1)
                            v.wait_ge(lnd.sem, lnd.at(t, 2))
                            v.tensor_scalar(vare[:, :], mv[:, 1:2], LN_EPS, None, ALU.add).then_inc(lnd.sem, 1)
                            v.wait_ge(rooted.sem, rooted.at(t))
                            v.tensor_scalar(ln[:, :], misc[:, 2 * P:3 * P], mv[:, 0:1], rstd[:, 0:1], ALU.subtract, ALU.mult).then_inc(lnd.sem, 1)
                            for c, (at, size) in enumerate(HC):
                                v.wait_ge(gelu_in.sem, gelu_in.at(t, c + 1))
                                v.scalar_tensor_tensor(out=hT[0:size, c, :], in0=wide[0:size, 1, c * P:(c + 1) * P], scalar=b_1[0:size, 0, c:c + 1],
                                                       in1=gg[0:size, c, :], op0=ALU.add, op1=ALU.mult).then_inc(h_in.sem, 1)
                            v.wait_ge(f_up.sem, f_up.at(t))
                            v.tensor_tensor(tile(t), misc[:, 0:DIM], x1[:, :], ALU.add).then_inc(tile_done.sem, 1)
            st.restart()


def attention0(nc, g, d):
    H, HD, LH, WIN, LAT = 16, 8, 8, 32, 64
    G, LG = H // 4, LH // 4
    CHUNK = SEQ // LAT
    HD2 = HD + 2
    ALL = H + LH
    s, ident, identb, xnT = g["s"], g["ident"], g["identb"], g["xnT"]
    with Stage(nc, "a0") as st:
        wqs = st.sb("wqs", [P, G, 4, 32])
        wks = st.sb("wks", [P, G, 4, 32])
        wgqs = st.sb("wgqs", [P, LG, 4, 32])
        wgks = st.sb("wgks", [P, LG, 4, 32])
        wq = st.sb("wq", [P, DIM])
        wv = st.sb("wv", [P, DIM])
        wgv = st.sb("wgv", [P, LAT])
        wr = st.sb("wr", [LAT, DIM])
        wo = st.sb("wo", [P, DIM])
        gw = st.sb("gw", [P, 2, DIM])
        mask = st.sb("mask", [P, 2, WIN + P], BF16)
        maskt = st.sb("maskt", [P, 2, 2, P], BF16)
        maskl = st.sb("maskl", [P, TPB, LAT], BF16)
        masklt = st.sb("masklt", [LAT, TPB, P], BF16)
        sel = st.sb("sel", [2 * ALL, ALL, P], BF16)
        xb = st.sb("xb", [P, SEQ])
        qz = st.sb("qz", [P, H, SEQ])
        kT = st.sb("kT", [P, G, SEQ])
        gqz = st.sb("gqz", [P, LH, SEQ])
        gkT = st.sb("gkT", [P, LG, LAT])
        gvT = st.sb("gvT", [LAT, LAT])
        va = st.sb("va", [P, TPB, H, HD2])
        vc = st.sb("vc", [WIN, TPB, H, HD2])
        gva = st.sb("gva", [LAT, LH, HD2])
        gprod = st.sb("gprod", [P, 2, DIM])
        logit = st.sb("logit", [P, TPB, 2, H])
        gates = st.sb("gates", [P, TPB, 2, H])
        nmax = st.sb("nmax", [P, ALL])
        hl = st.sb("hl", [P, 2, ALL], BF16)
        nmT = st.sb("nmT", [2 * ALL, P], BF16)
        pt = st.sb("pt", [P, H, P])
        pc = st.sb("pc", [WIN, H, WIN])
        ptl = st.sb("ptl", [LAT, LH, P])
        rden = st.sb("rden", [P, ALL])
        loc = st.sb("loc", [P, DIM])
        rem = st.sb("rem", [P, LAT])
        remT = st.sb("remT", [LAT, P])
        remg = st.sb("remg", [P, DIM])
        mix = st.sb("mix", [P, DIM])
        mixT = st.sb("mixT", [P, P])
        all8 = st.bank("all8", [P, 8, 512])
        bank = [all8[:, i, :] for i in range(8)]
        loaded, zeroed = st.sem("loaded"), st.sem("zeroed")
        with nc.Block() as block:
            @block.gpsimd
            def _(pool):
                for z in (wqs, wks, wgqs, wgks):
                    pool.memset(z[:, :, :, :], 0.0).then_inc(zeroed, 1)
                pool.memset(qz[:, :, :], 0.0).then_inc(zeroed, 1)
                pool.memset(gqz[:, :, :], 0.0).then_inc(zeroed, 1)
                pool.memset(va[:, :, :, :], 1.0).then_inc(zeroed, 1)
                pool.memset(gva[:, :, :], 1.0).then_inc(zeroed, 1)

            @block.sync
            def _(sp):
                sp.wait_ge(zeroed, 4)
                for dst, name, groups in ((wqs, "wq", G), (wks, "wk", G), (wgqs, "wgq", LG), (wgks, "wgk", LG)):
                    for c in range(groups):
                        sp.dma_start(dst[:, c, :, 0:HD], d[f"L0_attn_{name}"][:, c * 32:(c + 1) * 32].rearrange("p (j e) -> p j e", e=HD)).then_inc(loaded, 16)
                sp.dma_start(wq[:, :], d["L0_attn_wq"]).then_inc(loaded, 16)
                sp.dma_start(wv[:, :], d["L0_attn_wv"]).then_inc(loaded, 16)
                sp.dma_start(wgv[:, :], d["L0_attn_wgv"]).then_inc(loaded, 16)
                sp.dma_start(wr[:, :], d["L0_attn_r_out_w"]).then_inc(loaded, 16)
                sp.dma_start(wo[:, :], d["L0_attn_w_out"]).then_inc(loaded, 16)
                for k, name in enumerate(("local", "remote")):
                    sp.dma_start(gw[:, k, :], d[f"L0_attn_gate_{name}_w"].rearrange("h e -> (h e)").rearrange("(a n) -> a n", a=1).to_broadcast([P, DIM])).then_inc(loaded, 16)
                sp.dma_start(mask[:, :, :], d["c_mask31"]).then_inc(loaded, 16)
                sp.dma_start(maskt[:, :, :, :], d["c_maskt31"]).then_inc(loaded, 16)
                sp.dma_start(maskl[:, :, :], d["c_maskl"]).then_inc(loaded, 16)
                sp.dma_start(masklt[:, :, :], d["c_masklt"]).then_inc(loaded, 16)
                sp.dma_start(sel[:, :, :], d["c_sel24"]).then_inc(loaded, 16)
                sp.wait_ge(loaded, (2 * G + 2 * LG + 12) * 16)

        xb_in = st.event("xb_in")
        proj = st.event("proj")
        even_in = st.event("even_in")
        odd_in = st.event("odd_in")
        lat_up = st.event("lat_up")
        lat_in = st.event("lat_in")
        carried = st.event("carried")
        gate_up = st.event("gate_up")
        gate_mul = st.event("gate_mul")
        gate_sum = st.event("gate_sum")
        gates_in = st.event("gates_in")
        with nc.Fori(0, BATCH) as b:
            JOBS = ([("q", c) for c in range(G)] + [("k", c) for c in range(G)] + [("gq", 0), ("gk", 0), ("gq", 1), ("gk", 1)]
                    + [("v", 0), ("gv", 0)] + [("v", t) for t in range(1, TPB)])
            NP = len(JOBS)
            with nc.Block() as block:
                @block.gpsimd
                def _(pool):
                    pool.tensor_copy(xb[:, :], xnT[:, bass.ds(b * SEQ, SEQ)]).then_inc(xb_in.sem, 1)

                @block.tensor
                def _(pe):
                    pe.wait_ge(xb_in.sem, 1)
                    for n in range(NP):
                        if n >= 8:
                            pe.wait_ge((even_in, odd_in)[n % 2].sem, (n - 8) // 2 + 1)
                        kind, c = JOBS[n]
                        if kind == "gv":
                            m = pe.matmul(bank[n % 8][0:LAT, :], wgv[:, :], xb[:, :], start=True, stop=True)
                        elif kind == "v":
                            m = pe.matmul(bank[n % 8][:, 0:DIM], xb[:, c * P:(c + 1) * P], wv[:, :], start=True, stop=True)
                        else:
                            w = {"q": wqs, "k": wks, "gq": wgqs, "gk": wgks}[kind]
                            m = pe.matmul(bank[n % 8], w[:, c, :, :].rearrange("p j e -> p (j e)"), xb[:, :], start=True, stop=True)
                        m.then_inc(proj.sem, 1)
                    pe.wait_ge(even_in.sem, (NP + 1) // 2)
                    pe.wait_ge(odd_in.sem, NP // 2)
                    pe.transpose(bank[0][0:LAT, 0:LAT], gvT[:, :], ident[0:LAT, 0:LAT]).then_inc(lat_up.sem, 1)
                    for t in range(TPB):
                        pe.matmul(bank[1 + t][:, 0:DIM], xb[:, t * P:(t + 1) * P], wq[:, :], start=True, stop=True).then_inc(gate_up.sem, 1)

                def place(n, copy, pooled):
                    src = bank[n % 8]
                    kind, c = JOBS[n]
                    if kind in ("q", "gq"):
                        dst, scale = (qz, HD ** -0.5) if kind == "q" else (gqz, HD ** -0.5 / CHUNK)
                        for j in range(4):
                            m = copy(dst[32 * j:32 * j + 32, 4 * c + j, :], src[32 * j:32 * j + 32], scale)
                        return m
                    if kind == "k":
                        return copy(kT[:, c, :], src, 1.0)
                    if kind == "gk":
                        return pooled(gkT[:, c, :], src)
                    if kind == "gv":
                        return pooled(gvT[:, :], src[0:LAT, :])
                    return copy(va[:, c, :, 0:HD], src[:, 0:DIM].rearrange("p (h e) -> p h e", e=HD), 1.0)

                @block.scalar
                def _(act):
                    for n in range(0, NP, 2):
                        act.wait_ge(proj.sem, n + 1)
                        place(n, lambda dst, src, k: act.activation(dst, src, ACT.Copy, scale=k), None).then_inc(even_in.sem, 1)
                    act.wait_ge(even_in.sem, (NP + 1) // 2)
                    act.wait_ge(odd_in.sem, NP // 2)
                    for t in range(1, TPB):
                        act.activation(vc[:, t, :, :], va[P - WIN:P, t - 1, :, :], ACT.Copy).then_inc(carried.sem, 1)
                    act.wait_ge(gate_sum.sem, TPB)
                    act.activation(gates[:, :, :, :], logit[:, :, :, :], ACT.Sigmoid).then_inc(gates_in.sem, 1)

                @block.vector
                def _(v):
                    def pooled(dst, src):
                        return v.tensor_reduce(dst, src.rearrange("p (n k) -> p n k", k=CHUNK), X, ALU.add)

                    for n in range(1, NP, 2):
                        v.wait_ge(proj.sem, n + 1)
                        place(n, lambda dst, src, k: v.tensor_scalar(dst, src, k, None, ALU.mult), pooled).then_inc(odd_in.sem, 1)
                    v.wait_ge(lat_up.sem, 1)
                    v.tensor_scalar(gva[:, :, 0:HD], bank[0][0:LAT, 0:LAT].rearrange("p (h e) -> p h e", e=HD), 1.0 / CHUNK, None, ALU.mult).then_inc(lat_in.sem, 1)
                    for t in range(TPB):
                        v.wait_ge(gate_up.sem, t + 1)
                        if t:
                            v.wait_ge(gate_sum.sem, t)
                        v.tensor_tensor(gprod[:, :, :], gw[:, :, :], spread(bank[1 + t][:, 0:DIM], 1, 2), ALU.mult).then_inc(gate_mul.sem, 1)
                        v.wait_ge(gate_mul.sem, t + 1)
                        v.tensor_reduce(logit[:, t, :, :].rearrange("p a h -> p (a h)"), gprod[:, :, :].rearrange("p a (h e) -> p (a h) e", e=HD),
                                        X, ALU.add).then_inc(gate_sum.sem, 1)
            st.restart()

            t_scored = st.event("t_scored", 4)
            t_maxed = st.event("t_maxed", 4)
            t_split = st.event("t_split", 2)
            t_m_up = st.event("t_m_up", 1)
            t_m_in = st.event("t_m_in", 1)
            t_shifted = st.event("t_shifted", 3)
            t_exped = st.event("t_exped", 3)
            t_weighed = st.event("t_weighed", 1)
            t_norm = st.event("t_norm", 4)
            t_remT_up = st.event("t_remT_up", 1)
            t_remT_in = st.event("t_remT_in", 1)
            t_rem_up = st.event("t_rem_up", 1)
            t_mix = st.event("t_mix", 2)
            t_mixT_up = st.event("t_mixT_up", 1)
            t_mixT_in = st.event("t_mixT_in", 1)
            t_y_up = st.event("t_y_up", 1)
            t_done = st.event("t_done", 1)
            KEYS = WIN + P
            PER = 512 // KEYS
            GROUPS = [(0, 3, 0, PER), (3, 2, 3 * PER, PER), (5, 1, 5 * PER, H - 5 * PER)]
            SCORE_LAT, CARRIED, SHIFT_LAT, REST = 6, 4, 5, 7
            with nc.Block() as block:
                @block.tensor
                def _(pe):
                    def score(t):
                        own, lo = slice(t * P, (t + 1) * P), 0 if t else WIN
                        for first_bank, banks, h0, per in GROUPS:
                            for k in range(banks):
                                out = bank[first_bank + k][:, 0:per * KEYS].rearrange("p (a k) -> p a k", a=per)[:, :, lo:]
                                pe.matmul(out, identb[:, :], spread(mask[:, min(t, 1), lo:], 1, per), start=True, stop=False, skip_group_check=True)
                                for a in range(per):
                                    h = h0 + k * per + a
                                    m = pe.matmul(out[:, a, :], qz[:, h, own], kT[:, h // 4, t * P - (WIN - lo):(t + 1) * P],
                                                  start=False, stop=True, skip_group_check=True)
                            m.then_inc(t_scored.sem, 1)
                        out = bank[SCORE_LAT].rearrange("p (h k) -> p h k", h=LH)
                        pe.matmul(out, identb[:, :], spread(maskl[:, t, :], 1, LH), start=True, stop=False, skip_group_check=True)
                        for h in range(LH):
                            m = pe.matmul(out[:, h, :], gqz[:, h, own], gkT[:, h // 4, :], start=False, stop=True, skip_group_check=True)
                        m.then_inc(t_scored.sem, 1)

                    score(0)
                    for t in range(TPB):
                        own = slice(t * P, (t + 1) * P)
                        pe.wait_ge(t_split.sem, t_split.at(t, 2))
                        if t:
                            pe.wait_ge(t_done.sem, t_done.at(t - 1))
                        pe.transpose(bank[REST].bitcast(BF16)[0:2 * ALL, 0:P], hl[:, :, :].rearrange("p a h -> p (a h)"), identb[:, :]).then_inc(t_m_up.sem, 1)
                        pe.wait_ge(t_m_in.sem, t_m_in.at(t))
                        if t:
                            out = bank[CARRIED][0:WIN].rearrange("p (h k) -> p h k", h=H)
                            pe.matmul(out, identb[:, 0:WIN], spread(maskt[:, 1, 1, 0:WIN], 1, H), start=True, stop=False, skip_group_check=True)
                            for h in range(H):
                                pe.matmul(out[:, h, :], sel[:, h, 0:WIN], nmT[:, 0:WIN], start=False, stop=False, skip_group_check=True)
                                pe.matmul(out[:, h, :], kT[:, h // 4, t * P - WIN:t * P], qz[:, h, t * P:t * P + WIN],
                                          start=False, stop=True, skip_group_check=True)
                        for c in range(G):
                            out = bank[c].rearrange("p (j k) -> p j k", j=4)
                            pe.matmul(out, identb[:, :], spread(maskt[:, 1, 0, :], 1, 4), start=True, stop=False, skip_group_check=True)
                            for j in range(4):
                                h = 4 * c + j
                                pe.matmul(out[:, j, :], sel[:, h, :], nmT[:, :], start=False, stop=False, skip_group_check=True)
                                m = pe.matmul(out[:, j, :], kT[:, c, own], qz[:, h, own], start=False, stop=True, skip_group_check=True)
                            if c % 2:
                                m.then_inc(t_shifted.sem, 1)
                        for c in range(LG):
                            out = bank[SHIFT_LAT + c][0:LAT].rearrange("p (j k) -> p j k", j=4)
                            pe.matmul(out, identb[0:LAT, 0:LAT], spread(masklt[:, t, :], 1, 4), start=True, stop=False, skip_group_check=True)
                            for j in range(4):
                                h = 4 * c + j
                                pe.matmul(out[:, j, :], sel[:, H + h, 0:LAT], nmT[:, :], start=False, stop=False, skip_group_check=True)
                                m = pe.matmul(out[:, j, :], gkT[:, c, :], gqz[:, h, own], start=False, stop=True, skip_group_check=True)
                        m.then_inc(t_shifted.sem, 1)
                        for h in range(H):
                            if h % 8 == 0:
                                pe.wait_ge(t_exped.sem, t_exped.at(t, h // 8 + 1))
                            out = bank[REST][:, h * HD2:(h + 1) * HD2]
                            pe.matmul(out, pt[:, h, :], va[:, t, h, :], start=True, stop=not t, skip_group_check=True)
                            if t:
                                pe.matmul(out[0:WIN], pc[:, h, :], vc[:, t, h, :], start=False, stop=True, skip_group_check=True)
                        pe.wait_ge(t_exped.sem, t_exped.at(t, 3))
                        for h in range(LH):
                            m = pe.matmul(bank[REST][:, (H + h) * HD2:(H + h + 1) * HD2], ptl[:, h, :], gva[:, h, :], start=True, stop=True,
                                          skip_group_check=True)
                        m.then_inc(t_weighed.sem, 1)
                        if t + 1 < TPB:
                            score(t + 1)
                        pe.wait_ge(t_norm.sem, t_norm.at(t, 4))
                        pe.transpose(bank[REST][0:LAT, 256:256 + P], rem[:, :], ident[:, :]).then_inc(t_remT_up.sem, 1)
                        pe.wait_ge(t_remT_in.sem, t + 1)
                        pe.matmul(bank[REST][:, 384:384 + DIM], remT[:, :], wr[:, :], start=True, stop=True).then_inc(t_rem_up.sem, 1)
                        pe.wait_ge(t_mix.sem, t_mix.at(t, 2))
                        pe.transpose(bank[REST][:, 256:256 + P], mix[:, :], ident[:, :]).then_inc(t_mixT_up.sem, 1)
                        pe.wait_ge(t_mixT_in.sem, t + 1)
                        pe.matmul(bank[REST][:, 384:384 + DIM], mixT[:, :], wo[:, :], start=True, stop=True).then_inc(t_y_up.sem, 1)

                @block.scalar
                def _(act):
                    for t in range(TPB):
                        act.wait_ge(t_shifted.sem, t_shifted.at(t, 1))
                        if t:
                            act.wait_ge(t_weighed.sem, t_weighed.at(t - 1))
                            act.activation(pc[:, :, :].rearrange("p h k -> p (h k)"), bank[CARRIED][0:WIN], ACT.Exp)
                        for k in range(2):
                            act.wait_ge(t_shifted.sem, t_shifted.at(t, k + 1))
                            act.activation(pt[:, 8 * k:8 * k + 8, :].rearrange("p (c j) k -> p c (j k)", c=2), all8[:, 2 * k:2 * k + 2, :],
                                           ACT.Exp).then_inc(t_exped.sem, 1)
                        act.wait_ge(t_shifted.sem, t_shifted.at(t, 3))
                        act.activation(ptl[:, :, :].rearrange("p (c j) k -> p c (j k)", c=LG), all8[0:LAT, SHIFT_LAT:SHIFT_LAT + LG, :],
                                       ACT.Exp).then_inc(t_exped.sem, 1)
                        act.wait_ge(t_remT_up.sem, t + 1)
                        act.activation(remT[:, :], bank[REST][0:LAT, 256:256 + P], ACT.Copy).then_inc(t_remT_in.sem, 1)
                        act.wait_ge(t_mixT_up.sem, t + 1)
                        act.activation(mixT[:, :], bank[REST][:, 256:256 + P], ACT.Copy).then_inc(t_mixT_in.sem, 1)

                @block.vector
                def _(v):
                    def maxima(t):
                        lo = 0 if t else WIN
                        for k, (first_bank, banks, h0, per) in enumerate(GROUPS):
                            v.wait_ge(t_scored.sem, t_scored.at(t, k + 1))
                            v.tensor_reduce(nmax[:, h0:h0 + banks * per].rearrange("p (b a) -> p b a", b=banks),
                                            all8[:, first_bank:first_bank + banks, 0:per * KEYS].rearrange("p b (a k) -> p b a k", a=per)[:, :, :, lo:],
                                            X, ALU.max, negate=True).then_inc(t_maxed.sem, 1)
                        v.wait_ge(t_scored.sem, t_scored.at(t, 4))
                        v.tensor_reduce(nmax[:, H:ALL], bank[SCORE_LAT].rearrange("p (h k) -> p h k", h=LH), X, ALU.max, negate=True).then_inc(t_maxed.sem, 1)
                        v.wait_ge(t_maxed.sem, t_maxed.at(t, 4))
                        v.tensor_copy(hl[:, 0, :], nmax[:, :]).then_inc(t_split.sem, 1)
                        v.wait_ge(t_split.sem, t_split.at(t, 1))
                        v.tensor_tensor(hl[:, 1, :], nmax[:, :], hl[:, 0, :], ALU.subtract).then_inc(t_split.sem, 1)

                    maxima(0)
                    for t in range(TPB):
                        v.wait_ge(t_m_up.sem, t_m_up.at(t))
                        v.tensor_copy(nmT[:, :], bank[REST].bitcast(BF16)[0:2 * ALL, 0:P]).then_inc(t_m_in.sem, 1)
                        v.wait_ge(t_weighed.sem, t_weighed.at(t))
                        out = bank[REST][:, 0:ALL * HD2].rearrange("p (h e) -> p h e", e=HD2)
                        v.reciprocal(rden[:, :], out[:, :, HD]).then_inc(t_norm.sem, 1)
                        v.wait_ge(t_norm.sem, t_norm.at(t, 1))
                        v.tensor_tensor(rden[:, 0:H], rden[:, 0:H], gates[:, t, 0, :], ALU.mult).then_inc(t_norm.sem, 1)
                        v.wait_ge(t_norm.sem, t_norm.at(t, 2))
                        v.tensor_tensor(loc[:, :].rearrange("p (h e) -> p h e", e=HD), out[:, 0:H, 0:HD], spread(rden[:, 0:H], 2, HD), ALU.mult).then_inc(t_norm.sem, 1)
                        v.tensor_tensor(rem[:, :].rearrange("p (h e) -> p h e", e=HD), out[:, H:ALL, 0:HD], spread(rden[:, H:ALL], 2, HD), ALU.mult).then_inc(t_norm.sem, 1)
                        if t + 1 < TPB:
                            maxima(t + 1)
                        v.wait_ge(t_rem_up.sem, t + 1)
                        v.tensor_tensor(remg[:, :].rearrange("p (h e) -> p h e", e=HD), bank[REST][:, 384:384 + DIM].rearrange("p (h e) -> p h e", e=HD),
                                        spread(gates[:, t, 1, :], 2, HD), ALU.mult).then_inc(t_mix.sem, 1)
                        v.wait_ge(t_mix.sem, t_mix.at(t, 1))
                        v.tensor_tensor(mix[:, :], loc[:, :], remg[:, :], ALU.add).then_inc(t_mix.sem, 1)
                        v.wait_ge(t_y_up.sem, t + 1)
                        v.tensor_copy(s[:, bass.ds(b * TPB + t, 1), :].rearrange("p a c -> p (a c)"), bank[REST][:, 384:384 + DIM]).then_inc(t_done.sem, 1)
            st.restart()


def ffn0(nc, g, d):
    HID, BL = 352, 16
    HC = [(c, min(P, HID - c)) for c in range(0, HID, P)]
    u, ident, xn = g["u"], g["ident"], g["xn"]
    MAXN = TPB * HID
    with Stage(nc, "f0") as st:
        wgu = st.sb("wgu", [P, 2, len(HC), DIM])
        wd = st.sb("wd", [P, HID])
        wguT = st.sb("wguT", [P, 2, HID])
        wdT = st.sb("wdT", [P, len(HC), DIM])
        src = st.sb("src", [P, MAXN])
        mag = st.sb("mag", [P, MAXN])
        sgn = st.sb("sgn", [P, MAXN])
        acc = st.sb("acc", [P, MAXN])
        low = st.sb("low", [P, MAXN])
        scale = st.sb("scale", [P, MAXN // BL])
        inverse = st.sb("inverse", [P, MAXN // BL])
        xqT = st.sb("xqT", [P, SEQ])
        sil = st.sb("sil", [P, 2, HID])
        hqT = st.sb("hqT", [P, len(HC), SEQ])
        bank = [st.bank(f"bank{i}") for i in range(8)]
        loaded = st.sem("loaded")
        zeroed = st.sem("zeroed")

        STEPS = 14

        def round_fp4(v, stepped, base, signed, sign_at, n):
            a, q, lo = (z[:, 0:n] for z in (mag, acc, low))
            blk = lambda z: z.rearrange("p (k e) -> p k e", e=BL)
            sc = scale[:, 0:n // BL]
            k = base

            def step(m):
                nonlocal k
                k += 1
                m.then_inc(stepped.sem, 1)
                v.wait_ge(stepped.sem, k)

            v.wait_ge(signed.sem, sign_at)
            step(v.tensor_reduce(sc, blk(a), X, ALU.max))
            step(v.tensor_scalar(sc, sc, 1.0 / 6.0, 1e-12, ALU.mult, ALU.max))
            step(v.reciprocal(inverse[:, 0:n // BL], sc))
            step(v.tensor_tensor(blk(a), blk(a), spread(inverse[:, 0:n // BL], 2, BL), ALU.mult))
            step(v.tensor_scalar(q, a, 5.0, 2.0, ALU.is_gt, ALU.mult))
            for mid in (3.5, 2.5):
                step(v.scalar_tensor_tensor(out=q, in0=a, scalar=mid, in1=q, op0=ALU.is_gt, op1=ALU.add))
            step(v.tensor_scalar(lo, a, 1.75, None, ALU.is_gt))
            for mid in (1.25, 0.75, 0.25):
                step(v.scalar_tensor_tensor(out=lo, in0=a, scalar=mid, in1=lo, op0=ALU.is_gt, op1=ALU.add))
            step(v.scalar_tensor_tensor(out=q, in0=lo, scalar=0.5, in1=q, op0=ALU.mult, op1=ALU.add))
            step(v.tensor_tensor(q, q, sgn[:, 0:n], ALU.mult))
            step(v.tensor_tensor(blk(q), blk(q), spread(sc, 2, BL), ALU.mult))

        stepped = st.event("stepped")
        staged = st.event("staged")
        signed = st.event("signed")
        turned = st.event("turned")
        placed = st.event("placed")
        NW = 2 * len(HC) * DIM
        with nc.Block() as block:
            @block.gpsimd
            def _(pool):
                pool.memset(wgu[:, :, :, :], 0.0).then_inc(zeroed, 1)

            @block.sync
            def _(sp):
                sp.wait_ge(zeroed, 1)
                for k, name in enumerate(("gate", "up")):
                    w = d[f"L0_ffn_w_{name}"]
                    sp.dma_start(wgu[:, k, 0:2, :], w[0:2 * P, :].rearrange("(c p) n -> p c n", p=P)).then_inc(loaded, 16)
                    sp.dma_start(wgu[0:HID - 2 * P, k, 2, :], w[2 * P:HID, :]).then_inc(loaded, 16)
                sp.dma_start(wd[:, :], d["L0_ffn_w_down"]).then_inc(loaded, 16)
                sp.wait_ge(loaded, 5 * 16)

            @block.vector
            def _(v):
                v.wait_ge(loaded, 5 * 16)
                v.wait_ge(zeroed, 1)
                v.tensor_copy(src[:, 0:NW], wgu[:, :, :, :].rearrange("p a c n -> p (a c n)")).then_inc(staged.sem, 1)
                v.tensor_copy(src[:, NW:NW + HID], wd[:, :]).then_inc(staged.sem, 1)
                v.wait_ge(staged.sem, 2)
                round_fp4(v, stepped, 0, signed, 2, NW + HID)

            @block.scalar
            def _(act):
                act.wait_ge(staged.sem, 2)
                act.activation(mag[:, 0:NW + HID], src[:, 0:NW + HID], ACT.Abs).then_inc(signed.sem, 1)
                act.activation(sgn[:, 0:NW + HID], src[:, 0:NW + HID], ACT.Sign).then_inc(signed.sem, 1)
                for k in range(2):
                    act.wait_ge(turned.sem, k + 1)
                    act.activation(wguT[:, k, :], bank[k][:, 0:HID], ACT.Copy).then_inc(placed.sem, 1)
                act.wait_ge(turned.sem, 3)
                for c, (at, size) in enumerate(HC):
                    act.activation(wdT[0:size, c, :], bank[2][0:size, c * P:(c + 1) * P], ACT.Copy).then_inc(placed.sem, 1)

            @block.tensor
            def _(pe):
                pe.wait_ge(stepped.sem, STEPS)
                for k in range(2):
                    for c, (at, size) in enumerate(HC):
                        lo = (k * len(HC) + c) * DIM
                        m = pe.transpose(bank[k][:, at:at + size], acc[0:size, lo:lo + DIM], ident[0:size, 0:size])
                    m.then_inc(turned.sem, 1)
                for c, (at, size) in enumerate(HC):
                    m = pe.transpose(bank[2][0:size, c * P:c * P + P], acc[:, NW + at:NW + at + size], ident[:, :])
                m.then_inc(turned.sem, 1)
        st.restart()

        xqT_up = st.event("xqT_up")
        xqT_in = st.event("xqT_in")
        hid_up = st.event("hid_up")
        silued = st.event("silued")
        hid_in = st.event("hid_in")
        hqT_up = st.event("hqT_up")
        hqT_in = st.event("hqT_in")
        y_up = st.event("y_up")
        y_in = st.event("y_in")
        with nc.Fori(0, BATCH) as b:
            with nc.Block() as block:
                @block.vector
                def _(v):
                    v.tensor_copy(src[:, 0:TPB * DIM], xn[:, bass.ds(b * TPB, TPB), :].rearrange("p t c -> p (t c)")).then_inc(staged.sem, 1)
                    v.wait_ge(staged.sem, 1)
                    round_fp4(v, stepped, 0, signed, 2, TPB * DIM)
                    for t in range(TPB):
                        v.wait_ge(silued.sem, t + 1)
                        v.tensor_tensor(src[:, t * HID:(t + 1) * HID], sil[:, t % 2, :], bank[2 * (t % 2) + 1][:, 0:HID], ALU.mult).then_inc(hid_in.sem, 1)
                    v.wait_ge(hid_in.sem, TPB)
                    v.wait_ge(xqT_up.sem, 1)
                    round_fp4(v, stepped, STEPS, signed, 4, MAXN)
                    for t in range(TPB):
                        v.wait_ge(y_up.sem, t + 1)
                        v.tensor_copy(u[:, bass.ds(b * TPB + t, 1), :].rearrange("p a c -> p (a c)"), bank[4 + t][:, 0:DIM]).then_inc(y_in.sem, 1)

                @block.scalar
                def _(act):
                    act.wait_ge(staged.sem, 1)
                    act.activation(mag[:, 0:TPB * DIM], src[:, 0:TPB * DIM], ACT.Abs).then_inc(signed.sem, 1)
                    act.activation(sgn[:, 0:TPB * DIM], src[:, 0:TPB * DIM], ACT.Sign).then_inc(signed.sem, 1)
                    act.wait_ge(xqT_up.sem, 1)
                    act.activation(xqT[:, :], bank[4][:, :], ACT.Copy).then_inc(xqT_in.sem, 1)
                    for t in range(TPB):
                        act.wait_ge(hid_up.sem, t + 1)
                        if t >= 2:
                            act.wait_ge(hid_in.sem, t - 1)
                        act.activation(sil[:, t % 2, :], bank[2 * (t % 2)][:, 0:HID], ACT.Silu).then_inc(silued.sem, 1)
                    act.wait_ge(hid_in.sem, TPB)
                    act.activation(mag[:, :], src[:, :], ACT.Abs).then_inc(signed.sem, 1)
                    act.activation(sgn[:, :], src[:, :], ACT.Sign).then_inc(signed.sem, 1)
                    for c, (at, size) in enumerate(HC):
                        act.wait_ge(hqT_up.sem, c + 1)
                        act.activation(hqT[0:size, c, :], bank[c][0:size, :], ACT.Copy).then_inc(hqT_in.sem, 1)

                @block.tensor
                def _(pe):
                    pe.wait_ge(stepped.sem, STEPS)
                    for t in range(TPB):
                        m = pe.transpose(bank[4][:, t * P:(t + 1) * P], acc[:, t * DIM:(t + 1) * DIM], ident[:, :])
                    m.then_inc(xqT_up.sem, 1)
                    pe.wait_ge(xqT_in.sem, 1)
                    for t in range(TPB):
                        if t >= 2:
                            pe.wait_ge(hid_in.sem, t - 1)
                        pe.matmul(bank[2 * (t % 2)][:, 0:HID], xqT[:, t * P:(t + 1) * P], wguT[:, 0, :], start=True, stop=True)
                        pe.matmul(bank[2 * (t % 2) + 1][:, 0:HID], xqT[:, t * P:(t + 1) * P], wguT[:, 1, :], start=True, stop=True).then_inc(hid_up.sem, 1)
                    pe.wait_ge(stepped.sem, 2 * STEPS)
                    for c, (at, size) in enumerate(HC):
                        for t in range(TPB):
                            m = pe.transpose(bank[c][0:size, t * P:(t + 1) * P], acc[:, t * HID + at:t * HID + at + size], ident[:, :])
                        m.then_inc(hqT_up.sem, 1)
                    pe.wait_ge(hqT_in.sem, len(HC))
                    for t in range(TPB):
                        for c, (at, size) in enumerate(HC):
                            m = pe.matmul(bank[4 + t][:, 0:DIM], hqT[0:size, c, t * P:(t + 1) * P], wdT[0:size, c, :],
                                          start=(c == 0), stop=(c == len(HC) - 1))
                        m.then_inc(y_up.sem, 1)
            st.restart()


def attention1(nc, g, d):
    H, HD = 16, 64
    PAIRS = H // 2
    s, ident, identb, xnT = g["s"], g["ident"], g["identb"], g["xnT"]
    with Stage(nc, "a1") as st:
        wq = st.sb("wq", [P, H * HD])
        wk = st.sb("wk", [P, H * HD])
        wv = st.sb("wv", [P, H * HD])
        wu = st.sb("wu", [P, PAIRS, DIM])
        bu = st.sb("bu", [1, DIM])
        ones = st.sb("ones", [1, P])
        maskq = st.sb("maskq", [P, P], BF16)
        maskk = st.sb("maskk", [P, P], BF16)
        sel = st.sb("sel", [2 * H, H, P], BF16)
        xb = st.sb("xb", [P, SEQ])
        qz = st.sb("qz", [P, H, SEQ])
        kT = st.sb("kT", [P, PAIRS, SEQ])
        va = st.sb("va", [P, TPB, H, HD + 2])
        nmax = st.sb("nmax", [P, TPB, H])
        hl = st.sb("hl", [P, TPB, 2, H], BF16)
        nmT = st.sb("nmT", [2 * H, SEQ], BF16)
        pt = st.sb("pt", [P, 2, TPB, SEQ])
        rden = st.sb("rden", [P, 2, TPB])
        o = st.sb("o", [P, TPB, H * HD])
        oT = st.sb("oT", [P, 2, PAIRS, P])
        bank = [st.bank(f"bank{i}") for i in range(8)]
        loaded = st.sem("loaded")
        zeroed = st.sem("zeroed")
        xb_in = st.event("xb_in")
        NPROJ = 2 * PAIRS + 2 * TPB
        proj = st.event("proj", NPROJ)
        proj_in = st.event("proj_in")
        projv_in = st.event("projv_in")
        scored = st.event("scored")
        maxed = st.event("maxed")
        split = st.event("split")
        m_up = st.event("m_up")
        m_in = st.event("m_in")
        shifted = st.event("shifted")
        exped = st.event("exped", 3)
        weighed = st.event("weighed")
        recip = st.event("recip")
        o_in = st.event("o_in")
        oT_up = st.event("oT_up")
        oT_in = st.event("oT_in")
        y_up = st.event("y_up")
        y_in = st.event("y_in")

        with nc.Block() as block:
            @block.sync
            def _(sp):
                sp.dma_start(wq[:, :], d["L1_attn_w_q"]).then_inc(loaded, 16)
                sp.dma_start(wk[:, :], d["L1_attn_w_k"]).then_inc(loaded, 16)
                sp.dma_start(wv[:, :], d["L1_attn_w_v"]).then_inc(loaded, 16)
                sp.dma_start(wu[:, :, :], d["L1_attn_w_u"].rearrange("(c p) n -> p c n", p=P)).then_inc(loaded, 16)
                sp.dma_start(bu[:, :], d["L1_attn_b_u"].rearrange("(a n) -> a n", a=1)).then_inc(loaded, 16)
                sp.dma_start(maskq[:, :], d["c_causal"][0]).then_inc(loaded, 16)
                sp.dma_start(maskk[:, :], d["c_causal"][1]).then_inc(loaded, 16)
                sp.dma_start(sel[:, :, :], d["c_sel16"]).then_inc(loaded, 16)
                sp.wait_ge(loaded, 8 * 16)

            @block.gpsimd
            def _(pool):
                pool.memset(va[:, :, :, :], 1.0).then_inc(zeroed, 1)
                pool.memset(ones[:, :], 1.0).then_inc(zeroed, 1)
                pool.memset(qz[:, :, :], 0.0).then_inc(zeroed, 1)

        def spot(j):
            return {0: (0, 0), 1: (1, 0), 2: (2, 0), 3: (1, 3 * P)}[j]

        with nc.Fori(0, BATCH) as b:
            with nc.Block() as block:
                @block.tensor
                def _(pe):
                    pe.wait_ge(xb_in.sem, 1)
                    for n in range(NPROJ):
                        if n >= 8:
                            pe.wait_ge((proj_in, projv_in)[n % 2].sem, (n - 8) // 2 + 1)
                        if n < 2 * PAIRS:
                            w = (wq, wk)[n // PAIRS]
                            c = n % PAIRS
                            m = pe.matmul(bank[n % 8][:, :], w[:, c * P:(c + 1) * P], xb[:, :], start=True, stop=True)
                        else:
                            t, c = divmod(n - 2 * PAIRS, 2)
                            m = pe.matmul(bank[n % 8][:, :], xb[:, t * P:(t + 1) * P], wv[:, c * 512:(c + 1) * 512], start=True, stop=True)
                        m.then_inc(proj.sem, 1)
                    pe.wait_ge(proj_in.sem, NPROJ // 2)
                    pe.wait_ge(projv_in.sem, NPROJ // 2)
                    for t in range(TPB):
                        for c in range(PAIRS):
                            n = t * PAIRS + c
                            if n >= 4:
                                pe.wait_ge(maxed.sem, n - 3)
                            for p in range(2):
                                out = bank[2 * (n % 4) + p]
                                pe.matmul(out[:, 0:(t + 1) * P], qz[:, 2 * c + p, t * P:(t + 1) * P], kT[:, c, 0:(t + 1) * P],
                                          start=True, stop=False, skip_group_check=True)
                                m = pe.matmul(out[:, t * P:(t + 1) * P], identb[:, :], maskq[:, :],
                                              start=False, stop=True, skip_group_check=True)
                            m.then_inc(scored.sem, 1)
                    pe.wait_ge(split.sem, 2)
                    for t in range(TPB):
                        m = pe.transpose(bank[7][:, 0:SEQ // 2].bitcast(BF16)[0:2 * H, t * P:(t + 1) * P], hl[:, t, :, :].rearrange("p a h -> p (a h)"),
                                         identb[:, :])
                    m.then_inc(m_up.sem, 1)
                    pe.wait_ge(m_in.sem, 1)

                    def shift(h):
                        p, c = h % 2, h // 2
                        if h >= 2:
                            pe.wait_ge(exped.sem, 3 * (h - 1))
                        for j in range(TPB):
                            k, at = spot(j)
                            n = (TPB - j) * P
                            out = bank[3 * p + k][:, at:at + n]
                            pe.matmul(out, sel[:, h, :], nmT[:, j * P:SEQ], start=True, stop=False, skip_group_check=True)
                            pe.matmul(out[:, 0:P], identb[:, :], maskk[:, :], start=False, stop=False, skip_group_check=True)
                            m = pe.matmul(out, kT[:, c, j * P:(j + 1) * P], qz[:, h, j * P:SEQ],
                                          start=False, stop=True, skip_group_check=True)
                        m.then_inc(shifted.sem, 1)

                    def weigh(h):
                        pe.wait_ge(exped.sem, 3 * (h + 1))
                        if h >= 2:
                            pe.wait_ge(o_in.sem, h - 1)
                        for i in range(TPB):
                            for j in range(i + 1):
                                m = pe.matmul(bank[6 + h % 2][:, i * (HD + 2):(i + 1) * (HD + 2)], pt[:, h % 2, j, i * P:(i + 1) * P], va[:, j, h, :],
                                              start=(j == 0), stop=(j == i), skip_group_check=True)
                        m.then_inc(weighed.sem, 1)

                    for h in range(H + 1):
                        if h < H:
                            shift(h)
                        if h >= 1:
                            weigh(h - 1)
                    pe.wait_ge(o_in.sem, H)
                    for t in range(TPB):
                        for half in range(2):
                            n = 2 * t + half
                            if n >= 4:
                                pe.wait_ge(oT_in.sem, n - 3)
                            for j in range(4):
                                c = 4 * half + j
                                m = pe.transpose(bank[n % 4][:, j * P:(j + 1) * P], o[:, t, c * P:(c + 1) * P], ident[:, :])
                            m.then_inc(oT_up.sem, 1)
                        pe.wait_ge(oT_in.sem, 2 * t + 2)
                        if t >= 2:
                            pe.wait_ge(y_in.sem, t - 1)
                        for c in range(PAIRS):
                            pe.matmul(bank[4 + t % 2][:, 0:DIM], oT[:, t % 2, c, :], wu[:, c, :], start=(c == 0), stop=False)
                        pe.matmul(bank[4 + t % 2][:, 0:DIM], ones[:, :], bu[:, :], start=False, stop=True).then_inc(y_up.sem, 1)

                def evacuate(n, copy):
                    src = bank[n % 8]
                    if n < PAIRS:
                        copy(qz[0:HD, 2 * n, :], src[0:HD, :], 1.0 / HD)
                        return copy(qz[HD:P, 2 * n + 1, :], src[HD:P, :], 1.0 / HD)
                    if n < 2 * PAIRS:
                        return copy(kT[:, n - PAIRS, :], src[:, :], 1.0)
                    t, c = divmod(n - 2 * PAIRS, 2)
                    return copy(va[:, t, 8 * c:8 * c + 8, 0:HD], src[:, :].rearrange("p (h d) -> p h d", h=8), 1.0)

                @block.scalar
                def _(act):
                    act.activation(xb[:, :], xnT[:, bass.ds(b * SEQ, SEQ)], ACT.Copy).then_inc(xb_in.sem, 1)
                    for n in range(0, NPROJ, 2):
                        act.wait_ge(proj.sem, n + 1)
                        evacuate(n, lambda dst, src, k: act.activation(dst, src, ACT.Copy, scale=k)).then_inc(proj_in.sem, 1)
                    for h in range(H):
                        act.wait_ge(shifted.sem, h + 1)
                        if h >= 2:
                            act.wait_ge(weighed.sem, h - 1)
                        for js in ((0,), (1, 3), (2,)):
                            for j in js:
                                k, at = spot(j)
                                m = act.activation(pt[:, h % 2, j, j * P:SEQ], bank[3 * (h % 2) + k][:, at:at + (TPB - j) * P], ACT.Exp)
                            m.then_inc(exped.sem, 1)
                    for n in range(2 * TPB):
                        act.wait_ge(oT_up.sem, n + 1)
                        if n >= 4:
                            act.wait_ge(y_in.sem, n // 2 - 1)
                        act.activation(oT[:, (n // 2) % 2, 4 * (n % 2):4 * (n % 2) + 4, :].rearrange("p a b -> p (a b)"), bank[n % 4][:, :],
                                       ACT.Copy).then_inc(oT_in.sem, 1)

                @block.vector
                def _(v):
                    for n in range(1, NPROJ, 2):
                        v.wait_ge(proj.sem, n + 1)
                        evacuate(n, lambda dst, src, k: v.tensor_scalar(dst, src, k, None, ALU.mult)).then_inc(projv_in.sem, 1)
                    for t in range(TPB):
                        for c in range(PAIRS):
                            n = t * PAIRS + c
                            v.wait_ge(scored.sem, n + 1)
                            for p in range(2):
                                m = v.tensor_reduce(nmax[:, t, 2 * c + p:2 * c + p + 1], bank[2 * (n % 4) + p][:, 0:(t + 1) * P], X, ALU.max, negate=True)
                            m.then_inc(maxed.sem, 1)
                    v.wait_ge(maxed.sem, TPB * PAIRS)
                    v.tensor_copy(hl[:, :, 0, :], nmax[:, :, :]).then_inc(split.sem, 1)
                    v.wait_ge(split.sem, 1)
                    v.tensor_tensor(hl[:, :, 1, :], nmax[:, :, :], hl[:, :, 0, :], ALU.subtract).then_inc(split.sem, 1)
                    v.wait_ge(m_up.sem, 1)
                    v.tensor_copy(nmT[:, :], bank[7][:, 0:SEQ // 2].bitcast(BF16)[0:2 * H, :]).then_inc(m_in.sem, 1)
                    for h in range(H):
                        v.wait_ge(weighed.sem, h + 1)
                        out = bank[6 + h % 2][:, 0:TPB * (HD + 2)].rearrange("p (t e) -> p t e", t=TPB)
                        v.reciprocal(rden[:, h % 2, :], out[:, :, HD]).then_inc(recip.sem, 1)
                        v.wait_ge(recip.sem, h + 1)
                        v.tensor_tensor(o[:, :, h * HD:(h + 1) * HD], out[:, :, 0:HD], spread(rden[:, h % 2, :], 2, HD), ALU.mult).then_inc(o_in.sem, 1)
                    for t in range(TPB):
                        v.wait_ge(y_up.sem, t + 1)
                        v.tensor_copy(s[:, bass.ds(b * TPB + t, 1), :].rearrange("p a c -> p (a c)"), bank[4 + t % 2][:, 0:DIM]).then_inc(y_in.sem, 1)
            st.restart()


def ffn1(nc, g, d):
    HID, C = 512, 4
    u, xnT = g["u"], g["xnT"]
    with Stage(nc, "f1") as st:
        w1 = st.sb("w1", [P, HID])
        w2 = st.sb("w2", [P, HID])
        h1 = st.sb("h1", [P, C, HID])
        h2 = st.sb("h2", [P, C, HID])
        w3 = st.sb("w3", [P, C, DIM])
        sc = st.sb("sc", [P, 4, C])
        s3 = st.sb("s3", [P, DIM])
        xb = st.sb("xb", [P, SEQ])
        a1 = st.sb("a1", [P, C, SEQ])
        a2 = st.sb("a2", [P, C, SEQ])
        a3 = st.sb("a3", [P, C, SEQ])
        bank = [st.bank(f"bank{i}") for i in range(8)]
        loaded = st.sem("loaded")
        xb_in = st.event("xb_in")
        first = st.event("first", C)
        silued = st.event("silued", C)
        gated = st.event("gated", C)
        second = st.event("second", C)
        gelu1 = st.event("gelu1", C)
        third = st.event("third", C)
        gelu2 = st.event("gelu2", C)
        y_up = st.event("y_up", TPB)
        y_in = st.event("y_in", TPB)
        with nc.Block() as block:
            @block.sync
            def _(sp):
                sp.dma_start(w1[:, :], d["t_L1_ffn_w1_w"]).then_inc(loaded, 16)
                sp.dma_start(w2[:, :], d["t_L1_ffn_w2_w"]).then_inc(loaded, 16)
                sp.dma_start(h1[:, :, :], d["t_L1_ffn_h1_w"].rearrange("(c p) n -> p c n", p=P)).then_inc(loaded, 16)
                sp.dma_start(h2[:, :, :], d["t_L1_ffn_h2_w"].rearrange("(c p) n -> p c n", p=P)).then_inc(loaded, 16)
                sp.dma_start(w3[:, :, :], d["t_L1_ffn_w3_w"].rearrange("(c p) n -> p c n", p=P)).then_inc(loaded, 16)
                for k, name in enumerate(("w1", "w2", "h1", "h2")):
                    sp.dma_start(sc[:, k, :], d[f"L1_ffn_{name}_s"].rearrange("(c p) -> p c", p=P), allow_slow_non_contiguous=True).then_inc(loaded, 16)
                sp.dma_start(s3[:, :], d["L1_ffn_w3_s"].rearrange("(a n) -> a n", a=1).to_broadcast([P, DIM])).then_inc(loaded, 16)
                sp.wait_ge(loaded, 10 * 16)

        with nc.Fori(0, BATCH) as b:
            with nc.Block() as block:
                @block.gpsimd
                def _(pool):
                    pool.tensor_copy(xb[:, :], xnT[:, bass.ds(b * SEQ, SEQ)]).then_inc(xb_in.sem, 1)

                @block.tensor
                def _(pe):
                    pe.wait_ge(xb_in.sem, 1)
                    for c in range(C):
                        pe.matmul(bank[2 * c][:, :], w1[:, c * P:(c + 1) * P], xb[:, :], start=True, stop=True)
                        pe.matmul(bank[2 * c + 1][:, :], w2[:, c * P:(c + 1) * P], xb[:, :], start=True, stop=True).then_inc(first.sem, 1)
                    for w, src, ready, done, last in ((h1, a2, gated, second, gated), (h2, a3, gelu1, third, gelu1)):
                        pe.wait_ge(ready.sem, C)
                        for c in range(C):
                            out = bank[c if w is h1 else 4 + c]
                            for k in range(C):
                                m = pe.matmul(out[:, :], w[:, k, c * P:(c + 1) * P], src[:, k, :], start=(k == 0), stop=(k == C - 1))
                            m.then_inc(done.sem, 1)
                    pe.wait_ge(gelu2.sem, C)
                    for t in range(TPB):
                        for k in range(C):
                            m = pe.matmul(bank[t][:, 0:DIM], a2[:, k, t * P:(t + 1) * P], w3[:, k, :], start=(k == 0), stop=(k == C - 1))
                        m.then_inc(y_up.sem, 1)

                @block.scalar
                def _(act):
                    for c in range(C):
                        act.wait_ge(first.sem, c + 1)
                        act.activation(a1[:, c, :], bank[2 * c][:, :], ACT.Silu, scale=sc[:, 0, c:c + 1]).then_inc(silued.sem, 1)
                    for c in range(C):
                        act.wait_ge(second.sem, c + 1)
                        act.activation(a3[:, c, :], bank[c][:, :], ACT.Gelu, scale=sc[:, 2, c:c + 1]).then_inc(gelu1.sem, 1)
                    for c in range(C):
                        act.wait_ge(third.sem, c + 1)
                        act.activation(a2[:, c, :], bank[4 + c][:, :], ACT.Gelu, scale=sc[:, 3, c:c + 1]).then_inc(gelu2.sem, 1)

                @block.vector
                def _(v):
                    for c in range(C):
                        v.wait_ge(silued.sem, c + 1)
                        v.scalar_tensor_tensor(out=a2[:, c, :], in0=bank[2 * c + 1][:, :], scalar=sc[:, 1, c:c + 1], in1=a1[:, c, :],
                                               op0=ALU.mult, op1=ALU.mult).then_inc(gated.sem, 1)
                    for t in range(TPB):
                        v.wait_ge(y_up.sem, t + 1)
                        v.tensor_tensor(u[:, bass.ds(b * TPB + t, 1), :].rearrange("p a c -> p (a c)"), bank[t][:, 0:DIM], s3[:, :],
                                        ALU.mult).then_inc(y_in.sem, 1)
            st.restart()


def attention2(nc, g, d):
    HD, NQ, NKV = 8, 32, 8
    GH = NQ // NKV
    TOK = SEQ // NKV
    LAMBDA_INIT = 0.8 - 0.6 * float(np.exp(-0.3))
    QG, KG = 2 * DIM // HD, NKV * HD // HD
    ROWS = 9 * HD
    FG = 512 // TOK
    NF = (QG + KG) // FG
    KVB = 4
    UNITS = KVB * BATCH
    s, ident, identb, xnT = g["s"], g["ident"], g["identb"], g["xnT"]
    with Stage(nc, "a2") as st:
        w = st.sb("w", [P, 2 * DIM + 2 * NKV * HD + 32])
        w9 = st.sb("w9", [P, QG + KG, ROWS])
        wp = st.sb("wp", [P, DIM])
        lam = st.sb("lam", [P, 4, NKV * HD])
        lprod = st.sb("lprod", [P, 2, NKV * HD])
        lsum = st.sb("lsum", [P, 2])
        lexp = st.sb("lexp", [P, 2])
        nlam = st.sb("nlam", [P, 1])
        maskq = st.sb("maskq", [P, P], BF16)
        maskk = st.sb("maskk", [P, P], BF16)
        sel = st.sb("sel", [2 * GH, GH, P], BF16)
        part = st.sb("part", [ROWS, 2, 2])
        vT = st.sb("vT", [P, NKV * SEQ])
        va = st.sb("va", [P, NKV, TPB, BATCH, HD + 2])
        xs = st.sb("xs", [ROWS, 2, 512])
        x_hi = st.sb("x_hi", [ROWS, 2, 512], BF16)
        ys = st.sb("ys", [ROWS, 2, 512])
        y_hi = st.sb("y_hi", [ROWS, 2, 512], BF16)
        zs = st.sb("zs", [ROWS, 2, 512])
        q9 = st.sb("q9", [ROWS, 3, GH * SEQ], BF16)
        k9 = st.sb("k9", [ROWS, 3, SEQ], BF16)
        nmax = st.sb("nmax", [P, TPB, GH])
        hl = st.sb("hl", [P, TPB, 2, GH], BF16)
        nmT = st.sb("nmT", [2 * GH, SEQ], BF16)
        pt = st.sb("pt", [P, 2, 10 * P])
        rden = st.sb("rden", [P, 2, GH, TPB])
        on = st.sb("on", [P, 2, GH, TPB, HD])
        att = st.sb("att", [P, BATCH, TPB, DIM])
        attT = st.sb("attT", [P, SEQ])
        y1 = st.sb("y1", [P, TPB, DIM])
        y2T = st.sb("y2T", [P, SEQ])
        bank = [st.bank(f"bank{i}") for i in range(8)]
        loaded = st.sem("loaded")
        zeroed = st.sem("zeroed")
        copied = st.sem("copied")
        lamd = st.sem("lamd")
        lamx = st.sem("lamx")

        vproj = st.event("vproj")
        vg_in = st.event("vg_in")
        v_up = st.event("v_up")
        with nc.Block() as block:
            @block.gpsimd
            def _(pool):
                pool.memset(w[:, 2 * DIM + 2 * NKV * HD:], 0.0).then_inc(zeroed, 1)
                pool.memset(va[:, :, :, :, :], 1.0).then_inc(zeroed, 1)
                pool.wait_ge(loaded, 10 * 16)
                groups = w[:, 0:(QG + KG) * HD].rearrange("p (n e) -> p n e", e=HD)
                pool.tensor_copy(w9[:, :, :].rearrange("p n (c e) -> p n c e", e=HD), spread(groups, 2, ROWS // HD)).then_inc(copied, 1)

            @block.sync
            def _(sp):
                sp.dma_start(w[:, 0:2 * DIM + 2 * NKV * HD], d["L2_attn_Wqkv"]).then_inc(loaded, 16)
                sp.dma_start(wp[:, :], d["L2_attn_Wproj"]).then_inc(loaded, 16)
                for k, name in enumerate(("q1", "k1", "q2", "k2")):
                    sp.dma_start(lam[:, k, :], d[f"L2_attn_lambda_{name}"].rearrange("(a n) -> a n", a=1).to_broadcast([P, NKV * HD])).then_inc(loaded, 16)
                sp.dma_start(maskq[:, :], d["c_causal"][0]).then_inc(loaded, 16)
                sp.dma_start(maskk[:, :], d["c_causal"][1]).then_inc(loaded, 16)
                sp.dma_start(sel[:, :, :], d["c_sel4"]).then_inc(loaded, 16)
                sp.dma_start(part[:, :, :], d["c_part"]).then_inc(loaded, 16)
                sp.wait_ge(loaded, 10 * 16)

            @block.tensor
            def _(pe):
                pe.wait_ge(loaded, 10 * 16)
                pe.wait_ge(zeroed, 2)
                for n in range(KG):
                    at = (QG + KG + n) * HD
                    for b in range(BATCH):
                        m = pe.matmul(bank[n][32 * b:32 * b + 32, :], w[:, at:at + 32], xnT[:, b * SEQ:(b + 1) * SEQ],
                                      start=True, stop=True, tile_position=(0, 32 * b))
                    m.then_inc(vproj.sem, 1)
                pe.wait_ge(vg_in.sem, KG)
                for h in range(NKV):
                    for t in range(TPB):
                        m = pe.transpose(bank[h][:, t * P:(t + 1) * P], vT[:, h * SEQ + t * P:h * SEQ + (t + 1) * P], ident[:, :])
                    m.then_inc(v_up.sem, 1)

            @block.scalar
            def _(act):
                for n in range(KG):
                    act.wait_ge(vproj.sem, n + 1)
                    act.activation(vT[:, :].rearrange("p (t r) -> p t r", r=KG)[:, :, n], bank[n][:, :], ACT.Copy).then_inc(vg_in.sem, 1)
                act.wait_ge(lamd, 2)
                act.activation(lexp[:, :], lsum[:, :], ACT.Exp).then_inc(lamx, 1)

            @block.vector
            def _(v):
                v.wait_ge(loaded, 10 * 16)
                lm = lam[:, :, :].rearrange("p (a c) n -> p a c n", c=2)
                v.tensor_tensor(lprod[:, :, :], lm[:, :, 0, :], lm[:, :, 1, :], ALU.mult).then_inc(lamd, 1)
                v.wait_ge(lamd, 1)
                v.tensor_reduce(lsum[:, :], lprod[:, :, :], X, ALU.add).then_inc(lamd, 1)
                v.wait_ge(zeroed, 2)
                for h in range(NKV):
                    v.wait_ge(v_up.sem, h + 1)
                    v.tensor_copy(va[:, h, :, :, 0:HD].rearrange("p t b e -> p (t b) e"),
                                  bank[h][:, :].rearrange("p (x e) -> p x e", e=32)[:, :, 0:HD])
                v.wait_ge(lamx, 1)
                v.tensor_tensor(nlam[:, :], lexp[:, 1:2], lexp[:, 0:1], ALU.subtract).then_inc(lamd, 1)
                v.wait_ge(lamd, 3)
                v.tensor_scalar(nlam[:, :], nlam[:, :], -LAMBDA_INIT, None, ALU.add)
        st.restart()

        SCORES = [(0, 0, 4), (1, 0, 2), (1, 2, 2)] + [(t, h, 1) for t in (2, 3) for h in range(GH)]
        NS = len(SCORES)
        SHIFTS = [[(0, 0)], [(1, 0), (3, 3 * P)], [(2, 0)]]
        WIDTH = [4 * P, 4 * P, 2 * P]
        START = {j: sum(WIDTH[:k]) + at for k, tiles in enumerate(SHIFTS) for j, at in tiles}
        work, score_banks, shift_banks, out_bank = bank[0], bank[1:4], bank[4:7], bank[7]
        fill_up = st.event("fill_up", NF)
        xs_in = st.event("xs_in", NF)
        x_hi_in = st.event("x_hi_in", NF)
        ys_in = st.event("ys_in", NF)
        y_hi_in = st.event("y_hi_in", NF)
        zs_in = st.event("zs_in", NF)
        parts_in = st.event("parts_in", NF)
        scored = st.event("scored", NS)
        maxed = st.event("maxed", NS)
        split = st.event("split", 2)
        m_up = st.event("m_up", 1)
        m_in = st.event("m_in", 1)
        shifted = st.event("shifted", 3 * GH)
        exped = st.event("exped", 3 * GH)
        weighed = st.event("weighed", GH)
        recip = st.event("recip", 1)
        normed = st.event("normed", 1)
        attended = st.event("attended", 1)

        with nc.Fori(0, NKV // KVB) as i:
            with nc.Block() as block:
                @block.tensor
                def _(pe):
                    def project(u, f):
                        k, b = divmod(u, BATCH)
                        if f:
                            pe.wait_ge(xs_in.sem, xs_in.at(u, f))
                        elif u:
                            pe.wait_ge(xs_in.sem, xs_in.at(u - 1, NF))
                        if f == 0 and u >= 2:
                            pe.wait_ge(m_in.sem, m_in.at(u - 2))
                        for c in range(FG):
                            m = pe.matmul(work[0:ROWS, c * TOK:(c + 1) * TOK], w9[:, f * FG + c, :],
                                          xnT[:, bass.ds(i * (KVB * TOK) + (b * SEQ + k * TOK), TOK)], start=True, stop=True)
                        m.then_inc(fill_up.sem, 1)

                    def score(u, n):
                        t, h0, nh = SCORES[n]
                        if n == 0:
                            pe.wait_ge(parts_in.sem, parts_in.at(u, NF))
                        total = u * NS + n
                        if total >= 3:
                            pe.wait_ge(maxed.sem, total - 2)
                        keys = (t + 1) * P
                        for h in range(nh):
                            out = score_banks[total % 3][:, h * keys:(h + 1) * keys]
                            at = (h0 + h) * SEQ + t * P
                            pe.matmul(out, q9[:, u % 3, at:at + P], k9[:, u % 3, 0:keys], start=True, stop=False, skip_group_check=True)
                            m = pe.matmul(out[:, t * P:keys], identb[:, :], maskq[:, :], start=False, stop=True, skip_group_check=True)
                        m.then_inc(scored.sem, 1)

                    def turn_maxima(u):
                        pe.wait_ge(split.sem, split.at(u, 2))
                        pe.wait_ge(xs_in.sem, xs_in.at(min(u + 1, UNITS - 1), NF))
                        for t in range(TPB):
                            m = pe.transpose(work[:, 0:SEQ // 2].bitcast(BF16)[0:2 * GH, t * P:(t + 1) * P],
                                             hl[:, t, :, :].rearrange("p a h -> p (a h)"), identb[:, :])
                        m.then_inc(m_up.sem, 1)

                    def shift(u, h):
                        if h == 0:
                            pe.wait_ge(m_in.sem, m_in.at(u))
                        for k, tiles in enumerate(SHIFTS):
                            x = u * GH + h
                            if x:
                                pe.wait_ge(exped.sem, 3 * (x - 1) + k + 1)
                            for j, at in tiles:
                                n = (TPB - j) * P
                                out = shift_banks[k][:, at:at + n]
                                pe.matmul(out, sel[:, h, :], nmT[:, j * P:SEQ], start=True, stop=False, skip_group_check=True)
                                pe.matmul(out[:, 0:P], identb[:, :], maskk[:, :], start=False, stop=False, skip_group_check=True)
                                m = pe.matmul(out, k9[:, u % 3, j * P:(j + 1) * P], q9[:, u % 3, h * SEQ + j * P:(h + 1) * SEQ],
                                              start=False, stop=True, skip_group_check=True)
                            m.then_inc(shifted.sem, 1)

                    def weigh(u, h):
                        k, b = divmod(u, BATCH)
                        pe.wait_ge(exped.sem, exped.at(u, 3 * (h + 1)))
                        if h == 0 and u:
                            pe.wait_ge(normed.sem, normed.at(u - 1))
                        for q in range(TPB):
                            for j in range(q + 1):
                                at = (h * TPB + q) * (HD + 2)
                                first = START[j] + (q - j) * P
                                m = pe.matmul(out_bank[:, at:at + HD + 2], pt[:, h % 2, first:first + P],
                                              va[:, bass.ds(i * KVB + k, 1), j, b, :].rearrange("p a e -> p (a e)"),
                                              start=(j == 0), stop=(j == q), skip_group_check=True)
                        m.then_inc(weighed.sem, 1)

                    for t in range(-2, UNITS):
                        for h in range(GH + 1):
                            if t + 2 < UNITS and h < NF:
                                project(t + 2, h)
                            if t >= 0 and h < GH:
                                shift(t, h)
                            if 0 <= t + 1 < UNITS:
                                for n in range(4 * h, min(4 * h + 4, NS)):
                                    score(t + 1, n)
                            if h == GH and 0 <= t + 1 < UNITS:
                                turn_maxima(t + 1)
                            if t >= 0 and h:
                                weigh(t, h - 1)

                @block.scalar
                def _(act):
                    def part_step(u, f, step):
                        z = (u * NF + f) % 2
                        if step == 0:
                            act.wait_ge(fill_up.sem, fill_up.at(u, f + 1))
                            act.activation(xs[:, z, :], work[0:ROWS, :], ACT.Copy, scale=HD ** -0.5 if f * FG < QG else 1.0).then_inc(xs_in.sem, 1)
                            act.wait_ge(xs_in.sem, xs_in.at(u, f + 1))
                            act.activation(x_hi[:, z, :], xs[:, z, :], ACT.Copy).then_inc(x_hi_in.sem, 1)
                        elif step == 1:
                            act.wait_ge(ys_in.sem, ys_in.at(u, f + 1))
                            act.activation(y_hi[:, z, :], ys[:, z, :], ACT.Copy).then_inc(y_hi_in.sem, 1)
                        else:
                            act.wait_ge(zs_in.sem, zs_in.at(u, f + 1))
                            if u >= 3:
                                act.wait_ge(shifted.sem, shifted.at(u - 3, 3 * GH))
                            q = f * FG < QG
                            dst, groups, r = (q9[:, u % 3, :], QG, f * FG) if q else (k9[:, u % 3, :], KG, f * FG - QG)
                            act.activation(dst.rearrange("p (t r) -> p r t", r=groups)[:, r:r + FG, :],
                                           zs[:, z, :].rearrange("p (r t) -> p r t", r=FG), ACT.Copy).then_inc(parts_in.sem, 1)

                    for t in range(-2, UNITS):
                        for h in range(GH + 1):
                            for step in range(3):
                                if t + 2 < UNITS and h < NF:
                                    part_step(t + 2, h, step)
                                if t >= 0 and h < GH:
                                    act.wait_ge(shifted.sem, shifted.at(t, 3 * h + step + 1))
                                    x = t * GH + h
                                    if step == 0 and x >= 2:
                                        act.wait_ge(weighed.sem, x - 1)
                                    first = sum(WIDTH[:step])
                                    act.activation(pt[:, h % 2, first:first + WIDTH[step]], shift_banks[step][:, 0:WIDTH[step]],
                                                   ACT.Exp).then_inc(exped.sem, 1)

                @block.vector
                def _(v):
                    def rest(u, f, step):
                        z = (u * NF + f) % 2
                        total = u * NF + f
                        sign = part[:, 0 if f * FG < QG else 1, step:step + 1]
                        if step == 0:
                            v.wait_ge(x_hi_in.sem, x_hi_in.at(u, f + 1))
                            v.scalar_tensor_tensor(out=ys[:, z, :], in0=x_hi[:, z, :], scalar=sign, in1=xs[:, z, :],
                                                   op0=ALU.mult, op1=ALU.add).then_inc(ys_in.sem, 1)
                        else:
                            v.wait_ge(y_hi_in.sem, y_hi_in.at(u, f + 1))
                            if total >= 2:
                                v.wait_ge(parts_in.sem, total - 1)
                            v.scalar_tensor_tensor(out=zs[:, z, :], in0=y_hi[:, z, :], scalar=sign, in1=ys[:, z, :],
                                                   op0=ALU.mult, op1=ALU.add).then_inc(zs_in.sem, 1)

                    def maxima(u, n):
                        t, h0, nh = SCORES[n]
                        v.wait_ge(scored.sem, scored.at(u, n + 1))
                        v.tensor_reduce(nmax[:, t, h0:h0 + nh], score_banks[(u * NS + n) % 3][:, 0:nh * (t + 1) * P].rearrange("p (h k) -> p h k", h=nh),
                                        X, ALU.max, negate=True).then_inc(maxed.sem, 1)

                    def finish(u):
                        k, b = divmod(u, BATCH)
                        v.wait_ge(weighed.sem, weighed.at(u, GH))
                        out = out_bank[:, 0:GH * TPB * (HD + 2)].rearrange("p (x e) -> p x e", e=HD + 2)
                        rd = rden[:, u % 2].rearrange("p h t -> p (h t)")
                        v.reciprocal(rd, out[:, :, HD]).then_inc(recip.sem, 1)
                        v.wait_ge(recip.sem, recip.at(u))
                        v.tensor_tensor(on[:, u % 2].rearrange("p h t e -> p (h t) e"), out[:, :, 0:HD], spread(rd, 2, HD), ALU.mult).then_inc(normed.sem, 1)
                        v.wait_ge(normed.sem, normed.at(u))
                        for pair in range(2):
                            m = v.scalar_tensor_tensor(out=att[:, b, :, bass.ds(i * (KVB * 2 * HD) + (k * 2 + pair) * HD, HD)], in0=on[:, u % 2, 2 * pair + 1],
                                                       scalar=nlam[:, 0:1], in1=on[:, u % 2, 2 * pair], op0=ALU.mult, op1=ALU.add)
                        m.then_inc(attended.sem, 1)

                    for t in range(-2, UNITS + 1):
                        if t >= 1:
                            finish(t - 1)
                        for h in range(GH + 1):
                            for step in range(2):
                                if t + 2 < UNITS and h < NF:
                                    rest(t + 2, h, step)
                                if 0 <= t + 1 < UNITS:
                                    for n in range(4 * h + 2 * step, min(4 * h + 2 * step + 2, NS)):
                                        maxima(t + 1, n)
                            if h == GH - 2 and 0 <= t + 1 < UNITS:
                                v.wait_ge(maxed.sem, maxed.at(t + 1, NS))
                                v.tensor_copy(hl[:, :, 0, :], nmax[:, :, :]).then_inc(split.sem, 1)
                                v.wait_ge(split.sem, split.at(t + 1, 1))
                                v.tensor_tensor(hl[:, :, 1, :], nmax[:, :, :], hl[:, :, 0, :], ALU.subtract).then_inc(split.sem, 1)
                        if 0 <= t + 1 < UNITS:
                            v.wait_ge(m_up.sem, m_up.at(t + 1))
                            if t >= 0:
                                v.wait_ge(shifted.sem, shifted.at(t, 3 * GH))
                            v.tensor_copy(nmT[:, :], work[:, 0:SEQ // 2].bitcast(BF16)[0:2 * GH, :]).then_inc(m_in.sem, 1)
            st.restart()

        at_up = st.event("at_up")
        at_in = st.event("at_in")
        y1_up = st.event("y1_up")
        y1_in = st.event("y1_in")
        y2_up = st.event("y2_up")
        y2_in = st.event("y2_in")
        y3_up = st.event("y3_up")
        y3_in = st.event("y3_in")
        with nc.Block() as block:
            @block.tensor
            def _(pe):
                for b in range(BATCH):
                    for t in range(TPB):
                        m = pe.transpose(bank[0][:, t * P:(t + 1) * P], att[:, b, t, :], ident[:, :])
                    m.then_inc(at_up.sem, 1)
                    pe.wait_ge(at_in.sem, b + 1)
                    for t in range(TPB):
                        m = pe.matmul(bank[1][:, t * P:(t + 1) * P], attT[:, t * P:(t + 1) * P], wp[:, :], start=True, stop=True)
                    m.then_inc(y1_up.sem, 1)
                    pe.wait_ge(y1_in.sem, b + 1)
                    pe.matmul(bank[2][:, :], wp[:, :], y1[:, :, :].rearrange("p t m -> p (t m)"), start=True, stop=True).then_inc(y2_up.sem, 1)
                    pe.wait_ge(y2_in.sem, b + 1)
                    for t in range(TPB):
                        m = pe.transpose(bank[3][:, t * P:(t + 1) * P], y2T[:, t * P:(t + 1) * P], ident[:, :])
                    m.then_inc(y3_up.sem, 1)
                    pe.wait_ge(y3_in.sem, b + 1)

            @block.scalar
            def _(act):
                for b in range(BATCH):
                    act.wait_ge(at_up.sem, b + 1)
                    act.activation(attT[:, :], bank[0][:, :], ACT.Copy, scale=1.0 - LAMBDA_INIT).then_inc(at_in.sem, 1)
                    act.wait_ge(y2_up.sem, b + 1)
                    act.activation(y2T[:, :].rearrange("p (m t) -> p t m", t=TPB), bank[2][:, :].rearrange("p (t m) -> p t m", t=TPB),
                                   ACT.Copy).then_inc(y2_in.sem, 1)

            @block.vector
            def _(v):
                for b in range(BATCH):
                    v.wait_ge(y1_up.sem, b + 1)
                    v.tensor_copy(y1[:, :, :].rearrange("p t m -> p (t m)"), bank[1][:, :]).then_inc(y1_in.sem, 1)
                    v.wait_ge(y3_up.sem, b + 1)
                    v.tensor_copy(s[:, b * TPB:(b + 1) * TPB, :].rearrange("p t m -> p (t m)"), bank[3][:, :]).then_inc(y3_in.sem, 1)


def attention3(nc, g, d):
    N, T = 16, 16
    CH = SEQ // T
    R = BATCH * CH
    s, ident, xnT = g["s"], g["ident"], g["xnT"]
    with Stage(nc, "a3") as st:
        A = st.sb("A", [P, N, N])
        Bp = st.sb("Bp", [P, N])
        Cp = st.sb("Cp", [P, N])
        Dp = st.sb("Dp", [P, 1])
        wg = st.sb("wg", [P, P])
        bg = st.sb("bg", [P, 1])
        gam = st.sb("gam", [P, DIM])
        bet = st.sb("bet", [P, DIM])
        gate = st.sb("gate", [P, TILES * P])
        xg = st.sb("xg", [P, TILES * P])
        V = st.sb("V", [P, T, N])
        W = st.sb("W", [P, T + 1, N])
        h = st.sb("h", [P, T])
        h0 = st.sb("h0", [P, 1])
        pw = st.sb("pw", [P, 2, N, N])
        prod = st.sb("prod", [P, N, N, N])
        tmp = st.sb("tmp", [P, N, N])
        y = st.sb("y", [P, R, T])
        U = st.sb("U", [P, N, R])
        S = st.sb("S", [P, CH + 1, BATCH, N])
        rec = st.sb("rec", [P, BATCH, N])
        stats = st.sb("stats", [P, TPB, 6])
        mv = st.sb("mv", [P, TPB, 2])
        vare = st.sb("vare", [P, TPB])
        rstd = st.sb("rstd", [P, TPB])
        ln = st.sb("ln", [P, TPB, DIM])
        bank = [st.bank(f"bank{i}") for i in range(8)]
        loaded = st.sem("loaded")

        gated_up = st.event("gated_up")
        sig_in = st.event("sig_in")
        xg_in = st.event("xg_in")
        did = st.event("did")
        powd = st.event("powd")
        with nc.Block() as block:
            @block.sync
            def _(sp):
                sp.dma_start(A[:, :, :], d["L3_attn_A"]).then_inc(loaded, 16)
                sp.dma_start(Bp[:, :], d["L3_attn_Bp"]).then_inc(loaded, 16)
                sp.dma_start(Cp[:, :], d["L3_attn_Cp"]).then_inc(loaded, 16)
                sp.dma_start(Dp[:, :], d["L3_attn_Dp"].rearrange("(p a) -> p a", a=1)).then_inc(loaded, 16)
                sp.dma_start(wg[:, :], d["t_L3_attn_Wg"]).then_inc(loaded, 16)
                sp.dma_start(bg[:, :], d["L3_attn_bg"].rearrange("(p a) -> p a", a=1)).then_inc(loaded, 16)
                sp.dma_start(gam[:, :], d["L3_attn_gamma"].rearrange("(a n) -> a n", a=1).to_broadcast([P, DIM])).then_inc(loaded, 16)
                sp.dma_start(bet[:, :], d["L3_attn_beta"].rearrange("(a n) -> a n", a=1).to_broadcast([P, DIM])).then_inc(loaded, 16)
                sp.wait_ge(loaded, 8 * 16)

            @block.tensor
            def _(pe):
                pe.wait_ge(loaded, 8 * 16)
                for b in range(BATCH):
                    pe.matmul(bank[b][:, :], wg[:, :], xnT[:, b * SEQ:(b + 1) * SEQ], start=True, stop=True).then_inc(gated_up.sem, 1)

            @block.scalar
            def _(act):
                for b in range(BATCH):
                    act.wait_ge(gated_up.sem, b + 1)
                    act.activation(gate[:, b * SEQ:(b + 1) * SEQ], bank[b][:, :], ACT.Sigmoid, bias=bg[:, :]).then_inc(sig_in.sem, 1)

            @block.gpsimd
            def _(pool):
                pool.wait_ge(loaded, 8 * 16)
                for b in range(BATCH):
                    pool.wait_ge(sig_in.sem, b + 1)
                    if b:
                        pool.wait_ge(xg_in.sem, b)
                    pool.tensor_tensor(xg[:, b * SEQ:(b + 1) * SEQ], xnT[:, b * SEQ:(b + 1) * SEQ], gate[:, b * SEQ:(b + 1) * SEQ],
                                       ALU.mult).then_inc(xg_in.sem, 1)

            @block.vector
            def _(v):
                n = 0

                def step(m):
                    nonlocal n
                    n += 1
                    m.then_inc(did.sem, 1)
                    v.wait_ge(did.sem, n)

                v.wait_ge(loaded, 8 * 16)
                At = A[:, :, :].rearrange("p n m -> p m n")
                step(v.tensor_copy(V[:, 0, :], Bp[:, :]))
                step(v.tensor_copy(W[:, 0, :], Cp[:, :]))
                for k in range(1, T + 1):
                    if k < T:
                        step(v.tensor_tensor(tmp[:, :, :], At, spread(V[:, k - 1, :], 1, N), ALU.mult))
                        step(v.tensor_reduce(V[:, k, :], tmp[:, :, :], X, ALU.add))
                    step(v.tensor_tensor(tmp[:, :, :], A[:, :, :], spread(W[:, k - 1, :], 1, N), ALU.mult))
                    step(v.tensor_reduce(W[:, k, :], tmp[:, :, :], X, ALU.add))
                step(v.tensor_tensor(tmp[:, :, :], V[:, :, :], spread(Cp[:, :], 1, T), ALU.mult))
                step(v.tensor_reduce(h[:, :], tmp[:, :, :], X, ALU.add))
                src = A
                for k in range(4):
                    a = A[:, :, :] if k == 0 else pw[:, (k - 1) % 2]
                    step(v.tensor_tensor(prod[:, :, :, :], spread(a, 2, N), spread(a.rearrange("p n m -> p m n"), 1, N), ALU.mult))
                    step(v.tensor_reduce(pw[:, k % 2], prod[:, :, :, :], X, ALU.add))
                step(v.tensor_scalar(h0[:, :], h[:, 0:1], Dp[:, 0:1], 1.0, ALU.add, ALU.add))
                v.wait_ge(xg_in.sem, BATCH)
                x = xg[:, :].rearrange("p (r t) -> p r t", t=T)
                step(v.tensor_scalar(y[:, :, :], x, h0[:, 0:1], None, ALU.mult))
                for k in range(1, T):
                    step(v.scalar_tensor_tensor(out=y[:, :, k:T], in0=x[:, :, 0:T - k], scalar=h[:, k:k + 1], in1=y[:, :, k:T],
                                                op0=ALU.mult, op1=ALU.add))
                step(v.memset(S[:, 0, :, :], 0.0))
        st.restart()

        added = st.event("added")
        with nc.Fori(0, N // 2) as m:
            with nc.Block() as block:
                @block.vector
                def _(v):
                    x = xg[:, :].rearrange("p (r t) -> p r t", t=T)
                    for j in range(T):
                        if j:
                            v.wait_ge(added.sem, j)
                        for k in range(2):
                            out = U[:, bass.ds(2 * m + k, 1), :].rearrange("p a r -> p (a r)")
                            vk = V[:, T - 1 - j, bass.ds(2 * m + k, 1)]
                            if j == 0:
                                i = v.tensor_scalar(out, x[:, :, j], vk, None, ALU.mult)
                            else:
                                i = v.scalar_tensor_tensor(out=out, in0=x[:, :, j], scalar=vk, in1=out, op0=ALU.mult, op1=ALU.add)
                        i.then_inc(added.sem, 1)
            st.restart()

        multiplied = st.event("multiplied", 3)
        UNROLL = 4
        with nc.Fori(0, CH // UNROLL) as c:
            with nc.Block() as block:
                @block.vector
                def _(v):
                    last = pw[:, 1]
                    Uc = U[:, :, :].rearrange("p n (b c) -> p c b n", b=BATCH)
                    for k in range(UNROLL):
                        if k:
                            v.wait_ge(multiplied.sem, 3 * k)
                        now = S[:, bass.ds(UNROLL * c + k, 1), :, :].rearrange("p a b n -> p (a b) n")
                        nxt = S[:, bass.ds(UNROLL * c + k + 1, 1), :, :].rearrange("p a b n -> p (a b) n")
                        v.tensor_tensor(prod[:, 0:BATCH, :, :], spread(now, 2, N), spread(last.rearrange("p n m -> p m n"), 1, BATCH),
                                        ALU.mult).then_inc(multiplied.sem, 1)
                        v.wait_ge(multiplied.sem, 3 * k + 1)
                        v.tensor_reduce(rec[:, :, :], prod[:, 0:BATCH, :, :], X, ALU.add).then_inc(multiplied.sem, 1)
                        v.wait_ge(multiplied.sem, 3 * k + 2)
                        v.tensor_tensor(nxt, rec[:, :, :], Uc[:, bass.ds(UNROLL * c + k, 1), :, :].rearrange("p a b n -> p (a b) n"), ALU.add).then_inc(multiplied.sem, 1)
            st.restart()

        with nc.Fori(0, T // 2) as i:
            with nc.Block() as block:
                @block.vector
                def _(v):
                    yv = y[:, :, :].rearrange("p (b c) t -> p b c t", b=BATCH)
                    Sv = S[:, 0:CH, :, :].rearrange("p c b n -> p b c n")
                    for n in range(N):
                        if n:
                            v.wait_ge(added.sem, n)
                        for k in range(2):
                            out = yv[:, :, :, bass.ds(2 * i + k, 1)].rearrange("p b c a -> p b (c a)")
                            m = v.scalar_tensor_tensor(out=out, in0=Sv[:, :, :, n], scalar=W[:, bass.ds(2 * i + k + 1, 1), n],
                                                       in1=out, op0=ALU.mult, op1=ALU.add)
                        m.then_inc(added.sem, 1)
            st.restart()

        yT_up = st.event("yT_up")
        stepped = st.event("stepped")
        rooted = st.event("rooted")
        with nc.Fori(0, BATCH) as b:
            with nc.Block() as block:
                @block.gpsimd
                def _(pool):
                    pool.tensor_copy(gate[:, 0:SEQ], y[:, bass.ds(b * CH, CH), :].rearrange("p r t -> p (r t)")).then_inc(powd.sem, 1)
                    pool.wait_ge(stepped.sem, 3)
                    pool.tensor_tensor(rstd[:, :], vare[:, :], g["half"][:, 0:TPB], ALU.pow).then_inc(rooted.sem, 1)

                @block.tensor
                def _(pe):
                    pe.wait_ge(powd.sem, 1)
                    for t in range(TPB):
                        m = pe.transpose(bank[0][:, t * P:(t + 1) * P], gate[:, t * P:(t + 1) * P], ident[:, :])
                    m.then_inc(yT_up.sem, 1)

                @block.vector
                def _(v):
                    v.wait_ge(yT_up.sem, 1)
                    for t in range(TPB):
                        m = v.bn_stats(stats[:, t, :], bank[0][:, t * P:(t + 1) * P])
                    m.then_inc(stepped.sem, 1)
                    v.wait_ge(stepped.sem, 1)
                    for t in range(TPB):
                        m = v.bn_aggr(mv[:, t, :], stats[:, t, :])
                    m.then_inc(stepped.sem, 1)
                    v.wait_ge(stepped.sem, 2)
                    v.tensor_scalar(vare[:, :], mv[:, :, 1], LN_EPS, None, ALU.add).then_inc(stepped.sem, 1)
                    v.wait_ge(rooted.sem, 1)
                    for t in range(TPB):
                        m = v.tensor_scalar(ln[:, t, :], bank[0][:, t * P:(t + 1) * P], mv[:, t, 0:1], rstd[:, t:t + 1], ALU.subtract, ALU.mult)
                    m.then_inc(stepped.sem, 1)
                    v.wait_ge(stepped.sem, 4)
                    v.tensor_tensor(ln[:, :, :], ln[:, :, :], spread(gam[:, :], 1, TPB), ALU.mult).then_inc(stepped.sem, 1)
                    v.wait_ge(stepped.sem, 5)
                    v.tensor_tensor(s[:, bass.ds(b * TPB, TPB), :], ln[:, :, :], spread(bet[:, :], 1, TPB), ALU.add).then_inc(stepped.sem, 1)
            st.restart()


def program(nc, dram, out):
    with ExitStack() as ctx:
        def keep(name, shape, dt=F32):
            return ctx.enter_context(nc.sbuf_tensor(name, shape, dt))

        g = {
            "x": keep("x", [P, TILES, DIM]),
            "xn": keep("xn", [P, TILES, DIM]),
            "xnT": keep("xnT", [P, TILES * P]),
            "s": keep("s", [P, TILES, DIM]),
            "u": keep("u", [P, TILES, DIM]),
            "half": keep("half", [P, 32]),
            "ident": keep("ident", [P, P]),
            "identb": keep("identb", [P, P], BF16),
        }
        load_inputs(nc, g, dram)
        for layer in range(4):
            layer_norm(nc, g, f"norm{layer}")
            ATTENTION[layer](nc, g, dram)
            FFN[layer](nc, g, dram)
            combine(nc, g, f"combine{layer}")
        store_output(nc, g, out)


def copy_xn(nc, g, name):
    with Stage(nc, name) as st:
        with nc.Block() as block:

            @block.vector
            def _(v):
                v.tensor_copy(g["u"][:, :, :], g["xn"][:, :, :])


def ffn2(nc, g, d):
    copy_xn(nc, g, "copy2")
    transformer(nc, g, d, "t2", 6, 16, 32, 341, d["L2_ffn_Wqkv"], d["L2_ffn_q_scale"], d["L2_ffn_k_scale"], d["L2_ffn_Wo"],
                d["L2_ffn_ln_g"], d["L2_ffn_ln_b"], d["L2_ffn_W1"], d["L2_ffn_b1"], d["L2_ffn_W2"], d["L2_ffn_b2"])


def ffn3(nc, g, d):
    copy_xn(nc, g, "copy3")
    transformer(nc, g, d, "t3", 2, 8, 64, 341, d["L3_ffn_wqkv"], d["L3_ffn_q_scale"], d["L3_ffn_k_scale"], d["L3_ffn_wo"],
                d["L3_ffn_ln_g"], d["L3_ffn_ln_b"], d["L3_ffn_w1"], d["L3_ffn_b1"], d["L3_ffn_w2"], d["L3_ffn_b2"])


ATTENTION = [attention0, attention1, attention2, attention3]
FFN = [ffn0, ffn1, ffn2, ffn3]


def rotary_table(window):
    half = np.arange(0, 64, 2, dtype=np.float32)
    inv_freq = (1.0 / np.float32(10000.0) ** (half / 64)).astype(np.float32)
    t = np.arange(SEQ, dtype=np.float32)
    freqs = t[:, None] * inv_freq[None, :]
    freqs = np.concatenate([freqs, freqs], -1)
    base = ((half + np.float32(0.4 * 64)) / np.float32(1.4 * 64)).astype(np.float32)
    power = (t - SEQ // 2) / np.float32(window // 2)
    scale = (base[None, :] ** power[:, None]).astype(np.float32)
    scale = np.concatenate([scale, scale], -1)
    cos, sin = np.cos(freqs), np.sin(freqs)
    sin = np.concatenate([-sin[:, :32], sin[:, 32:]], -1)
    tab = np.stack([cos * scale * 8, sin * scale * 8, cos / scale, sin / scale])
    return np.ascontiguousarray(tab.reshape(4, TPB, P, 64).transpose(2, 0, 1, 3).astype(np.float32))


def band_masks(window, first):
    q = np.arange(P)[:, None]
    k = np.arange(window + P)[None, :] - window
    ok = (k <= q) & (k >= q - first)
    tiles = []
    for i in range(2):
        m = ok & (k >= 0) if i == 0 else ok
        tiles.append(np.where(m, 0.0, MASKED))
    m = np.stack(tiles, 1).astype(np.dtype("bfloat16"))
    mt = np.zeros((P, 2, 2, P), m.dtype)
    mt[:, :, 0] = m[:, :, window:].transpose(2, 1, 0)
    mt[:window, :, 1] = m[:, :, :window].transpose(2, 1, 0)
    return m, mt


def shape_constants():
    bf = np.dtype("bfloat16")
    c = {"c_ident": np.eye(P, dtype=np.float32), "c_identb": np.eye(P, dtype=np.float32).astype(bf)}
    for window in (32, 64):
        c[f"c_rot{window}"] = rotary_table(window)
        c[f"c_mask{window}"], c[f"c_maskt{window}"] = band_masks(window, window)
        k, q = np.arange(P)[:, None] - P, np.arange(window)[None, :]
        c[f"c_maskp{window}"] = np.where(k >= q - window, 0.0, MASKED).astype(bf)
    c["c_mask31"], c["c_maskt31"] = band_masks(32, 31)
    q, n, t = np.arange(P)[:, None, None], np.arange(64)[None, None, :], np.arange(TPB)[None, :, None]
    latent = np.where(n <= (t * P + q) // 8, 0.0, MASKED)
    c["c_maskl"] = latent.astype(bf)
    c["c_masklt"] = np.ascontiguousarray(latent.transpose(2, 1, 0)).astype(bf)
    q, k = np.arange(P)[:, None], np.arange(P)[None, :]
    c["c_causal"] = np.stack([np.where(k <= q, 0.0, MASKED), np.where(q <= k, 0.0, MASKED)]).astype(bf)
    for heads in (4, 8, 16, 24):
        sel = np.zeros((2, heads, heads, P), np.float32)
        for h in range(heads):
            sel[:, h, h, :] = 1.0
        c[f"c_sel{heads}"] = sel.reshape(2 * heads, heads, P).astype(bf)
    row = np.arange(72)
    of = np.stack([row // 24, row // 8 % 3], 1)
    c["c_part"] = -np.stack([of >= 1, of == 2], -1).astype(np.float32)
    return c


TRANSPOSED = ["L3_attn_Wg", "L1_ffn_w1_w", "L1_ffn_w2_w", "L1_ffn_h1_w", "L1_ffn_h2_w", "L1_ffn_w3_w"]


def kernel(**inputs):
    import concourse.bacc as _bacc
    from concourse.bass_utils import run_bass_kernel_spmd as _run

    nc = _bacc.Bacc("TRN2", target_bir_lowering=False, num_devices=1)
    arrays, dram = {}, {}
    for name in list(inputs):
        a = np.ascontiguousarray(inputs[name])
        arrays[f"in_{name}"] = a
        dram[name] = nc.dram_tensor(f"in_{name}", a.shape, mybir.dt.from_np(a.dtype), kind="ExternalInput").ap()
    for name in TRANSPOSED:
        arrays[f"t_{name}"] = a = np.ascontiguousarray(inputs[name].T)
        dram[f"t_{name}"] = nc.dram_tensor(f"t_{name}", a.shape, mybir.dt.from_np(a.dtype), kind="ExternalInput").ap()
    for name, a in shape_constants().items():
        arrays[name] = a
        dram[name] = nc.dram_tensor(name, a.shape, mybir.dt.from_np(a.dtype), kind="ExternalInput").ap()
    out = nc.dram_tensor("out_0_dram", (BATCH, SEQ, DIM), F32, kind="ExternalOutput").ap()
    program(nc, dram, out)
    r = _run(nc, [arrays], core_ids=[0])
    return r.results[0]["out_0_dram"]
```
